# Optimizing a Trainium2 kernel written in Bass

```python
import numpy as np
import jax
import jax.numpy as jnp

def _softmax(x, axis=-1):
    return jax.nn.softmax(x, axis=axis)

def _gelu(x):
    return jax.nn.gelu(x, approximate=True)

def _silu(x):
    return jax.nn.silu(x)

def _sigmoid(x):
    return jax.nn.sigmoid(x)

def _layernorm(x, axis=-1, eps=1e-05):
    m = jnp.mean(x, axis=axis, keepdims=True)
    v = jnp.var(x, axis=axis, keepdims=True)
    return (x - m) / jnp.sqrt(v + eps)

def _scatter_add(tgt, idx, src, axis=0):
    return tgt.at[idx].add(src)

def _segment_sum(src, seg, n):
    return jax.ops.segment_sum(src, seg, n)
kernel_name = 'mk_lm_tower_d4_tok_ids256_r4_4acf28'

def setup_inputs(seed: int=0):
    np.random.seed(seed)
    _w = jnp.asarray

    def _rec_inputs():
        import jax
        import jax.numpy as jnp
        _rk = jax.random.key(seed)
        x = jax.random.randint(jax.random.fold_in(_rk, 1), (64, 128), 0, 64, jnp.int32)
        return x
    x = _rec_inputs()

    def _L0_tok_setup():
        import jax, jax.numpy as jnp
        import numpy as np
        PRIME = 31
        VOCAB = 125000
        NGRAM_SIZES = (2, 3, 4)

        def _ngram_hash(byte_ids, n):
            T = byte_ids.shape[1]
            powers = PRIME ** jnp.arange(n - 1, -1, -1, dtype=jnp.int64) % VOCAB
            windows = jnp.stack([byte_ids[:, i:T - n + 1 + i] for i in range(n)], axis=-1)
            return (windows.astype(jnp.int64) * powers).sum(axis=-1) % VOCAB
        key = jax.random.key(seed)
        k0, k1, k2, k3 = jax.random.split(key, 4)
        byte_ids = jax.random.randint(k0, (8, 1024), 0, 64, dtype=jnp.int64)
        emb_2 = jax.random.normal(k1, (VOCAB, 64), dtype=jnp.float32)
        emb_3 = jax.random.normal(k2, (VOCAB, 64), dtype=jnp.float32)
        emb_4 = jax.random.normal(k3, (VOCAB, 64), dtype=jnp.float32)
        return {'byte_ids': byte_ids, 'emb_2': emb_2, 'emb_3': emb_3, 'emb_4': emb_4}
    _L0_tok_all = _L0_tok_setup()
    _L0_tok_in = {k: v for k, v in _L0_tok_all.items() if k in ('emb_2', 'emb_3', 'emb_4')}
    del _L0_tok_all

    def _L0_attn_setup():
        import jax, jax.numpy as jnp
        import numpy as np
        H = 8
        key = jax.random.key(seed)
        ks = jax.random.split(key, 10)
        B, N, D, E = (1, 1024, 64, 16384)
        s = 0.02
        return {'x': jax.random.normal(ks[0], (B, N, D), jnp.float32), 'edge_index': jax.random.randint(ks[1], (2, E), 0, N, jnp.int32), 'edge_attr': jax.random.normal(ks[2], (E, 3), jnp.float32), 'Wq': jax.random.normal(ks[3], (D, D), jnp.float32) * s, 'bq': jnp.zeros((D,), jnp.float32), 'Wk': jax.random.normal(ks[4], (D, D), jnp.float32) * s, 'bk': jnp.zeros((D,), jnp.float32), 'Wv': jax.random.normal(ks[5], (D, D), jnp.float32) * s, 'bv': jnp.zeros((D,), jnp.float32), 'Wo': jax.random.normal(ks[6], (D, D), jnp.float32) * s, 'bo': jnp.zeros((D,), jnp.float32), 'We': jax.random.normal(ks[7], (3, H), jnp.float32) * s, 'be': jnp.zeros((H,), jnp.float32)}
    _L0_attn_all = _L0_attn_setup()
    _L0_attn_in = {k: v for k, v in _L0_attn_all.items() if k in ('edge_index', 'edge_attr', 'Wq', 'bq', 'Wk', 'bk', 'Wv', 'bv', 'Wo', 'bo', 'We', 'be')}
    del _L0_attn_all

    def _L0_ffn_setup():
        import jax, jax.numpy as jnp
        import numpy as np
        DIM = 64
        H = 8
        D = 64
        G = 64
        INNER = H * D
        SCALE = D ** (-0.5)
        key = jax.random.key(seed)
        ks = jax.random.split(key, 12)
        B, N = (4, 4096)
        x = jax.random.normal(ks[0], (B, N, DIM), dtype=jnp.float32)
        s = lambda fan_in: 1.0 / np.sqrt(fan_in)
        W_fx = jax.random.normal(ks[1], (DIM, INNER), dtype=jnp.float32) * s(DIM)
        b_fx = jnp.zeros((INNER,), dtype=jnp.float32)
        W_x = jax.random.normal(ks[2], (DIM, INNER), dtype=jnp.float32) * s(DIM)
        b_x = jnp.zeros((INNER,), dtype=jnp.float32)
        A = jax.random.normal(ks[3], (G, D), dtype=jnp.float32)
        Q, _ = jnp.linalg.qr(A.T)
        W_slice = Q[:, :G].astype(jnp.float32)
        b_slice = jnp.zeros((G,), dtype=jnp.float32)
        W_q = jax.random.normal(ks[4], (D, D), dtype=jnp.float32) * s(D)
        W_k = jax.random.normal(ks[5], (D, D), dtype=jnp.float32) * s(D)
        W_v = jax.random.normal(ks[6], (D, D), dtype=jnp.float32) * s(D)
        W_out = jax.random.normal(ks[7], (INNER, DIM), dtype=jnp.float32) * s(INNER)
        b_out = jnp.zeros((DIM,), dtype=jnp.float32)
        temperature = jnp.ones((1, H, 1, 1), dtype=jnp.float32) * 0.5
        return {'x': x, 'W_fx': W_fx, 'b_fx': b_fx, 'W_x': W_x, 'b_x': b_x, 'W_slice': W_slice, 'b_slice': b_slice, 'W_q': W_q, 'W_k': W_k, 'W_v': W_v, 'W_out': W_out, 'b_out': b_out, 'temperature': temperature}
    _L0_ffn_all = _L0_ffn_setup()
    _L0_ffn_in = {k: v for k, v in _L0_ffn_all.items() if k in ('W_fx', 'b_fx', 'W_x', 'b_x', 'W_slice', 'b_slice', 'W_q', 'W_k', 'W_v', 'W_out', 'b_out', 'temperature')}
    del _L0_ffn_all

    def _L1_attn_setup():
        import jax, jax.numpy as jnp
        import numpy as np
        BS = 32
        NUM_HOPS = 1

        def _connectivity(edge_index, edge_values, positions, nb):
            rows, cols = (edge_index[0], edge_index[1])
            br, bc = (rows // BS, cols // BS)
            in_block = (br == bc) & (br < nb)
            r_l, c_l = (rows % BS, cols % BS)
            b_safe = jnp.where(in_block, br, nb)
            dx = positions[cols] - positions[rows]
            ef_flat = jnp.concatenate([dx, edge_values[:, None]], axis=1)
            adj = jnp.zeros((nb, BS, BS), jnp.float32).at[b_safe, r_l, c_l].set(1.0, mode='drop')
            eye = jnp.eye(BS, dtype=jnp.float32)
            reachable = jnp.broadcast_to(eye[None], (nb, BS, BS))
            cur = adj
            for _ in range(NUM_HOPS):
                reachable = jnp.clip(reachable + cur, 0.0, 1.0)
                cur = jnp.matmul(cur, adj)
            attn_mask = jnp.concatenate([reachable, jnp.ones((nb, BS, 1), jnp.float32)], axis=2)
            edge_feats = jnp.zeros((nb, BS, BS + 1, 4), jnp.float32)
            edge_feats = edge_feats.at[b_safe, r_l, c_l, :].set(ef_flat, mode='drop')
            return (attn_mask, edge_feats)
        key = jax.random.key(seed)
        ks = jax.random.split(key, 10)
        B, N, C, H = (1, 32768, 64, 4)
        E = 8 * N
        x = jax.random.normal(ks[0], (B, N, C), dtype=jnp.float32)
        rows = jax.random.randint(ks[1], (E,), 0, N)
        offs = jax.random.randint(ks[2], (E,), 0, BS)
        cols = rows // BS * BS + offs
        edge_index = jnp.stack([rows, cols]).astype(jnp.int64)
        edge_values = jax.random.normal(ks[3], (E,), dtype=jnp.float32)
        positions = jax.random.uniform(ks[4], (N, 3), dtype=jnp.float32)
        qkv_w = jax.random.normal(ks[5], (3 * C, C), dtype=jnp.float32) * 0.02
        qkv_b = jnp.zeros((3 * C,), dtype=jnp.float32)
        proj_w = jax.random.normal(ks[6], (C, C), dtype=jnp.float32) * 0.02
        proj_b = jnp.zeros((C,), dtype=jnp.float32)
        gate_w = jax.random.normal(ks[7], (H, 4), dtype=jnp.float32) * 0.01
        gate_b = jnp.zeros((H,), dtype=jnp.float32)
        return {'x': x, 'edge_index': edge_index, 'edge_values': edge_values, 'positions': positions, 'qkv_w': qkv_w, 'qkv_b': qkv_b, 'proj_w': proj_w, 'proj_b': proj_b, 'gate_w': gate_w, 'gate_b': gate_b}
    _L1_attn_all = _L1_attn_setup()
    _L1_attn_in = {k: v for k, v in _L1_attn_all.items() if k in ('edge_index', 'edge_values', 'positions', 'qkv_w', 'qkv_b', 'proj_w', 'proj_b', 'gate_w', 'gate_b')}
    del _L1_attn_all

    def _L1_ffn_setup():
        import jax, jax.numpy as jnp
        import numpy as np
        B, S, H, NH, NE = (4, 256, 64, 4, 4)
        D = H // NH
        EPS = 1e-08

        def layernorm(x, g, b):
            m = jnp.mean(x, axis=-1, keepdims=True)
            v = jnp.mean((x - m) ** 2, axis=-1, keepdims=True)
            return (x - m) / jnp.sqrt(v + EPS) * g + b
        key = jax.random.key(seed)
        ks = jax.random.split(key, 18)
        sc = 0.05
        return {'x': jax.random.normal(ks[0], (B, S, H), jnp.float32), 'hl_w': jax.random.normal(ks[1], (NH, D, H), jnp.float32) * sc, 'hl_b': jax.random.normal(ks[2], (NH, D), jnp.float32) * sc, 'wq': jax.random.normal(ks[3], (NH, NE, D, D), jnp.float32) * sc, 'wk': jax.random.normal(ks[4], (NH, D, D), jnp.float32) * sc, 'wv': jax.random.normal(ks[5], (NH, D, D), jnp.float32) * sc, 'gate_w': jax.random.normal(ks[6], (NH, NE, NE * D), jnp.float32) * sc, 'gate_b': jax.random.normal(ks[7], (NH, NE), jnp.float32) * sc, 'ln_g': jnp.ones((D,), jnp.float32), 'ln_b': jnp.zeros((D,), jnp.float32), 'fc1_w': jax.random.normal(ks[8], (D, D), jnp.float32) * sc, 'fc1_b': jax.random.normal(ks[9], (D,), jnp.float32) * sc, 'fc2_w': jax.random.normal(ks[10], (D, D), jnp.float32) * sc, 'fc2_b': jax.random.normal(ks[11], (D,), jnp.float32) * sc, 'fnorm_g': jnp.ones((D,), jnp.float32), 'fnorm_b': jnp.zeros((D,), jnp.float32), 'fgate_w': jax.random.normal(ks[12], (NH, H), jnp.float32) * sc}
    _L1_ffn_all = _L1_ffn_setup()
    _L1_ffn_in = {k: v for k, v in _L1_ffn_all.items() if k in ('hl_w', 'hl_b', 'wq', 'wk', 'wv', 'gate_w', 'gate_b', 'ln_g', 'ln_b', 'fc1_w', 'fc1_b', 'fc2_w', 'fc2_b', 'fnorm_g', 'fnorm_b', 'fgate_w')}
    del _L1_ffn_all

    def _L2_attn_setup():
        import jax, jax.numpy as jnp
        import numpy as np
        IN_CH, OUT_CH, HEADS, DIM = (64, 64, 8, 64)

        def _xavier(key, shape, fan_in, fan_out):
            upper = np.sqrt(6.0) / np.sqrt(float(fan_in + fan_out))
            return jax.random.uniform(key, shape, jnp.float32) * (2.0 * upper) - upper
        key = jax.random.key(seed)
        kf, kq, kk, kv, ko = jax.random.split(key, 5)
        features = jax.random.normal(kf, (8, 256, IN_CH), jnp.float32)
        weight_q = _xavier(kq, (IN_CH, HEADS, DIM), IN_CH, HEADS * DIM)
        weight_k = _xavier(kk, (IN_CH, HEADS, DIM), IN_CH, HEADS * DIM)
        weight_v = _xavier(kv, (IN_CH, HEADS, DIM), IN_CH, HEADS * DIM)
        weight_out = _xavier(ko, (OUT_CH, HEADS, DIM), HEADS * DIM, OUT_CH)
        return {'features': features, 'weight_q': weight_q, 'weight_k': weight_k, 'weight_v': weight_v, 'weight_out': weight_out}
    _L2_attn_all = _L2_attn_setup()
    _L2_attn_in = {k: v for k, v in _L2_attn_all.items() if k in ('weight_q', 'weight_k', 'weight_v', 'weight_out')}
    del _L2_attn_all

    def _L2_ffn_setup():
        import jax, jax.numpy as jnp
        import numpy as np
        B, S, D, F, E, K = (8, 512, 64, 256, 8, 2)
        key = jax.random.key(seed)
        ks = jax.random.split(key, 10)
        s = 0.02
        return {'x': jax.random.normal(ks[0], (B, S, D), dtype=jnp.float32), 'Wr': jax.random.normal(ks[1], (D, E), dtype=jnp.float32) * s, 'W1s': jax.random.normal(ks[2], (D, F), dtype=jnp.float32) * s, 'b1s': jnp.zeros((F,), dtype=jnp.float32), 'W2s': jax.random.normal(ks[3], (F, D), dtype=jnp.float32) * s, 'b2s': jnp.zeros((D,), dtype=jnp.float32), 'W1p': jax.random.normal(ks[4], (E, D, F), dtype=jnp.float32) * s, 'b1p': jnp.zeros((E, F), dtype=jnp.float32), 'W2p': jax.random.normal(ks[5], (E, F, D), dtype=jnp.float32) * s, 'b2p': jnp.zeros((E, D), dtype=jnp.float32)}
    _L2_ffn_all = _L2_ffn_setup()
    _L2_ffn_in = {k: v for k, v in _L2_ffn_all.items() if k in ('Wr', 'W1s', 'b1s', 'W2s', 'b2s', 'W1p', 'b1p', 'W2p', 'b2p')}
    del _L2_ffn_all

    def _L3_attn_setup():
        import jax, jax.numpy as jnp
        import numpy as np
        DIM = 64
        HEADS = 8
        DIM_HEAD = 32
        INNER = HEADS * DIM_HEAD
        K_NEIGHBORS = 16
        TEMPERATURE = 1.0
        SCALE = DIM_HEAD ** (-0.5)
        BATCH = 128
        N_FEATURES = 32
        key = jax.random.key(seed)
        ks = jax.random.split(key, 6)
        s = 0.02
        return {'x': jax.random.normal(ks[0], (BATCH, N_FEATURES, DIM), dtype=jnp.float32), 'W_qkv': jax.random.normal(ks[1], (DIM, 3 * INNER), dtype=jnp.float32) * s, 'W_out': jax.random.normal(ks[2], (INNER, DIM), dtype=jnp.float32) * s, 'b_out': jnp.zeros((DIM,), dtype=jnp.float32), 'W_repr': jax.random.normal(ks[3], (DIM, DIM), dtype=jnp.float32) * s, 'b_repr': jnp.zeros((DIM,), dtype=jnp.float32)}
    _L3_attn_all = _L3_attn_setup()
    _L3_attn_in = {k: v for k, v in _L3_attn_all.items() if k in ('W_qkv', 'W_out', 'b_out', 'W_repr', 'b_repr')}
    del _L3_attn_all

    def _L3_ffn_setup():
        import jax, jax.numpy as jnp
        import numpy as np
        TOP_K = 2
        LN_EPS = 1e-05
        key = jax.random.key(seed)
        ks = jax.random.split(key, 8)
        B, S, D, E, H = (16, 256, 64, 8, 256)
        x = jax.random.normal(ks[0], (B, S, D), dtype=jnp.float32)
        Wr = jax.random.normal(ks[1], (D, E), dtype=jnp.float32) * 0.1
        br = jnp.zeros((E,), dtype=jnp.float32)
        ln_g = jnp.ones((E, D), dtype=jnp.float32)
        ln_b = jnp.zeros((E, D), dtype=jnp.float32)
        W1 = jax.random.normal(ks[2], (E, D, H), dtype=jnp.float32) * (1.0 / np.sqrt(D))
        b1 = jnp.zeros((E, H), dtype=jnp.float32)
        W2 = jax.random.normal(ks[3], (E, H, D), dtype=jnp.float32) * (1.0 / np.sqrt(H))
        b2 = jnp.zeros((E, D), dtype=jnp.float32)
        return {'x': x, 'Wr': Wr, 'br': br, 'ln_g': ln_g, 'ln_b': ln_b, 'W1': W1, 'b1': b1, 'W2': W2, 'b2': b2}
    _L3_ffn_all = _L3_ffn_setup()
    _L3_ffn_in = {k: v for k, v in _L3_ffn_all.items() if k in ('Wr', 'br', 'ln_g', 'ln_b', 'W1', 'b1', 'W2', 'b2')}
    del _L3_ffn_all
    return {'x': x, 'L0_tok_emb_2': _L0_tok_in['emb_2'], 'L0_tok_emb_3': _L0_tok_in['emb_3'], 'L0_tok_emb_4': _L0_tok_in['emb_4'], 'L0_attn_edge_index': _L0_attn_in['edge_index'], 'L0_attn_edge_attr': _L0_attn_in['edge_attr'], 'L0_attn_Wq': _L0_attn_in['Wq'], 'L0_attn_bq': _L0_attn_in['bq'], 'L0_attn_Wk': _L0_attn_in['Wk'], 'L0_attn_bk': _L0_attn_in['bk'], 'L0_attn_Wv': _L0_attn_in['Wv'], 'L0_attn_bv': _L0_attn_in['bv'], 'L0_attn_Wo': _L0_attn_in['Wo'], 'L0_attn_bo': _L0_attn_in['bo'], 'L0_attn_We': _L0_attn_in['We'], 'L0_attn_be': _L0_attn_in['be'], 'L0_ffn_W_fx': _L0_ffn_in['W_fx'], 'L0_ffn_b_fx': _L0_ffn_in['b_fx'], 'L0_ffn_W_x': _L0_ffn_in['W_x'], 'L0_ffn_b_x': _L0_ffn_in['b_x'], 'L0_ffn_W_slice': _L0_ffn_in['W_slice'], 'L0_ffn_b_slice': _L0_ffn_in['b_slice'], 'L0_ffn_W_q': _L0_ffn_in['W_q'], 'L0_ffn_W_k': _L0_ffn_in['W_k'], 'L0_ffn_W_v': _L0_ffn_in['W_v'], 'L0_ffn_W_out': _L0_ffn_in['W_out'], 'L0_ffn_b_out': _L0_ffn_in['b_out'], 'L0_ffn_temperature': _L0_ffn_in['temperature'], 'L1_attn_edge_index': _L1_attn_in['edge_index'], 'L1_attn_edge_values': _L1_attn_in['edge_values'], 'L1_attn_positions': _L1_attn_in['positions'], 'L1_attn_qkv_w': _L1_attn_in['qkv_w'], 'L1_attn_qkv_b': _L1_attn_in['qkv_b'], 'L1_attn_proj_w': _L1_attn_in['proj_w'], 'L1_attn_proj_b': _L1_attn_in['proj_b'], 'L1_attn_gate_w': _L1_attn_in['gate_w'], 'L1_attn_gate_b': _L1_attn_in['gate_b'], 'L1_ffn_hl_w': _L1_ffn_in['hl_w'], 'L1_ffn_hl_b': _L1_ffn_in['hl_b'], 'L1_ffn_wq': _L1_ffn_in['wq'], 'L1_ffn_wk': _L1_ffn_in['wk'], 'L1_ffn_wv': _L1_ffn_in['wv'], 'L1_ffn_gate_w': _L1_ffn_in['gate_w'], 'L1_ffn_gate_b': _L1_ffn_in['gate_b'], 'L1_ffn_ln_g': _L1_ffn_in['ln_g'], 'L1_ffn_ln_b': _L1_ffn_in['ln_b'], 'L1_ffn_fc1_w': _L1_ffn_in['fc1_w'], 'L1_ffn_fc1_b': _L1_ffn_in['fc1_b'], 'L1_ffn_fc2_w': _L1_ffn_in['fc2_w'], 'L1_ffn_fc2_b': _L1_ffn_in['fc2_b'], 'L1_ffn_fnorm_g': _L1_ffn_in['fnorm_g'], 'L1_ffn_fnorm_b': _L1_ffn_in['fnorm_b'], 'L1_ffn_fgate_w': _L1_ffn_in['fgate_w'], 'L2_attn_weight_q': _L2_attn_in['weight_q'], 'L2_attn_weight_k': _L2_attn_in['weight_k'], 'L2_attn_weight_v': _L2_attn_in['weight_v'], 'L2_attn_weight_out': _L2_attn_in['weight_out'], 'L2_ffn_Wr': _L2_ffn_in['Wr'], 'L2_ffn_W1s': _L2_ffn_in['W1s'], 'L2_ffn_b1s': _L2_ffn_in['b1s'], 'L2_ffn_W2s': _L2_ffn_in['W2s'], 'L2_ffn_b2s': _L2_ffn_in['b2s'], 'L2_ffn_W1p': _L2_ffn_in['W1p'], 'L2_ffn_b1p': _L2_ffn_in['b1p'], 'L2_ffn_W2p': _L2_ffn_in['W2p'], 'L2_ffn_b2p': _L2_ffn_in['b2p'], 'L3_attn_W_qkv': _L3_attn_in['W_qkv'], 'L3_attn_W_out': _L3_attn_in['W_out'], 'L3_attn_b_out': _L3_attn_in['b_out'], 'L3_attn_W_repr': _L3_attn_in['W_repr'], 'L3_attn_b_repr': _L3_attn_in['b_repr'], 'L3_ffn_Wr': _L3_ffn_in['Wr'], 'L3_ffn_br': _L3_ffn_in['br'], 'L3_ffn_ln_g': _L3_ffn_in['ln_g'], 'L3_ffn_ln_b': _L3_ffn_in['ln_b'], 'L3_ffn_W1': _L3_ffn_in['W1'], 'L3_ffn_b1': _L3_ffn_in['b1'], 'L3_ffn_W2': _L3_ffn_in['W2'], 'L3_ffn_b2': _L3_ffn_in['b2']}

def reference(x, L0_tok_emb_2, L0_tok_emb_3, L0_tok_emb_4, L0_attn_edge_index, L0_attn_edge_attr, L0_attn_Wq, L0_attn_bq, L0_attn_Wk, L0_attn_bk, L0_attn_Wv, L0_attn_bv, L0_attn_Wo, L0_attn_bo, L0_attn_We, L0_attn_be, L0_ffn_W_fx, L0_ffn_b_fx, L0_ffn_W_x, L0_ffn_b_x, L0_ffn_W_slice, L0_ffn_b_slice, L0_ffn_W_q, L0_ffn_W_k, L0_ffn_W_v, L0_ffn_W_out, L0_ffn_b_out, L0_ffn_temperature, L1_attn_edge_index, L1_attn_edge_values, L1_attn_positions, L1_attn_qkv_w, L1_attn_qkv_b, L1_attn_proj_w, L1_attn_proj_b, L1_attn_gate_w, L1_attn_gate_b, L1_ffn_hl_w, L1_ffn_hl_b, L1_ffn_wq, L1_ffn_wk, L1_ffn_wv, L1_ffn_gate_w, L1_ffn_gate_b, L1_ffn_ln_g, L1_ffn_ln_b, L1_ffn_fc1_w, L1_ffn_fc1_b, L1_ffn_fc2_w, L1_ffn_fc2_b, L1_ffn_fnorm_g, L1_ffn_fnorm_b, L1_ffn_fgate_w, L2_attn_weight_q, L2_attn_weight_k, L2_attn_weight_v, L2_attn_weight_out, L2_ffn_Wr, L2_ffn_W1s, L2_ffn_b1s, L2_ffn_W2s, L2_ffn_b2s, L2_ffn_W1p, L2_ffn_b1p, L2_ffn_W2p, L2_ffn_b2p, L3_attn_W_qkv, L3_attn_W_out, L3_attn_b_out, L3_attn_W_repr, L3_attn_b_repr, L3_ffn_Wr, L3_ffn_br, L3_ffn_ln_g, L3_ffn_ln_b, L3_ffn_W1, L3_ffn_b1, L3_ffn_W2, L3_ffn_b2):
    import jax
    import jax.numpy as jnp

    def _L0_tok_ref(byte_ids, emb_2, emb_3, emb_4):
        import jax, jax.numpy as jnp
        import numpy as np
        PRIME = 31
        VOCAB = 125000
        NGRAM_SIZES = (2, 3, 4)

        def _ngram_hash(byte_ids, n):
            T = byte_ids.shape[1]
            powers = PRIME ** jnp.arange(n - 1, -1, -1, dtype=jnp.int64) % VOCAB
            windows = jnp.stack([byte_ids[:, i:T - n + 1 + i] for i in range(n)], axis=-1)
            return (windows.astype(jnp.int64) * powers).sum(axis=-1) % VOCAB
        tables = {2: emb_2, 3: emb_3, 4: emb_4}
        B, T = byte_ids.shape
        D = emb_2.shape[1]
        out = jnp.zeros((B, T, D), dtype=emb_2.dtype)
        for n in NGRAM_SIZES:
            idx = _ngram_hash(byte_ids, n)
            gathered = tables[n][idx]
            out = out + jnp.pad(gathered, ((0, 0), (n - 1, 0), (0, 0)))
        return out / (len(NGRAM_SIZES) + 1)

    def _L0_attn_ref(x, edge_index, edge_attr, Wq, bq, Wk, bk, Wv, bv, Wo, bo, We, be):
        import jax, jax.numpy as jnp
        import numpy as np
        H = 8
        B, N, D = x.shape
        hd = D // H
        q = (x @ Wq + bq).reshape(B, N, H, hd)
        k = (x @ Wk + bk).reshape(B, N, H, hd)
        v = (x @ Wv + bv).reshape(B, N, H, hd)
        scores = jnp.einsum('bihd,bjhd->bhij', q, k) / jnp.sqrt(jnp.asarray(hd, x.dtype))
        eb = edge_attr @ We + be
        edge_tgt = edge_index[1]
        col_bias = jnp.zeros((H, N), x.dtype).at[:, edge_tgt].set(eb.T)
        scores = scores + col_bias[None, :, None, :]
        attn = jax.nn.softmax(scores, axis=-1)
        out = jnp.einsum('bhij,bjhd->bihd', attn, v).reshape(B, N, D)
        return out @ Wo + bo

    def _L0_ffn_ref(x, W_fx, b_fx, W_x, b_x, W_slice, b_slice, W_q, W_k, W_v, W_out, b_out, temperature):
        import jax, jax.numpy as jnp
        import numpy as np
        DIM = 64
        H = 8
        D = 64
        G = 64
        INNER = H * D
        SCALE = D ** (-0.5)
        B, N, _ = x.shape
        fx_mid = (x @ W_fx + b_fx).reshape(B, N, H, D).transpose(0, 2, 1, 3)
        x_mid = (x @ W_x + b_x).reshape(B, N, H, D).transpose(0, 2, 1, 3)
        temp = jnp.clip(temperature, 0.1, 5.0)
        slice_weights = jax.nn.softmax((x_mid @ W_slice + b_slice) / temp, axis=-1)
        slice_norm = slice_weights.sum(axis=2)
        slice_token = jnp.einsum('bhnc,bhng->bhgc', fx_mid, slice_weights)
        slice_token = slice_token / (slice_norm[..., None] + 1e-05)
        q = slice_token @ W_q
        k = slice_token @ W_k
        v = slice_token @ W_v
        attn = jax.nn.softmax(jnp.einsum('bhgc,bhkc->bhgk', q, k) * SCALE, axis=-1)
        out_slice = jnp.einsum('bhgk,bhkc->bhgc', attn, v)
        out_x = jnp.einsum('bhgc,bhng->bhnc', out_slice, slice_weights)
        out_x = out_x.transpose(0, 2, 1, 3).reshape(B, N, INNER)
        return out_x @ W_out + b_out

    def _L1_attn_ref(x, edge_index, edge_values, positions, qkv_w, qkv_b, proj_w, proj_b, gate_w, gate_b):
        import jax, jax.numpy as jnp
        import numpy as np
        BS = 32
        NUM_HOPS = 1

        def _connectivity(edge_index, edge_values, positions, nb):
            rows, cols = (edge_index[0], edge_index[1])
            br, bc = (rows // BS, cols // BS)
            in_block = (br == bc) & (br < nb)
            r_l, c_l = (rows % BS, cols % BS)
            b_safe = jnp.where(in_block, br, nb)
            dx = positions[cols] - positions[rows]
            ef_flat = jnp.concatenate([dx, edge_values[:, None]], axis=1)
            adj = jnp.zeros((nb, BS, BS), jnp.float32).at[b_safe, r_l, c_l].set(1.0, mode='drop')
            eye = jnp.eye(BS, dtype=jnp.float32)
            reachable = jnp.broadcast_to(eye[None], (nb, BS, BS))
            cur = adj
            for _ in range(NUM_HOPS):
                reachable = jnp.clip(reachable + cur, 0.0, 1.0)
                cur = jnp.matmul(cur, adj)
            attn_mask = jnp.concatenate([reachable, jnp.ones((nb, BS, 1), jnp.float32)], axis=2)
            edge_feats = jnp.zeros((nb, BS, BS + 1, 4), jnp.float32)
            edge_feats = edge_feats.at[b_safe, r_l, c_l, :].set(ef_flat, mode='drop')
            return (attn_mask, edge_feats)
        B, N, C = x.shape
        H = gate_w.shape[0]
        hd = C // H
        scale = hd ** (-0.5)
        nb = N // BS
        attn_mask, edge_feats = _connectivity(edge_index, edge_values, positions, nb)
        x_blk = x.reshape(B, nb, BS, C)
        block_node = x_blk.mean(axis=2, keepdims=True)
        kv = jnp.concatenate([x_blk, block_node], axis=2)
        qkv_q = x_blk @ qkv_w.T + qkv_b
        qkv_kv = kv @ qkv_w.T + qkv_b
        q = qkv_q[..., :C].reshape(B, nb, BS, H, hd)
        k = qkv_kv[..., C:2 * C].reshape(B, nb, BS + 1, H, hd)
        v = qkv_kv[..., 2 * C:].reshape(B, nb, BS + 1, H, hd)
        scores = jnp.einsum('bnqhd,bnkhd->bnqkh', q, k) * scale
        ar = jnp.arange(BS)
        bias_physics = edge_feats.at[:, :, BS, :].set(0.0).at[:, :, BS, 3].set(1.0)
        bias_physics = bias_physics.at[:, ar, ar, :].set(0.0).at[:, ar, ar, 3].set(1.0)
        scores = scores + bias_physics[None, ..., 3:4]
        mask = attn_mask[None, :, :, :, None]
        scores = jnp.where(mask == 0, -jnp.inf, scores)
        attn_probs = jax.nn.softmax(scores, axis=3)
        gate = bias_physics @ gate_w.T + gate_b
        gate = jnp.where(mask == 0, 0.0, gate[None])
        combined = attn_probs + gate
        x_out = jnp.einsum('bnqkh,bnkhd->bnqhd', combined, v).reshape(B, nb, BS, C)
        out = x_out.reshape(B, N, C) @ proj_w.T + proj_b
        return out

    def _L1_ffn_ref(x, hl_w, hl_b, wq, wk, wv, gate_w, gate_b, ln_g, ln_b, fc1_w, fc1_b, fc2_w, fc2_b, fnorm_g, fnorm_b, fgate_w):
        import jax, jax.numpy as jnp
        import numpy as np
        B, S, H, NH, NE = (4, 256, 64, 4, 4)
        D = H // NH
        EPS = 1e-08

        def layernorm(x, g, b):
            m = jnp.mean(x, axis=-1, keepdims=True)
            v = jnp.mean((x - m) ** 2, axis=-1, keepdims=True)
            return (x - m) / jnp.sqrt(v + EPS) * g + b
        b, s, h = x.shape
        nh, d, _ = wk.shape
        ne = wq.shape[1]
        sx = jnp.einsum('bsh,ndh->bnsd', x, hl_w) + hl_b[None, :, None, :]
        pad = sx == 0
        q = jnp.einsum('bnsd,neod->bneso', sx, wq)
        k = jnp.einsum('bnsd,nod->bnso', sx, wk)
        v = jnp.einsum('bnsd,nod->bnso', sx, wv)
        causal = jnp.where(jnp.tril(jnp.ones((s, s), bool)), 0.0, -jnp.inf).astype(x.dtype)
        scores = jnp.einsum('bnesd,bntd->bnest', q, k) * d ** 0.5 + causal
        att = jax.nn.softmax(scores, axis=-1)
        qkv = jnp.einsum('bnest,bntd->bnesd', att, v)
        qkv = jnp.where(pad[:, :, None], 0.0, qkv)
        out = jnp.transpose(qkv, (0, 1, 3, 2, 4)).reshape(b, nh, s, ne * d)
        gs = jax.nn.softmax(jnp.einsum('bnsf,nef->bnse', out, gate_w) + gate_b[None, :, None, :], axis=-1)
        mixed = jnp.einsum('bnsed,bnse->bnsd', out.reshape(b, nh, s, ne, d), gs)
        resid = sx[jnp.arange(nh), jnp.arange(nh)]
        hn = layernorm(mixed + resid, ln_g, ln_b)
        f_n = jnp.transpose(hn, (0, 2, 1, 3)).reshape(b, s, h)
        fx = f_n.reshape(b, s, nh, d)
        pm = fx == 0
        hx = jnp.where(pm, 0.0, fx @ fc1_w.T + fc1_b)
        hx = jax.nn.relu(hx)
        hx = jnp.where(pm, 0.0, hx @ fc2_w.T + fc2_b)
        hx = layernorm(hx + fx, fnorm_g, fnorm_b)
        fout = hx.reshape(b, s, h)
        fg = jax.nn.softmax(fout @ fgate_w.T, axis=-1)
        return (fout.reshape(b, s, nh, d) * fg[..., None]).reshape(b, s, h)

    def _L2_attn_ref(features, weight_q, weight_k, weight_v, weight_out):
        import jax, jax.numpy as jnp
        import numpy as np
        IN_CH, OUT_CH, HEADS, DIM = (64, 64, 8, 64)

        def _xavier(key, shape, fan_in, fan_out):
            upper = np.sqrt(6.0) / np.sqrt(float(fan_in + fan_out))
            return jax.random.uniform(key, shape, jnp.float32) * (2.0 * upper) - upper
        q = jnp.einsum('bnc,chd->bnhd', features, weight_q)
        k = jnp.einsum('bnc,chd->bnhd', features, weight_k)
        v = jnp.einsum('bnc,chd->bnhd', features, weight_v)
        qk = jnp.einsum('bihd,bjhd->bijh', q, k) / jnp.sqrt(jnp.asarray(DIM, q.dtype))
        qk_softmax = jax.nn.softmax(qk, axis=1)
        attn_weight = jnp.sum(qk_softmax, axis=2)
        applied = v * attn_weight[:, :, :, None]
        out = jnp.einsum('bihd,ohd->bio', applied, weight_out)
        return out

    def _L2_ffn_ref(x, Wr, W1s, b1s, W2s, b2s, W1p, b1p, W2p, b2p):
        import jax, jax.numpy as jnp
        import numpy as np
        B, S, D, F, E, K = (8, 512, 64, 256, 8, 2)
        gelu = lambda t: jax.nn.gelu(t, approximate=False)
        shared = gelu(x @ W1s + b1s) @ W2s + b2s
        rw = jax.nn.softmax(x @ Wr, axis=-1)
        topw, topi = jax.lax.top_k(rw, K)
        topw = topw / jnp.sum(topw, axis=-1, keepdims=True)
        mask = jnp.sum(jax.nn.one_hot(topi, E, dtype=topw.dtype) * topw[..., None], axis=-2)
        h = gelu(jnp.einsum('bsd,edf->bsef', x, W1p) + b1p)
        priv = jnp.einsum('bsef,efd->bsed', h, W2p) + b2p
        routed = jnp.einsum('bsed,bse->bsd', priv, mask)
        return shared + routed

    def _L3_attn_ref(x, W_qkv, W_out, b_out, W_repr, b_repr):
        import jax, jax.numpy as jnp
        import numpy as np
        DIM = 64
        HEADS = 8
        DIM_HEAD = 32
        INNER = HEADS * DIM_HEAD
        K_NEIGHBORS = 16
        TEMPERATURE = 1.0
        SCALE = DIM_HEAD ** (-0.5)
        BATCH = 128
        N_FEATURES = 32
        B, n, d = x.shape
        reprs = jnp.mean(x, axis=1) @ W_repr + b_repr
        normed = reprs / jnp.linalg.norm(reprs, axis=-1, keepdims=True)
        sim_mat = normed @ normed.T / TEMPERATURE
        k_actual = min(K_NEIGHBORS + 1, B)
        _, knn_idx = jax.lax.top_k(sim_mat, k_actual)
        neg_inf = jnp.float32(-jnp.inf)
        mask = jnp.full((B, B), neg_inf, dtype=jnp.float32)
        mask = mask.at[jnp.arange(B)[:, None], knn_idx].set(0.0)
        qkv = x @ W_qkv
        q, k, v = jnp.split(qkv, 3, axis=-1)

        def to_bhnd(t):
            return t.reshape(B, n, HEADS, DIM_HEAD).transpose(0, 2, 1, 3)
        q, k, v = (to_bhnd(q), to_bhnd(k), to_bhnd(v))
        sim = jnp.einsum('bhnd,Bhnd->nbhB', q, k) * SCALE
        sim = sim + mask[None, :, None, :]
        attn = jax.nn.softmax(sim, axis=-1)
        out = jnp.einsum('nbhB,Bhnd->bnhd', attn, v)
        out = out.reshape(B, n, INNER)
        return out @ W_out + b_out

    def _L3_ffn_ref(x, Wr, br, ln_g, ln_b, W1, b1, W2, b2):
        import jax, jax.numpy as jnp
        import numpy as np
        TOP_K = 2
        LN_EPS = 1e-05
        B, S, D = x.shape
        N = B * S
        xt = x.reshape(N, D)
        logits = xt @ Wr + br
        probs = jax.nn.softmax(logits, axis=-1)
        top_p, top_idx = jax.lax.top_k(probs, TOP_K)
        weights = top_p / top_p.sum(axis=-1, keepdims=True)
        mu = xt.mean(axis=-1, keepdims=True)
        var = ((xt - mu) ** 2).mean(axis=-1, keepdims=True)
        xn = (xt - mu) * jax.lax.rsqrt(var + LN_EPS)
        xe = xn[None, :, :] * ln_g[:, None, :] + ln_b[:, None, :]
        h = jax.nn.gelu(jnp.einsum('end,edh->enh', xe, W1) + b1[:, None, :], approximate=False)
        y = jnp.einsum('enh,ehd->end', h, W2) + b2[:, None, :]
        y_tok = jnp.transpose(y, (1, 0, 2))
        sel = jnp.take_along_axis(y_tok, top_idx[:, :, None], axis=1)
        out = (weights[:, :, None] * sel).sum(axis=1)
        return out.reshape(B, S, D)
    h = _L0_tok_ref(x, L0_tok_emb_2, L0_tok_emb_3, L0_tok_emb_4)
    h = h + _L0_attn_ref(_layernorm(h, axis=-1), L0_attn_edge_index, L0_attn_edge_attr, L0_attn_Wq, L0_attn_bq, L0_attn_Wk, L0_attn_bk, L0_attn_Wv, L0_attn_bv, L0_attn_Wo, L0_attn_bo, L0_attn_We, L0_attn_be)
    h = h + _L0_ffn_ref(_layernorm(h, axis=-1), L0_ffn_W_fx, L0_ffn_b_fx, L0_ffn_W_x, L0_ffn_b_x, L0_ffn_W_slice, L0_ffn_b_slice, L0_ffn_W_q, L0_ffn_W_k, L0_ffn_W_v, L0_ffn_W_out, L0_ffn_b_out, L0_ffn_temperature)
    h = h + _L1_attn_ref(_layernorm(h, axis=-1), L1_attn_edge_index, L1_attn_edge_values, L1_attn_positions, L1_attn_qkv_w, L1_attn_qkv_b, L1_attn_proj_w, L1_attn_proj_b, L1_attn_gate_w, L1_attn_gate_b)
    h = h + _L1_ffn_ref(_layernorm(h, axis=-1), L1_ffn_hl_w, L1_ffn_hl_b, L1_ffn_wq, L1_ffn_wk, L1_ffn_wv, L1_ffn_gate_w, L1_ffn_gate_b, L1_ffn_ln_g, L1_ffn_ln_b, L1_ffn_fc1_w, L1_ffn_fc1_b, L1_ffn_fc2_w, L1_ffn_fc2_b, L1_ffn_fnorm_g, L1_ffn_fnorm_b, L1_ffn_fgate_w)
    h = h + _L2_attn_ref(_layernorm(h, axis=-1), L2_attn_weight_q, L2_attn_weight_k, L2_attn_weight_v, L2_attn_weight_out)
    h = h + _L2_ffn_ref(_layernorm(h, axis=-1), L2_ffn_Wr, L2_ffn_W1s, L2_ffn_b1s, L2_ffn_W2s, L2_ffn_b2s, L2_ffn_W1p, L2_ffn_b1p, L2_ffn_W2p, L2_ffn_b2p)
    h = h + _L3_attn_ref(_layernorm(h, axis=-1), L3_attn_W_qkv, L3_attn_W_out, L3_attn_b_out, L3_attn_W_repr, L3_attn_b_repr)
    h = h + _L3_ffn_ref(_layernorm(h, axis=-1), L3_ffn_Wr, L3_ffn_br, L3_ffn_ln_g, L3_ffn_ln_b, L3_ffn_W1, L3_ffn_b1, L3_ffn_W2, L3_ffn_b2)
    return h

_drawn_inputs = setup_inputs


def setup_inputs(seed=0):
    import zlib

    import numpy as np

    out = dict(_drawn_inputs(seed))
    spreads = {'L0_attn_bq': (0.0, 0.524),
     'L0_attn_bk': (0.0, 2.0),
     'L0_attn_bv': (0.0, 0.1),
     'L0_attn_bo': (0.0, 0.1),
     'L0_attn_be': (0.0, 2.0),
     'L0_ffn_b_fx': (0.0, 0.1),
     'L0_ffn_b_x': (0.0, 0.1),
     'L0_ffn_b_slice': (0.0, 0.1),
     'L0_ffn_b_out': (0.0, 0.1),
     'L0_ffn_temperature': (0.5, 0.2),
     'L1_attn_qkv_b': (0.0, 0.1),
     'L1_attn_proj_b': (0.0, 0.1),
     'L1_attn_gate_b': (0.0, 0.1),
     'L1_ffn_ln_g': (1.0, 0.2),
     'L1_ffn_ln_b': (0.0, 0.1),
     'L1_ffn_fnorm_g': (1.0, 0.2),
     'L1_ffn_fnorm_b': (0.0, 0.1),
     'L2_ffn_b1s': (0.0, 0.1),
     'L2_ffn_b2s': (0.0, 0.1),
     'L2_ffn_b1p': (0.0, 0.1),
     'L2_ffn_b2p': (0.0, 0.1),
     'L3_attn_b_out': (0.0, 0.1),
     'L3_attn_b_repr': (0.0, 2.0),
     'L3_ffn_br': (0.0, 0.1),
     'L3_ffn_ln_g': (1.0, 0.2),
     'L3_ffn_ln_b': (0.0, 0.1),
     'L3_ffn_b1': (0.0, 0.1),
     'L3_ffn_b2': (0.0, 0.1)}
    factors = {'L0_attn_edge_attr': 6.836,
     'L0_attn_Wq': 8.0,
     'L0_attn_Wk': 4.375,
     'L0_attn_We': 8.0,
     'L1_attn_positions': 4.32,
     'L1_attn_gate_w': 3.07,
     'L1_ffn_wq': 3.926,
     'L1_ffn_wk': 3.784,
     'L1_ffn_gate_w': 25.05,
     'L1_ffn_gate_b': 8.0}
    for name, (base, spread) in spreads.items():
        noise = np.random.default_rng([zlib.crc32(name.encode()), seed]).standard_normal(out[name].shape)
        drawn = base * np.exp(spread * noise) if base else spread * noise
        out[name] = jnp.asarray(drawn.astype(out[name].dtype))
    for name, factor in factors.items():
        out[name] = (out[name] * factor).astype(out[name].dtype)
    return out
```

```python
from contextlib import ExitStack

import concourse.bass as bass
from concourse import mybir

F32 = mybir.dt.float32
BF16 = mybir.dt.bfloat16
I32 = mybir.dt.int32
U32 = mybir.dt.uint32
ALU = mybir.AluOpType
ACT = mybir.ActivationFunctionType
AX = mybir.AxisListType.X

P = 128
SEQS = 64
N = 128
D = 64
GROUP = 4
GROUPS = SEQS // GROUP
TOK = GROUP * N
LN_EPS = 1e-5
BANK = 512
MASKED = -1e30


class Core:

    def __init__(self, nc, w, out):
        self.nc, self.w, self.out = nc, w, out


class Scope:

    psum = None
    next_bank = 0

    def __init__(self, nc, stage):
        self.nc, self.stage, self.ctx = nc, stage, ExitStack()
        self.first_bank, self.sems = Scope.next_bank, []

    def __enter__(self):
        return self

    def __exit__(self, *a):
        Scope.next_bank = self.first_bank
        self.ctx.close()
        if self.sems:
            self.nc.clear_and_free_semaphores(self.sems)
            self.nc.all_engine_barrier()

    def sb(self, name, shape, dt=F32):
        return self.ctx.enter_context(self.nc.sbuf_tensor(f"{self.stage}_{name}", shape, dt))

    def ps(self, name, shape, dt=F32):
        size = 1
        for n in shape[1:]:
            size *= n
        words = size if dt == F32 else size // 2
        start = Scope.next_bank * BANK
        Scope.next_bank += -(-words // BANK)
        assert Scope.next_bank <= 8, name
        flat = Scope.psum[0:shape[0], start:start + words]
        if dt != F32:
            flat = flat.bitcast(dt)
        axes = "abcd"[:len(shape) - 1]
        return flat.rearrange(f"p ({' '.join(axes)}) -> p {' '.join(axes)}", **dict(zip(axes, shape[1:])))

    def sem(self, name):
        self.sems.append(self.nc.alloc_semaphore(name=f"{self.stage}_{name}"))
        return self.sems[-1]

    def block(self):
        return self.ctx.enter_context(self.nc.Block())


class Link:

    def __init__(self, eng, sem, base=0, per=None):
        self.eng, self.sem, self.base, self.n, self.per = eng, sem, base, 0, per

    def __call__(self, ins):
        ins.then_inc(self.sem, 1)
        self.n += 1
        self.eng.wait_ge(self.sem, self.base + self.n)

    def close(self):
        assert self.per is None or self.n == self.per, (self.n, self.per)


def bc(ap, shape):
    return ap.to_broadcast(shape)


def stage_constants(k):
    nc = k.nc
    with Scope(nc, "const") as s:
        made = s.sem("ident_step")
        block = s.block()

        @block.gpsimd
        def _(pool):
            link = Link(pool, made)
            link(nc.gpsimd.memset(k.ident[:], 0.0))
            link(nc.gpsimd.affine_select(out=k.ident[:], in_=k.ident[:], compare_op=ALU.not_equal, fill=1.0,
                                         base=0, pattern=[[-1, P]], channel_multiplier=1))


def stage_tokens(k):
    nc, w = k.nc, k.w
    PRIME, VOCAB = 31, 125000
    with Scope(nc, "tok") as s:
        ids_i = s.sb("ids_i", [SEQS, N], I32)
        ids = s.sb("ids", [SEQS, N + 3])
        acc = s.sb("acc", [SEQS, 3, N])
        over = s.sb("over", [SEQS, 3, N])
        index = s.sb("index", [P, 3, SEQS], U32)
        rows = [s.sb(f"rows{n}", [P, SEQS, D]) for n in range(2)]
        keep = s.sb("keep", [P, 3])
        ones = s.sb("ones", [P, 3])
        turned = s.ps("turned", [P, 3, SEQS])
        loaded, step, hashed, transposed = s.sem("loaded"), s.sem("step"), s.sem("hashed"), s.sem("transposed")
        indexed, kept, one = s.sem("indexed"), s.sem("kept"), s.sem("one")
        landed = k.rows_landed
        block = s.block()
        dest = [k.h, rows[0], rows[1]]

        @block.sync
        def _(sp):
            sp.dma_start(ids_i[:], w["x"]).then_inc(loaded, 16)

        @block.gpsimd
        def _(pool):
            link = Link(pool, one)
            link(nc.gpsimd.memset(ones[:], 0.25))
            link(nc.gpsimd.affine_select(out=keep[:], in_=ones[:], compare_op=ALU.is_ge, fill=0.0, base=-1,
                                         pattern=[[-1, 3]], channel_multiplier=1))
            nc.gpsimd.sem_inc(kept, 1)
            pool.wait_ge(indexed, 1)
            for g in range(3):
                for b in range(SEQS):
                    nc.gpsimd.indirect_dma_start(
                        dest[g][:, b, :], None, w[f"L0_tok_emb_{g + 2}"],
                        bass.IndirectOffsetOnAxis(index[:, g, b:b + 1], 0)).then_inc(landed[g], 16)

        @block.vector
        def _(dve):
            link = Link(dve, step)
            link(nc.vector.memset(ids[:], 0.0))
            dve.wait_ge(loaded, 16)
            link(nc.vector.tensor_copy(ids[:, 3:], ids_i[:]))
            for g in range(3):
                link(nc.vector.tensor_copy(acc[:, g, :], ids[:, 3:]))
                for j in range(1, g + 2):
                    link(nc.vector.scalar_tensor_tensor(out=acc[:, g, :], in0=ids[:, 3 - j:3 - j + N],
                                                        scalar=float(PRIME ** j % VOCAB), in1=acc[:, g, :],
                                                        op0=ALU.mult, op1=ALU.add))
            for bit in range(7, -1, -1):
                m = float(VOCAB << bit)
                link(nc.vector.tensor_scalar(over[:], acc[:], m, m, ALU.is_ge, ALU.mult))
                link(nc.vector.tensor_tensor(acc[:], acc[:], over[:], ALU.subtract))
            nc.vector.sem_inc(hashed, 1)
            dve.wait_ge(transposed, 1)
            nc.vector.tensor_copy(index[:], turned[:]).then_inc(indexed, 1)
            dve.wait_ge(kept, 1)
            for g in range(3):
                dve.wait_ge(landed[g], 16 * SEQS)
                if g == 0:
                    link(nc.vector.tensor_scalar(k.h[:], k.h[:], keep[:, 0:1], None, ALU.mult))
                else:
                    link(nc.vector.scalar_tensor_tensor(out=k.h[:], in0=dest[g][:], scalar=keep[:, g:g + 1],
                                                        in1=k.h[:], op0=ALU.mult, op1=ALU.add))

        @block.tensor
        def _(pe):
            pe.wait_ge(hashed, 1)
            for g in range(3):
                ins = nc.tensor.transpose(turned[:, g, :], acc[:, g, :], k.ident[0:SEQS, 0:SEQS])
            ins.then_inc(transposed, 1)


def stage_center(k, tag):
    nc = k.nc
    with Scope(nc, f"ln{tag}") as s:
        sq = s.sb("sq", [P, SEQS, D])
        mean = s.sb("mean", [P, SEQS, 1])
        std = s.sb("std", [P, SEQS, 1])
        eps = s.sb("eps", [P, 1])
        step, summed, rooted = s.sem("step"), s.sem("summed"), s.sem("rooted")
        block = s.block()

        @block.scalar
        def _(act):
            act.wait_ge(summed, 1)
            nc.scalar.activation(std[:], mean[:], ACT.Sqrt, bias=eps[:, 0:1], scale=1.0 / D).then_inc(rooted, 1)

        @block.vector
        def _(dve):
            link = Link(dve, step)
            link(nc.vector.memset(eps[:], LN_EPS))
            link(nc.vector.tensor_reduce(mean[:, :, 0], k.h[:], AX, ALU.add))
            link(nc.vector.tensor_scalar(mean[:], mean[:], 1.0 / D, None, ALU.mult))
            link(nc.vector.tensor_tensor(k.xc[:], k.h[:], bc(mean[:], [P, SEQS, D]), ALU.subtract))
            link(nc.vector.tensor_tensor(sq[:], k.xc[:], k.xc[:], ALU.mult))
            nc.vector.tensor_reduce(mean[:, :, 0], sq[:], AX, ALU.add).then_inc(summed, 1)
            dve.wait_ge(rooted, 1)
            link(nc.vector.reciprocal(k.rstd[:], std[:]))


def front_dve(k, dve, xs, t, normed):
    g = bass.ds(GROUP * t, GROUP)
    return k.nc.vector.tensor_tensor(xs[:, :, 0:D], k.xc[:, g, :], bc(k.rstd[:, g, :], [P, GROUP, D]), ALU.mult).then_inc(normed, 1)


def stage_edge_bias(k):
    nc, w = k.nc, k.w
    EDGES = w["L0_attn_edge_index"].shape[1]
    F = EDGES // P
    HEADS, CH = 8, 32
    with Scope(nc, "ebias") as s:
        tgt_i = s.sb("tgt_i", [P, 1, F], I32)
        tgt = s.sb("tgt", [P, 1, F])
        number = s.sb("number", [P, 1, F])
        token = s.sb("token", [P, N, 1])
        hit = s.sb("hit", [P, CH, F])
        best = s.sb("best", [P, N])
        last = s.sb("last", [P, 1])
        found = s.sb("found", [P, 1])
        row = s.sb("row", [P, 1])
        row_u = s.sb("row_u", [P, 1], U32)
        attr = s.sb("attr", [P, 3])
        we = s.sb("we", [P, 3, HEADS])
        be = s.sb("be", [P, HEADS])
        eb = s.sb("eb", [P, HEADS])
        spread = s.sb("spread", [P, 2, 4, 32])
        turned = s.ps("turned", [P, N])
        placed = s.ps("placed", [P, 2, N])
        loaded, counted, step, bested = s.sem("loaded"), s.sem("counted"), s.sem("step"), s.sem("bested")
        transposed, rowed, fetched, spreaded = s.sem("transposed"), s.sem("rowed"), k.attr_fetched, s.sem("spreaded")
        block = s.block()

        @block.sync
        def _(sp):
            sp.dma_start(tgt_i[:, 0, :], w["L0_attn_edge_index"][1].rearrange("(p f) -> p f", p=P)).then_inc(loaded, 16)
            sp.dma_start(we[:], w["L0_attn_We"].partition_broadcast(P)).then_inc(loaded, 16)
            sp.dma_start(be[:], w["L0_attn_be"].partition_broadcast(P)).then_inc(loaded, 16)

        @block.gpsimd
        def _(pool):
            nc.gpsimd.iota(number[:, 0, :], [[1, F]], 1, F, allow_small_or_imprecise_dtypes=True).then_inc(counted, 1)
            nc.gpsimd.iota(token[:, :, 0], [[1, N]], 0, 0, allow_small_or_imprecise_dtypes=True).then_inc(counted, 1)
            pool.wait_ge(rowed, 1)
            nc.gpsimd.indirect_dma_start(attr[:], None, w["L0_attn_edge_attr"],
                                         bass.IndirectOffsetOnAxis(row_u[:, 0:1], 0)).then_inc(fetched, 16)

        @block.vector
        def _(dve):
            link = Link(dve, step)
            link(nc.vector.memset(spread[:], 0.0))
            dve.wait_ge(loaded, 48)
            dve.wait_ge(counted, 2)
            link(nc.vector.tensor_copy(tgt[:], tgt_i[:]))
            for c in range(0, N, CH):
                link(nc.vector.tensor_tensor(hit[:], bc(tgt[:], [P, CH, F]), bc(token[:, c:c + CH, :], [P, CH, F]), ALU.is_equal))
                link(nc.vector.tensor_tensor(hit[:], hit[:], bc(number[:], [P, CH, F]), ALU.mult))
                link(nc.vector.tensor_reduce(best[:, c:c + CH], hit[:], AX, ALU.max))
            nc.vector.sem_inc(bested, 1)
            dve.wait_ge(transposed, 1)
            link(nc.vector.tensor_reduce(last[:], turned[:], AX, ALU.max))
            link(nc.vector.tensor_scalar(found[:], last[:], 1.0, None, ALU.is_ge))
            link(nc.vector.tensor_tensor(row[:], last[:], found[:], ALU.subtract))
            nc.vector.tensor_copy(row_u[:], row[:]).then_inc(rowed, 1)
            dve.wait_ge(fetched, 16)
            link(nc.vector.tensor_copy(eb[:], be[:]))
            for j in range(3):
                link(nc.vector.scalar_tensor_tensor(out=eb[:], in0=we[:, j, :], scalar=attr[:, j:j + 1], in1=eb[:],
                                                    op0=ALU.mult, op1=ALU.add))
            nc.vector.tensor_scalar(spread[:, :, :, 8], eb[:].rearrange("p (g h) -> p g h", g=2), found[:, 0:1], None,
                                    ALU.mult).then_inc(spreaded, 1)
            dve.wait_ge(transposed, 2)
            link(nc.vector.tensor_copy(k.colbias[:], placed[:]))

        @block.tensor
        def _(pe):
            pe.wait_ge(bested, 1)
            nc.tensor.transpose(turned[:], best[:], k.ident[:]).then_inc(transposed, 1)
            pe.wait_ge(spreaded, 1)
            for g in range(2):
                ins = nc.tensor.transpose(placed[:, g, :], spread[:, g].rearrange("p h c -> p (h c)"), k.ident[:])
            ins.then_inc(transposed, 1)


def in_turn(eng, prelude, body):
    prelude()
    body(0, 0, True, False, True)
    with eng.Fori(0, (GROUPS - 2) // 2) as i:
        body(2 * i + 1, 1, True, True, True)
        body(2 * i + 2, 0, True, True, True)
    body(GROUPS - 1, 1, True, True, False)
    body(GROUPS, 0, False, True, False)


def stage_l0_attn(k):
    nc, w = k.nc, k.w
    HEADS, HD, HP = 8, 8, 32
    UNITS = GROUP * 2
    with Scope(nc, "l0a") as s:
        wq = s.sb("wq", [P, 2, 4, HP])
        wk = s.sb("wk", [P, 2, 4, HP])
        wv = s.sb("wv", [P, D])
        wo = s.sb("wo", [P, D])
        k.colbias = s.sb("colbias", [P, 2, N])
        stage_edge_bias(k)
        compact = s.sb("compact", [P, 4, HD + 1])
        xs = s.sb("xs", [P, GROUP, P])
        xt = s.sb("xt", [P, TOK])
        q = s.sb("q", [P, 2, 2, TOK])
        keys = s.sb("keys", [P, 2, 2, GROUP, 4, N])
        v = s.sb("v", [P, 2, GROUP, HEADS, HP])
        top = s.sb("top", [P, 4, 4])
        probs = s.sb("probs", [P, 4, 4, N])
        probs_t = s.sb("probs_t", [P, 2, 4, N])
        ot = s.sb("ot", [P, 2, TOK])
        rden = s.sb("rden", [P, GROUP, HEADS, 1])
        mixed = s.sb("mixed", [P, GROUP, P])
        mt = s.sb("mt", [P, TOK])
        ps = s.ps("ps", [P, 8, 512])
        SC, TU, OT, X, Y = 0, 2, 4, 6, 7
        names = ("loaded step ready normed xt_made xt_ready projected q_ready k_ready v_ready scored topped exped turned "
                 "turned_ready valued ot_ready back inverted mixed_ready mt_made mt_ready outed added apart").split()
        S = {n: s.sem(n) for n in names}
        loaded, step, ready = S["loaded"], S["step"], S["ready"]
        block = s.block()

        def heads(flat):
            return flat.rearrange("p (h n) -> p h n", h=4)

        def seqs(flat):
            return flat.rearrange("p (b n) -> p b n", b=GROUP)

        @block.sync
        def _(sp):
            sp.wait_ge(ready, 1)
            for g in range(2):
                for wt, n in ((wq, "q"), (wk, "k")):
                    sp.dma_start(wt[0:D, g, :, 0:HD],
                                 w[f"L0_attn_W{n}"].rearrange("i (g h c) -> g i h c", g=2, c=HD)[g]).then_inc(loaded, 16)
                    sp.dma_start(wt[D:D + 1, g, :, 0:HD],
                                 w[f"L0_attn_b{n}"].rearrange("(o g h c) -> g o h c", o=1, g=2, c=HD)[g]).then_inc(loaded, 16)
            for wt, n in ((wv, "v"), (wo, "o")):
                sp.dma_start(wt[0:D, :], w[f"L0_attn_W{n}"]).then_inc(loaded, 16)
                sp.dma_start(wt[D:D + 1, :], w[f"L0_attn_b{n}"].rearrange("(o d) -> o d", o=1)).then_inc(loaded, 16)

        LOADED = 16 * 12

        @block.gpsimd
        def _(pool):
            nc.gpsimd.memset(v[:], 0.0).then_inc(S["v_ready"], 1)
            pool.wait_ge(S["v_ready"], 1)
            nc.gpsimd.memset(v[:, :, :, :, HD:HD + 1], 1.0).then_inc(S["v_ready"], 1)

        @block.vector
        def _(dve):
            vec = nc.vector
            link = Link(dve, step)
            vec.memset(wo[:], 0.0)
            vec.memset(wv[:], 0.0)
            vec.memset(wq[:], 0.0)
            link(vec.memset(wk[:], 0.0))
            vec.sem_inc(ready, 1)
            vec.memset(xs[:], 0.0)
            vec.memset(mixed[:], 0.0)
            link(vec.memset(keys[:], 0.0))
            link(vec.memset(xs[:, :, D:D + 1], 1.0))
            link(vec.memset(mixed[:, :, D:D + 1], 1.0))
            for h in range(4):
                r = slice(HP * h, HP * h + HP)
                for par in range(2):
                    for g in range(2):
                        ins = vec.tensor_copy(keys[r, par, g, :, h, :], bc(k.colbias[r, g:g + 1, :], [HP, GROUP, N]))
            link(vec.tensor_copy(compact[:], k.ident[:].rearrange("p (h c) -> p h c", h=4)[:, :, 0:HD + 1]))
            dve.wait_ge(loaded, LOADED)
            link(vec.tensor_scalar(wq[:], wq[:], HD ** -0.5, None, ALU.mult))
            link(vec.memset(wq[D:D + 1, :, :, HD:HD + 1], 1.0))
            vec.sem_inc(ready, 1)

            def front(t):
                front_dve(k, dve, xs[:], t, S["normed"])

            def keep_keys(t, par, g):
                dve.wait_ge(S["projected"], 5 * t + 3 + g)
                for h in range(2):
                    r = slice(HP * h, HP * h + HD)
                    ins = vec.tensor_copy(keys[r, par, g, :, h, :], seqs(ps[r, X, :]))
                ins.then_inc(S["k_ready"], 1)

            def prelude():
                front(0)
                keep_keys(0, 0, 0)
                keep_keys(0, 0, 1)

            def maximum(t, u):
                dve.wait_ge(S["scored"], UNITS * t + u + 1)
                vec.tensor_reduce(top[:, u % 4], heads(ps[:, SC + u % 2, :]), AX, ALU.max, negate=True).then_inc(S["topped"], 1)

            def keep_turned(t, u):
                dve.wait_ge(S["turned"], UNITS * t + u + 1)
                if not (isinstance(t, int) and t == 0 and u < 2):
                    dve.wait_ge(S["valued"], UNITS * t + u - 1)
                vec.tensor_copy(probs_t[:, u % 2], heads(ps[:, TU + u % 2, :])).then_inc(S["turned_ready"], 1)

            def normalize(t):
                dve.wait_ge(S["back"], t + 1)
                o = ps[:, Y, 0:GROUP * HEADS * (HD + 1)].rearrange("p (b h c) -> p b h c", b=GROUP, h=HEADS)
                vec.reciprocal(rden[:], o[:, :, :, HD:HD + 1]).then_inc(S["inverted"], 1)
                dve.wait_ge(S["inverted"], t + 1)
                vec.tensor_tensor(mixed[:, :, 0:D].rearrange("p b (h c) -> p b h c", h=HEADS), o[:, :, :, 0:HD],
                                  bc(rden[:], [P, GROUP, HEADS, HD]), ALU.mult).then_inc(S["mixed_ready"], 1)

            def add(t):
                dve.wait_ge(S["outed"], t + 1)
                g = bass.ds(GROUP * t, GROUP)
                vec.tensor_tensor(k.h[:, g, :], k.h[:, g, :], ps[:, Y, 0:GROUP * D].rearrange("p (b d) -> p b d", b=GROUP),
                                  ALU.add).then_inc(S["added"], 1)

            def body(t, par, cur, prev, nxt):
                for u in range(UNITS):
                    if cur:
                        maximum(t, u)
                    if u >= 2 and cur:
                        keep_turned(t, u - 2)
                    if u < 2 and prev:
                        keep_turned(t - 1, UNITS + u - 2)
                    if u == 0 and nxt:
                        front(t + 1)
                    if u in (4, 5) and nxt:
                        keep_keys(t + 1, 1 - par, u - 4)
                    if u == 3 and prev:
                        normalize(t - 1)
                    if u == 7 and prev:
                        add(t - 1)

            in_turn(dve, prelude, body)

        @block.scalar
        def _(act):
            act.wait_ge(S["v_ready"], 2)

            def keep_x(t):
                act.wait_ge(S["xt_made"], t + 1)
                nc.scalar.copy(xt[:], ps[:, X, :]).then_inc(S["xt_ready"], 1)

            def keep_q(t, par, g):
                act.wait_ge(S["projected"], 5 * t + g + 1)
                nc.scalar.copy(q[:, par, g, :], ps[:, X, :]).then_inc(S["q_ready"], 1)

            def keep_keys(t, par, g):
                act.wait_ge(S["projected"], 5 * t + 3 + g)
                for h in range(2, 4):
                    r = slice(HP * h, HP * h + HD)
                    ins = nc.scalar.copy(keys[r, par, g, :, h, :], seqs(ps[r, X, :]))
                ins.then_inc(S["k_ready"], 1)

            def keep_v(t, par):
                act.wait_ge(S["projected"], 5 * t + 5)
                nc.scalar.copy(v[:, par, :, :, 0:HD], ps[:, X, 0:GROUP * D].rearrange("p (b h c) -> p b h c", b=GROUP, c=HD)).then_inc(S["v_ready"], 1)

            def prelude():
                keep_x(0)
                keep_q(0, 0, 0)
                keep_q(0, 0, 1)
                keep_keys(0, 0, 0)
                keep_keys(0, 0, 1)
                keep_v(0, 0)

            def exponential(t, u):
                act.wait_ge(S["topped"], UNITS * t + u + 1)
                if not (isinstance(t, int) and t == 0 and u < 4):
                    act.wait_ge(S["turned"], UNITS * t + u - 3)
                for h in range(4):
                    ins = nc.scalar.activation(probs[:, u % 4, h], ps[:, SC + u % 2, h * N:(h + 1) * N], ACT.Exp, bias=top[:, u % 4, h:h + 1])
                ins.then_inc(S["exped"], 1)

            def keep_output(t, g):
                act.wait_ge(S["valued"], UNITS * t + 4 * g + 4)
                nc.scalar.copy(ot[:, g], ps[:, OT + g, :]).then_inc(S["ot_ready"], 1)

            def body(t, par, cur, prev, nxt):
                for u in range(UNITS):
                    if cur:
                        exponential(t, u)
                    if u == 1 and nxt:
                        keep_x(t + 1)
                    if u in (2, 3) and nxt:
                        keep_q(t + 1, 1 - par, u - 2)
                    if u == 2 and prev:
                        keep_output(t - 1, 1)
                    if u in (4, 5) and nxt:
                        keep_keys(t + 1, 1 - par, u - 4)
                    if u == 6 and nxt:
                        keep_v(t + 1, 1 - par)
                    if u == 6 and cur:
                        keep_output(t, 0)
                    if u == 5 and prev:
                        act.wait_ge(S["mt_made"], t)
                        nc.scalar.copy(mt[:], ps[:, Y, :]).then_inc(S["mt_ready"], 1)

            in_turn(act, prelude, body)

        @block.tensor
        def _(pe):
            mm = nc.tensor.matmul

            def turn_x(t):
                pe.wait_ge(S["normed"], t + 1)
                if not (isinstance(t, int) and t == 0):
                    pe.wait_ge(S["v_ready"], t + 2)
                for b in range(GROUP):
                    ins = nc.tensor.transpose(ps[:, X, b * N:(b + 1) * N], xs[:, b, :], k.ident[:])
                ins.then_inc(S["xt_made"], 1)

            def project(t, n):
                if n == 0:
                    pe.wait_ge(S["xt_ready"], t + 1)
                elif n <= 2:
                    pe.wait_ge(S["q_ready"], 2 * t + n)
                else:
                    pe.wait_ge(S["k_ready"], 4 * t + 2 * (n - 2))
                if n < 4:
                    wt = (wq, wk)[n // 2][:, n % 2].rearrange("p h c -> p (h c)")
                    ins = mm(ps[:, X, :], wt, xt[:], start=True, stop=True)
                else:
                    for b in range(GROUP):
                        ins = mm(ps[:, X, b * D:(b + 1) * D], xt[:, b * N:(b + 1) * N], wv[:], start=True, stop=True)
                ins.then_inc(S["projected"], 1)

            def prelude():
                pe.wait_ge(ready, 2)
                turn_x(0)
                for n in range(5):
                    project(0, n)

            def scores(t, par, u):
                g, b = u // 4, u % 4
                if u == 0:
                    pe.wait_ge(S["q_ready"], 2 * t + 2)
                    pe.wait_ge(S["k_ready"], 4 * t + 4)
                if not (isinstance(t, int) and t == 0 and u < 2):
                    pe.wait_ge(S["exped"], UNITS * t + u - 1)
                mm(ps[:, SC + u % 2, :], q[:, par, g, b * N:(b + 1) * N], keys[:, par, g, b].rearrange("p h n -> p (h n)"),
                   start=True, stop=True).then_inc(S["scored"], 1)

            def turn(t, u):
                pe.wait_ge(S["exped"], UNITS * t + u + 1)
                if not (isinstance(t, int) and t == 0 and u < 2):
                    pe.wait_ge(S["turned_ready"], UNITS * t + u - 1)
                for h in range(4):
                    ins = nc.tensor.transpose(ps[:, TU + u % 2, h * N:(h + 1) * N], probs[:, u % 4, h], k.ident[:])
                ins.then_inc(S["turned"], 1)

            def values(t, par, u):
                g, b = u // 4, u % 4
                pe.wait_ge(S["turned_ready"], UNITS * t + u + 1)
                if u == 0:
                    pe.wait_ge(S["v_ready"], t + 3)
                if b == 0 and not (isinstance(t, int) and t == 0):
                    pe.wait_ge(S["ot_ready"], 2 * t + g - 1)
                nc.tensor.sem_inc(S["apart"], 1)
                for h in range(4):
                    ins = mm(ps[HP * h:HP * h + HP, OT + g, b * N:(b + 1) * N], v[:, par, b, 4 * g + h, :], probs_t[:, u % 2, h],
                             start=True, stop=True, tile_position=(0, HP * h))
                ins.then_inc(S["valued"], 1)

            def turn_back(t):
                pe.wait_ge(S["ot_ready"], 2 * t + 2)
                if not (isinstance(t, int) and t == 0):
                    pe.wait_ge(S["added"], t)
                for b in range(GROUP):
                    for g in range(2):
                        c = (2 * b + g) * 4 * (HD + 1)
                        ins = mm(ps[:, Y, c:c + 4 * (HD + 1)], ot[:, g, b * N:(b + 1) * N], compact[:].rearrange("p h c -> p (h c)"),
                                 start=True, stop=True)
                ins.then_inc(S["back"], 1)

            def turn_mixed(t):
                pe.wait_ge(S["mixed_ready"], t + 1)
                for b in range(GROUP):
                    ins = nc.tensor.transpose(ps[:, Y, b * N:(b + 1) * N], mixed[:, b, :], k.ident[:])
                ins.then_inc(S["mt_made"], 1)

            def outputs(t):
                pe.wait_ge(S["mt_ready"], t + 1)
                for b in range(GROUP):
                    ins = mm(ps[:, Y, b * D:(b + 1) * D], mt[:, b * N:(b + 1) * N], wo[:], start=True, stop=True)
                ins.then_inc(S["outed"], 1)

            def body(t, par, cur, prev, nxt):
                for u in range(UNITS):
                    if cur:
                        scores(t, par, u)
                    if u >= 2 and cur:
                        turn(t, u - 2)
                    if u < 2 and prev:
                        turn(t - 1, UNITS + u - 2)
                    if u >= 3 and cur:
                        values(t, par, u - 3)
                    if u < 3 and prev:
                        values(t - 1, 1 - par, UNITS + u - 3)
                    if u == 1 and nxt:
                        turn_x(t + 1)
                    if 2 <= u <= 6 and nxt:
                        project(t + 1, u - 2)
                    if u == 3 and prev:
                        turn_back(t - 1)
                    if u == 5 and prev:
                        turn_mixed(t - 1)
                    if u == 7 and prev:
                        outputs(t - 1)

            in_turn(pe, prelude, body)


def stage_l0_ffn(k):
    nc, w = k.nc, k.w
    H, G, A1 = 8, 64, D + 1
    PAIRS = H // 2
    with Scope(nc, "l0f") as s:
        slice_map = s.sb("slice_map", [A1, H, G])
        pair_map = s.sb("pair_map", [A1, H, A1])
        value_map = s.sb("value_map", [A1, H, D])
        fold_l0_ffn(k, slice_map, pair_map, value_map)
        xs = s.sb("xs", [P, GROUP, A1])
        xt = s.sb("xt", [A1, TOK])
        sw = s.sb("sw", [P, GROUP, H, G])
        sw_t = s.sb("sw_t", [P, GROUP, PAIRS, N])
        top = s.sb("top", [P, GROUP, H, 1])
        den = s.sb("den", [P, GROUP, H, 1])
        rden = s.sb("rden", [P, GROUP, H, 1])
        znorm = s.sb("znorm", [P, GROUP, PAIRS, 1])
        z = s.sb("z", [P, GROUP, PAIRS, A1])
        z_t = s.sb("z_t", [A1, GROUP, H, G])
        za = s.sb("za", [A1, GROUP, H, G])
        vals = s.sb("vals", [P, GROUP, 2, 2, D])
        att = s.sb("att", [P, GROUP, PAIRS, G])
        atop = s.sb("atop", [P, GROUP, PAIRS, 1])
        aden = s.sb("aden", [P, GROUP, PAIRS, 1])
        att_t = s.sb("att_t", [P, GROUP, 2, P])
        y = s.sb("y", [P, GROUP, PAIRS, D])
        ps = s.ps("ps", [P, 8, 512])
        names = ("step normed xt_made xt_ready logit shifted exped weighted swt_made swt_ready z_made z_ready zt_made zt_ready "
                 "za_made za_ready val_made val_ready sc_made sc_shifted sc_exped att_ready att_made att_t_ready y_made y_ready outed apart").split()
        S = {n: s.sem(n) for n in names}
        block = s.block()

        def view(bank, cols, *dims):
            a = ps[:, bank, 0:cols]
            if len(dims) == 1:
                return a.rearrange("p (a b) -> p a b", b=dims[0])
            return a.rearrange("p (a b c) -> p a b c", b=dims[0], c=dims[1])

        XT, LOG, SWT, Z, ZT, ZA, VAL, SC, AT, Y, OUT = 0, 1, 3, 5, (7, 0), 1, 3, 5, (7, 0), 1, 3

        @block.vector
        def _(dve):
            link = Link(dve, S["step"])
            link(nc.vector.memset(xs[:, :, D:A1], 1.0))
            PER = 1 + GROUP * 10
            with dve.Fori(0, GROUPS) as t:
                link = Link(dve, S["step"], 1 + PER * t, PER)
                front_dve(k, dve, xs[:], t, S["normed"])

                def shift(b):
                    dve.wait_ge(S["logit"], GROUP * t + b + 1)
                    lg = view(LOG + b % 2, 512, G)
                    link(nc.vector.tensor_reduce(top[:, b, :, 0], lg, AX, ALU.max))
                    nc.vector.tensor_tensor(sw[:, b], lg, bc(top[:, b], [P, H, G]), ALU.subtract).then_inc(S["shifted"], 1)

                def weigh(b):
                    dve.wait_ge(S["exped"], GROUP * t + b + 1)
                    link(nc.vector.tensor_reduce(den[:, b, :, 0], sw[:, b], AX, ALU.add))
                    link(nc.vector.reciprocal(rden[:, b], den[:, b]))
                    link(nc.vector.tensor_tensor(sw[:, b], sw[:, b], bc(rden[:, b], [P, H, G]), ALU.mult))
                    nc.vector.sem_inc(S["weighted"], 1)

                for b in range(GROUP + 1):
                    if b < GROUP:
                        shift(b)
                    if b >= 1:
                        weigh(b - 1)
                for b in range(GROUP):
                    dve.wait_ge(S["z_made"], GROUP * t + b + 1)
                    zz = view(Z + b % 2, PAIRS * A1, A1)
                    link(nc.vector.tensor_scalar(znorm[:, b], zz[:, :, D:A1], 1e-5, None, ALU.add))
                    link(nc.vector.reciprocal(znorm[:, b], znorm[:, b]))
                    link(nc.vector.tensor_tensor(z[:, b], zz, bc(znorm[:, b], [P, PAIRS, A1]), ALU.mult))
                    nc.vector.sem_inc(S["z_ready"], 1)
                for b in range(GROUP):
                    dve.wait_ge(S["val_made"], GROUP * t + b + 1)
                    nc.vector.tensor_copy(vals[:, b], view(VAL + b % 2, 256, 2, D)).then_inc(S["val_ready"], 1)

                def sc_shift(b):
                    dve.wait_ge(S["sc_made"], GROUP * t + b + 1)
                    sc = view(SC + b % 2, 256, G)
                    link(nc.vector.tensor_reduce(atop[:, b, :, 0], sc, AX, ALU.max))
                    nc.vector.tensor_tensor(att[:, b], sc, bc(atop[:, b], [P, PAIRS, G]), ALU.subtract).then_inc(S["sc_shifted"], 1)

                def sc_weigh(b):
                    dve.wait_ge(S["sc_exped"], GROUP * t + b + 1)
                    link(nc.vector.tensor_reduce(aden[:, b, :, 0], att[:, b], AX, ALU.add))
                    link(nc.vector.reciprocal(aden[:, b], aden[:, b]))

                for b in range(GROUP + 1):
                    if b < GROUP:
                        sc_shift(b)
                    if b >= 1:
                        sc_weigh(b - 1)
                for b in range(GROUP):
                    dve.wait_ge(S["y_made"], GROUP * t + b + 1)
                    for q in range(2):
                        yy = view(Y + 2 * (b % 2) + q, 128, D)
                        ins = nc.vector.tensor_tensor(y[:, b].rearrange("p (j q) o -> p q j o", q=2)[:, q], yy,
                                                      bc(aden[:, b].rearrange("p (j q) o -> p q j o", q=2)[:, q], [P, 2, D]), ALU.mult)
                    ins.then_inc(S["y_ready"], 1)
                dve.wait_ge(S["outed"], t + 1)
                g = bass.ds(GROUP * t, GROUP)
                link(nc.vector.tensor_tensor(k.h[:, g, :], k.h[:, g, :], view(OUT + 2, 256, D), ALU.add))
                link.close()

        @block.scalar
        def _(act):
            with act.Fori(0, GROUPS) as t:
                act.wait_ge(S["xt_made"], t + 1)
                nc.scalar.copy(xt[:], ps[0:A1, XT, :]).then_inc(S["xt_ready"], 1)
                for b in range(GROUP):
                    act.wait_ge(S["shifted"], GROUP * t + b + 1)
                    nc.scalar.activation(sw[:, b], sw[:, b], ACT.Exp).then_inc(S["exped"], 1)
                for b in range(GROUP):
                    act.wait_ge(S["swt_made"], GROUP * t + b + 1)
                    nc.scalar.copy(sw_t[:, b], view(SWT + b % 2, 512, N)).then_inc(S["swt_ready"], 1)
                for b in range(GROUP):
                    act.wait_ge(S["zt_made"], GROUP * t + b + 1)
                    nc.scalar.copy(z_t[:, b], view(ZT[b % 2], 512, G)[0:A1]).then_inc(S["zt_ready"], 1)
                for b in range(GROUP):
                    act.wait_ge(S["za_made"], GROUP * t + b + 1)
                    nc.scalar.copy(za[:, b], view(ZA + b % 2, 512, G)[0:A1]).then_inc(S["za_ready"], 1)
                for b in range(GROUP):
                    act.wait_ge(S["sc_shifted"], GROUP * t + b + 1)
                    nc.scalar.activation(att[:, b], att[:, b], ACT.Exp).then_inc(S["sc_exped"], 1)
                for b in range(GROUP):
                    act.wait_ge(S["att_made"], GROUP * t + b + 1)
                    nc.scalar.copy(att_t[:, b], view(AT[b % 2], 256, P)).then_inc(S["att_t_ready"], 1)

        @block.tensor
        def _(pe):
            mm = nc.tensor.matmul
            with pe.Fori(0, GROUPS) as t:
                def free(sem, b):
                    if b >= 2:
                        pe.wait_ge(S[sem], GROUP * t + b - 1)

                pe.wait_ge(S["normed"], t + 1)
                for b in range(GROUP):
                    ins = nc.tensor.transpose(ps[0:A1, XT, b * N:(b + 1) * N], xs[:, b, :], k.ident[:])
                ins.then_inc(S["xt_made"], 1)
                pe.wait_ge(S["xt_ready"], t + 1)
                for b in range(GROUP):
                    free("shifted", b)
                    mm(ps[:, LOG + b % 2, :], xt[:, b * N:(b + 1) * N], slice_map[:].rearrange("p h g -> p (h g)"),
                       start=True, stop=True).then_inc(S["logit"], 1)
                for b in range(GROUP):
                    pe.wait_ge(S["weighted"], GROUP * t + b + 1)
                    free("swt_ready", b)
                    for q in range(PAIRS):
                        ins = nc.tensor.transpose(view(SWT + b % 2, 512, N)[:, q], sw[:, b, 2 * q:2 * q + 2].rearrange("p h g -> p (h g)"), k.ident[:])
                    ins.then_inc(S["swt_made"], 1)
                    free("z_ready", b)
                    for q in range(PAIRS):
                        ins = mm(view(Z + b % 2, PAIRS * A1, A1)[:, q], sw[:, b, 2 * q:2 * q + 2].rearrange("p h g -> p (h g)"),
                                 xs[:, b, :], start=True, stop=True)
                    ins.then_inc(S["z_made"], 1)
                for b in range(GROUP):
                    pe.wait_ge(S["z_ready"], GROUP * t + b + 1)
                    free("zt_ready", b)
                    for q in range(PAIRS):
                        ins = nc.tensor.transpose(view(ZT[b % 2], 512, N)[0:A1, q], z[:, b, q], k.ident[:])
                    ins.then_inc(S["zt_made"], 1)
                for b in range(GROUP):
                    pe.wait_ge(S["zt_ready"], GROUP * t + b + 1)
                    free("za_ready", b)
                    for h in range(H):
                        ins = mm(view(ZA + b % 2, 512, G)[0:A1, h], pair_map[:, h], z_t[:, b, h], start=True, stop=True)
                    ins.then_inc(S["za_made"], 1)
                    free("val_ready", b)
                    if b < 2:
                        pe.wait_ge(S["swt_ready"], GROUP * t + GROUP)
                    for h in range(H):
                        pr, sub = h // 2, h % 2
                        r = 64 * (pr % 2)
                        ins = mm(view(VAL + b % 2, 256, 2, D)[r:r + 64, pr // 2, sub], z_t[:, b, h], value_map[:, h], start=True, stop=True)
                    ins.then_inc(S["val_made"], 1)
                for b in range(GROUP):
                    pe.wait_ge(S["za_ready"], GROUP * t + b + 1)
                    free("sc_shifted", b)
                    for h in range(H):
                        r = 64 * (h % 2)
                        ins = mm(view(SC + b % 2, 256, G)[r:r + 64, h // 2], za[:, b, h], z_t[:, b, h], start=True, stop=True)
                    ins.then_inc(S["sc_made"], 1)
                for b in range(GROUP):
                    pe.wait_ge(S["sc_exped"], GROUP * t + b + 1)
                    free("att_t_ready", b)
                    for j in range(2):
                        ins = nc.tensor.transpose(view(AT[b % 2], 256, P)[:, j], att[:, b, 2 * j:2 * j + 2].rearrange("p a g -> p (a g)"), k.ident[:])
                    ins.then_inc(S["att_made"], 1)
                for b in range(GROUP):
                    pe.wait_ge(S["att_t_ready"], GROUP * t + b + 1)
                    if b == 0:
                        pe.wait_ge(S["val_ready"], GROUP * t + GROUP)
                    free("y_ready", b)
                    nc.tensor.sem_inc(S["apart"], 1)
                    for h in range(H):
                        pr, sub = h // 2, h % 2
                        r, o = 64 * (pr % 2), 64 * sub
                        ins = mm(view(Y + 2 * (b % 2) + pr % 2, 128, D)[o:o + 64, pr // 2], att_t[r:r + 64, b, pr // 2, o:o + 64],
                                 vals[r:r + 64, b, pr // 2, sub], start=True, stop=True, tile_position=(r, o))
                    ins.then_inc(S["y_made"], 1)
                for b in range(GROUP):
                    pe.wait_ge(S["y_ready"], GROUP * t + b + 1)
                    for q in range(PAIRS):
                        ins = mm(view(OUT + 2, 256, D)[:, b], sw_t[:, b, q], y[:, b, q], start=(q == 0), stop=(q == PAIRS - 1))
                ins.then_inc(S["outed"], 1)


def fold_l0_ffn(k, slice_map, pair_map, value_map):
    nc, w = k.nc, k.w
    H, G, A1 = 8, 64, D + 1
    with Scope(nc, "l0fold") as s:
        fx = s.sb("fx", [A1, H, D])
        wx = s.sb("wx", [A1, H, D])
        fx_t = s.sb("fx_t", [D, H, A1])
        wx_t = s.sb("wx_t", [D, H, A1])
        wsl, wq, wk, wv = (s.sb(n, [D, D]) for n in ("wsl", "wq", "wk", "wv"))
        wout = s.sb("wout", [D, H, D])
        bsl = s.sb("bsl", [A1, G])
        temp = s.sb("temp", [A1, H, 1])
        bout = s.sb("bout", [P, 1, D])
        proj = s.sb("proj", [D, 3, H, A1])
        ps = s.ps("ps", [P, 8, 512])
        loaded, step, made, ready = s.sem("loaded"), s.sem("step"), s.sem("made"), s.sem("ready")
        block = s.block()

        def maps(first):
            return [ps[0:D, first + j, 0:4 * A1].rearrange("p (h c) -> p h c", c=A1) for j in range(2)]

        @block.sync
        def _(sp):
            n = 0
            for dst, src in ((fx, "fx"), (wx, "x")):
                sp.dma_start(dst[0:D], w[f"L0_ffn_W_{src}"].rearrange("i (h d) -> i h d", d=D)).then_inc(loaded, 16)
                sp.dma_start(dst[D:A1], w[f"L0_ffn_b_{src}"].rearrange("(o h d) -> o h d", o=1, d=D)).then_inc(loaded, 16)
            for dst, src in ((wsl, "W_slice"), (wq, "W_q"), (wk, "W_k"), (wv, "W_v")):
                sp.dma_start(dst[:], w[f"L0_ffn_{src}"]).then_inc(loaded, 16)
            sp.dma_start(wout[:], w["L0_ffn_W_out"].rearrange("(h d) o -> d h o", d=D)).then_inc(loaded, 16)
            sp.dma_start(bsl[D:A1, :], w["L0_ffn_b_slice"].rearrange("(o g) -> o g", o=1)).then_inc(loaded, 16)
            sp.dma_start(temp[:, :, 0], w["L0_ffn_temperature"].rearrange("a h b c -> (a h b c)").partition_broadcast(A1)).then_inc(loaded, 16)
            sp.dma_start(bout[:, 0, :], w["L0_ffn_b_out"].partition_broadcast(P)).then_inc(loaded, 16)

        LOADED = 16 * 12

        @block.vector
        def _(dve):
            link = Link(dve, step)
            dve.wait_ge(loaded, LOADED)
            link(nc.vector.tensor_tensor(k.h[:], k.h[:], bc(bout[:], [P, SEQS, D]), ALU.add))
            link(nc.vector.tensor_scalar(temp[:], temp[:], 0.1, 5.0, ALU.max, ALU.min))
            link(nc.vector.reciprocal(temp[:], temp[:]))
            dve.wait_ge(made, 1)
            for j in range(2):
                link(nc.vector.tensor_copy(fx_t[:, 4 * j:4 * j + 4], maps(0)[j]))
                link(nc.vector.tensor_copy(wx_t[:, 4 * j:4 * j + 4], maps(2)[j]))
            nc.vector.sem_inc(ready, 1)
            dve.wait_ge(made, 2)
            for n in range(3):
                for j in range(2):
                    src = maps(2 * n)[j]
                    if n == 0:
                        link(nc.vector.tensor_scalar(proj[:, n, 4 * j:4 * j + 4], src, D ** -0.5, None, ALU.mult))
                    else:
                        link(nc.vector.tensor_copy(proj[:, n, 4 * j:4 * j + 4], src))
            sl = ps[0:A1, 6, :].rearrange("p (h g) -> p h g", g=G)
            link(nc.vector.tensor_copy(slice_map[:], sl))
            link(nc.vector.tensor_tensor(slice_map[D:A1], slice_map[D:A1],
                                         bc(bsl[D:A1, :].rearrange("p (o g) -> p o g", o=1), [1, H, G]), ALU.add))
            link(nc.vector.tensor_tensor(slice_map[:], slice_map[:], bc(temp[:], [A1, H, G]), ALU.mult))
            nc.vector.sem_inc(ready, 1)
            dve.wait_ge(made, 3)
            for j in range(2):
                link(nc.vector.tensor_copy(pair_map[:, 4 * j:4 * j + 4], ps[0:A1, j, 0:4 * A1].rearrange("p (h c) -> p h c", c=A1)))
            link(nc.vector.tensor_copy(value_map[:], ps[0:A1, 2, :].rearrange("p (h o) -> p h o", o=D)))

        @block.tensor
        def _(pe):
            mm = nc.tensor.matmul
            pe.wait_ge(loaded, LOADED)
            for h in range(H):
                nc.tensor.transpose(maps(0)[h // 4][:, h % 4], fx[:, h], k.ident[0:A1, 0:A1])
                ins = nc.tensor.transpose(maps(2)[h // 4][:, h % 4], wx[:, h], k.ident[0:A1, 0:A1])
            ins.then_inc(made, 1)
            pe.wait_ge(ready, 1)
            for n, wt in enumerate((wq, wk, wv)):
                for j in range(2):
                    mm(maps(2 * n)[j], wt[:], fx_t[:, 4 * j:4 * j + 4], start=True, stop=True)
            for h in range(H):
                ins = mm(ps[0:A1, 6, h * G:(h + 1) * G], wx_t[:, h], wsl[:], start=True, stop=True)
            ins.then_inc(made, 1)
            pe.wait_ge(ready, 2)
            for h in range(H):
                mm(ps[0:A1, h // 4, (h % 4) * A1:(h % 4 + 1) * A1], proj[:, 0, h], proj[:, 1, h], start=True, stop=True)
                ins = mm(ps[0:A1, 2, h * D:(h + 1) * D], proj[:, 2, h], wout[:, h], start=True, stop=True)
            ins.then_inc(made, 1)


def stage_edge_cells(k):
    nc, w = k.nc, k.w
    E = w["L1_attn_edge_index"].shape[1]
    BS = 32
    LANE = E // P
    CPL = LANE // P
    UN = 2
    CB = UN * CPL
    STEPS = P // (2 * UN)
    HEADS = 4
    assert CPL == 16
    keys_dram = nc.dram_tensor("edge_keys", (E // P, P), F32).ap()
    with Scope(nc, "cells") as s:
        r_t = s.sb("r_t", [P, P, CPL, 1], BF16)
        c_t = s.sb("c_t", [P, P, CPL, 1], BF16)
        stored = s.sem("stored")
        with Scope(nc, "cellkeys") as s1:
            rows = s1.sb("rows", [P, LANE], I32)
            cols = s1.sb("cols", [P, LANE], I32)
            away = s1.sb("away", [P, LANE], I32)
            key = s1.sb("key", [P, LANE])
            rf = s1.sb("rf", [P, LANE])
            rb = s1.sb("rb", [P, CPL, P], BF16)
            cb = s1.sb("cb", [P, CPL, P], BF16)
            identb = s1.sb("identb", [P, P], BF16)
            ps = s1.ps("ps", [P, 4, 8, P], BF16)
            loaded, step, keyed, turned, copied = (s1.sem(n) for n in "loaded step keyed turned copied".split())
            block = s1.block()

            @block.sync
            def _(sp):
                sp.dma_start(rows[:], w["L1_attn_edge_index"][0].rearrange("(p f) -> p f", p=P)).then_inc(loaded, 16)
                sp.dma_start(cols[:], w["L1_attn_edge_index"][1].rearrange("(p f) -> p f", p=P)).then_inc(loaded, 16)
                sp.wait_ge(keyed, 1)
                sp.dma_start(keys_dram.rearrange("(p c) f -> p (c f)", p=P), key[:]).then_inc(stored, 16)
                sp.wait_ge(stored, 16)

            @block.vector
            def _(dve):
                link = Link(dve, step)
                link(nc.vector.tensor_copy(identb[:], k.ident[:]))
                dve.wait_ge(loaded, 32)
                link(nc.vector.tensor_tensor(away[:], rows[:], cols[:], ALU.bitwise_xor))
                link(nc.vector.tensor_scalar(away[:], away[:], 5, None, ALU.logical_shift_right))
                link(nc.vector.tensor_scalar(cols[:], cols[:], BS - 1, None, ALU.bitwise_and))
                link(nc.vector.tensor_scalar(rf[:], away[:], 1.0, 128.0, ALU.min, ALU.mult))
                link(nc.vector.tensor_tensor(rf[:], rf[:], rows[:], ALU.add))
                link(nc.vector.tensor_scalar(rf[:], rf[:], 128.0, None, ALU.min))
                link(nc.vector.scalar_tensor_tensor(out=key[:], in0=rf[:], scalar=float(BS), in1=cols[:], op0=ALU.mult, op1=ALU.add))
                nc.vector.tensor_copy(rb[:].rearrange("p c f -> p (c f)"), rf[:]).then_inc(keyed, 1)
                nc.vector.tensor_copy(cb[:].rearrange("p c f -> p (c f)"), cols[:]).then_inc(keyed, 1)
                for n in range(4):
                    dst = (r_t, c_t)[n // 2]
                    dve.wait_ge(turned, n + 1)
                    nc.vector.tensor_copy(dst[:, :, 8 * (n % 2):8 * (n % 2) + 8, 0].rearrange("f p c -> f c p"), ps[:, n]).then_inc(copied, 1)
                dve.wait_ge(copied, 4)

            @block.tensor
            def _(pe):
                pe.wait_ge(keyed, 2)
                for n in range(4):
                    src = (rb, cb)[n // 2]
                    for j in range(8):
                        ins = nc.tensor.transpose(ps[:, n, j], src[:, 8 * (n % 2) + j], identb[:])
                    ins.then_inc(turned, 1)

        with Scope(nc, "cellhits") as s2:
            hits = s2.sb("hits", [P, P, BS])
            with Scope(nc, "cellcount") as s3:
                tok_i = s3.sb("tok_i", [P, 1, P])
                tok = s3.sb("tok", [P, 1, P], BF16)
                power = s3.sb("power", [P, 1, CPL, 1], BF16)
                rhot = s3.sb("rhot", [P, 2, CB, P], BF16)
                chot = s3.sb("chot", [P, 2, UN, CPL, BS], BF16)
                ps = s3.ps("ps", [P, 2, 512])
                step, iotad, hot, counted, taken = (s3.sem(n) for n in "step iotad hot counted taken".split())
                block = s3.block()

                @block.gpsimd
                def _(pool):
                    nc.gpsimd.iota(tok_i[:, 0, :], [[1, P]], 0, 0, allow_small_or_imprecise_dtypes=True).then_inc(iotad, 1)

                @block.vector
                def _(dve):
                    link = Link(dve, step)
                    for b in range(CPL):
                        link(nc.vector.memset(power[:, :, b, :], 2.0 ** (8 * (b - 8))))
                    dve.wait_ge(iotad, 1)
                    link(nc.vector.tensor_copy(tok[:], tok_i[:]))
                    BASE = CPL + 1
                    with dve.Fori(0, STEPS) as t:
                        link = Link(dve, step, BASE + 2 * t, 2)
                        for j in range(2):
                            lanes = bass.ds(2 * UN * t + UN * j, UN)
                            rr = r_t[:, lanes].rearrange("p l c o -> p (l c) o")
                            nc.vector.tensor_tensor(rhot[:, j], bc(rr, [P, CB, P]), bc(tok[:], [P, CB, P]), ALU.is_equal).then_inc(hot, 1)
                            cc = c_t[:, lanes]
                            link(nc.vector.tensor_tensor(chot[:, j].rearrange("p l c k -> p (l c) k"),
                                                         bc(cc.rearrange("p l c o -> p (l c) o"), [P, CB, BS]),
                                                         bc(tok[:, :, 0:BS], [P, CB, BS]), ALU.is_equal))
                            nc.vector.tensor_tensor(chot[:, j], chot[:, j], bc(power[:], [P, UN, CPL, BS]), ALU.mult).then_inc(hot, 1)
                            dve.wait_ge(counted, 2 * t + j + 1)
                        link.close()

                @block.tensor
                def _(pe):
                    with pe.Fori(0, STEPS) as t:
                        for j in range(2):
                            pe.wait_ge(hot, 2 * (2 * t + j) + 2)
                            for l in range(UN):
                                for b in range(CPL):
                                    ins = nc.tensor.matmul(ps[:, j, l * BS:(l + 1) * BS], rhot[:, j, l * CPL + b], chot[:, j, l, b],
                                                           start=(b == 0), stop=(b == CPL - 1))
                            ins.then_inc(counted, 1)
                            pe.wait_ge(taken, 2 * t + j + 1)

                @block.scalar
                def _(act):
                    with act.Fori(0, STEPS) as t:
                        for j in range(2):
                            act.wait_ge(counted, 2 * t + j + 1)
                            nc.scalar.copy(hits[:, bass.ds(2 * UN * t + UN * j, UN), :],
                                           ps[:, j, 0:UN * BS].rearrange("p (l k) -> p l k", l=UN)).then_inc(taken, 1)

            with Scope(nc, "cellfind") as s4:
                expo = s4.sb("expo", [P, P, BS], I32)
                lane = s4.sb("lane", [P, P, 1])
                last = s4.sb("last", [P, BS])
                found = s4.sb("found", [P, BS])
                number = s4.sb("number", [P, BS])
                last_i = s4.sb("last_i", [P, 2, BS], I32)
                chunk = s4.sb("chunk", [P, BS], U32)
                keys = s4.sb("keys", [P, BS, P])
                vals = s4.sb("vals", [P, BS, P])
                cell = s4.sb("cell", [P, BS, 1])
                place = s4.sb("place", [P, 1, P])
                at = s4.sb("at", [P, BS, 1])
                col = s4.sb("col", [P, BS])
                row_i = s4.sb("row_i", [P, 1], I32)
                row_f = s4.sb("row_f", [P, 1])
                diag = s4.sb("diag", [P, BS])
                off = s4.sb("off", [P, BS])
                mask = s4.sb("mask", [P, BS + 1])
                feats = s4.sb("feats", [P, 4, BS + 1])
                pos = s4.sb("pos", [P, BS, 3])
                pos_r = s4.sb("pos_r", [P, 3])
                gw = s4.sb("gw", [P, HEADS, 4])
                gb = s4.sb("gb", [P, HEADS])
                loaded, iotad, step, chunked = (s4.sem(n) for n in "loaded iotad step chunked".split())
                fetched = k.chunks_fetched
                block = s4.block()

                @block.sync
                def _(sp):
                    for n in range(P // BS):
                        sp.dma_start(pos[n * BS:(n + 1) * BS].rearrange("p c x -> p (c x)"),
                                     w["L1_attn_positions"][n * BS:(n + 1) * BS].rearrange("c x -> (c x)").partition_broadcast(BS)).then_inc(loaded, 16)
                    sp.dma_start(pos_r[:], w["L1_attn_positions"][0:P]).then_inc(loaded, 16)
                    sp.dma_start(gw[:], w["L1_attn_gate_w"].partition_broadcast(P)).then_inc(loaded, 16)
                    sp.dma_start(gb[:], w["L1_attn_gate_b"].partition_broadcast(P)).then_inc(loaded, 16)

                @block.gpsimd
                def _(pool):
                    imp = dict(allow_small_or_imprecise_dtypes=True)
                    nc.gpsimd.iota(lane[:, :, 0], [[256, P]], 0, 0, **imp).then_inc(iotad, 1)
                    nc.gpsimd.iota(cell[:, :, 0], [[1, BS]], 0, BS, **imp).then_inc(iotad, 1)
                    nc.gpsimd.iota(place[:, 0, :], [[1, P]], 1, 0, **imp).then_inc(iotad, 1)
                    nc.gpsimd.iota(col[:], [[1, BS]], 0, 0, **imp).then_inc(iotad, 1)
                    nc.gpsimd.iota(row_i[:], [[0, 1]], 0, 1).then_inc(iotad, 1)
                    pool.wait_ge(chunked, 1)
                    for c in range(BS):
                        index = bass.IndirectOffsetOnAxis(chunk[:, c:c + 1], 0)
                        nc.gpsimd.indirect_dma_start(keys[:, c, :], None, keys_dram, index).then_inc(fetched, 16)
                        nc.gpsimd.indirect_dma_start(vals[:, c, :], None, w["L1_attn_edge_values"].rearrange("(c f) -> c f", f=P),
                                                     index).then_inc(fetched, 16)

                @block.vector
                def _(dve):
                    link = Link(dve, step)
                    v = nc.vector
                    full = [P, P, BS]
                    dve.wait_ge(iotad, 5)
                    link(v.tensor_scalar(expo[:], hits[:].bitcast(I32), 23, None, ALU.logical_shift_right))
                    link(v.scalar_tensor_tensor(out=hits[:], in0=expo[:], scalar=1.0, in1=bc(lane[:], full), op0=ALU.min, op1=ALU.mult))
                    link(v.tensor_tensor(hits[:], hits[:], expo[:], ALU.add))
                    link(v.tensor_reduce(last[:], hits[:].rearrange("r p c -> r c p"), AX, ALU.max))
                    link(v.tensor_scalar(found[:], last[:], 1.0, None, ALU.min))
                    link(v.tensor_copy(last_i[:, 0], last[:]))
                    link(v.tensor_scalar(last_i[:, 1], last_i[:, 0], 255, None, ALU.bitwise_and))
                    link(v.tensor_scalar(last_i[:, 0], last_i[:, 0], 8, None, ALU.logical_shift_right))
                    link(v.tensor_scalar(number[:], last_i[:, 1], -63.0, 0.0, ALU.add, ALU.max))
                    link(v.tensor_copy(last_i[:, 1], number[:]))
                    link(v.tensor_scalar(last_i[:, 1], last_i[:, 1], 3, None, ALU.logical_shift_right))
                    link(v.scalar_tensor_tensor(out=number[:], in0=last_i[:, 0], scalar=float(CPL), in1=last_i[:, 1], op0=ALU.mult, op1=ALU.add))
                    v.tensor_copy(chunk[:], number[:]).then_inc(chunked, 1)
                    link(v.tensor_scalar(row_i[:], row_i[:], BS - 1, None, ALU.bitwise_and))
                    link(v.tensor_copy(row_f[:], row_i[:]))
                    link(v.tensor_scalar(diag[:], col[:], row_f[:, 0:1], None, ALU.is_equal))
                    link(v.tensor_scalar(off[:], diag[:], -1.0, 1.0, ALU.mult, ALU.add))
                    link(v.memset(mask[:], 1.0))
                    link(v.tensor_tensor(mask[:, 0:BS], diag[:], found[:], ALU.max))
                    link(v.tensor_tensor(off[:], off[:], found[:], ALU.mult))
                    link(v.memset(feats[:], 0.0))
                    link(v.memset(feats[:, 3, BS:BS + 1], 1.0))
                    dve.wait_ge(loaded, 16 * 7)
                    for x in range(3):
                        link(v.tensor_scalar(feats[:, x, 0:BS], pos[:, :, x], pos_r[:, x:x + 1], None, ALU.subtract))
                        link(v.tensor_tensor(feats[:, x, 0:BS], feats[:, x, 0:BS], off[:], ALU.mult))
                    dve.wait_ge(fetched, 16 * 2 * BS)
                    one = [P, BS, P]
                    link(v.tensor_tensor(keys[:], keys[:], bc(cell[:], one), ALU.is_equal))
                    link(v.tensor_tensor(keys[:], keys[:], bc(place[:], one), ALU.mult))
                    link(v.tensor_reduce(at[:, :, 0], keys[:], AX, ALU.max))
                    link(v.tensor_scalar(at[:], at[:], 1.0, None, ALU.max))
                    link(v.tensor_tensor(keys[:], bc(place[:], one), bc(at[:], one), ALU.is_equal))
                    link(v.tensor_tensor(vals[:], vals[:], keys[:], ALU.mult))
                    link(v.tensor_reduce(number[:], vals[:], AX, ALU.add))
                    link(v.tensor_tensor(number[:], number[:], off[:], ALU.mult))
                    link(v.tensor_tensor(feats[:, 3, 0:BS], number[:], diag[:], ALU.add))
                    link(v.tensor_scalar(k.edge_score[:], mask[:], -MASKED, MASKED, ALU.mult, ALU.add))
                    link(v.tensor_tensor(k.edge_score[:], k.edge_score[:], feats[:, 3], ALU.add))
                    for h in range(HEADS):
                        g = k.edge_gate[:, h]
                        link(v.tensor_scalar(g, feats[:, 0], gw[:, h, 0:1], gb[:, h:h + 1], ALU.mult, ALU.add))
                        for x in range(1, 4):
                            link(v.scalar_tensor_tensor(out=g, in0=feats[:, x], scalar=gw[:, h, x:x + 1], in1=g, op0=ALU.mult, op1=ALU.add))
                        link(v.tensor_tensor(g, g, mask[:], ALU.mult))


def stage_l1_attn(k):
    nc, w = k.nc, k.w
    HEADS, HD, BS, A1 = 4, 16, 32, D + 1
    NB = N // BS
    KEYS = BS + 1
    with Scope(nc, "l1a") as s:
        k.edge_score = s.sb("edge_score", [P, 1, KEYS])
        k.edge_gate = s.sb("edge_gate", [P, HEADS, 1, KEYS])
        score_view, gate_view = k.edge_score, k.edge_gate
        k.edge_score, k.edge_gate = k.edge_score[:, 0], k.edge_gate[:, :, 0]
        stage_edge_cells(k)
        wnat = s.sb("wnat", [D, 4, A1])
        wq = s.sb("wq", [A1, HEADS, 32])
        wk = s.sb("wk", [A1, HEADS, 32])
        wv = s.sb("wv", [A1, D])
        wo = s.sb("wo", [A1, D])
        blockmean = s.sb("blockmean", [P, P])
        xs = s.sb("xs", [P, GROUP, A1])
        xkv = s.sb("xkv", [A1, TOK + GROUP * NB])
        q = s.sb("q", [P, GROUP * NB, BS])
        kk = s.sb("kk", [P, GROUP * NB, KEYS])
        v = s.sb("v", [P, GROUP, D])
        sc = s.sb("sc", [P, HEADS, GROUP, KEYS])
        top = s.sb("top", [P, HEADS, GROUP, 1])
        den = s.sb("den", [P, HEADS, GROUP, 1])
        sct = s.sb("sct", [P, HEADS, GROUP, BS])
        scn = s.sb("scn", [P, HEADS, GROUP, BS])
        mixed = s.sb("mixed", [P, GROUP, A1])
        node = s.sb("node", [P, GROUP, HEADS, HD])
        mt = s.sb("mt", [A1, TOK])
        ps = s.ps("ps", [P, 8, 512])
        names = ("loaded step wturned wready normed xt_made xt_ready mean_ready projected q_ready k_ready v_ready "
                 "scored shifted exped combined noded valued mixed_ready mt_made mt_ready outed apart").split()
        S = {n: s.sem(n) for n in names}
        block = s.block()

        @block.sync
        def _(sp):
            qkv = w["L1_attn_qkv_w"].rearrange("(n o) i -> o n i", o=D)
            sp.dma_start(wnat[:, 0:3, 0:D], qkv).then_inc(S["loaded"], 16)
            sp.dma_start(wnat[:, 3, 0:D], w["L1_attn_proj_w"]).then_inc(S["loaded"], 16)
            for n in range(3):
                sp.dma_start(wnat[:, n, D:A1], w["L1_attn_qkv_b"].rearrange("(n o u) -> n o u", o=D, u=1)[n]).then_inc(S["loaded"], 16)
            sp.dma_start(wnat[:, 3, D:A1], w["L1_attn_proj_b"].rearrange("(o u) -> o u", u=1)).then_inc(S["loaded"], 16)

        @block.vector
        def _(dve):
            vec = nc.vector
            link = Link(dve, S["step"])
            link(vec.memset(wq[:], 0.0))
            link(vec.memset(wk[:], 0.0))
            link(vec.memset(xs[:, :, D:A1], 1.0))
            link(vec.memset(mixed[:, :, D:A1], 1.0))
            link(vec.memset(blockmean[:], 0.0))
            for n in range(NB):
                link(vec.memset(blockmean[n * BS:(n + 1) * BS, n * BS:(n + 1) * BS], 1.0 / BS))
            dve.wait_ge(S["wturned"], 1)
            wt = ps[0:A1, 0, 0:4 * D].rearrange("p (n h c) -> p n h c", n=4, h=HEADS)
            link(vec.tensor_scalar(wq[:, :, 0:HD], wt[:, 0], HD ** -0.5, None, ALU.mult))
            link(vec.tensor_copy(wk[:, :, 0:HD], wt[:, 1]))
            link(vec.tensor_copy(wv[:].rearrange("p (h c) -> p h c", h=HEADS), wt[:, 2]))
            link(vec.tensor_copy(wo[:].rearrange("p (h c) -> p h c", h=HEADS), wt[:, 3]))
            vec.sem_inc(S["wready"], 1)
            BASE = 5 + NB + 4
            PER = 10
            with dve.Fori(0, GROUPS) as t:
                link = Link(dve, S["step"], BASE + PER * t, PER)
                front_dve(k, dve, xs[:], t, S["normed"])
                dve.wait_ge(S["xt_ready"], t + 1)
                link(vec.tensor_reduce(xkv[:, TOK:], xkv[:, 0:TOK].rearrange("p (n c) -> p n c", c=BS), AX, ALU.add))
                link(vec.tensor_scalar(xkv[:, TOK:], xkv[:, TOK:], 1.0 / BS, None, ALU.mult))
                vec.sem_inc(S["mean_ready"], 1)
                dve.wait_ge(S["projected"], 4 * t + 3)
                vec.tensor_copy(kk[:, :, 0:BS], ps[:, 2, :].rearrange("p (n c) -> p n c", c=BS)).then_inc(S["k_ready"], 1)
                vec.tensor_copy(kk[:, :, BS], ps[:, 3, 0:GROUP * NB]).then_inc(S["k_ready"], 1)
                full = [P, HEADS, GROUP, KEYS]
                dve.wait_ge(S["scored"], t + 1)
                psc = ps[:, 4:8, 0:GROUP * KEYS].rearrange("p h (b c) -> p h b c", c=KEYS)
                for h in range(HEADS):
                    ins = vec.tensor_tensor(sc[:, h], psc[:, h], bc(score_view[:], [P, GROUP, KEYS]), ALU.add)
                link(ins)
                link(vec.tensor_reduce(top[:, :, :, 0], sc[:], AX, ALU.max))
                vec.tensor_tensor(sc[:], sc[:], bc(top[:], full), ALU.subtract).then_inc(S["shifted"], 1)
                dve.wait_ge(S["exped"], t + 1)
                link(vec.tensor_reduce(den[:, :, :, 0], sc[:], AX, ALU.add))
                link(vec.reciprocal(den[:], den[:]))
                link(vec.tensor_tensor(sc[:], sc[:], bc(den[:], full), ALU.mult))
                link(vec.tensor_tensor(sc[:], sc[:], bc(gate_view[:], full), ALU.add))
                link(vec.tensor_copy(scn[:], sc[:, :, :, 0:BS]))
                vec.transpose(sct[:].rearrange("p h b c -> p (h b c)"), scn[:].rearrange("p h b c -> p (h b c)")).then_inc(S["combined"], 1)
                dve.wait_ge(S["valued"], 2 * t + 1)
                weight = sc[:, :, :, BS:KEYS].rearrange("p h b c -> p b h c")
                vec.tensor_tensor(node[:], ps[:, 1, 0:256].rearrange("p (b h c) -> p b h c", b=GROUP, h=HEADS),
                                  bc(weight, [P, GROUP, HEADS, HD]), ALU.mult).then_inc(S["noded"], 1)
                dve.wait_ge(S["noded"], t + 1)
                dve.wait_ge(S["valued"], 2 * t + 2)
                vec.tensor_tensor(mixed[:, :, 0:D], ps[:, 2, 0:256].rearrange("p (b d) -> p b d", b=GROUP),
                                  node[:].rearrange("p b h c -> p b (h c)"), ALU.add).then_inc(S["mixed_ready"], 1)
                dve.wait_ge(S["outed"], t + 1)
                g = bass.ds(GROUP * t, GROUP)
                link(vec.tensor_tensor(k.h[:, g, :], k.h[:, g, :], ps[:, 3, 0:256].rearrange("p (b d) -> p b d", b=GROUP), ALU.add))
                link.close()

        @block.scalar
        def _(act):
            with act.Fori(0, GROUPS) as t:
                act.wait_ge(S["xt_made"], t + 1)
                nc.scalar.copy(xkv[:, 0:TOK], ps[0:A1, 0, :]).then_inc(S["xt_ready"], 1)
                act.wait_ge(S["projected"], 4 * t + 1)
                nc.scalar.copy(q[:].rearrange("p n c -> p (n c)"), ps[:, 1, :]).then_inc(S["q_ready"], 1)
                act.wait_ge(S["projected"], 4 * t + 4)
                nc.scalar.copy(v[:], ps[:, 0, 0:256].rearrange("p (b d) -> p b d", b=GROUP)).then_inc(S["v_ready"], 1)
                act.wait_ge(S["shifted"], t + 1)
                nc.scalar.activation(sc[:], sc[:], ACT.Exp).then_inc(S["exped"], 1)
                act.wait_ge(S["mt_made"], t + 1)
                nc.scalar.copy(mt[:], ps[0:A1, 0, :]).then_inc(S["mt_ready"], 1)

        @block.tensor
        def _(pe):
            mm = nc.tensor.matmul
            pe.wait_ge(S["loaded"], 16 * 6)
            for n in range(4):
                ins = nc.tensor.transpose(ps[0:A1, 0, n * D:(n + 1) * D], wnat[:, n, :], k.ident[0:D, 0:D])
            ins.then_inc(S["wturned"], 1)
            pe.wait_ge(S["wready"], 1)
            with pe.Fori(0, GROUPS) as t:
                pe.wait_ge(S["normed"], t + 1)
                for b in range(GROUP):
                    ins = nc.tensor.transpose(ps[0:A1, 0, b * N:(b + 1) * N], xs[:, b, :], k.ident[:])
                ins.then_inc(S["xt_made"], 1)
                pe.wait_ge(S["xt_ready"], t + 1)
                mm(ps[:, 1, :], wq[:].rearrange("p h c -> p (h c)"), xkv[:, 0:TOK], start=True, stop=True).then_inc(S["projected"], 1)
                pe.wait_ge(S["mean_ready"], t + 1)
                mm(ps[:, 2, :], wk[:].rearrange("p h c -> p (h c)"), xkv[:, 0:TOK], start=True, stop=True).then_inc(S["projected"], 1)
                mm(ps[:, 3, 0:GROUP * NB], wk[:].rearrange("p h c -> p (h c)"), xkv[:, TOK:], start=True, stop=True).then_inc(S["projected"], 1)
                for b in range(GROUP):
                    ins = mm(ps[:, 0, b * D:(b + 1) * D], xkv[:, b * N:(b + 1) * N], wv[:], start=True, stop=True)
                ins.then_inc(S["projected"], 1)
                pe.wait_ge(S["q_ready"], t + 1)
                pe.wait_ge(S["k_ready"], 2 * t + 2)
                nc.tensor.sem_inc(S["apart"], 1)
                for b in range(GROUP):
                    for n in range(NB):
                        for h in range(HEADS):
                            ins = mm(ps[n * BS:(n + 1) * BS, 4 + h, b * KEYS:(b + 1) * KEYS],
                                     q[32 * h:32 * h + 32, b * NB + n, :], kk[32 * h:32 * h + 32, b * NB + n, :],
                                     start=True, stop=True, tile_position=(32 * h, n * BS))
                ins.then_inc(S["scored"], 1)
                pe.wait_ge(S["v_ready"], t + 1)
                mm(ps[:, 1, 0:256], blockmean[:], v[:].rearrange("p b d -> p (b d)"), start=True, stop=True).then_inc(S["valued"], 1)
                pe.wait_ge(S["combined"], t + 1)
                nc.tensor.sem_inc(S["apart"], 1)
                for b in range(GROUP):
                    for h in range(HEADS):
                        for n in range(NB):
                            r = slice(n * BS, (n + 1) * BS)
                            ins = mm(ps[r, 2, b * D + h * HD:b * D + (h + 1) * HD], sct[r, h, b, :], v[r, b, h * HD:(h + 1) * HD],
                                     start=True, stop=True, tile_position=(n * BS, n * BS))
                ins.then_inc(S["valued"], 1)
                pe.wait_ge(S["mixed_ready"], t + 1)
                for b in range(GROUP):
                    ins = nc.tensor.transpose(ps[0:A1, 0, b * N:(b + 1) * N], mixed[:, b, :], k.ident[:])
                ins.then_inc(S["mt_made"], 1)
                pe.wait_ge(S["mt_ready"], t + 1)
                for b in range(GROUP):
                    ins = mm(ps[:, 3, b * D:(b + 1) * D], mt[:, b * N:(b + 1) * N], wo[:], start=True, stop=True)
                ins.then_inc(S["outed"], 1)


def stage_l1_ffn(k):
    nc, w = k.nc, k.w
    HEADS, SETS, HD, A1 = 4, 4, 16, D + 1
    UNITS = GROUP * HEADS
    with Scope(nc, "l1f") as s:
        wq = s.sb("wq", [A1, SETS, HEADS, 32])
        wk = s.sb("wk", [A1, HEADS, 32])
        wvs = s.sb("wvs", [A1, 2, HEADS, HD])
        fc1 = s.sb("fc1", [A1, D])
        fc2 = s.sb("fc2", [A1, D])
        gate_w = s.sb("gate_w", [P, 2, 8])
        fgate_w = s.sb("fgate_w", [D, HEADS])
        gate_b = s.sb("gate_b", [P, 1, HEADS * SETS])
        norms = s.sb("norms", [P, 4, 1, HD])
        causal = s.sb("causal", [P, 4, N], BF16)
        identb = s.sb("identb", [P, P], BF16)
        resid = s.sb("resid", [P, HEADS, HD])
        nhalf = s.sb("nhalf", [P, GROUP * HEADS, 1])
        fold_l1_ffn(k, wq, wk, wvs, fc1, fc2, gate_w, fgate_w, gate_b, norms, causal, identb, resid, nhalf)
        xs = s.sb("xs", [P, GROUP, A1])
        xt = s.sb("xt", [A1, TOK])
        q = s.sb("q", [P, SETS, TOK])
        kk = s.sb("kk", [P, TOK])
        v = s.sb("v", [P, GROUP, HEADS, HD + 1])
        live = s.sb("live", [P, GROUP, HEADS, 1, HD])
        top = s.sb("top", [P, 2, 4, 1])
        probs = s.sb("probs", [P, 2, 4, N])
        probs_t = s.sb("probs_t", [P, 2, 4, N])
        rden = s.sb("rden", [P, GROUP, HEADS, SETS, 1])
        out = s.sb("out", [P, GROUP, HEADS, SETS, HD])
        out_t = s.sb("out_t", [P, GROUP, 2, N])
        gs = s.sb("gs", [P, GROUP * HEADS, SETS, 1])
        gtop = s.sb("gtop", [P, GROUP * HEADS, 1])
        fx = s.sb("fx", [P, GROUP, A1])
        fh = s.sb("fh", [P, GROUP * HEADS, HD])
        sq = s.sb("sq", [P, GROUP * HEADS, HD])
        mom = s.sb("mom", [P, GROUP * HEADS, 1])
        var = s.sb("var", [P, GROUP * HEADS, 1])
        rstd = s.sb("rstd", [P, GROUP * HEADS, 1])
        nz = s.sb("nz", [P, GROUP, D])
        fx_t = s.sb("fx_t", [A1, TOK])
        nz_t = s.sb("nz_t", [D, TOK])
        h1_t = s.sb("h1_t", [A1, TOK])
        fo_t = s.sb("fo_t", [A1, TOK])
        fg = s.sb("fg", [P, GROUP, HEADS, 1])
        ftop = s.sb("ftop", [P, GROUP, 1])
        ps = s.ps("ps", [P, 8, 512])
        names = ("step normed xt_made xt_ready projected q_ready kv_ready scored topped shifted exped turned turned_ready valued "
                 "out_ready out_made out_t_ready gated gs_shifted gs_exped var_ready rooted fx_ready fx_made fx_t_ready h1_made "
                 "h1_ready h2_made fo_ready fo_made fo_t_ready fg_made fg_shifted fg_exped").split()
        S = {n: s.sem(n) for n in names}
        block = s.block()
        OB = (5, 6, 7, 0)

        def o_bank(b):
            return ps[:, OB[b], 0:HEADS * SETS * (HD + 1)].rearrange("p (h e c) -> p h e c", h=HEADS, e=SETS)

        def seqs(bank, cols):
            return ps[:, bank, 0:GROUP * cols].rearrange("p (b d) -> p b d", b=GROUP)

        @block.gpsimd
        def _(pool):
            with pool.Fori(0, GROUPS) as t:
                for j in range(2):
                    pool.wait_ge(S["var_ready"], 2 * t + j + 1)
                    nc.gpsimd.tensor_tensor(rstd[:], var[:], nhalf[:], ALU.pow).then_inc(S["rooted"], 1)

        @block.vector
        def _(dve):
            vec = nc.vector
            link = Link(dve, S["step"])
            link(vec.memset(xs[:, :, D:A1], 1.0))
            link(vec.memset(fx[:, :, D:A1], 1.0))
            link(vec.memset(h1_t[D:A1, :], 1.0))
            link(vec.memset(v[:, :, :, HD:HD + 1], 1.0))
            PER = 46
            with dve.Fori(0, GROUPS) as t:
                link = Link(dve, S["step"], 4 + PER * t, PER)

                def layernorm(x, j, dst, gain, shift):
                    full = [P, GROUP * HEADS, HD]
                    link(vec.tensor_reduce(mom[:, :, 0], x, AX, ALU.add))
                    link(vec.tensor_scalar(mom[:], mom[:], 1.0 / HD, None, ALU.mult))
                    link(vec.tensor_tensor(x, x, bc(mom[:], full), ALU.subtract))
                    link(vec.tensor_tensor(sq[:], x, x, ALU.mult))
                    link(vec.tensor_reduce(var[:, :, 0], sq[:], AX, ALU.add))
                    vec.tensor_scalar(var[:], var[:], 1.0 / HD, 1e-8, ALU.mult, ALU.add).then_inc(S["var_ready"], 1)
                    dve.wait_ge(S["rooted"], 2 * t + j + 1)
                    link(vec.tensor_tensor(x, x, bc(rstd[:], full), ALU.mult))
                    link(vec.tensor_tensor(x, x, bc(norms[:, gain], full), ALU.mult))
                    link(vec.tensor_tensor(dst, x, bc(norms[:, shift], full), ALU.add))

                front_dve(k, dve, xs[:], t, S["normed"])
                dve.wait_ge(S["projected"], 6 * t + 6)
                vec.tensor_copy(kk[:], ps[:, 5, :]).then_inc(S["kv_ready"], 1)
                vs = ps[:, 6, :].rearrange("p (b z h c) -> p b z h c", b=GROUP, z=2, h=HEADS)
                vec.tensor_copy(v[:, :, :, 0:HD], vs[:, :, 0]).then_inc(S["kv_ready"], 1)
                for b in range(GROUP):
                    ins = vec.tensor_scalar(live[:, b, :, 0, :], vs[:, b, 1], 0.0, None, ALU.not_equal)
                ins.then_inc(S["kv_ready"], 1)
                for u in range(UNITS):
                    dve.wait_ge(S["scored"], UNITS * t + u + 1)
                    bank = ps[:, 1 + u % 2, :].rearrange("p (e n) -> p e n", e=SETS)
                    vec.tensor_reduce(top[:, u % 2, :, 0], bank, AX, ALU.max).then_inc(S["topped"], 1)
                    if u >= 2:
                        dve.wait_ge(S["turned"], UNITS * t + u - 1)
                    dve.wait_ge(S["topped"], UNITS * t + u + 1)
                    vec.tensor_tensor(probs[:, u % 2], bank, bc(top[:, u % 2], [P, 4, N]), ALU.subtract).then_inc(S["shifted"], 1)
                for b in range(GROUP):
                    dve.wait_ge(S["valued"], UNITS * t + HEADS * (b + 1))
                    o = o_bank(b)
                    link(vec.reciprocal(rden[:, b], o[:, :, :, HD:HD + 1]))
                    link(vec.tensor_tensor(out[:, b], o[:, :, :, 0:HD], bc(rden[:, b], [P, HEADS, SETS, HD]), ALU.mult))
                    link(vec.tensor_tensor(out[:, b], out[:, b], bc(live[:, b], [P, HEADS, SETS, HD]), ALU.mult))
                    vec.sem_inc(S["out_ready"], 1)
                dve.wait_ge(S["gated"], t + 1)
                glog = ps[:, 3, 0:GROUP * 16]
                gflat = gs[:].rearrange("p m e o -> p (m e o)")
                link(vec.tensor_tensor(gflat.rearrange("p (b g) -> p b g", b=GROUP), glog.rearrange("p (b g) -> p b g", b=GROUP),
                                       bc(gate_b[:], [P, GROUP, 16]), ALU.add))
                link(vec.tensor_reduce(gtop[:, :, 0], gs[:, :, :, 0], AX, ALU.max))
                vec.tensor_tensor(gs[:, :, :, 0], gs[:, :, :, 0], bc(gtop[:], [P, 16, SETS]), ALU.subtract).then_inc(S["gs_shifted"], 1)
                dve.wait_ge(S["gs_exped"], t + 1)
                link(vec.tensor_reduce(gtop[:, :, 0], gs[:, :, :, 0], AX, ALU.add))
                link(vec.reciprocal(gtop[:], gtop[:]))
                link(vec.tensor_tensor(gs[:, :, :, 0], gs[:, :, :, 0], bc(gtop[:], [P, 16, SETS]), ALU.mult))
                om = out[:].rearrange("p b h e c -> p (b h) e c")
                link(vec.tensor_tensor(om, om, bc(gs[:], [P, 16, SETS, HD]), ALU.mult))
                link(vec.tensor_reduce(fh[:], om.rearrange("p m e c -> p m c e"), AX, ALU.add))
                link(vec.tensor_tensor(fh[:].rearrange("p (b h) c -> p b (h c)", b=GROUP), fh[:].rearrange("p (b h) c -> p b (h c)", b=GROUP),
                                       bc(resid[:].rearrange("p (o h) c -> p o (h c)", o=1), [P, GROUP, D]), ALU.add))
                layernorm(fh[:], 0, fh[:], 0, 1)
                vec.tensor_copy(fx[:, :, 0:D], fh[:].rearrange("p (b h) c -> p b (h c)", b=GROUP)).then_inc(S["fx_ready"], 1)
                dve.wait_ge(S["fx_ready"], t + 1)
                link(vec.tensor_scalar(nz[:], fx[:, :, 0:D], 0.0, None, ALU.not_equal))
                dve.wait_ge(S["fx_t_ready"], t + 1)
                link(vec.tensor_scalar(nz_t[:], fx_t[0:D, :], 0.0, None, ALU.not_equal))
                dve.wait_ge(S["h1_made"], t + 1)
                vec.scalar_tensor_tensor(out=h1_t[0:D, :], in0=ps[0:D, 5, :], scalar=0.0, in1=nz_t[:],
                                         op0=ALU.max, op1=ALU.mult).then_inc(S["h1_ready"], 1)
                dve.wait_ge(S["h2_made"], t + 1)
                f4 = fh[:].rearrange("p (b h) c -> p b (h c)", b=GROUP)
                link(vec.tensor_tensor(f4, seqs(6, D), nz[:], ALU.mult))
                link(vec.tensor_tensor(f4, f4, fx[:, :, 0:D], ALU.add))
                layernorm(fh[:], 1, fh[:], 2, 3)
                vec.tensor_copy(fx[:, :, 0:D], f4).then_inc(S["fo_ready"], 1)
                dve.wait_ge(S["fg_made"], t + 1)
                link(vec.tensor_reduce(ftop[:, :, 0], seqs(0, HEADS), AX, ALU.max))
                vec.tensor_tensor(fg[:, :, :, 0], seqs(0, HEADS), bc(ftop[:], [P, GROUP, HEADS]), ALU.subtract).then_inc(S["fg_shifted"], 1)
                dve.wait_ge(S["fg_exped"], t + 1)
                link(vec.tensor_reduce(ftop[:, :, 0], fg[:, :, :, 0], AX, ALU.add))
                link(vec.reciprocal(ftop[:], ftop[:]))
                link(vec.tensor_tensor(fg[:, :, :, 0], fg[:, :, :, 0], bc(ftop[:], [P, GROUP, HEADS]), ALU.mult))
                f3 = fh[:]
                link(vec.tensor_tensor(f3, f3, bc(fg[:].rearrange("p b h o -> p (b h) o"), [P, GROUP * HEADS, HD]), ALU.mult))
                g = bass.ds(GROUP * t, GROUP)
                link(vec.tensor_tensor(k.h[:, g, :], k.h[:, g, :], f4, ALU.add))
                link.close()

        @block.scalar
        def _(act):
            with act.Fori(0, GROUPS) as t:
                act.wait_ge(S["xt_made"], t + 1)
                nc.scalar.copy(xt[:], ps[0:A1, 0, :]).then_inc(S["xt_ready"], 1)
                for e in range(SETS):
                    act.wait_ge(S["projected"], 6 * t + e + 1)
                    nc.scalar.copy(q[:, e, :], ps[:, 1 + e, :]).then_inc(S["q_ready"], 1)

                def copy_turned(u):
                    act.wait_ge(S["turned"], UNITS * t + u + 1)
                    if u >= 2:
                        act.wait_ge(S["valued"], UNITS * t + u - 1)
                    nc.scalar.copy(probs_t[:, u % 2], ps[:, 3 + u % 2, :].rearrange("p (e n) -> p e n", e=SETS)).then_inc(S["turned_ready"], 1)

                for u in range(UNITS):
                    act.wait_ge(S["shifted"], UNITS * t + u + 1)
                    nc.scalar.activation(probs[:, u % 2], probs[:, u % 2], ACT.Exp).then_inc(S["exped"], 1)
                    if u >= 1:
                        copy_turned(u - 1)
                copy_turned(UNITS - 1)
                for j in range(2):
                    act.wait_ge(S["out_made"], 2 * t + j + 1)
                    nc.scalar.copy(out_t[:, 2 * j:2 * j + 2], ps[:, 1 + j, :].rearrange("p (b z n) -> p b z n", b=2, z=2)).then_inc(S["out_t_ready"], 1)
                act.wait_ge(S["gs_shifted"], t + 1)
                nc.scalar.activation(gs[:], gs[:], ACT.Exp).then_inc(S["gs_exped"], 1)
                act.wait_ge(S["fx_made"], t + 1)
                nc.scalar.copy(fx_t[:], ps[0:A1, 4, :]).then_inc(S["fx_t_ready"], 1)
                act.wait_ge(S["fo_made"], t + 1)
                nc.scalar.copy(fo_t[:], ps[0:A1, 7, :]).then_inc(S["fo_t_ready"], 1)
                act.wait_ge(S["fg_shifted"], t + 1)
                nc.scalar.activation(fg[:], fg[:], ACT.Exp).then_inc(S["fg_exped"], 1)

        @block.tensor
        def _(pe):
            mm = nc.tensor.matmul
            with pe.Fori(0, GROUPS) as t:
                pe.wait_ge(S["normed"], t + 1)
                for b in range(GROUP):
                    ins = nc.tensor.transpose(ps[0:A1, 0, b * N:(b + 1) * N], xs[:, b, :], k.ident[:])
                ins.then_inc(S["xt_made"], 1)
                pe.wait_ge(S["xt_ready"], t + 1)
                for e in range(SETS):
                    mm(ps[:, 1 + e, :], wq[:, e].rearrange("p h c -> p (h c)"), xt[:], start=True, stop=True).then_inc(S["projected"], 1)
                mm(ps[:, 5, :], wk[:].rearrange("p h c -> p (h c)"), xt[:], start=True, stop=True).then_inc(S["projected"], 1)
                for b in range(GROUP):
                    ins = mm(ps[:, 6, b * P:(b + 1) * P], xt[:, b * N:(b + 1) * N], wvs[:].rearrange("p z h c -> p (z h c)"), start=True, stop=True)
                ins.then_inc(S["projected"], 1)
                pe.wait_ge(S["q_ready"], 4 * t + 4)
                pe.wait_ge(S["kv_ready"], 3 * t + 3)

                def scores(u):
                    b, h = u // HEADS, u % HEADS
                    if u >= 2:
                        pe.wait_ge(S["shifted"], UNITS * t + u - 1)
                    mm(ps[:, 1 + u % 2, :], identb[:], causal[:].rearrange("p e n -> p (e n)"), start=True, stop=False)
                    for e in range(SETS):
                        ins = mm(ps[:, 1 + u % 2, e * N:(e + 1) * N], q[32 * h:32 * h + 32, e, b * N:(b + 1) * N],
                                 kk[32 * h:32 * h + 32, b * N:(b + 1) * N], start=False, stop=(e == SETS - 1), tile_position=(32 * h, 0))
                    ins.then_inc(S["scored"], 1)

                def turn(u):
                    pe.wait_ge(S["exped"], UNITS * t + u + 1)
                    if u >= 2:
                        pe.wait_ge(S["turned_ready"], UNITS * t + u - 1)
                    for e in range(SETS):
                        ins = nc.tensor.transpose(ps[:, 3 + u % 2, e * N:(e + 1) * N], probs[:, u % 2, e, :], k.ident[:])
                    ins.then_inc(S["turned"], 1)

                def values(u):
                    b, h = u // HEADS, u % HEADS
                    pe.wait_ge(S["turned_ready"], UNITS * t + u + 1)
                    for e in range(SETS):
                        ins = mm(o_bank(b)[:, h, e], probs_t[:, u % 2, e, :], v[:, b, h, :], start=True, stop=True)
                    ins.then_inc(S["valued"], 1)

                for u in range(UNITS + 2):
                    if u < UNITS:
                        scores(u)
                    if 1 <= u <= UNITS:
                        turn(u - 1)
                    if u >= 2:
                        values(u - 2)
                for b in range(GROUP):
                    pe.wait_ge(S["out_ready"], GROUP * t + b + 1)
                    ob = out[:, b].rearrange("p h e c -> p (h e c)")
                    for z in range(2):
                        ins = nc.tensor.transpose(ps[:, 1 + b // 2, (2 * (b % 2) + z) * N:(2 * (b % 2) + z + 1) * N], ob[:, z * N:(z + 1) * N], k.ident[:])
                    if b % 2:
                        ins.then_inc(S["out_made"], 1)
                pe.wait_ge(S["out_t_ready"], 2 * t + 2)
                for b in range(GROUP):
                    for z in range(2):
                        ins = mm(ps[:, 3, b * 16 + z * 8:b * 16 + z * 8 + 8], out_t[:, b, z], gate_w[:, z, :], start=True, stop=True)
                ins.then_inc(S["gated"], 1)
                pe.wait_ge(S["fx_ready"], t + 1)
                for b in range(GROUP):
                    ins = nc.tensor.transpose(ps[0:A1, 4, b * N:(b + 1) * N], fx[:, b, :], k.ident[:])
                ins.then_inc(S["fx_made"], 1)
                pe.wait_ge(S["fx_t_ready"], t + 1)
                mm(ps[0:D, 5, :], fc1[:], fx_t[:], start=True, stop=True).then_inc(S["h1_made"], 1)
                pe.wait_ge(S["h1_ready"], t + 1)
                for b in range(GROUP):
                    ins = mm(ps[:, 6, b * D:(b + 1) * D], h1_t[:, b * N:(b + 1) * N], fc2[:], start=True, stop=True)
                ins.then_inc(S["h2_made"], 1)
                pe.wait_ge(S["fo_ready"], t + 1)
                for b in range(GROUP):
                    ins = nc.tensor.transpose(ps[0:A1, 7, b * N:(b + 1) * N], fx[:, b, :], k.ident[:])
                ins.then_inc(S["fo_made"], 1)
                pe.wait_ge(S["fo_t_ready"], t + 1)
                for b in range(GROUP):
                    ins = mm(ps[:, 0, b * HEADS:(b + 1) * HEADS], fo_t[0:D, b * N:(b + 1) * N], fgate_w[:], start=True, stop=True)
                ins.then_inc(S["fg_made"], 1)


def fold_l1_ffn(k, wq, wk, wvs, fc1, fc2, gate_w, fgate_w, gate_b, norms, causal, identb, resid, nhalf):
    nc, w = k.nc, k.w
    HEADS, SETS, HD, A1 = 4, 4, 16, D + 1
    with Scope(nc, "l1fold") as s:
        hl = s.sb("hl", [D, A1])
        nat = s.sb("nat", [D, 8, D])
        turned = s.sb("turned", [D, 8, D])
        gnat = s.sb("gnat", [8, 2, 2, D])
        fgnat = s.sb("fgnat", [HEADS, D])
        xs = s.sb("xs", [P, HEADS, A1])
        xt = s.sb("xt", [A1, TOK])
        maskf = s.sb("maskf", [P, 4, N])
        ps = s.ps("ps", [P, 8, 512])
        zeroed, loaded, step, made, ready, masked = (s.sem(n) for n in "zeroed loaded step made ready masked".split())
        block = s.block()
        LOADS = 2 + HEADS * (SETS + 7) + 2 + 4

        @block.sync
        def _(sp):
            sent = [0]

            def load(dst, src):
                sp.dma_start(dst, src).then_inc(loaded, 16)
                sent[0] += 1

            sp.wait_ge(zeroed, 1)
            load(hl[:, 0:D], w["L1_ffn_hl_w"].rearrange("n d i -> (n d) i"))
            load(hl[:, D:A1], w["L1_ffn_hl_b"].rearrange("n (d u) -> (n d) u", u=1))
            for n in range(HEADS):
                r = slice(n * HD, (n + 1) * HD)
                for e in range(SETS):
                    load(nat[r, e, r], w["L1_ffn_wq"][n, e])
                load(nat[r, 4, r], w["L1_ffn_wk"][n])
                load(nat[r, 5, r], w["L1_ffn_wv"][n])
                load(nat[r, 6, r], w["L1_ffn_fc1_w"])
                load(nat[r, 7, r], w["L1_ffn_fc2_w"])
                load(gnat[(n % 2) * 4:(n % 2) * 4 + 4, n // 2, n % 2, :], w["L1_ffn_gate_w"][n])
                load(fc1[D:A1, r], w["L1_ffn_fc1_b"].rearrange("(o d) -> o d", o=1))
                load(fc2[D:A1, r], w["L1_ffn_fc2_b"].rearrange("(o d) -> o d", o=1))
            load(fgnat[:], w["L1_ffn_fgate_w"])
            load(gate_b[:, 0, :], w["L1_ffn_gate_b"].rearrange("n e -> (n e)").partition_broadcast(P))
            for n, name in enumerate(("ln_g", "ln_b", "fnorm_g", "fnorm_b")):
                load(norms[:, n, 0, :], w[f"L1_ffn_{name}"].partition_broadcast(P))
            assert sent[0] == LOADS, (sent, LOADS)

        @block.gpsimd
        def _(pool):
            link = Link(pool, masked)
            link(nc.gpsimd.memset(maskf[:], 0.0))
            link(nc.gpsimd.affine_select(out=maskf[:], in_=maskf[:], compare_op=ALU.is_ge, fill=MASKED, base=0,
                                         pattern=[[0, 4], [-1, N]], channel_multiplier=1))

        @block.vector
        def _(dve):
            vec = nc.vector
            link = Link(dve, step)
            link(vec.memset(nat[:], 0.0))
            link(vec.memset(gnat[:], 0.0))
            vec.sem_inc(zeroed, 1)
            link(vec.memset(wq[:], 0.0))
            link(vec.memset(wk[:], 0.0))
            link(vec.memset(nhalf[:], -0.5))
            link(vec.tensor_copy(identb[:], k.ident[:]))
            link(vec.memset(xs[:, :, D:A1], 1.0))
            link(vec.tensor_tensor(xs[:, :, 0:D], k.xc[:, 0:HEADS, :], bc(k.rstd[:, 0:HEADS, :], [P, HEADS, D]), ALU.mult))
            vec.sem_inc(ready, 1)
            dve.wait_ge(masked, 2)
            link(vec.tensor_copy(causal[:], maskf[:]))
            dve.wait_ge(made, 1)
            link(vec.tensor_copy(turned[:], ps[0:D, 0, :].rearrange("p (n c) -> p n c", n=8)))
            link(vec.tensor_copy(fc1[0:D, :], ps[0:D, 0, 6 * D:7 * D]))
            link(vec.tensor_copy(fc2[0:D, :], ps[0:D, 0, 7 * D:8 * D]))
            link(vec.tensor_copy(wvs[:, 1], ps[0:A1, 1, 0:D].rearrange("p (h c) -> p h c", h=HEADS)))
            link(vec.tensor_copy(gate_w[:], ps[:, 2, 0:16].rearrange("p (z g) -> p z g", z=2)))
            link(vec.tensor_copy(fgate_w[:], ps[0:D, 3, 0:HEADS]))
            link(vec.tensor_copy(xt[:], ps[0:A1, 4, :]))
            vec.sem_inc(ready, 1)
            dve.wait_ge(made, 2)
            f = ps[0:A1, 5, 0:6 * D].rearrange("p (n h c) -> p n h c", n=6, h=HEADS)
            link(vec.tensor_scalar(wq[:, :, :, 0:HD], f[:, 0:4], HD ** 0.5, None, ALU.mult))
            link(vec.tensor_copy(wk[:, :, 0:HD], f[:, 4]))
            link(vec.tensor_copy(wvs[:, 0], f[:, 5]))
            for n in range(HEADS):
                link(vec.tensor_copy(resid[:, n, :], ps[:, 6, n * D + n * HD:n * D + (n + 1) * HD]))

        @block.tensor
        def _(pe):
            mm = nc.tensor.matmul
            pe.wait_ge(loaded, 16 * LOADS)
            pe.wait_ge(ready, 1)
            for n in range(8):
                nc.tensor.transpose(ps[0:D, 0, n * D:(n + 1) * D], nat[:, n, :], k.ident[0:D, 0:D])
            nc.tensor.transpose(ps[0:A1, 1, 0:D], hl[:], k.ident[0:D, 0:D])
            for z in range(2):
                nc.tensor.transpose(ps[:, 2, 8 * z:8 * z + 8], gnat[:, z].rearrange("p a f -> p (a f)"), k.ident[0:8, 0:8])
            nc.tensor.transpose(ps[0:D, 3, 0:HEADS], fgnat[:], k.ident[0:HEADS, 0:HEADS])
            for b in range(HEADS):
                ins = nc.tensor.transpose(ps[0:A1, 4, b * N:(b + 1) * N], xs[:, b, :], k.ident[:])
            ins.then_inc(made, 1)
            pe.wait_ge(ready, 2)
            mm(ps[0:A1, 5, 0:6 * D], hl[:], turned[:, 0:6].rearrange("p n c -> p (n c)"), start=True, stop=True)
            for b in range(HEADS):
                ins = mm(ps[:, 6, b * D:(b + 1) * D], xt[:, b * N:(b + 1) * N], wvs[:, 1].rearrange("p h c -> p (h c)"), start=True, stop=True)
            ins.then_inc(made, 1)


def stage_l2_attn(k):
    nc, w = k.nc, k.w
    HEADS, HD = 8, 64
    PAIRS = HEADS // 2
    UNITS = GROUP * 2
    with Scope(nc, "l2a") as s:
        pair_map = s.sb("pair_map", [D, HEADS, HD])
        value_map = s.sb("value_map", [D, HEADS, D])
        with Scope(nc, "l2fold") as s1:
            nat = s1.sb("nat", [D, 4, HEADS, HD])
            turned = s1.sb("turned", [D, 4, HEADS, HD])
            ps = s1.ps("ps", [P, 8, 512])
            loaded, step, made, ready = (s1.sem(n) for n in "loaded step made ready".split())
            block = s1.block()

            @block.sync
            def _(sp):
                for n, name in enumerate(("q", "k", "v", "out")):
                    sp.dma_start(nat[:, n], w[f"L2_attn_weight_{name}"]).then_inc(loaded, 16)

            @block.tensor
            def _(pe):
                pe.wait_ge(loaded, 64)
                for n in range(4):
                    for h in range(HEADS):
                        ins = nc.tensor.transpose(ps[0:D, n, h * HD:(h + 1) * HD], nat[:, n, h], k.ident[0:D, 0:D])
                ins.then_inc(made, 1)
                pe.wait_ge(ready, 1)
                for h in range(HEADS):
                    nc.tensor.matmul(ps[0:D, 4, h * HD:(h + 1) * HD], turned[:, 0, h], turned[:, 1, h], start=True, stop=True)
                    ins = nc.tensor.matmul(ps[0:D, 5, h * HD:(h + 1) * HD], turned[:, 2, h], turned[:, 3, h], start=True, stop=True)
                ins.then_inc(made, 1)

            @block.vector
            def _(dve):
                link = Link(dve, step)
                dve.wait_ge(made, 1)
                for n in range(4):
                    link(nc.vector.tensor_copy(turned[:, n], ps[0:D, n, :].rearrange("p (h c) -> p h c", h=HEADS)))
                nc.vector.sem_inc(ready, 1)
                dve.wait_ge(made, 2)
                link(nc.vector.tensor_scalar(pair_map[:], ps[0:D, 4, :].rearrange("p (h c) -> p h c", h=HEADS), HD ** -0.5, None, ALU.mult))
                link(nc.vector.tensor_copy(value_map[:], ps[0:D, 5, :].rearrange("p (h c) -> p h c", h=HEADS)))

        xs = s.sb("xs", [P, GROUP, 2, D])
        xt = s.sb("xt", [P, TOK])
        xm = s.sb("xm", [P, PAIRS, TOK])
        top = s.sb("top", [P, 2, 4])
        probs = s.sb("probs", [P, 2, 4, N])
        total = s.sb("total", [P, 2, 4])
        rtotal = s.sb("rtotal", [P, 2, 4])
        weight = s.sb("weight", [P, 2, HEADS, 1])
        part = s.sb("part", [P, 2, HEADS, D])
        summed = s.sb("summed", [P, 2, D])
        ps = s.ps("ps", [P, 8, 512])
        names = "step normed xt_made xt_ready projected xm_ready scored topped exped inverted weighed taken xv_made combined".split()
        S = {n: s.sem(n) for n in names}
        block = s.block()

        def weights(b):
            return ps[:, (7, 0)[b % 2], 0:HEADS]

        @block.vector
        def _(dve):
            vec = nc.vector
            PER = UNITS + 4 * GROUP
            with dve.Fori(0, GROUPS) as t:
                link = Link(dve, S["step"], PER * t, PER)
                g = bass.ds(GROUP * t, GROUP)
                for half in range(2):
                    vec.tensor_tensor(xs[:, :, half, :], k.xc[:, g, :], bc(k.rstd[:, g, :], [P, GROUP, D]), ALU.mult).then_inc(S["normed"], 1)

                def invert(u):
                    dve.wait_ge(S["exped"], 4 * (UNITS * t + u) + 4)
                    if u >= 2:
                        dve.wait_ge(S["weighed"], UNITS * t + u - 1)
                    vec.reciprocal(rtotal[:, u % 2], total[:, u % 2]).then_inc(S["inverted"], 1)

                def combine(b):
                    dve.wait_ge(S["weighed"], UNITS * t + 2 * b + 2)
                    dve.wait_ge(S["xv_made"], GROUP * t + b + 1)
                    link(vec.tensor_copy(weight[:, b % 2].rearrange("p h o -> p (h o)"), weights(b)))
                    link(vec.tensor_tensor(part[:, b % 2], ps[:, 1 + b % 2, :].rearrange("p (h d) -> p h d", h=HEADS),
                                           bc(weight[:, b % 2], [P, HEADS, D]), ALU.mult))
                    vec.sem_inc(S["taken"], 1)
                    link(vec.tensor_reduce(summed[:, b % 2], part[:, b % 2].rearrange("p h d -> p d h"), AX, ALU.add))
                    one = bass.ds(GROUP * t + b, 1)
                    link(vec.tensor_tensor(k.h[:, one, :], k.h[:, one, :], summed[:, b % 2:b % 2 + 1, :], ALU.add))

                for u in range(UNITS + 1):
                    if u < UNITS:
                        dve.wait_ge(S["scored"], UNITS * t + u + 1)
                        if u >= 2:
                            dve.wait_ge(S["exped"], 4 * (UNITS * t + u - 1))
                        link(vec.tensor_reduce(top[:, u % 2], ps[:, 5 + u % 2, :].rearrange("p (a n) -> p a n", a=4), AX, ALU.max, negate=True))
                        vec.sem_inc(S["topped"], 1)
                    if u >= 1:
                        invert(u - 1)
                    if u >= 3 and u % 2:
                        combine(u // 2 - 1)
                combine(GROUP - 1)
                link.close()

        @block.scalar
        def _(act):
            with act.Fori(0, GROUPS) as t:
                act.wait_ge(S["xt_made"], t + 1)
                nc.scalar.copy(xt[:], ps[:, 0, :]).then_inc(S["xt_ready"], 1)
                for p in range(PAIRS):
                    act.wait_ge(S["projected"], PAIRS * t + p + 1)
                    nc.scalar.copy(xm[:, p, :], ps[:, 1 + p, :]).then_inc(S["xm_ready"], 1)
                for u in range(UNITS):
                    act.wait_ge(S["topped"], UNITS * t + u + 1)
                    if u >= 2:
                        act.wait_ge(S["weighed"], UNITS * t + u - 1)
                        act.wait_ge(S["inverted"], UNITS * t + u - 1)
                    for a in range(4):
                        nc.scalar.activation(probs[:, u % 2, a], ps[:, 5 + u % 2, a * N:(a + 1) * N], ACT.Exp, bias=top[:, u % 2, a:a + 1],
                                             accum_out=total[:, u % 2, a:a + 1]).then_inc(S["exped"], 1)

        @block.tensor
        def _(pe):
            mm = nc.tensor.matmul
            with pe.Fori(0, GROUPS) as t:
                pe.wait_ge(S["normed"], 2 * t + 2)
                for b in range(GROUP):
                    ins = nc.tensor.transpose(ps[:, 0, b * N:(b + 1) * N], xs[:, b].rearrange("p z d -> p (z d)"), k.ident[:])
                ins.then_inc(S["xt_made"], 1)
                pe.wait_ge(S["xt_ready"], t + 1)
                for p in range(PAIRS):
                    mm(ps[:, 1 + p, :], pair_map[:, 2 * p:2 * p + 2].rearrange("c h d -> c (h d)"), xt[0:D, :],
                       start=True, stop=True).then_inc(S["projected"], 1)
                pe.wait_ge(S["xm_ready"], PAIRS * t + PAIRS)

                def scores(u):
                    b, r = u // 2, D * (u % 2)
                    if u >= 2:
                        pe.wait_ge(S["exped"], 4 * (UNITS * t + u - 1))
                    mm(ps[:, 5 + u % 2, :], xt[r:r + D, b * N:(b + 1) * N], xm[r:r + D, :, b * N:(b + 1) * N],
                       start=True, stop=True).then_inc(S["scored"], 1)

                def weigh(u):
                    b = u // 2
                    if u % 2 == 0 and b >= 2:
                        pe.wait_ge(S["taken"], GROUP * t + b - 1)
                    pe.wait_ge(S["inverted"], UNITS * t + u + 1)
                    for a in range(4):
                        ins = mm(weights(b)[:, 2 * a + u % 2:2 * a + u % 2 + 1], probs[:, u % 2, a, :], rtotal[:, u % 2, a:a + 1],
                                 start=True, stop=True)
                    ins.then_inc(S["weighed"], 1)
                    if u % 2:
                        mm(ps[:, 1 + b % 2, :], xt[0:D, b * N:(b + 1) * N], value_map[:].rearrange("c h o -> c (h o)"),
                           start=True, stop=True).then_inc(S["xv_made"], 1)

                for u in range(UNITS + 1):
                    if u < UNITS:
                        scores(u)
                    if u >= 1:
                        weigh(u - 1)


def turn_all(k, tag, xt, router=None, logits=None, by_token=False):
    nc = k.nc
    rows = xt.shape[0]
    with Scope(nc, f"turn{tag}") as s:
        xs = s.sb("xs", [P, 2, GROUP, P])
        xg = s.sb("xg", [P, 2, TOK])
        ps = s.ps("ps", [P, 4, 512])
        names = "step normed made ready kept routed taken".split()
        S = {n: s.sem(n) for n in names}
        block = s.block()
        E = router.shape[1] if router is not None else 0

        @block.vector
        def _(dve):
            link = Link(dve, S["step"])
            link(nc.vector.memset(xs[:], 0.0))
            link(nc.vector.memset(xs[:, :, :, D:D + 1], 1.0))
            with dve.Fori(0, GROUPS // 2) as i:
                for j in range(2):
                    dve.wait_ge(S["taken"], 2 * i + j + 1)
                    front_dve(k, dve, xs[:, j], 2 * i + j, S["normed"])
                for j in range(2):
                    t = 2 * i + j
                    g = bass.ds(GROUP * t, GROUP)
                    dve.wait_ge(S["ready"], t + 1)
                    src = xg[:, j].rearrange("p (b n) -> p b n", b=GROUP)
                    dst = xt[:, :, g].rearrange("p n b -> p b n") if by_token else xt[:, g, :]
                    nc.vector.tensor_copy(dst, src[0:rows]).then_inc(S["kept"], 1)
                    if E:
                        dve.wait_ge(S["routed"], t + 1)
                        nc.vector.tensor_copy(logits[:, g, :], ps[:, 2 + j, 0:GROUP * E].rearrange("p (b e) -> p b e", b=GROUP)).then_inc(S["kept"], 1)

        @block.scalar
        def _(act):
            with act.Fori(0, GROUPS // 2) as i:
                for j in range(2):
                    t = 2 * i + j
                    act.wait_ge(S["made"], t + 1)
                    nc.scalar.copy(xg[:, j], ps[:, j, :]).then_inc(S["ready"], 1)

        @block.tensor
        def _(pe):
            nc.tensor.sem_inc(S["taken"], 2)
            with pe.Fori(0, GROUPS // 2) as i:
                for j in range(2):
                    t = 2 * i + j
                    pe.wait_ge(S["normed"], t + 1)
                    for b in range(GROUP):
                        ins = nc.tensor.transpose(ps[:, j, b * N:(b + 1) * N], xs[:, j, b, :], k.ident[:])
                    ins.then_inc(S["made"], 1)
                for j in range(2):
                    t = 2 * i + j
                    pe.wait_ge(S["ready"], t + 1)
                    if E:
                        for b in range(GROUP):
                            ins = nc.tensor.matmul(ps[:, 2 + j, b * E:(b + 1) * E], xg[:, j, b * N:(b + 1) * N], router[:], start=True, stop=True)
                        ins.then_inc(S["routed"], 1)
                    nc.tensor.sem_inc(S["taken"], 1)


def route(k, tag, logits, share):
    nc = k.nc
    E = logits.shape[2]
    with Scope(nc, f"route{tag}") as s:
        shape = [P, SEQS, E]
        top = s.sb("top", [P, SEQS, 1])
        prob = s.sb("prob", [P, SEQS * E, 1])
        before = s.sb("before", [P, SEQS, E, E])
        tie = s.sb("tie", [P, SEQS, E, E])
        lower_f = s.sb("lower_f", [P, E, E])
        rank = s.sb("rank", shape)
        step, shifted, exped, made = (s.sem(n) for n in "step shifted exped made".split())
        block = s.block()
        p3 = prob[:].rearrange("p (s e) o -> p s (e o)", e=E)

        @block.gpsimd
        def _(pool):
            link = Link(pool, made)
            link(nc.gpsimd.memset(lower_f[:], 1.0))
            link(nc.gpsimd.affine_select(out=lower_f[:], in_=lower_f[:], compare_op=ALU.is_gt, fill=0.0, base=0,
                                         pattern=[[1, E], [-1, E]], channel_multiplier=0))

        @block.scalar
        def _(act):
            act.wait_ge(shifted, 1)
            nc.scalar.activation(p3, p3, ACT.Exp).then_inc(exped, 1)

        @block.vector
        def _(dve):
            vec = nc.vector
            link = Link(dve, step)
            link(vec.tensor_reduce(top[:, :, 0], logits[:], AX, ALU.max))
            vec.tensor_tensor(p3, logits[:], bc(top[:], shape), ALU.subtract).then_inc(shifted, 1)
            dve.wait_ge(exped, 1)
            dve.wait_ge(made, 2)
            for e in range(E):
                mine = bc(p3[:, :, e:e + 1], shape)
                vec.tensor_tensor(before[:, :, e, :], p3, mine, ALU.is_gt)
                ins = vec.tensor_tensor(tie[:, :, e, :], p3, mine, ALU.is_equal)
            link(ins)
            flat = [P, SEQS, E * E]
            t3 = tie[:].rearrange("p s e f -> p s (e f)")
            link(vec.tensor_tensor(t3, t3, bc(lower_f[:].rearrange("p (o e) f -> p o (e f)", o=1), flat), ALU.mult))
            link(vec.tensor_tensor(before[:], before[:], tie[:], ALU.add))
            link(vec.tensor_reduce(rank[:], before[:], AX, ALU.add))
            link(vec.tensor_scalar(rank[:], rank[:], 1.5, None, ALU.is_lt))
            link(vec.tensor_tensor(rank[:], rank[:], p3, ALU.mult))
            link(vec.tensor_reduce(top[:, :, 0], rank[:], AX, ALU.add))
            link(vec.reciprocal(top[:], top[:]))
            link(vec.tensor_tensor(share[:], rank[:], bc(top[:], shape), ALU.mult))


def split_shares(k, tag, share, parts_t):
    nc = k.nc
    E = share.shape[2]
    PARTS = 3
    with Scope(nc, f"split{tag}") as s:
        parts = s.sb("parts", [P, SEQS, PARTS * E], BF16)
        rest = s.sb("rest", [P, SEQS, E])
        now = s.sb("now", [P, 2, GROUP, PARTS * E], BF16)
        identb = s.sb("identb", [P, P], BF16)
        ps = s.ps("ps", [PARTS * E, 2, 2 * BANK], BF16)
        step, ready, taken, kept, apart = (s.sem(n) for n in "step ready taken kept apart".split())
        block = s.block()

        @block.vector
        def _(dve):
            vec = nc.vector
            link = Link(dve, step)
            link(vec.tensor_copy(identb[:], k.ident[:]))
            link(vec.memset(parts_t[:], 0.0))
            link(vec.tensor_copy(parts[:, :, 0:E], share[:]))
            link(vec.tensor_tensor(rest[:], share[:], parts[:, :, 0:E], ALU.subtract))
            link(vec.tensor_copy(parts[:, :, E:2 * E], rest[:]))
            link(vec.tensor_tensor(rest[:], rest[:], parts[:, :, E:2 * E], ALU.subtract))
            link(vec.tensor_copy(parts[:, :, 2 * E:3 * E], rest[:]))
            with dve.Fori(0, GROUPS // 2) as i:
                for j in range(2):
                    t = 2 * i + j
                    dve.wait_ge(taken, t + 1)
                    vec.tensor_copy(now[:, j], parts[:, bass.ds(GROUP * t, GROUP), :]).then_inc(ready, 1)

        @block.tensor
        def _(pe):
            nc.tensor.sem_inc(taken, 2)
            nc.tensor.sem_inc(kept, 2)
            with pe.Fori(0, GROUPS // 2) as i:
                for j in range(2):
                    pe.wait_ge(ready, 2 * i + j + 1)
                    pe.wait_ge(kept, 2 * i + j + 1)
                    nc.tensor.sem_inc(apart, 1)
                    for b in range(GROUP):
                        ins = nc.tensor.transpose(ps[:, j, b * N:(b + 1) * N], now[:, j, b, :], identb[:])
                    ins.then_inc(taken, 1)

        @block.scalar
        def _(act):
            with act.Fori(0, GROUPS // 2) as i:
                for j in range(2):
                    act.wait_ge(taken, 2 * i + j + 3)
                    nc.scalar.copy(parts_t[0:PARTS * E, bass.ds(GROUP * (2 * i + j), GROUP), :],
                                   ps[:, j, 0:TOK].rearrange("p (b n) -> p b n", b=GROUP)).then_inc(kept, 1)


def mix_experts(k, tag, xt, share, w1, w2, b2, shared):
    nc = k.nc
    HC, E, PARTS = 2, 8, 3
    ALL = E + (1 if shared else 0)
    with Scope(nc, f"mix{tag}") as s:
        parts_t = s.sb("parts_t", [P, SEQS, N], BF16)
        split_shares(k, tag, share, parts_t)
        pick_f = s.sb("pick_f", [P, E, P])
        pick = s.sb("pick", [P, E, P], BF16)
        b2x = s.sb("b2x", [P, D])
        b2rest = s.sb("b2rest", [P, D])
        b2_parts = s.sb("b2_parts", [P, PARTS, D], BF16)
        halves = s.sb("halves", [P, D])
        act_t = s.sb("act_t", [P, 3, HC, TOK])
        scaled = s.sb("scaled", [P, 2, HC, TOK])
        y_t = s.sb("y_t", [P, TOK])
        ps = s.ps("ps", [P, 8, 512])
        names = "step picked loaded ready hidden active spread scaled output y_ready back added apart".split()
        S = {n: s.sem(n) for n in names}
        block = s.block()
        NH = ALL * HC
        HIDDEN, SPREAD, Y, BACK = 0, 3, 5, 6
        HB = 3 if NH % 3 == 0 else 2

        @block.sync
        def _(sp):
            sp.wait_ge(S["ready"], 1)
            for n in range(PARTS):
                sp.dma_start(b2x[n * E:(n + 1) * E, :], b2).then_inc(S["loaded"], 16)

        @block.gpsimd
        def _(pool):
            link = Link(pool, S["picked"])
            link(nc.gpsimd.memset(pick_f[:], 0.0))
            for n in range(PARTS):
                link(nc.gpsimd.affine_select(out=pick_f[:], in_=pick_f[:], compare_op=ALU.not_equal, fill=1.0,
                                             base=-n * E, pattern=[[-1, E], [0, P]], channel_multiplier=1))

        @block.vector
        def _(dve):
            vec = nc.vector
            link = Link(dve, S["step"])
            link(vec.memset(b2x[:], 0.0))
            vec.sem_inc(S["ready"], 1)
            for n in range(2):
                link(vec.tensor_copy(halves[n * D:(n + 1) * D, :], k.ident[n * D:(n + 1) * D, n * D:(n + 1) * D]))
            dve.wait_ge(S["loaded"], 16 * PARTS)
            link(vec.tensor_copy(b2_parts[:, 0], b2x[:]))
            link(vec.tensor_tensor(b2rest[:], b2x[:], b2_parts[:, 0], ALU.subtract))
            link(vec.tensor_copy(b2_parts[:, 1], b2rest[:]))
            link(vec.tensor_tensor(b2rest[:], b2rest[:], b2_parts[:, 1], ALU.subtract))
            link(vec.tensor_copy(b2_parts[:, 2], b2rest[:]))
            dve.wait_ge(S["picked"], 1 + PARTS)
            link(vec.tensor_copy(pick[:], pick_f[:]))
            vec.sem_inc(S["ready"], 1)

            def keep(t):
                g = bass.ds(GROUP * t, GROUP)
                dve.wait_ge(S["back"], t + 1)
                vec.tensor_tensor(k.h[:, g, :], k.h[:, g, :], ps[:, BACK, 0:GROUP * D].rearrange("p (b d) -> p b d", b=GROUP), ALU.add).then_inc(S["added"], 1)

            def group(t, first):
                for e in range(E):
                    if e == 1 and not first:
                        keep(t - 1)
                    dve.wait_ge(S["spread"], E * t + e + 1)
                    dve.wait_ge(S["active"], NH * t + HC * e + HC)
                    if e >= 2:
                        dve.wait_ge(S["output"], ALL * t + e - 1)
                    vec.tensor_tensor(scaled[:, e % 2], act_t[:, e % 3],
                                      bc(ps[:, SPREAD + e % 2, :].rearrange("p (o n) -> p o n", o=1), [P, HC, TOK]), ALU.mult).then_inc(S["scaled"], 1)
                dve.wait_ge(S["output"], ALL * t + ALL)
                if not first:
                    dve.wait_ge(S["back"], t)
                vec.tensor_copy(y_t[:], ps[:, Y, :]).then_inc(S["y_ready"], 1)

            group(0, True)
            with dve.Fori(1, GROUPS) as t:
                group(t, False)
            keep(GROUPS - 1)

        @block.scalar
        def _(act):
            with act.Fori(0, GROUPS) as t:
                for n in range(NH):
                    e, c = n // HC, n % HC
                    act.wait_ge(S["hidden"], NH * t + n + 1)
                    if n >= 3 * HC and c == 0:
                        act.wait_ge(S["scaled"], E * t + e - 2)
                    nc.scalar.activation(act_t[:, e % 3, c, :], ps[:, HIDDEN + n % HB, :], ACT.Gelu).then_inc(S["active"], 1)

        @block.tensor
        def _(pe):
            mm = nc.tensor.matmul
            pe.wait_ge(S["ready"], 2)

            def back(t):
                pe.wait_ge(S["y_ready"], t + 1)
                for b in range(GROUP):
                    ins = mm(ps[:, BACK, b * D:(b + 1) * D], y_t[:, b * N:(b + 1) * N], halves[:], start=True, stop=True)
                ins.then_inc(S["back"], 1)

            def group(t, first):
                g = bass.ds(GROUP * t, GROUP)
                x = xt[:, g, :].rearrange("p b n -> p (b n)")
                parts = parts_t[:, g, :].rearrange("p b n -> p (b n)")

                def hidden(e):
                    for c in range(HC):
                        n = HC * e + c
                        if n >= HB:
                            pe.wait_ge(S["active"], NH * t + n - HB + 1)
                        mm(ps[:, HIDDEN + n % HB, :], w1[:, e, c * P:(c + 1) * P], x, start=True, stop=True).then_inc(S["hidden"], 1)

                def spread(e):
                    if e >= 2:
                        pe.wait_ge(S["scaled"], E * t + e - 1)
                    mm(ps[:, SPREAD + e % 2, :], pick[:, e, :], parts, start=True, stop=True).then_inc(S["spread"], 1)

                def output(e):
                    src = scaled[:, e % 2] if e < E else act_t[:, e % 3]
                    if e < E:
                        pe.wait_ge(S["scaled"], E * t + e + 1)
                    else:
                        pe.wait_ge(S["active"], NH * t + NH)
                    for c in range(HC):
                        ins = mm(ps[c * D:(c + 1) * D, Y, :], w2[:, e, c, :], src[:, c, :], start=(e == 0 and c == 1), stop=(e == ALL - 1),
                                 skip_group_check=True, tile_position=(0, c * D))
                    return ins.then_inc(S["output"], 1)

                spread(0)
                hidden(0)
                if not first:
                    back(t - 1)
                for n in range(PARTS):
                    mm(ps[0:D, Y, :], b2_parts[:, n, :], parts, start=(n == 0), stop=False, skip_group_check=True, tile_position=(0, 0))
                for e in range(1, ALL):
                    hidden(e)
                    if e < E:
                        spread(e)
                    output(e - 1)
                output(ALL - 1)

            group(0, True)
            with pe.Fori(1, GROUPS) as t:
                group(t, False)
            back(GROUPS - 1)


def stage_l2_ffn(k):
    nc, w = k.nc, k.w
    E, F, A1 = 8, 256, D + 1
    with Scope(nc, "l2f") as s:
        share = s.sb("share", [P, SEQS, E])
        xt = s.sb("xt", [P, SEQS, N])
        w1 = s.sb("w1", [P, E + 1, F])
        w2 = s.sb("w2", [P, E + 1, 2, D])
        with Scope(nc, "l2froute") as s1:
            wr = s1.sb("wr", [P, E])
            bshared = s1.sb("bshared", [P, 1, D])
            logits = s1.sb("logits", [P, SEQS, E])
            with Scope(nc, "l2fload") as s2:
                loaded, zeroed, added = s2.sem("loaded"), s2.sem("zeroed"), s2.sem("added")
                block = s2.block()

                @block.sync
                def _(sp):
                    sp.wait_ge(zeroed, 1)
                    sp.dma_start(w1[0:D, 0:E], w["L2_ffn_W1p"].rearrange("e d f -> d e f")).then_inc(loaded, 16)
                    sp.dma_start(w1[0:D, E], w["L2_ffn_W1s"]).then_inc(loaded, 16)
                    sp.dma_start(w1[D:A1, 0:E], w["L2_ffn_b1p"].rearrange("(o e) f -> o e f", o=1)).then_inc(loaded, 16)
                    sp.dma_start(w1[D:A1, E], w["L2_ffn_b1s"].rearrange("(o f) -> o f", o=1)).then_inc(loaded, 16)
                    for c in range(2):
                        sp.dma_start(w2[:, 0:E, c], w["L2_ffn_W2p"].rearrange("e (c f) d -> c f e d", c=2)[c]).then_inc(loaded, 16)
                    sp.dma_start(w2[:, E], w["L2_ffn_W2s"].rearrange("(c f) d -> f c d", c=2)).then_inc(loaded, 16)
                    sp.dma_start(bshared[:, 0, :], w["L2_ffn_b2s"].partition_broadcast(P)).then_inc(loaded, 16)
                    sp.dma_start(wr[0:D, :], w["L2_ffn_Wr"]).then_inc(loaded, 16)

                @block.vector
                def _(dve):
                    nc.vector.memset(wr[D:P, :], 0.0)
                    nc.vector.memset(w1[D:P], 0.0).then_inc(zeroed, 1)
                    dve.wait_ge(loaded, 144)
                    nc.vector.tensor_tensor(k.h[:], k.h[:], bc(bshared[:], [P, SEQS, D]), ALU.add).then_inc(added, 1)
                    dve.wait_ge(added, 1)
            turn_all(k, "l2f", xt, wr, logits)
            route(k, "l2f", logits, share)
        mix_experts(k, "l2f", xt, share, w1, w2, w["L2_ffn_b2p"], True)


def stage_neighbours(k, xt, mask):
    nc, w = k.nc, k.w
    A1, NEAR = D + 1, 17
    with Scope(nc, "knn") as s:
        wr = s.sb("wr", [A1, D])
        mean_t = s.sb("mean_t", [A1, SEQS])
        reprs = s.sb("reprs", [SEQS, D])
        sq = s.sb("sq", [SEQS, D])
        norm = s.sb("norm", [SEQS, 1])
        unit_t = s.sb("unit_t", [D, SEQS])
        sim = s.sb("sim", [SEQS, 1, SEQS])
        before = s.sb("before", [SEQS, SEQS, SEQS])
        tie = s.sb("tie", [SEQS, SEQS, SEQS])
        lower = s.sb("lower", [SEQS, SEQS, SEQS])
        rank = s.sb("rank", [SEQS, SEQS])
        ps = s.ps("ps", [SEQS, 4, 512])
        loaded, step, meaned, made, squared, rooted, united, lowered = (s.sem(n) for n in "loaded step meaned made squared rooted united lowered".split())
        block = s.block()

        @block.sync
        def _(sp):
            sp.dma_start(wr[0:D, :], w["L3_attn_W_repr"]).then_inc(loaded, 16)
            sp.dma_start(wr[D:A1, :], w["L3_attn_b_repr"].rearrange("(o d) -> o d", o=1)).then_inc(loaded, 16)

        @block.gpsimd
        def _(pool):
            link = Link(pool, lowered)
            link(nc.gpsimd.memset(lower[:], 1.0))
            link(nc.gpsimd.affine_select(out=lower[:], in_=lower[:], compare_op=ALU.is_gt, fill=0.0, base=0,
                                         pattern=[[1, SEQS], [-1, SEQS]], channel_multiplier=0))

        @block.scalar
        def _(act):
            act.wait_ge(squared, 1)
            nc.scalar.activation(norm[:], norm[:], ACT.Sqrt).then_inc(rooted, 1)

        @block.tensor
        def _(pe):
            pe.wait_ge(loaded, 32)
            pe.wait_ge(meaned, 1)
            nc.tensor.matmul(ps[:, 0, 0:D], mean_t[:], wr[:], start=True, stop=True).then_inc(made, 1)
            pe.wait_ge(united, 1)
            nc.tensor.transpose(ps[:, 1, 0:SEQS], reprs[:], k.ident[0:SEQS, 0:SEQS]).then_inc(made, 1)
            pe.wait_ge(united, 2)
            nc.tensor.matmul(ps[:, 2, 0:SEQS], unit_t[:], unit_t[:], start=True, stop=True).then_inc(made, 1)

        @block.vector
        def _(dve):
            vec = nc.vector
            link = Link(dve, step)
            link(vec.memset(mean_t[D:A1, :], 1.0))
            link(vec.tensor_reduce(mean_t[0:D, :], xt[0:D].rearrange("d n b -> d b n"), AX, ALU.add))
            link(vec.tensor_scalar(mean_t[0:D, :], mean_t[0:D, :], 1.0 / N, None, ALU.mult))
            vec.sem_inc(meaned, 1)
            dve.wait_ge(made, 1)
            link(vec.tensor_copy(reprs[:], ps[:, 0, 0:D]))
            link(vec.tensor_tensor(sq[:], reprs[:], reprs[:], ALU.mult))
            vec.tensor_reduce(norm[:], sq[:], AX, ALU.add).then_inc(squared, 1)
            dve.wait_ge(rooted, 1)
            link(vec.reciprocal(norm[:], norm[:]))
            vec.tensor_scalar(reprs[:], reprs[:], norm[:, 0:1], None, ALU.mult).then_inc(united, 1)
            dve.wait_ge(made, 2)
            vec.tensor_copy(unit_t[:], ps[:, 1, 0:SEQS]).then_inc(united, 1)
            dve.wait_ge(made, 3)
            link(vec.tensor_copy(sim[:, 0, :], ps[:, 2, 0:SEQS]))
            cube = [SEQS, SEQS, SEQS]
            mine = bc(sim[:, 0, :].rearrange("p (b o) -> p b o", o=1), cube)
            vec.tensor_tensor(before[:], bc(sim[:], cube), mine, ALU.is_gt)
            link(vec.tensor_tensor(tie[:], bc(sim[:], cube), mine, ALU.is_equal))
            dve.wait_ge(lowered, 2)
            link(vec.tensor_tensor(tie[:], tie[:], lower[:], ALU.mult))
            link(vec.tensor_tensor(before[:], before[:], tie[:], ALU.add))
            link(vec.tensor_reduce(rank[:], before[:], AX, ALU.add))
            link(vec.tensor_scalar(rank[:], rank[:], NEAR - 0.5, MASKED, ALU.is_gt, ALU.mult))
            link(vec.tensor_copy(mask[:], bc(rank[:].rearrange("p (o b) -> p o b", o=1), [SEQS, 8, SEQS])))


def stage_l3_attn(k):
    with Scope(k.nc, "l3") as s:
        xt = s.sb("xt", [D, N, SEQS])
        yt = s.sb("yt", [D, SEQS, N])
        mask = s.sb("mask", [SEQS, 8, SEQS], BF16)
        turn_all(k, "l3a", xt, by_token=True)
        stage_neighbours(k, xt, mask)
        attend_sequences(k, xt, yt, mask)
        add_turned_back(k, "l3a", yt)


def attend_sequences(k, xt, yt, mask):
    nc, w = k.nc, k.w
    HEADS, HD = 8, 32
    NG = 8
    STEPS = N // NG
    COLS = NG * SEQS
    with Scope(nc, "l3a") as s:
        twice = s.sb("twice", [SEQS, 2, SEQS], BF16)
        wqkv = s.sb("wqkv", [D, 3, 2, P])
        wo = s.sb("wo", [P, 2, D])
        bo = s.sb("bo", [D, 1])
        xg = s.sb("xg", [D, COLS])
        q = s.sb("q", [P, 2, COLS])
        kk = s.sb("kk", [P, 2, COLS])
        v = s.sb("v", [P, NG, P])
        top = s.sb("top", [P, 2, 8, 1])
        probs = s.sb("probs", [P, 2, 8, SEQS])
        probs_t = s.sb("probs_t", [P, 2, 4, P])
        den = s.sb("den", [P, 4, 4, 2, 1])
        mixed = s.sb("mixed", [P, 4, 2, 4, HD])
        mt = s.sb("mt", [P, 2, 4, P])
        ps = s.ps("ps", [P, 8, 512])
        names = ("loaded step x_in projected q_ready kv_ready scored shifted exped summed turned turned_ready valued mixed_ready "
                 "mt_made mt_ready y_made y_kept apart").split()
        S = {n: s.sem(n) for n in names}
        block = s.block()
        UNITS = 4

        @block.sync
        def _(sp):
            sp.dma_start(wqkv[:], w["L3_attn_W_qkv"].rearrange("d (z g c) -> d z g c", z=3, g=2)).then_inc(S["loaded"], 16)
            sp.dma_start(wo[:], w["L3_attn_W_out"].rearrange("(g c) o -> c g o", g=2)).then_inc(S["loaded"], 16)
            sp.dma_start(bo[:], w["L3_attn_b_out"].rearrange("(o u) -> o u", u=1)).then_inc(S["loaded"], 16)

        @block.vector
        def _(dve):
            vec = nc.vector
            link = Link(dve, S["step"])
            dve.wait_ge(S["loaded"], 48)
            for z in range(2):
                link(vec.tensor_copy(twice[:, z, :], k.ident[0:SEQS, 0:SEQS]))
            link(vec.tensor_scalar(wqkv[:, 0], wqkv[:, 0], HD ** -0.5, None, ALU.mult))
            PER = UNITS * 2 + 1
            with dve.Fori(0, STEPS) as t:
                link = Link(dve, S["step"], 3 + PER * t, PER)
                vec.tensor_copy(xg[:], xt[:, bass.ds(NG * t, NG), :].rearrange("p n b -> p (n b)")).then_inc(S["x_in"], 1)
                for g in range(2):
                    dve.wait_ge(S["projected"], 6 * t + 3 + g)
                    vec.tensor_copy(kk[:, g, :], ps[:, 3 + g, :]).then_inc(S["kv_ready"], 1)
                for j in range(2):
                    dve.wait_ge(S["projected"], 6 * t + 5 + j)
                    vec.tensor_copy(v[:, 4 * j:4 * j + 4, :], ps[:, 5 + j, :].rearrange("p (n c) -> p n c", n=4)).then_inc(S["kv_ready"], 1)

                def shift(u):
                    dve.wait_ge(S["scored"], UNITS * t + u + 1)
                    bank = ps[:, 1 + u % 2, :].rearrange("p (s b) -> p s b", s=8)
                    link(vec.tensor_reduce(top[:, u % 2, :, 0], bank, AX, ALU.max))
                    if u >= 2:
                        dve.wait_ge(S["turned"], UNITS * t + u - 1)
                    vec.tensor_tensor(probs[:, u % 2], bank, bc(top[:, u % 2], [P, 8, SEQS]), ALU.subtract).then_inc(S["shifted"], 1)

                def total(u):
                    dve.wait_ge(S["exped"], UNITS * t + u + 1)
                    link(vec.tensor_reduce(den[:, u].rearrange("p a g o -> p (a g o)"), probs[:, u % 2], AX, ALU.add))

                for u in range(UNITS + 1):
                    if u < UNITS:
                        shift(u)
                    if u >= 1:
                        total(u - 1)
                link(vec.reciprocal(den[:], den[:]))
                dve.wait_ge(S["valued"], UNITS * t + UNITS)
                for g in range(2):
                    o = ps[:, (7, 0)[g], :].rearrange("p (a u c) -> p a u c", a=4, u=4)
                    r = den[:, :, :, g, :].rearrange("p u a o -> p a u o")
                    ins = vec.tensor_tensor(mixed[:, :, g], o, bc(r, [P, 4, 4, HD]), ALU.mult)
                ins.then_inc(S["mixed_ready"], 1)
                dve.wait_ge(S["y_made"], t + 1)
                vec.tensor_scalar(yt[:, :, bass.ds(NG * t, NG)].rearrange("p b n -> p n b"), ps[0:D, 5, :].rearrange("p (n b) -> p n b", n=NG),
                                  bo[:, 0:1], None, ALU.add).then_inc(S["y_kept"], 1)
                link.close()

        @block.scalar
        def _(act):
            with act.Fori(0, STEPS) as t:
                for g in range(2):
                    act.wait_ge(S["projected"], 6 * t + g + 1)
                    nc.scalar.copy(q[:, g, :], ps[:, 1 + g, :]).then_inc(S["q_ready"], 1)

                def copy_turned(u):
                    act.wait_ge(S["turned"], UNITS * t + u + 1)
                    if u >= 2:
                        act.wait_ge(S["valued"], UNITS * t + u - 1)
                    nc.scalar.copy(probs_t[:, u % 2], ps[:, 3 + u % 2, :].rearrange("p (a c) -> p a c", a=4)).then_inc(S["turned_ready"], 1)

                for u in range(UNITS):
                    act.wait_ge(S["shifted"], UNITS * t + u + 1)
                    nc.scalar.activation(probs[:, u % 2], probs[:, u % 2], ACT.Exp).then_inc(S["exped"], 1)
                    if u >= 1:
                        copy_turned(u - 1)
                copy_turned(UNITS - 1)
                for g in range(2):
                    act.wait_ge(S["mt_made"], 2 * t + g + 1)
                    nc.scalar.copy(mt[:, g], ps[:, 1 + g, :].rearrange("p (a c) -> p a c", a=4)).then_inc(S["mt_ready"], 1)

        @block.tensor
        def _(pe):
            mm = nc.tensor.matmul
            with pe.Fori(0, STEPS) as t:
                pe.wait_ge(S["x_in"], t + 1)
                for z in range(2):
                    for g in range(2):
                        mm(ps[:, 1 + 2 * z + g, :], wqkv[:, z, g, :], xg[:], start=True, stop=True).then_inc(S["projected"], 1)
                for n in range(NG):
                    for g in range(2):
                        ins = mm(ps[64 * g:64 * g + 64, 5 + n // 4, (n % 4) * P:(n % 4 + 1) * P], xg[:, n * SEQS:(n + 1) * SEQS],
                                 wqkv[:, 2, g, :], start=True, stop=True)
                    if n % 4 == 3:
                        ins.then_inc(S["projected"], 1)
                pe.wait_ge(S["q_ready"], 2 * t + 2)
                pe.wait_ge(S["kv_ready"], 4 * t + 4)

                def scores(u):
                    if u >= 2:
                        pe.wait_ge(S["shifted"], UNITS * t + u - 1)
                    bank = ps[:, 1 + u % 2, :]
                    nc.tensor.sem_inc(S["apart"], 1)
                    mm(bank, twice[:].rearrange("p z b -> p (z b)"), mask[:].rearrange("p s b -> p (s b)"), start=True, stop=False)
                    r = slice(32 * u, 32 * u + 32)
                    for a in range(4):
                        for g in range(2):
                            for par in range(2):
                                n = 2 * a + par
                                ins = mm(bank[64 * par:64 * par + 64, (2 * a + g) * SEQS:(2 * a + g + 1) * SEQS],
                                         q[r, g, n * SEQS:(n + 1) * SEQS], kk[r, g, n * SEQS:(n + 1) * SEQS],
                                         start=False, stop=(a == 3 and g == 1), tile_position=(32 * u, 64 * par))
                    ins.then_inc(S["scored"], 1)

                def turn(u):
                    pe.wait_ge(S["exped"], UNITS * t + u + 1)
                    if u >= 2:
                        pe.wait_ge(S["turned_ready"], UNITS * t + u - 1)
                    for a in range(4):
                        ins = nc.tensor.transpose(ps[:, 3 + u % 2, a * P:(a + 1) * P], probs[:, u % 2, 2 * a:2 * a + 2].rearrange("p s b -> p (s b)"), k.ident[:])
                    ins.then_inc(S["turned"], 1)

                def values(u):
                    pe.wait_ge(S["turned_ready"], UNITS * t + u + 1)
                    nc.tensor.sem_inc(S["apart"], 1)
                    for a in range(4):
                        for g in range(2):
                            for par in range(2):
                                r = slice(64 * g, 64 * g + 64)
                                o = 64 * par
                                ins = mm(ps[o:o + 64, (7, 0)[g], (a * 4 + u) * HD:(a * 4 + u + 1) * HD], probs_t[r, u % 2, a, o:o + 64],
                                         v[r, 2 * a + par, u * HD:(u + 1) * HD], start=True, stop=True, tile_position=(64 * g, o))
                    ins.then_inc(S["valued"], 1)

                for u in range(UNITS + 2):
                    if u < UNITS:
                        scores(u)
                    if 1 <= u <= UNITS:
                        turn(u - 1)
                    if u >= 2:
                        values(u - 2)
                pe.wait_ge(S["mixed_ready"], t + 1)
                for g in range(2):
                    for a in range(4):
                        ins = nc.tensor.transpose(ps[:, 1 + g, a * P:(a + 1) * P], mixed[:, a, g].rearrange("p u c -> p (u c)"), k.ident[:])
                    ins.then_inc(S["mt_made"], 1)
                pe.wait_ge(S["mt_ready"], 2 * t + 2)
                for g in range(2):
                    ins = mm(ps[0:D, 5, :], wo[:, g, :], mt[:, g].rearrange("p a c -> p (a c)"), start=(g == 0), stop=(g == 1))
                ins.then_inc(S["y_made"], 1)


def add_turned_back(k, tag, yt):
    nc = k.nc
    with Scope(nc, f"back{tag}") as s:
        yg = s.sb("yg", [D, 2, TOK])
        ps = s.ps("ps", [P, 2, 512])
        ready, made, added, apart, free = (s.sem(n) for n in "ready made added apart free".split())
        block = s.block()

        @block.vector
        def _(dve):
            nc.vector.sem_inc(added, 2)
            with dve.Fori(0, GROUPS // 2) as i:
                for j in range(2):
                    t = 2 * i + j
                    g = bass.ds(GROUP * t, GROUP)
                    dve.wait_ge(made, t + 1)
                    nc.vector.tensor_tensor(k.h[:, g, :], k.h[:, g, :], ps[:, j, 0:GROUP * D].rearrange("p (b d) -> p b d", b=GROUP), ALU.add).then_inc(added, 1)

        @block.scalar
        def _(act):
            with act.Fori(0, GROUPS // 2) as i:
                for j in range(2):
                    t = 2 * i + j
                    act.wait_ge(free, t + 1)
                    nc.scalar.copy(yg[:, j], yt[:, bass.ds(GROUP * t, GROUP), :].rearrange("p b n -> p (b n)")).then_inc(ready, 1)

        @block.tensor
        def _(pe):
            nc.tensor.sem_inc(free, 2)
            with pe.Fori(0, GROUPS // 2) as i:
                for j in range(2):
                    t = 2 * i + j
                    pe.wait_ge(ready, t + 1)
                    pe.wait_ge(added, t + 1)
                    nc.tensor.sem_inc(apart, 1)
                    for b in range(GROUP):
                        ins = nc.tensor.transpose(ps[:, j, b * D:(b + 1) * D], yg[:, j, b * N:(b + 1) * N], k.ident[0:D, 0:D])
                    ins.then_inc(made, 1)
                    pe.wait_ge(made, t + 1)
                    nc.tensor.sem_inc(free, 1)


def stage_l3_ffn(k):
    nc, w = k.nc, k.w
    E, F, A1 = 8, 256, D + 1
    with Scope(nc, "l3f") as s:
        share = s.sb("share", [P, SEQS, E])
        xt = s.sb("xt", [P, SEQS, N])
        w1 = s.sb("w1", [P, E, F])
        w2 = s.sb("w2", [P, E, 2, D])
        with Scope(nc, "l3froute") as s1:
            wr = s1.sb("wr", [P, E])
            logits = s1.sb("logits", [P, SEQS, E])
            with Scope(nc, "l3fload") as s2:
                gain = s2.sb("gain", [E, 2, D])
                gain_t = s2.sb("gain_t", [D, E])
                shift_t = s2.sb("shift_t", [D, E, A1])
                ps = s2.ps("ps", [P, 6, 512])
                loaded, step, made, ready, zeroed = (s2.sem(n) for n in "loaded step made ready zeroed".split())
                block = s2.block()

                @block.sync
                def _(sp):
                    sp.wait_ge(zeroed, 1)
                    sp.dma_start(w1[0:D], w["L3_ffn_W1"].rearrange("e d f -> d e f")).then_inc(loaded, 16)
                    sp.dma_start(w1[D:A1], w["L3_ffn_b1"].rearrange("(o e) f -> o e f", o=1)).then_inc(loaded, 16)
                    for c in range(2):
                        sp.dma_start(w2[:, :, c], w["L3_ffn_W2"].rearrange("e (c f) d -> c f e d", c=2)[c]).then_inc(loaded, 16)
                    sp.dma_start(wr[0:D, :], w["L3_ffn_Wr"]).then_inc(loaded, 16)
                    sp.dma_start(wr[D:A1, :], w["L3_ffn_br"].rearrange("(o e) -> o e", o=1)).then_inc(loaded, 16)
                    sp.dma_start(gain[:, 0, :], w["L3_ffn_ln_g"]).then_inc(loaded, 16)
                    sp.dma_start(gain[:, 1, :], w["L3_ffn_ln_b"]).then_inc(loaded, 16)

                @block.tensor
                def _(pe):
                    pe.wait_ge(loaded, 16 * 8)
                    for n in range(2):
                        ins = nc.tensor.transpose(ps[0:D, 0, E * n:E * n + E], gain[:, n, :], k.ident[0:E, 0:E])
                    ins.then_inc(made, 1)
                    pe.wait_ge(ready, 1)
                    for e in range(E):
                        ins = nc.tensor.matmul(ps[0:A1, 1 + e // 2, (e % 2) * F:(e % 2 + 1) * F], shift_t[:, e, :], w1[0:D, e, :], start=True, stop=True)
                    ins.then_inc(made, 1)

                @block.vector
                def _(dve):
                    vec = nc.vector
                    link = Link(dve, step)
                    link(vec.memset(wr[D:P, :], 0.0))
                    link(vec.memset(w1[D:P], 0.0))
                    vec.sem_inc(zeroed, 1)
                    link(vec.memset(shift_t[:], 0.0))
                    dve.wait_ge(made, 1)
                    link(vec.tensor_copy(gain_t[:], ps[0:D, 0, 0:E]))
                    link(vec.tensor_copy(shift_t[:, :, D], ps[0:D, 0, E:2 * E]))
                    vec.sem_inc(ready, 1)
                    dve.wait_ge(made, 2)
                    row = w1[D:A1].rearrange("p (a z) f -> p a z f", z=2)
                    link(vec.tensor_tensor(row, row, ps[D:A1, 1:5, :].rearrange("p a (z f) -> p a z f", z=2), ALU.add))
                    for e in range(E):
                        link(vec.tensor_scalar(w1[0:D, e, :], w1[0:D, e, :], gain_t[:, e:e + 1], None, ALU.mult))
            turn_all(k, "l3fr", xt, wr, logits)
            route(k, "l3f", logits, share)
        inner_center(k)
        turn_all(k, "l3fx", xt)
        mix_experts(k, "l3f", xt, share, w1, w2, w["L3_ffn_b2"], False)


def inner_center(k):
    nc = k.nc
    with Scope(nc, "inner") as s:
        sq = s.sb("sq", [P, SEQS, D])
        mean = s.sb("mean", [P, SEQS, 1])
        std = s.sb("std", [P, SEQS, 1])
        eps = s.sb("eps", [P, 1])
        step, summed, rooted = s.sem("step"), s.sem("summed"), s.sem("rooted")
        block = s.block()

        @block.scalar
        def _(act):
            act.wait_ge(summed, 1)
            nc.scalar.activation(std[:], mean[:], ACT.Sqrt, bias=eps[:, 0:1], scale=1.0 / D).then_inc(rooted, 1)

        @block.vector
        def _(dve):
            vec = nc.vector
            link = Link(dve, step)
            full = [P, SEQS, D]
            link(vec.memset(eps[:], LN_EPS))
            link(vec.tensor_tensor(k.xc[:], k.xc[:], bc(k.rstd[:], full), ALU.mult))
            link(vec.tensor_reduce(mean[:, :, 0], k.xc[:], AX, ALU.add))
            link(vec.tensor_scalar(mean[:], mean[:], 1.0 / D, None, ALU.mult))
            link(vec.tensor_tensor(k.xc[:], k.xc[:], bc(mean[:], full), ALU.subtract))
            link(vec.tensor_tensor(sq[:], k.xc[:], k.xc[:], ALU.mult))
            vec.tensor_reduce(mean[:, :, 0], sq[:], AX, ALU.add).then_inc(summed, 1)
            dve.wait_ge(rooted, 1)
            link(vec.reciprocal(k.rstd[:], std[:]))


def stage_store(k):
    nc = k.nc
    with Scope(nc, "store") as s:
        stored = s.sem("stored")
        block = s.block()

        @block.sync
        def _(sp):
            sp.dma_start(k.out.rearrange("b n d -> n b d"), k.h[:]).then_inc(stored, 16)
            sp.wait_ge(stored, 16)


def build(nc, w, out):
    k = Core(nc, w, out)
    with ExitStack() as ctx:
        k.h = ctx.enter_context(nc.sbuf_tensor("h", [P, SEQS, D], F32))
        k.xc = ctx.enter_context(nc.sbuf_tensor("xc", [P, SEQS, D], F32))
        k.rstd = ctx.enter_context(nc.sbuf_tensor("rstd", [P, SEQS, 1], F32))
        k.ident = ctx.enter_context(nc.sbuf_tensor("ident", [P, P], F32))
        k.rows_landed = [ctx.enter_context(nc.semaphore(f"rows_landed{n}")) for n in range(3)]
        k.attr_fetched = ctx.enter_context(nc.semaphore("attr_fetched"))
        k.chunks_fetched = ctx.enter_context(nc.semaphore("chunks_fetched"))
        Scope.psum = ctx.enter_context(nc.psum_tensor("psum", [P, 8 * BANK], F32))
        stage_constants(k)
        for name, run, normed in TOWER:
            if normed:
                stage_center(k, name)
            run(k)
        stage_store(k)


TOWER = [("tok", stage_tokens, False), ("L0a", stage_l0_attn, True), ("L0f", stage_l0_ffn, True), ("L1a", stage_l1_attn, True), ("L1f", stage_l1_ffn, True), ("L2a", stage_l2_attn, True), ("L2f", stage_l2_ffn, True), ("L3a", stage_l3_attn, True), ("L3f", stage_l3_ffn, True)]


def kernel(**inputs):
    import numpy as _np
    import concourse.bacc as _bacc
    from concourse import mybir as _mybir
    from concourse.bass_utils import run_bass_kernel_spmd as _run

    nc = _bacc.Bacc("TRN2", target_bir_lowering=False, num_devices=1)
    arrays, w = {}, {}
    for name, value in inputs.items():
        a = _np.ascontiguousarray(value)
        arrays[f"in_{name}"] = a
        w[name] = nc.dram_tensor(f"in_{name}", a.shape, _mybir.dt.from_np(a.dtype), kind="ExternalInput").ap()
    out = nc.dram_tensor("out", (SEQS, N, D), F32, kind="ExternalOutput").ap()
    build(nc, w, out)
    r = _run(nc, [arrays], core_ids=[0])
    return r.results[0]["out"]
```

```python
from contextlib import ExitStack

import concourse.bass as bass
from concourse import mybir

F32 = mybir.dt.float32
BF16 = mybir.dt.bfloat16
I32 = mybir.dt.int32
U32 = mybir.dt.uint32
ALU = mybir.AluOpType
ACT = mybir.ActivationFunctionType
AX = mybir.AxisListType.X

P = 128
SEQS = 64
N = 128
D = 64
GROUP = 4
GROUPS = SEQS // GROUP
TOK = GROUP * N
LN_EPS = 1e-5
BANK = 512
MASKED = -1e30


class Core:

    def __init__(self, nc, w, out):
        self.nc, self.w, self.out = nc, w, out


class Scope:

    psum = None
    next_bank = 0

    def __init__(self, nc, stage):
        self.nc, self.stage, self.ctx = nc, stage, ExitStack()
        self.first_bank, self.sems = Scope.next_bank, []

    def __enter__(self):
        return self

    def __exit__(self, *a):
        Scope.next_bank = self.first_bank
        self.ctx.close()
        if self.sems:
            self.nc.clear_and_free_semaphores(self.sems)
            self.nc.all_engine_barrier()

    def sb(self, name, shape, dt=F32):
        return self.ctx.enter_context(self.nc.sbuf_tensor(f"{self.stage}_{name}", shape, dt))

    def ps(self, name, shape, dt=F32):
        size = 1
        for n in shape[1:]:
            size *= n
        words = size if dt == F32 else size // 2
        start = Scope.next_bank * BANK
        Scope.next_bank += -(-words // BANK)
        assert Scope.next_bank <= 8, name
        flat = Scope.psum[0:shape[0], start:start + words]
        if dt != F32:
            flat = flat.bitcast(dt)
        axes = "abcd"[:len(shape) - 1]
        return flat.rearrange(f"p ({' '.join(axes)}) -> p {' '.join(axes)}", **dict(zip(axes, shape[1:])))

    def sem(self, name):
        self.sems.append(self.nc.alloc_semaphore(name=f"{self.stage}_{name}"))
        return self.sems[-1]

    def block(self):
        return self.ctx.enter_context(self.nc.Block())


class Link:

    def __init__(self, eng, sem, base=0, per=None):
        self.eng, self.sem, self.base, self.n, self.per = eng, sem, base, 0, per

    def __call__(self, ins):
        ins.then_inc(self.sem, 1)
        self.n += 1
        self.eng.wait_ge(self.sem, self.base + self.n)

    def close(self):
        assert self.per is None or self.n == self.per, (self.n, self.per)


def bc(ap, shape):
    return ap.to_broadcast(shape)


def stage_constants(k):
    nc = k.nc
    with Scope(nc, "const") as s:
        made = s.sem("ident_step")
        block = s.block()

        @block.gpsimd
        def _(pool):
            link = Link(pool, made)
            link(nc.gpsimd.memset(k.ident[:], 0.0))
            link(nc.gpsimd.affine_select(out=k.ident[:], in_=k.ident[:], compare_op=ALU.not_equal, fill=1.0,
                                         base=0, pattern=[[-1, P]], channel_multiplier=1))


def stage_tokens(k):
    nc, w = k.nc, k.w
    PRIME, VOCAB = 31, 125000
    with Scope(nc, "tok") as s:
        ids_i = s.sb("ids_i", [SEQS, N], I32)
        ids = s.sb("ids", [SEQS, N + 3])
        acc = s.sb("acc", [SEQS, 3, N])
        over = s.sb("over", [SEQS, 3, N])
        index = s.sb("index", [P, 3, SEQS], U32)
        rows = [s.sb(f"rows{n}", [P, SEQS, D]) for n in range(2)]
        keep = s.sb("keep", [P, 3])
        ones = s.sb("ones", [P, 3])
        turned = s.ps("turned", [P, 3, SEQS])
        loaded, step, hashed, transposed = s.sem("loaded"), s.sem("step"), s.sem("hashed"), s.sem("transposed")
        indexed, kept, one = s.sem("indexed"), s.sem("kept"), s.sem("one")
        landed = k.rows_landed
        block = s.block()
        dest = [k.h, rows[0], rows[1]]

        @block.sync
        def _(sp):
            sp.dma_start(ids_i[:], w["x"]).then_inc(loaded, 16)

        @block.gpsimd
        def _(pool):
            link = Link(pool, one)
            link(nc.gpsimd.memset(ones[:], 0.25))
            link(nc.gpsimd.affine_select(out=keep[:], in_=ones[:], compare_op=ALU.is_ge, fill=0.0, base=-1,
                                         pattern=[[-1, 3]], channel_multiplier=1))
            nc.gpsimd.sem_inc(kept, 1)
            pool.wait_ge(indexed, 1)
            for g in range(3):
                for b in range(SEQS):
                    nc.gpsimd.indirect_dma_start(
                        dest[g][:, b, :], None, w[f"L0_tok_emb_{g + 2}"],
                        bass.IndirectOffsetOnAxis(index[:, g, b:b + 1], 0)).then_inc(landed[g], 16)

        @block.vector
        def _(dve):
            link = Link(dve, step)
            link(nc.vector.memset(ids[:], 0.0))
            dve.wait_ge(loaded, 16)
            link(nc.vector.tensor_copy(ids[:, 3:], ids_i[:]))
            for g in range(3):
                link(nc.vector.tensor_copy(acc[:, g, :], ids[:, 3:]))
                for j in range(1, g + 2):
                    link(nc.vector.scalar_tensor_tensor(out=acc[:, g, :], in0=ids[:, 3 - j:3 - j + N],
                                                        scalar=float(PRIME ** j % VOCAB), in1=acc[:, g, :],
                                                        op0=ALU.mult, op1=ALU.add))
            for bit in range(7, -1, -1):
                m = float(VOCAB << bit)
                link(nc.vector.tensor_scalar(over[:], acc[:], m, m, ALU.is_ge, ALU.mult))
                link(nc.vector.tensor_tensor(acc[:], acc[:], over[:], ALU.subtract))
            nc.vector.sem_inc(hashed, 1)
            dve.wait_ge(transposed, 1)
            nc.vector.tensor_copy(index[:], turned[:]).then_inc(indexed, 1)
            dve.wait_ge(kept, 1)
            for g in range(3):
                dve.wait_ge(landed[g], 16 * SEQS)
                if g == 0:
                    link(nc.vector.tensor_scalar(k.h[:], k.h[:], keep[:, 0:1], None, ALU.mult))
                else:
                    link(nc.vector.scalar_tensor_tensor(out=k.h[:], in0=dest[g][:], scalar=keep[:, g:g + 1],
                                                        in1=k.h[:], op0=ALU.mult, op1=ALU.add))

        @block.tensor
        def _(pe):
            pe.wait_ge(hashed, 1)
            for g in range(3):
                ins = nc.tensor.transpose(turned[:, g, :], acc[:, g, :], k.ident[0:SEQS, 0:SEQS])
            ins.then_inc(transposed, 1)


def stage_center(k, tag):
    nc = k.nc
    with Scope(nc, f"ln{tag}") as s:
        sq = s.sb("sq", [P, SEQS, D])
        mean = s.sb("mean", [P, SEQS, 1])
        std = s.sb("std", [P, SEQS, 1])
        eps = s.sb("eps", [P, 1])
        step, summed, rooted = s.sem("step"), s.sem("summed"), s.sem("rooted")
        block = s.block()

        @block.scalar
        def _(act):
            act.wait_ge(summed, 1)
            nc.scalar.activation(std[:], mean[:], ACT.Sqrt, bias=eps[:, 0:1], scale=1.0 / D).then_inc(rooted, 1)

        @block.vector
        def _(dve):
            link = Link(dve, step)
            link(nc.vector.memset(eps[:], LN_EPS))
            link(nc.vector.tensor_reduce(mean[:, :, 0], k.h[:], AX, ALU.add))
            link(nc.vector.tensor_scalar(mean[:], mean[:], 1.0 / D, None, ALU.mult))
            link(nc.vector.tensor_tensor(k.xc[:], k.h[:], bc(mean[:], [P, SEQS, D]), ALU.subtract))
            link(nc.vector.tensor_tensor(sq[:], k.xc[:], k.xc[:], ALU.mult))
            nc.vector.tensor_reduce(mean[:, :, 0], sq[:], AX, ALU.add).then_inc(summed, 1)
            dve.wait_ge(rooted, 1)
            link(nc.vector.reciprocal(k.rstd[:], std[:]))


def front_dve(k, dve, xs, t, normed):
    g = bass.ds(GROUP * t, GROUP)
    return k.nc.vector.tensor_tensor(xs[:, :, 0:D], k.xc[:, g, :], bc(k.rstd[:, g, :], [P, GROUP, D]), ALU.mult).then_inc(normed, 1)


def stage_edge_bias(k):
    nc, w = k.nc, k.w
    EDGES = w["L0_attn_edge_index"].shape[1]
    F = EDGES // P
    HEADS, CH = 8, 32
    with Scope(nc, "ebias") as s:
        tgt_i = s.sb("tgt_i", [P, 1, F], I32)
        tgt = s.sb("tgt", [P, 1, F])
        number = s.sb("number", [P, 1, F])
        token = s.sb("token", [P, N, 1])
        hit = s.sb("hit", [P, CH, F])
        best = s.sb("best", [P, N])
        last = s.sb("last", [P, 1])
        found = s.sb("found", [P, 1])
        row = s.sb("row", [P, 1])
        row_u = s.sb("row_u", [P, 1], U32)
        attr = s.sb("attr", [P, 3])
        we = s.sb("we", [P, 3, HEADS])
        be = s.sb("be", [P, HEADS])
        eb = s.sb("eb", [P, HEADS])
        spread = s.sb("spread", [P, 2, 4, 32])
        turned = s.ps("turned", [P, N])
        placed = s.ps("placed", [P, 2, N])
        loaded, counted, step, bested = s.sem("loaded"), s.sem("counted"), s.sem("step"), s.sem("bested")
        transposed, rowed, fetched, spreaded = s.sem("transposed"), s.sem("rowed"), k.attr_fetched, s.sem("spreaded")
        block = s.block()

        @block.sync
        def _(sp):
            sp.dma_start(tgt_i[:, 0, :], w["L0_attn_edge_index"][1].rearrange("(p f) -> p f", p=P)).then_inc(loaded, 16)
            sp.dma_start(we[:], w["L0_attn_We"].partition_broadcast(P)).then_inc(loaded, 16)
            sp.dma_start(be[:], w["L0_attn_be"].partition_broadcast(P)).then_inc(loaded, 16)

        @block.gpsimd
        def _(pool):
            nc.gpsimd.iota(number[:, 0, :], [[1, F]], 1, F, allow_small_or_imprecise_dtypes=True).then_inc(counted, 1)
            nc.gpsimd.iota(token[:, :, 0], [[1, N]], 0, 0, allow_small_or_imprecise_dtypes=True).then_inc(counted, 1)
            pool.wait_ge(rowed, 1)
            nc.gpsimd.indirect_dma_start(attr[:], None, w["L0_attn_edge_attr"],
                                         bass.IndirectOffsetOnAxis(row_u[:, 0:1], 0)).then_inc(fetched, 16)

        @block.vector
        def _(dve):
            link = Link(dve, step)
            link(nc.vector.memset(spread[:], 0.0))
            dve.wait_ge(loaded, 48)
            dve.wait_ge(counted, 2)
            link(nc.vector.tensor_copy(tgt[:], tgt_i[:]))
            for c in range(0, N, CH):
                link(nc.vector.tensor_tensor(hit[:], bc(tgt[:], [P, CH, F]), bc(token[:, c:c + CH, :], [P, CH, F]), ALU.is_equal))
                link(nc.vector.tensor_tensor(hit[:], hit[:], bc(number[:], [P, CH, F]), ALU.mult))
                link(nc.vector.tensor_reduce(best[:, c:c + CH], hit[:], AX, ALU.max))
            nc.vector.sem_inc(bested, 1)
            dve.wait_ge(transposed, 1)
            link(nc.vector.tensor_reduce(last[:], turned[:], AX, ALU.max))
            link(nc.vector.tensor_scalar(found[:], last[:], 1.0, None, ALU.is_ge))
            link(nc.vector.tensor_tensor(row[:], last[:], found[:], ALU.subtract))
            nc.vector.tensor_copy(row_u[:], row[:]).then_inc(rowed, 1)
            dve.wait_ge(fetched, 16)
            link(nc.vector.tensor_copy(eb[:], be[:]))
            for j in range(3):
                link(nc.vector.scalar_tensor_tensor(out=eb[:], in0=we[:, j, :], scalar=attr[:, j:j + 1], in1=eb[:],
                                                    op0=ALU.mult, op1=ALU.add))
            nc.vector.tensor_scalar(spread[:, :, :, 8], eb[:].rearrange("p (g h) -> p g h", g=2), found[:, 0:1], None,
                                    ALU.mult).then_inc(spreaded, 1)
            dve.wait_ge(transposed, 2)
            link(nc.vector.tensor_copy(k.colbias[:], placed[:]))

        @block.tensor
        def _(pe):
            pe.wait_ge(bested, 1)
            nc.tensor.transpose(turned[:], best[:], k.ident[:]).then_inc(transposed, 1)
            pe.wait_ge(spreaded, 1)
            for g in range(2):
                ins = nc.tensor.transpose(placed[:, g, :], spread[:, g].rearrange("p h c -> p (h c)"), k.ident[:])
            ins.then_inc(transposed, 1)


def in_turn(eng, prelude, body):
    prelude()
    body(0, 0, True, False, True)
    with eng.Fori(0, (GROUPS - 2) // 2) as i:
        body(2 * i + 1, 1, True, True, True)
        body(2 * i + 2, 0, True, True, True)
    body(GROUPS - 1, 1, True, True, False)
    body(GROUPS, 0, False, True, False)


def stage_l0_attn(k):
    nc, w = k.nc, k.w
    HEADS, HD, HP = 8, 8, 32
    UNITS = GROUP * 2
    with Scope(nc, "l0a") as s:
        wq = s.sb("wq", [P, 2, 4, HP])
        wk = s.sb("wk", [P, 2, 4, HP])
        wv = s.sb("wv", [P, D])
        wo = s.sb("wo", [P, D])
        k.colbias = s.sb("colbias", [P, 2, N])
        stage_edge_bias(k)
        compact = s.sb("compact", [P, 4, HD + 1])
        xs = s.sb("xs", [P, GROUP, P])
        xt = s.sb("xt", [P, TOK])
        q = s.sb("q", [P, 2, 2, TOK])
        keys = s.sb("keys", [P, 2, 2, GROUP, 4, N])
        v = s.sb("v", [P, 2, GROUP, HEADS, HP])
        top = s.sb("top", [P, 4, 4])
        probs = s.sb("probs", [P, 4, 4, N])
        probs_t = s.sb("probs_t", [P, 2, 4, N])
        ot = s.sb("ot", [P, 2, TOK])
        rden = s.sb("rden", [P, GROUP, HEADS, 1])
        mixed = s.sb("mixed", [P, GROUP, P])
        mt = s.sb("mt", [P, TOK])
        ps = s.ps("ps", [P, 8, 512])
        SC, TU, OT, X, Y = 0, 2, 4, 6, 7
        names = ("loaded step ready normed xt_made xt_ready projected q_ready k_ready v_ready scored topped exped turned "
                 "turned_ready valued ot_ready back inverted mixed_ready mt_made mt_ready outed added apart").split()
        S = {n: s.sem(n) for n in names}
        loaded, step, ready = S["loaded"], S["step"], S["ready"]
        block = s.block()

        def heads(flat):
            return flat.rearrange("p (h n) -> p h n", h=4)

        def seqs(flat):
            return flat.rearrange("p (b n) -> p b n", b=GROUP)

        @block.sync
        def _(sp):
            sp.wait_ge(ready, 1)
            for g in range(2):
                for wt, n in ((wq, "q"), (wk, "k")):
                    sp.dma_start(wt[0:D, g, :, 0:HD],
                                 w[f"L0_attn_W{n}"].rearrange("i (g h c) -> g i h c", g=2, c=HD)[g]).then_inc(loaded, 16)
                    sp.dma_start(wt[D:D + 1, g, :, 0:HD],
                                 w[f"L0_attn_b{n}"].rearrange("(o g h c) -> g o h c", o=1, g=2, c=HD)[g]).then_inc(loaded, 16)
            for wt, n in ((wv, "v"), (wo, "o")):
                sp.dma_start(wt[0:D, :], w[f"L0_attn_W{n}"]).then_inc(loaded, 16)
                sp.dma_start(wt[D:D + 1, :], w[f"L0_attn_b{n}"].rearrange("(o d) -> o d", o=1)).then_inc(loaded, 16)

        LOADED = 16 * 12

        @block.gpsimd
        def _(pool):
            nc.gpsimd.memset(v[:], 0.0).then_inc(S["v_ready"], 1)
            pool.wait_ge(S["v_ready"], 1)
            nc.gpsimd.memset(v[:, :, :, :, HD:HD + 1], 1.0).then_inc(S["v_ready"], 1)

        @block.vector
        def _(dve):
            vec = nc.vector
            link = Link(dve, step)
            vec.memset(wo[:], 0.0)
            vec.memset(wv[:], 0.0)
            vec.memset(wq[:], 0.0)
            link(vec.memset(wk[:], 0.0))
            vec.sem_inc(ready, 1)
            vec.memset(xs[:], 0.0)
            vec.memset(mixed[:], 0.0)
            link(vec.memset(keys[:], 0.0))
            link(vec.memset(xs[:, :, D:D + 1], 1.0))
            link(vec.memset(mixed[:, :, D:D + 1], 1.0))
            for h in range(4):
                r = slice(HP * h, HP * h + HP)
                for par in range(2):
                    for g in range(2):
                        ins = vec.tensor_copy(keys[r, par, g, :, h, :], bc(k.colbias[r, g:g + 1, :], [HP, GROUP, N]))
            link(vec.tensor_copy(compact[:], k.ident[:].rearrange("p (h c) -> p h c", h=4)[:, :, 0:HD + 1]))
            dve.wait_ge(loaded, LOADED)
            link(vec.tensor_scalar(wq[:], wq[:], HD ** -0.5, None, ALU.mult))
            link(vec.memset(wq[D:D + 1, :, :, HD:HD + 1], 1.0))
            vec.sem_inc(ready, 1)

            def front(t):
                front_dve(k, dve, xs[:], t, S["normed"])

            def keep_keys(t, par, g):
                dve.wait_ge(S["projected"], 5 * t + 3 + g)
                for h in range(2):
                    r = slice(HP * h, HP * h + HD)
                    ins = vec.tensor_copy(keys[r, par, g, :, h, :], seqs(ps[r, X, :]))
                ins.then_inc(S["k_ready"], 1)

            def prelude():
                front(0)
                keep_keys(0, 0, 0)
                keep_keys(0, 0, 1)

            def maximum(t, u):
                dve.wait_ge(S["scored"], UNITS * t + u + 1)
                vec.tensor_reduce(top[:, u % 4], heads(ps[:, SC + u % 2, :]), AX, ALU.max, negate=True).then_inc(S["topped"], 1)

            def keep_turned(t, u):
                dve.wait_ge(S["turned"], UNITS * t + u + 1)
                if not (isinstance(t, int) and t == 0 and u < 2):
                    dve.wait_ge(S["valued"], UNITS * t + u - 1)
                vec.tensor_copy(probs_t[:, u % 2], heads(ps[:, TU + u % 2, :])).then_inc(S["turned_ready"], 1)

            def normalize(t):
                dve.wait_ge(S["back"], t + 1)
                o = ps[:, Y, 0:GROUP * HEADS * (HD + 1)].rearrange("p (b h c) -> p b h c", b=GROUP, h=HEADS)
                vec.reciprocal(rden[:], o[:, :, :, HD:HD + 1]).then_inc(S["inverted"], 1)
                dve.wait_ge(S["inverted"], t + 1)
                vec.tensor_tensor(mixed[:, :, 0:D].rearrange("p b (h c) -> p b h c", h=HEADS), o[:, :, :, 0:HD],
                                  bc(rden[:], [P, GROUP, HEADS, HD]), ALU.mult).then_inc(S["mixed_ready"], 1)

            def add(t):
                dve.wait_ge(S["outed"], t + 1)
                g = bass.ds(GROUP * t, GROUP)
                vec.tensor_tensor(k.h[:, g, :], k.h[:, g, :], ps[:, Y, 0:GROUP * D].rearrange("p (b d) -> p b d", b=GROUP),
                                  ALU.add).then_inc(S["added"], 1)

            def body(t, par, cur, prev, nxt):
                for u in range(UNITS):
                    if cur:
                        maximum(t, u)
                    if u >= 2 and cur:
                        keep_turned(t, u - 2)
                    if u < 2 and prev:
                        keep_turned(t - 1, UNITS + u - 2)
                    if u == 0 and nxt:
                        front(t + 1)
                    if u in (4, 5) and nxt:
                        keep_keys(t + 1, 1 - par, u - 4)
                    if u == 3 and prev:
                        normalize(t - 1)
                    if u == 7 and prev:
                        add(t - 1)

            in_turn(dve, prelude, body)

        @block.scalar
        def _(act):
            act.wait_ge(S["v_ready"], 2)

            def keep_x(t):
                act.wait_ge(S["xt_made"], t + 1)
                nc.scalar.copy(xt[:], ps[:, X, :]).then_inc(S["xt_ready"], 1)

            def keep_q(t, par, g):
                act.wait_ge(S["projected"], 5 * t + g + 1)
                nc.scalar.copy(q[:, par, g, :], ps[:, X, :]).then_inc(S["q_ready"], 1)

            def keep_keys(t, par, g):
                act.wait_ge(S["projected"], 5 * t + 3 + g)
                for h in range(2, 4):
                    r = slice(HP * h, HP * h + HD)
                    ins = nc.scalar.copy(keys[r, par, g, :, h, :], seqs(ps[r, X, :]))
                ins.then_inc(S["k_ready"], 1)

            def keep_v(t, par):
                act.wait_ge(S["projected"], 5 * t + 5)
                nc.scalar.copy(v[:, par, :, :, 0:HD], ps[:, X, 0:GROUP * D].rearrange("p (b h c) -> p b h c", b=GROUP, c=HD)).then_inc(S["v_ready"], 1)

            def prelude():
                keep_x(0)
                keep_q(0, 0, 0)
                keep_q(0, 0, 1)
                keep_keys(0, 0, 0)
                keep_keys(0, 0, 1)
                keep_v(0, 0)

            def exponential(t, u):
                act.wait_ge(S["topped"], UNITS * t + u + 1)
                if not (isinstance(t, int) and t == 0 and u < 4):
                    act.wait_ge(S["turned"], UNITS * t + u - 3)
                for h in range(4):
                    ins = nc.scalar.activation(probs[:, u % 4, h], ps[:, SC + u % 2, h * N:(h + 1) * N], ACT.Exp, bias=top[:, u % 4, h:h + 1])
                ins.then_inc(S["exped"], 1)

            def keep_output(t, g):
                act.wait_ge(S["valued"], UNITS * t + 4 * g + 4)
                nc.scalar.copy(ot[:, g], ps[:, OT + g, :]).then_inc(S["ot_ready"], 1)

            def body(t, par, cur, prev, nxt):
                for u in range(UNITS):
                    if cur:
                        exponential(t, u)
                    if u == 1 and nxt:
                        keep_x(t + 1)
                    if u in (2, 3) and nxt:
                        keep_q(t + 1, 1 - par, u - 2)
                    if u == 2 and prev:
                        keep_output(t - 1, 1)
                    if u in (4, 5) and nxt:
                        keep_keys(t + 1, 1 - par, u - 4)
                    if u == 6 and nxt:
                        keep_v(t + 1, 1 - par)
                    if u == 6 and cur:
                        keep_output(t, 0)
                    if u == 5 and prev:
                        act.wait_ge(S["mt_made"], t)
                        nc.scalar.copy(mt[:], ps[:, Y, :]).then_inc(S["mt_ready"], 1)

            in_turn(act, prelude, body)

        @block.tensor
        def _(pe):
            mm = nc.tensor.matmul

            def turn_x(t):
                pe.wait_ge(S["normed"], t + 1)
                if not (isinstance(t, int) and t == 0):
                    pe.wait_ge(S["v_ready"], t + 2)
                for b in range(GROUP):
                    ins = nc.tensor.transpose(ps[:, X, b * N:(b + 1) * N], xs[:, b, :], k.ident[:])
                ins.then_inc(S["xt_made"], 1)

            def project(t, n):
                if n == 0:
                    pe.wait_ge(S["xt_ready"], t + 1)
                elif n <= 2:
                    pe.wait_ge(S["q_ready"], 2 * t + n)
                else:
                    pe.wait_ge(S["k_ready"], 4 * t + 2 * (n - 2))
                if n < 4:
                    wt = (wq, wk)[n // 2][:, n % 2].rearrange("p h c -> p (h c)")
                    ins = mm(ps[:, X, :], wt, xt[:], start=True, stop=True)
                else:
                    for b in range(GROUP):
                        ins = mm(ps[:, X, b * D:(b + 1) * D], xt[:, b * N:(b + 1) * N], wv[:], start=True, stop=True)
                ins.then_inc(S["projected"], 1)

            def prelude():
                pe.wait_ge(ready, 2)
                turn_x(0)
                for n in range(5):
                    project(0, n)

            def scores(t, par, u):
                g, b = u // 4, u % 4
                if u == 0:
                    pe.wait_ge(S["q_ready"], 2 * t + 2)
                    pe.wait_ge(S["k_ready"], 4 * t + 4)
                if not (isinstance(t, int) and t == 0 and u < 2):
                    pe.wait_ge(S["exped"], UNITS * t + u - 1)
                mm(ps[:, SC + u % 2, :], q[:, par, g, b * N:(b + 1) * N], keys[:, par, g, b].rearrange("p h n -> p (h n)"),
                   start=True, stop=True).then_inc(S["scored"], 1)

            def turn(t, u):
                pe.wait_ge(S["exped"], UNITS * t + u + 1)
                if not (isinstance(t, int) and t == 0 and u < 2):
                    pe.wait_ge(S["turned_ready"], UNITS * t + u - 1)
                for h in range(4):
                    ins = nc.tensor.transpose(ps[:, TU + u % 2, h * N:(h + 1) * N], probs[:, u % 4, h], k.ident[:])
                ins.then_inc(S["turned"], 1)

            def values(t, par, u):
                g, b = u // 4, u % 4
                pe.wait_ge(S["turned_ready"], UNITS * t + u + 1)
                if u == 0:
                    pe.wait_ge(S["v_ready"], t + 3)
                if b == 0 and not (isinstance(t, int) and t == 0):
                    pe.wait_ge(S["ot_ready"], 2 * t + g - 1)
                nc.tensor.sem_inc(S["apart"], 1)
                for h in range(4):
                    ins = mm(ps[HP * h:HP * h + HP, OT + g, b * N:(b + 1) * N], v[:, par, b, 4 * g + h, :], probs_t[:, u % 2, h],
                             start=True, stop=True, tile_position=(0, HP * h))
                ins.then_inc(S["valued"], 1)

            def turn_back(t):
                pe.wait_ge(S["ot_ready"], 2 * t + 2)
                if not (isinstance(t, int) and t == 0):
                    pe.wait_ge(S["added"], t)
                for b in range(GROUP):
                    for g in range(2):
                        c = (2 * b + g) * 4 * (HD + 1)
                        ins = mm(ps[:, Y, c:c + 4 * (HD + 1)], ot[:, g, b * N:(b + 1) * N], compact[:].rearrange("p h c -> p (h c)"),
                                 start=True, stop=True)
                ins.then_inc(S["back"], 1)

            def turn_mixed(t):
                pe.wait_ge(S["mixed_ready"], t + 1)
                for b in range(GROUP):
                    ins = nc.tensor.transpose(ps[:, Y, b * N:(b + 1) * N], mixed[:, b, :], k.ident[:])
                ins.then_inc(S["mt_made"], 1)

            def outputs(t):
                pe.wait_ge(S["mt_ready"], t + 1)
                for b in range(GROUP):
                    ins = mm(ps[:, Y, b * D:(b + 1) * D], mt[:, b * N:(b + 1) * N], wo[:], start=True, stop=True)
                ins.then_inc(S["outed"], 1)

            def body(t, par, cur, prev, nxt):
                for u in range(UNITS):
                    if cur:
                        scores(t, par, u)
                    if u >= 2 and cur:
                        turn(t, u - 2)
                    if u < 2 and prev:
                        turn(t - 1, UNITS + u - 2)
                    if u >= 3 and cur:
                        values(t, par, u - 3)
                    if u < 3 and prev:
                        values(t - 1, 1 - par, UNITS + u - 3)
                    if u == 1 and nxt:
                        turn_x(t + 1)
                    if 2 <= u <= 6 and nxt:
                        project(t + 1, u - 2)
                    if u == 3 and prev:
                        turn_back(t - 1)
                    if u == 5 and prev:
                        turn_mixed(t - 1)
                    if u == 7 and prev:
                        outputs(t - 1)

            in_turn(pe, prelude, body)


def stage_l0_ffn(k):
    nc, w = k.nc, k.w
    H, G, A1 = 8, 64, D + 1
    PAIRS = H // 2
    with Scope(nc, "l0f") as s:
        slice_map = s.sb("slice_map", [A1, H, G])
        pair_map = s.sb("pair_map", [A1, H, A1])
        value_map = s.sb("value_map", [A1, H, D])
        fold_l0_ffn(k, slice_map, pair_map, value_map)
        xs = s.sb("xs", [P, GROUP, A1])
        xt = s.sb("xt", [A1, TOK])
        sw = s.sb("sw", [P, GROUP, H, G])
        sw_t = s.sb("sw_t", [P, GROUP, PAIRS, N])
        top = s.sb("top", [P, GROUP, H, 1])
        den = s.sb("den", [P, GROUP, H, 1])
        rden = s.sb("rden", [P, GROUP, H, 1])
        znorm = s.sb("znorm", [P, GROUP, PAIRS, 1])
        z = s.sb("z", [P, GROUP, PAIRS, A1])
        z_t = s.sb("z_t", [A1, GROUP, H, G])
        za = s.sb("za", [A1, GROUP, H, G])
        vals = s.sb("vals", [P, GROUP, 2, 2, D])
        att = s.sb("att", [P, GROUP, PAIRS, G])
        atop = s.sb("atop", [P, GROUP, PAIRS, 1])
        aden = s.sb("aden", [P, GROUP, PAIRS, 1])
        att_t = s.sb("att_t", [P, GROUP, 2, P])
        y = s.sb("y", [P, GROUP, PAIRS, D])
        ps = s.ps("ps", [P, 8, 512])
        names = ("step normed xt_made xt_ready logit shifted exped weighted swt_made swt_ready z_made z_ready zt_made zt_ready "
                 "za_made za_ready val_made val_ready sc_made sc_shifted sc_exped att_ready att_made att_t_ready y_made y_ready outed apart").split()
        S = {n: s.sem(n) for n in names}
        block = s.block()

        def view(bank, cols, *dims):
            a = ps[:, bank, 0:cols]
            if len(dims) == 1:
                return a.rearrange("p (a b) -> p a b", b=dims[0])
            return a.rearrange("p (a b c) -> p a b c", b=dims[0], c=dims[1])

        XT, LOG, SWT, Z, ZT, ZA, VAL, SC, AT, Y, OUT = 0, 1, 3, 5, (7, 0), 1, 3, 5, (7, 0), 1, 3

        @block.vector
        def _(dve):
            link = Link(dve, S["step"])
            link(nc.vector.memset(xs[:, :, D:A1], 1.0))
            PER = 1 + GROUP * 10
            with dve.Fori(0, GROUPS) as t:
                link = Link(dve, S["step"], 1 + PER * t, PER)
                front_dve(k, dve, xs[:], t, S["normed"])

                def shift(b):
                    dve.wait_ge(S["logit"], GROUP * t + b + 1)
                    lg = view(LOG + b % 2, 512, G)
                    link(nc.vector.tensor_reduce(top[:, b, :, 0], lg, AX, ALU.max))
                    nc.vector.tensor_tensor(sw[:, b], lg, bc(top[:, b], [P, H, G]), ALU.subtract).then_inc(S["shifted"], 1)

                def weigh(b):
                    dve.wait_ge(S["exped"], GROUP * t + b + 1)
                    link(nc.vector.tensor_reduce(den[:, b, :, 0], sw[:, b], AX, ALU.add))
                    link(nc.vector.reciprocal(rden[:, b], den[:, b]))
                    link(nc.vector.tensor_tensor(sw[:, b], sw[:, b], bc(rden[:, b], [P, H, G]), ALU.mult))
                    nc.vector.sem_inc(S["weighted"], 1)

                for b in range(GROUP + 1):
                    if b < GROUP:
                        shift(b)
                    if b >= 1:
                        weigh(b - 1)
                for b in range(GROUP):
                    dve.wait_ge(S["z_made"], GROUP * t + b + 1)
                    zz = view(Z + b % 2, PAIRS * A1, A1)
                    link(nc.vector.tensor_scalar(znorm[:, b], zz[:, :, D:A1], 1e-5, None, ALU.add))
                    link(nc.vector.reciprocal(znorm[:, b], znorm[:, b]))
                    link(nc.vector.tensor_tensor(z[:, b], zz, bc(znorm[:, b], [P, PAIRS, A1]), ALU.mult))
                    nc.vector.sem_inc(S["z_ready"], 1)
                for b in range(GROUP):
                    dve.wait_ge(S["val_made"], GROUP * t + b + 1)
                    nc.vector.tensor_copy(vals[:, b], view(VAL + b % 2, 256, 2, D)).then_inc(S["val_ready"], 1)

                def sc_shift(b):
                    dve.wait_ge(S["sc_made"], GROUP * t + b + 1)
                    sc = view(SC + b % 2, 256, G)
                    link(nc.vector.tensor_reduce(atop[:, b, :, 0], sc, AX, ALU.max))
                    nc.vector.tensor_tensor(att[:, b], sc, bc(atop[:, b], [P, PAIRS, G]), ALU.subtract).then_inc(S["sc_shifted"], 1)

                def sc_weigh(b):
                    dve.wait_ge(S["sc_exped"], GROUP * t + b + 1)
                    link(nc.vector.tensor_reduce(aden[:, b, :, 0], att[:, b], AX, ALU.add))
                    link(nc.vector.reciprocal(aden[:, b], aden[:, b]))

                for b in range(GROUP + 1):
                    if b < GROUP:
                        sc_shift(b)
                    if b >= 1:
                        sc_weigh(b - 1)
                for b in range(GROUP):
                    dve.wait_ge(S["y_made"], GROUP * t + b + 1)
                    for q in range(2):
                        yy = view(Y + 2 * (b % 2) + q, 128, D)
                        ins = nc.vector.tensor_tensor(y[:, b].rearrange("p (j q) o -> p q j o", q=2)[:, q], yy,
                                                      bc(aden[:, b].rearrange("p (j q) o -> p q j o", q=2)[:, q], [P, 2, D]), ALU.mult)
                    ins.then_inc(S["y_ready"], 1)
                dve.wait_ge(S["outed"], t + 1)
                g = bass.ds(GROUP * t, GROUP)
                link(nc.vector.tensor_tensor(k.h[:, g, :], k.h[:, g, :], view(OUT + 2, 256, D), ALU.add))
                link.close()

        @block.scalar
        def _(act):
            with act.Fori(0, GROUPS) as t:
                act.wait_ge(S["xt_made"], t + 1)
                nc.scalar.copy(xt[:], ps[0:A1, XT, :]).then_inc(S["xt_ready"], 1)
                for b in range(GROUP):
                    act.wait_ge(S["shifted"], GROUP * t + b + 1)
                    nc.scalar.activation(sw[:, b], sw[:, b], ACT.Exp).then_inc(S["exped"], 1)
                for b in range(GROUP):
                    act.wait_ge(S["swt_made"], GROUP * t + b + 1)
                    nc.scalar.copy(sw_t[:, b], view(SWT + b % 2, 512, N)).then_inc(S["swt_ready"], 1)
                for b in range(GROUP):
                    act.wait_ge(S["zt_made"], GROUP * t + b + 1)
                    nc.scalar.copy(z_t[:, b], view(ZT[b % 2], 512, G)[0:A1]).then_inc(S["zt_ready"], 1)
                for b in range(GROUP):
                    act.wait_ge(S["za_made"], GROUP * t + b + 1)
                    nc.scalar.copy(za[:, b], view(ZA + b % 2, 512, G)[0:A1]).then_inc(S["za_ready"], 1)
                for b in range(GROUP):
                    act.wait_ge(S["sc_shifted"], GROUP * t + b + 1)
                    nc.scalar.activation(att[:, b], att[:, b], ACT.Exp).then_inc(S["sc_exped"], 1)
                for b in range(GROUP):
                    act.wait_ge(S["att_made"], GROUP * t + b + 1)
                    nc.scalar.copy(att_t[:, b], view(AT[b % 2], 256, P)).then_inc(S["att_t_ready"], 1)

        @block.tensor
        def _(pe):
            mm = nc.tensor.matmul
            with pe.Fori(0, GROUPS) as t:
                def free(sem, b):
                    if b >= 2:
                        pe.wait_ge(S[sem], GROUP * t + b - 1)

                pe.wait_ge(S["normed"], t + 1)
                for b in range(GROUP):
                    ins = nc.tensor.transpose(ps[0:A1, XT, b * N:(b + 1) * N], xs[:, b, :], k.ident[:])
                ins.then_inc(S["xt_made"], 1)
                pe.wait_ge(S["xt_ready"], t + 1)
                for b in range(GROUP):
                    free("shifted", b)
                    mm(ps[:, LOG + b % 2, :], xt[:, b * N:(b + 1) * N], slice_map[:].rearrange("p h g -> p (h g)"),
                       start=True, stop=True).then_inc(S["logit"], 1)
                for b in range(GROUP):
                    pe.wait_ge(S["weighted"], GROUP * t + b + 1)
                    free("swt_ready", b)
                    for q in range(PAIRS):
                        ins = nc.tensor.transpose(view(SWT + b % 2, 512, N)[:, q], sw[:, b, 2 * q:2 * q + 2].rearrange("p h g -> p (h g)"), k.ident[:])
                    ins.then_inc(S["swt_made"], 1)
                    free("z_ready", b)
                    for q in range(PAIRS):
                        ins = mm(view(Z + b % 2, PAIRS * A1, A1)[:, q], sw[:, b, 2 * q:2 * q + 2].rearrange("p h g -> p (h g)"),
                                 xs[:, b, :], start=True, stop=True)
                    ins.then_inc(S["z_made"], 1)
                for b in range(GROUP):
                    pe.wait_ge(S["z_ready"], GROUP * t + b + 1)
                    free("zt_ready", b)
                    for q in range(PAIRS):
                        ins = nc.tensor.transpose(view(ZT[b % 2], 512, N)[0:A1, q], z[:, b, q], k.ident[:])
                    ins.then_inc(S["zt_made"], 1)
                for b in range(GROUP):
                    pe.wait_ge(S["zt_ready"], GROUP * t + b + 1)
                    free("za_ready", b)
                    for h in range(H):
                        ins = mm(view(ZA + b % 2, 512, G)[0:A1, h], pair_map[:, h], z_t[:, b, h], start=True, stop=True)
                    ins.then_inc(S["za_made"], 1)
                    free("val_ready", b)
                    if b < 2:
                        pe.wait_ge(S["swt_ready"], GROUP * t + GROUP)
                    for h in range(H):
                        pr, sub = h // 2, h % 2
                        r = 64 * (pr % 2)
                        ins = mm(view(VAL + b % 2, 256, 2, D)[r:r + 64, pr // 2, sub], z_t[:, b, h], value_map[:, h], start=True, stop=True)
                    ins.then_inc(S["val_made"], 1)
                for b in range(GROUP):
                    pe.wait_ge(S["za_ready"], GROUP * t + b + 1)
                    free("sc_shifted", b)
                    for h in range(H):
                        r = 64 * (h % 2)
                        ins = mm(view(SC + b % 2, 256, G)[r:r + 64, h // 2], za[:, b, h], z_t[:, b, h], start=True, stop=True)
                    ins.then_inc(S["sc_made"], 1)
                for b in range(GROUP):
                    pe.wait_ge(S["sc_exped"], GROUP * t + b + 1)
                    free("att_t_ready", b)
                    for j in range(2):
                        ins = nc.tensor.transpose(view(AT[b % 2], 256, P)[:, j], att[:, b, 2 * j:2 * j + 2].rearrange("p a g -> p (a g)"), k.ident[:])
                    ins.then_inc(S["att_made"], 1)
                for b in range(GROUP):
                    pe.wait_ge(S["att_t_ready"], GROUP * t + b + 1)
                    if b == 0:
                        pe.wait_ge(S["val_ready"], GROUP * t + GROUP)
                    free("y_ready", b)
                    nc.tensor.sem_inc(S["apart"], 1)
                    for h in range(H):
                        pr, sub = h // 2, h % 2
                        r, o = 64 * (pr % 2), 64 * sub
                        ins = mm(view(Y + 2 * (b % 2) + pr % 2, 128, D)[o:o + 64, pr // 2], att_t[r:r + 64, b, pr // 2, o:o + 64],
                                 vals[r:r + 64, b, pr // 2, sub], start=True, stop=True, tile_position=(r, o))
                    ins.then_inc(S["y_made"], 1)
                for b in range(GROUP):
                    pe.wait_ge(S["y_ready"], GROUP * t + b + 1)
                    for q in range(PAIRS):
                        ins = mm(view(OUT + 2, 256, D)[:, b], sw_t[:, b, q], y[:, b, q], start=(q == 0), stop=(q == PAIRS - 1))
                ins.then_inc(S["outed"], 1)


def fold_l0_ffn(k, slice_map, pair_map, value_map):
    nc, w = k.nc, k.w
    H, G, A1 = 8, 64, D + 1
    with Scope(nc, "l0fold") as s:
        fx = s.sb("fx", [A1, H, D])
        wx = s.sb("wx", [A1, H, D])
        fx_t = s.sb("fx_t", [D, H, A1])
        wx_t = s.sb("wx_t", [D, H, A1])
        wsl, wq, wk, wv = (s.sb(n, [D, D]) for n in ("wsl", "wq", "wk", "wv"))
        wout = s.sb("wout", [D, H, D])
        bsl = s.sb("bsl", [A1, G])
        temp = s.sb("temp", [A1, H, 1])
        bout = s.sb("bout", [P, 1, D])
        proj = s.sb("proj", [D, 3, H, A1])
        ps = s.ps("ps", [P, 8, 512])
        loaded, step, made, ready = s.sem("loaded"), s.sem("step"), s.sem("made"), s.sem("ready")
        block = s.block()

        def maps(first):
            return [ps[0:D, first + j, 0:4 * A1].rearrange("p (h c) -> p h c", c=A1) for j in range(2)]

        @block.sync
        def _(sp):
            n = 0
            for dst, src in ((fx, "fx"), (wx, "x")):
                sp.dma_start(dst[0:D], w[f"L0_ffn_W_{src}"].rearrange("i (h d) -> i h d", d=D)).then_inc(loaded, 16)
                sp.dma_start(dst[D:A1], w[f"L0_ffn_b_{src}"].rearrange("(o h d) -> o h d", o=1, d=D)).then_inc(loaded, 16)
            for dst, src in ((wsl, "W_slice"), (wq, "W_q"), (wk, "W_k"), (wv, "W_v")):
                sp.dma_start(dst[:], w[f"L0_ffn_{src}"]).then_inc(loaded, 16)
            sp.dma_start(wout[:], w["L0_ffn_W_out"].rearrange("(h d) o -> d h o", d=D)).then_inc(loaded, 16)
            sp.dma_start(bsl[D:A1, :], w["L0_ffn_b_slice"].rearrange("(o g) -> o g", o=1)).then_inc(loaded, 16)
            sp.dma_start(temp[:, :, 0], w["L0_ffn_temperature"].rearrange("a h b c -> (a h b c)").partition_broadcast(A1)).then_inc(loaded, 16)
            sp.dma_start(bout[:, 0, :], w["L0_ffn_b_out"].partition_broadcast(P)).then_inc(loaded, 16)

        LOADED = 16 * 12

        @block.vector
        def _(dve):
            link = Link(dve, step)
            dve.wait_ge(loaded, LOADED)
            link(nc.vector.tensor_tensor(k.h[:], k.h[:], bc(bout[:], [P, SEQS, D]), ALU.add))
            link(nc.vector.tensor_scalar(temp[:], temp[:], 0.1, 5.0, ALU.max, ALU.min))
            link(nc.vector.reciprocal(temp[:], temp[:]))
            dve.wait_ge(made, 1)
            for j in range(2):
                link(nc.vector.tensor_copy(fx_t[:, 4 * j:4 * j + 4], maps(0)[j]))
                link(nc.vector.tensor_copy(wx_t[:, 4 * j:4 * j + 4], maps(2)[j]))
            nc.vector.sem_inc(ready, 1)
            dve.wait_ge(made, 2)
            for n in range(3):
                for j in range(2):
                    src = maps(2 * n)[j]
                    if n == 0:
                        link(nc.vector.tensor_scalar(proj[:, n, 4 * j:4 * j + 4], src, D ** -0.5, None, ALU.mult))
                    else:
                        link(nc.vector.tensor_copy(proj[:, n, 4 * j:4 * j + 4], src))
            sl = ps[0:A1, 6, :].rearrange("p (h g) -> p h g", g=G)
            link(nc.vector.tensor_copy(slice_map[:], sl))
            link(nc.vector.tensor_tensor(slice_map[D:A1], slice_map[D:A1],
                                         bc(bsl[D:A1, :].rearrange("p (o g) -> p o g", o=1), [1, H, G]), ALU.add))
            link(nc.vector.tensor_tensor(slice_map[:], slice_map[:], bc(temp[:], [A1, H, G]), ALU.mult))
            nc.vector.sem_inc(ready, 1)
            dve.wait_ge(made, 3)
            for j in range(2):
                link(nc.vector.tensor_copy(pair_map[:, 4 * j:4 * j + 4], ps[0:A1, j, 0:4 * A1].rearrange("p (h c) -> p h c", c=A1)))
            link(nc.vector.tensor_copy(value_map[:], ps[0:A1, 2, :].rearrange("p (h o) -> p h o", o=D)))

        @block.tensor
        def _(pe):
            mm = nc.tensor.matmul
            pe.wait_ge(loaded, LOADED)
            for h in range(H):
                nc.tensor.transpose(maps(0)[h // 4][:, h % 4], fx[:, h], k.ident[0:A1, 0:A1])
                ins = nc.tensor.transpose(maps(2)[h // 4][:, h % 4], wx[:, h], k.ident[0:A1, 0:A1])
            ins.then_inc(made, 1)
            pe.wait_ge(ready, 1)
            for n, wt in enumerate((wq, wk, wv)):
                for j in range(2):
                    mm(maps(2 * n)[j], wt[:], fx_t[:, 4 * j:4 * j + 4], start=True, stop=True)
            for h in range(H):
                ins = mm(ps[0:A1, 6, h * G:(h + 1) * G], wx_t[:, h], wsl[:], start=True, stop=True)
            ins.then_inc(made, 1)
            pe.wait_ge(ready, 2)
            for h in range(H):
                mm(ps[0:A1, h // 4, (h % 4) * A1:(h % 4 + 1) * A1], proj[:, 0, h], proj[:, 1, h], start=True, stop=True)
                ins = mm(ps[0:A1, 2, h * D:(h + 1) * D], proj[:, 2, h], wout[:, h], start=True, stop=True)
            ins.then_inc(made, 1)


def stage_edge_cells(k):
    nc, w = k.nc, k.w
    E = w["L1_attn_edge_index"].shape[1]
    BS = 32
    LANE = E // P
    CPL = LANE // P
    UN = 2
    CB = UN * CPL
    STEPS = P // (2 * UN)
    HEADS = 4
    assert CPL == 16
    keys_dram = nc.dram_tensor("edge_keys", (E // P, P), F32).ap()
    with Scope(nc, "cells") as s:
        r_t = s.sb("r_t", [P, P, CPL, 1], BF16)
        c_t = s.sb("c_t", [P, P, CPL, 1], BF16)
        stored = s.sem("stored")
        with Scope(nc, "cellkeys") as s1:
            rows = s1.sb("rows", [P, LANE], I32)
            cols = s1.sb("cols", [P, LANE], I32)
            away = s1.sb("away", [P, LANE], I32)
            key = s1.sb("key", [P, LANE])
            rf = s1.sb("rf", [P, LANE])
            rb = s1.sb("rb", [P, CPL, P], BF16)
            cb = s1.sb("cb", [P, CPL, P], BF16)
            identb = s1.sb("identb", [P, P], BF16)
            ps = s1.ps("ps", [P, 4, 8, P], BF16)
            loaded, step, keyed, turned, copied = (s1.sem(n) for n in "loaded step keyed turned copied".split())
            block = s1.block()

            @block.sync
            def _(sp):
                sp.dma_start(rows[:], w["L1_attn_edge_index"][0].rearrange("(p f) -> p f", p=P)).then_inc(loaded, 16)
                sp.dma_start(cols[:], w["L1_attn_edge_index"][1].rearrange("(p f) -> p f", p=P)).then_inc(loaded, 16)
                sp.wait_ge(keyed, 1)
                sp.dma_start(keys_dram.rearrange("(p c) f -> p (c f)", p=P), key[:]).then_inc(stored, 16)
                sp.wait_ge(stored, 16)

            @block.vector
            def _(dve):
                link = Link(dve, step)
                link(nc.vector.tensor_copy(identb[:], k.ident[:]))
                dve.wait_ge(loaded, 32)
                link(nc.vector.tensor_tensor(away[:], rows[:], cols[:], ALU.bitwise_xor))
                link(nc.vector.tensor_scalar(away[:], away[:], 5, None, ALU.logical_shift_right))
                link(nc.vector.tensor_scalar(cols[:], cols[:], BS - 1, None, ALU.bitwise_and))
                link(nc.vector.tensor_scalar(rf[:], away[:], 1.0, 128.0, ALU.min, ALU.mult))
                link(nc.vector.tensor_tensor(rf[:], rf[:], rows[:], ALU.add))
                link(nc.vector.tensor_scalar(rf[:], rf[:], 128.0, None, ALU.min))
                link(nc.vector.scalar_tensor_tensor(out=key[:], in0=rf[:], scalar=float(BS), in1=cols[:], op0=ALU.mult, op1=ALU.add))
                nc.vector.tensor_copy(rb[:].rearrange("p c f -> p (c f)"), rf[:]).then_inc(keyed, 1)
                nc.vector.tensor_copy(cb[:].rearrange("p c f -> p (c f)"), cols[:]).then_inc(keyed, 1)
                for n in range(4):
                    dst = (r_t, c_t)[n // 2]
                    dve.wait_ge(turned, n + 1)
                    nc.vector.tensor_copy(dst[:, :, 8 * (n % 2):8 * (n % 2) + 8, 0].rearrange("f p c -> f c p"), ps[:, n]).then_inc(copied, 1)
                dve.wait_ge(copied, 4)

            @block.tensor
            def _(pe):
                pe.wait_ge(keyed, 2)
                for n in range(4):
                    src = (rb, cb)[n // 2]
                    for j in range(8):
                        ins = nc.tensor.transpose(ps[:, n, j], src[:, 8 * (n % 2) + j], identb[:])
                    ins.then_inc(turned, 1)

        with Scope(nc, "cellhits") as s2:
            hits = s2.sb("hits", [P, P, BS])
            with Scope(nc, "cellcount") as s3:
                tok_i = s3.sb("tok_i", [P, 1, P])
                tok = s3.sb("tok", [P, P, CB], BF16)
                power = s3.sb("power", [P, 1, UN, CPL], BF16)
                rhot = s3.sb("rhot", [P, 2, P, CB], BF16)
                chot = s3.sb("chot", [P, 2, BS, CB], BF16)
                ps = s3.ps("ps", [P, 2, 512])
                step, iotad, hot, counted, taken = (s3.sem(n) for n in "step iotad hot counted taken".split())
                block = s3.block()

                @block.gpsimd
                def _(pool):
                    nc.gpsimd.iota(tok_i[:, 0, :], [[1, P]], 0, 0, allow_small_or_imprecise_dtypes=True).then_inc(iotad, 1)

                @block.vector
                def _(dve):
                    link = Link(dve, step)
                    for b in range(CPL):
                        link(nc.vector.memset(power[:, :, :, b], 2.0 ** (8 * (b - 8))))
                    dve.wait_ge(iotad, 1)
                    link(nc.vector.tensor_copy(tok[:], bc(tok_i[:].rearrange("p o n -> p n o"), [P, P, CB])))
                    BASE = CPL + 1
                    with dve.Fori(0, STEPS) as t:
                        link = Link(dve, step, BASE + 2 * t, 2)
                        for j in range(2):
                            dve.wait_ge(counted, 2 * t + j + 1)
                            lanes = bass.ds(2 * UN * t + UN * j, UN)
                            rr = r_t[:, lanes].rearrange("p l c o -> p o (l c)")
                            cc = c_t[:, lanes].rearrange("p l c o -> p o (l c)")
                            nc.vector.tensor_tensor(rhot[:, j], bc(rr, [P, P, CB]), tok[:], ALU.is_equal).then_inc(hot, 1)
                            link(nc.vector.tensor_tensor(chot[:, j], bc(cc, [P, BS, CB]), tok[:, 0:BS], ALU.is_equal))
                            nc.vector.tensor_tensor(chot[:, j], chot[:, j], bc(power[:].rearrange("p o l c -> p o (l c)"), [P, BS, CB]), ALU.mult).then_inc(hot, 1)
                        link.close()

                @block.tensor
                def _(pe):
                    nc.tensor.sem_inc(counted, 2)
                    with pe.Fori(0, STEPS) as t:
                        for j in range(2):
                            pe.wait_ge(hot, 2 * (2 * t + j) + 2)
                            pe.wait_ge(taken, 2 * t + j + 1)
                            for l in range(UN):
                                for b in range(CPL):
                                    ins = nc.tensor.matmul(ps[:, j, l * BS:(l + 1) * BS], rhot[:, j, :, l * CPL + b], chot[:, j, :, l * CPL + b],
                                                           start=(b == 0), stop=(b == CPL - 1))
                            ins.then_inc(counted, 1)

                @block.scalar
                def _(act):
                    nc.scalar.sem_inc(taken, 2)
                    with act.Fori(0, STEPS) as t:
                        for j in range(2):
                            act.wait_ge(counted, 2 * t + j + 3)
                            nc.scalar.copy(hits[:, bass.ds(2 * UN * t + UN * j, UN), :],
                                           ps[:, j, 0:UN * BS].rearrange("p (l k) -> p l k", l=UN)).then_inc(taken, 1)

            with Scope(nc, "cellfind") as s4:
                expo = s4.sb("expo", [P, P, BS], I32)
                lane = s4.sb("lane", [P, P, 1])
                last = s4.sb("last", [P, BS])
                found = s4.sb("found", [P, BS])
                number = s4.sb("number", [P, BS])
                last_i = s4.sb("last_i", [P, 2, BS], I32)
                chunk = s4.sb("chunk", [P, BS], U32)
                keys = s4.sb("keys", [P, BS, P])
                vals = s4.sb("vals", [P, BS, P])
                cell = s4.sb("cell", [P, BS, 1])
                place = s4.sb("place", [P, 1, P])
                at = s4.sb("at", [P, BS, 1])
                col = s4.sb("col", [P, BS])
                row_i = s4.sb("row_i", [P, 1], I32)
                row_f = s4.sb("row_f", [P, 1])
                diag = s4.sb("diag", [P, BS])
                off = s4.sb("off", [P, BS])
                mask = s4.sb("mask", [P, BS + 1])
                feats = s4.sb("feats", [P, 4, BS + 1])
                pos = s4.sb("pos", [P, BS, 3])
                pos_r = s4.sb("pos_r", [P, 3])
                gw = s4.sb("gw", [P, HEADS, 4])
                gb = s4.sb("gb", [P, HEADS])
                loaded, iotad, step, chunked = (s4.sem(n) for n in "loaded iotad step chunked".split())
                fetched = k.chunks_fetched
                block = s4.block()

                @block.sync
                def _(sp):
                    for n in range(P // BS):
                        sp.dma_start(pos[n * BS:(n + 1) * BS].rearrange("p c x -> p (c x)"),
                                     w["L1_attn_positions"][n * BS:(n + 1) * BS].rearrange("c x -> (c x)").partition_broadcast(BS)).then_inc(loaded, 16)
                    sp.dma_start(pos_r[:], w["L1_attn_positions"][0:P]).then_inc(loaded, 16)
                    sp.dma_start(gw[:], w["L1_attn_gate_w"].partition_broadcast(P)).then_inc(loaded, 16)
                    sp.dma_start(gb[:], w["L1_attn_gate_b"].partition_broadcast(P)).then_inc(loaded, 16)

                @block.gpsimd
                def _(pool):
                    imp = dict(allow_small_or_imprecise_dtypes=True)
                    nc.gpsimd.iota(lane[:, :, 0], [[256, P]], 0, 0, **imp).then_inc(iotad, 1)
                    nc.gpsimd.iota(cell[:, :, 0], [[1, BS]], 0, BS, **imp).then_inc(iotad, 1)
                    nc.gpsimd.iota(place[:, 0, :], [[1, P]], 1, 0, **imp).then_inc(iotad, 1)
                    nc.gpsimd.iota(col[:], [[1, BS]], 0, 0, **imp).then_inc(iotad, 1)
                    nc.gpsimd.iota(row_i[:], [[0, 1]], 0, 1).then_inc(iotad, 1)
                    pool.wait_ge(chunked, 1)
                    for c in range(BS):
                        index = bass.IndirectOffsetOnAxis(chunk[:, c:c + 1], 0)
                        nc.gpsimd.indirect_dma_start(keys[:, c, :], None, keys_dram, index).then_inc(fetched, 16)
                        nc.gpsimd.indirect_dma_start(vals[:, c, :], None, w["L1_attn_edge_values"].rearrange("(c f) -> c f", f=P),
                                                     index).then_inc(fetched, 16)

                @block.vector
                def _(dve):
                    link = Link(dve, step)
                    v = nc.vector
                    full = [P, P, BS]
                    dve.wait_ge(iotad, 5)
                    link(v.tensor_scalar(expo[:], hits[:].bitcast(I32), 23, None, ALU.logical_shift_right))
                    link(v.scalar_tensor_tensor(out=hits[:], in0=expo[:], scalar=1.0, in1=bc(lane[:], full), op0=ALU.min, op1=ALU.mult))
                    link(v.tensor_tensor(hits[:], hits[:], expo[:], ALU.add))
                    link(v.tensor_reduce(last[:], hits[:].rearrange("r p c -> r c p"), AX, ALU.max))
                    link(v.tensor_scalar(found[:], last[:], 1.0, None, ALU.min))
                    link(v.tensor_copy(last_i[:, 0], last[:]))
                    link(v.tensor_scalar(last_i[:, 1], last_i[:, 0], 255, None, ALU.bitwise_and))
                    link(v.tensor_scalar(last_i[:, 0], last_i[:, 0], 8, None, ALU.logical_shift_right))
                    link(v.tensor_scalar(number[:], last_i[:, 1], -63.0, 0.0, ALU.add, ALU.max))
                    link(v.tensor_copy(last_i[:, 1], number[:]))
                    link(v.tensor_scalar(last_i[:, 1], last_i[:, 1], 3, None, ALU.logical_shift_right))
                    link(v.scalar_tensor_tensor(out=number[:], in0=last_i[:, 0], scalar=float(CPL), in1=last_i[:, 1], op0=ALU.mult, op1=ALU.add))
                    v.tensor_copy(chunk[:], number[:]).then_inc(chunked, 1)
                    link(v.tensor_scalar(row_i[:], row_i[:], BS - 1, None, ALU.bitwise_and))
                    link(v.tensor_copy(row_f[:], row_i[:]))
                    link(v.tensor_scalar(diag[:], col[:], row_f[:, 0:1], None, ALU.is_equal))
                    link(v.tensor_scalar(off[:], diag[:], -1.0, 1.0, ALU.mult, ALU.add))
                    link(v.memset(mask[:], 1.0))
                    link(v.tensor_tensor(mask[:, 0:BS], diag[:], found[:], ALU.max))
                    link(v.tensor_tensor(off[:], off[:], found[:], ALU.mult))
                    link(v.memset(feats[:], 0.0))
                    link(v.memset(feats[:, 3, BS:BS + 1], 1.0))
                    dve.wait_ge(loaded, 16 * 7)
                    for x in range(3):
                        link(v.tensor_scalar(feats[:, x, 0:BS], pos[:, :, x], pos_r[:, x:x + 1], None, ALU.subtract))
                        link(v.tensor_tensor(feats[:, x, 0:BS], feats[:, x, 0:BS], off[:], ALU.mult))
                    dve.wait_ge(fetched, 16 * 2 * BS)
                    one = [P, BS, P]
                    link(v.tensor_tensor(keys[:], keys[:], bc(cell[:], one), ALU.is_equal))
                    link(v.tensor_tensor(keys[:], keys[:], bc(place[:], one), ALU.mult))
                    link(v.tensor_reduce(at[:, :, 0], keys[:], AX, ALU.max))
                    link(v.tensor_scalar(at[:], at[:], 1.0, None, ALU.max))
                    link(v.tensor_tensor(keys[:], bc(place[:], one), bc(at[:], one), ALU.is_equal))
                    link(v.tensor_tensor(vals[:], vals[:], keys[:], ALU.mult))
                    link(v.tensor_reduce(number[:], vals[:], AX, ALU.add))
                    link(v.tensor_tensor(number[:], number[:], off[:], ALU.mult))
                    link(v.tensor_tensor(feats[:, 3, 0:BS], number[:], diag[:], ALU.add))
                    link(v.tensor_scalar(k.edge_score[:], mask[:], -MASKED, MASKED, ALU.mult, ALU.add))
                    link(v.tensor_tensor(k.edge_score[:], k.edge_score[:], feats[:, 3], ALU.add))
                    for h in range(HEADS):
                        g = k.edge_gate[:, h]
                        link(v.tensor_scalar(g, feats[:, 0], gw[:, h, 0:1], gb[:, h:h + 1], ALU.mult, ALU.add))
                        for x in range(1, 4):
                            link(v.scalar_tensor_tensor(out=g, in0=feats[:, x], scalar=gw[:, h, x:x + 1], in1=g, op0=ALU.mult, op1=ALU.add))
                        link(v.tensor_tensor(g, g, mask[:], ALU.mult))


def stage_l1_attn(k):
    nc, w = k.nc, k.w
    HEADS, HD, BS, A1 = 4, 16, 32, D + 1
    NB = N // BS
    KEYS = BS + 1
    with Scope(nc, "l1a") as s:
        k.edge_score = s.sb("edge_score", [P, 1, KEYS])
        k.edge_gate = s.sb("edge_gate", [P, HEADS, 1, KEYS])
        score_view, gate_view = k.edge_score, k.edge_gate
        k.edge_score, k.edge_gate = k.edge_score[:, 0], k.edge_gate[:, :, 0]
        stage_edge_cells(k)
        wnat = s.sb("wnat", [D, 4, A1])
        wq = s.sb("wq", [A1, HEADS, 32])
        wk = s.sb("wk", [A1, HEADS, 32])
        wv = s.sb("wv", [A1, D])
        wo = s.sb("wo", [A1, D])
        blockmean = s.sb("blockmean", [P, P])
        xs = s.sb("xs", [P, GROUP, A1])
        xkv = s.sb("xkv", [A1, TOK + GROUP * NB])
        q = s.sb("q", [P, GROUP * NB, BS])
        kk = s.sb("kk", [P, GROUP * NB, KEYS])
        v = s.sb("v", [P, GROUP, D])
        sc = s.sb("sc", [P, HEADS, GROUP, KEYS])
        top = s.sb("top", [P, HEADS, GROUP, 1])
        den = s.sb("den", [P, HEADS, GROUP, 1])
        sct = s.sb("sct", [P, HEADS, GROUP, BS])
        scn = s.sb("scn", [P, HEADS, GROUP, BS])
        mixed = s.sb("mixed", [P, GROUP, A1])
        node = s.sb("node", [P, GROUP, HEADS, HD])
        mt = s.sb("mt", [A1, TOK])
        ps = s.ps("ps", [P, 8, 512])
        names = ("loaded step wturned wready normed xt_made xt_ready mean_ready projected q_ready k_ready v_ready "
                 "scored shifted exped combined noded valued mixed_ready mt_made mt_ready outed apart").split()
        S = {n: s.sem(n) for n in names}
        block = s.block()

        @block.sync
        def _(sp):
            qkv = w["L1_attn_qkv_w"].rearrange("(n o) i -> o n i", o=D)
            sp.dma_start(wnat[:, 0:3, 0:D], qkv).then_inc(S["loaded"], 16)
            sp.dma_start(wnat[:, 3, 0:D], w["L1_attn_proj_w"]).then_inc(S["loaded"], 16)
            for n in range(3):
                sp.dma_start(wnat[:, n, D:A1], w["L1_attn_qkv_b"].rearrange("(n o u) -> n o u", o=D, u=1)[n]).then_inc(S["loaded"], 16)
            sp.dma_start(wnat[:, 3, D:A1], w["L1_attn_proj_b"].rearrange("(o u) -> o u", u=1)).then_inc(S["loaded"], 16)

        @block.vector
        def _(dve):
            vec = nc.vector
            link = Link(dve, S["step"])
            link(vec.memset(wq[:], 0.0))
            link(vec.memset(wk[:], 0.0))
            link(vec.memset(xs[:, :, D:A1], 1.0))
            link(vec.memset(mixed[:, :, D:A1], 1.0))
            link(vec.memset(blockmean[:], 0.0))
            for n in range(NB):
                link(vec.memset(blockmean[n * BS:(n + 1) * BS, n * BS:(n + 1) * BS], 1.0 / BS))
            dve.wait_ge(S["wturned"], 1)
            wt = ps[0:A1, 0, 0:4 * D].rearrange("p (n h c) -> p n h c", n=4, h=HEADS)
            link(vec.tensor_scalar(wq[:, :, 0:HD], wt[:, 0], HD ** -0.5, None, ALU.mult))
            link(vec.tensor_copy(wk[:, :, 0:HD], wt[:, 1]))
            link(vec.tensor_copy(wv[:].rearrange("p (h c) -> p h c", h=HEADS), wt[:, 2]))
            link(vec.tensor_copy(wo[:].rearrange("p (h c) -> p h c", h=HEADS), wt[:, 3]))
            vec.sem_inc(S["wready"], 1)
            BASE = 5 + NB + 4
            PER = 10
            with dve.Fori(0, GROUPS) as t:
                link = Link(dve, S["step"], BASE + PER * t, PER)
                front_dve(k, dve, xs[:], t, S["normed"])
                dve.wait_ge(S["xt_ready"], t + 1)
                link(vec.tensor_reduce(xkv[:, TOK:], xkv[:, 0:TOK].rearrange("p (n c) -> p n c", c=BS), AX, ALU.add))
                link(vec.tensor_scalar(xkv[:, TOK:], xkv[:, TOK:], 1.0 / BS, None, ALU.mult))
                vec.sem_inc(S["mean_ready"], 1)
                dve.wait_ge(S["projected"], 4 * t + 3)
                vec.tensor_copy(kk[:, :, 0:BS], ps[:, 2, :].rearrange("p (n c) -> p n c", c=BS)).then_inc(S["k_ready"], 1)
                vec.tensor_copy(kk[:, :, BS], ps[:, 3, 0:GROUP * NB]).then_inc(S["k_ready"], 1)
                full = [P, HEADS, GROUP, KEYS]
                dve.wait_ge(S["scored"], t + 1)
                psc = ps[:, 4:8, 0:GROUP * KEYS].rearrange("p h (b c) -> p h b c", c=KEYS)
                for h in range(HEADS):
                    ins = vec.tensor_tensor(sc[:, h], psc[:, h], bc(score_view[:], [P, GROUP, KEYS]), ALU.add)
                link(ins)
                link(vec.tensor_reduce(top[:, :, :, 0], sc[:], AX, ALU.max))
                vec.tensor_tensor(sc[:], sc[:], bc(top[:], full), ALU.subtract).then_inc(S["shifted"], 1)
                dve.wait_ge(S["exped"], t + 1)
                link(vec.tensor_reduce(den[:, :, :, 0], sc[:], AX, ALU.add))
                link(vec.reciprocal(den[:], den[:]))
                link(vec.tensor_tensor(sc[:], sc[:], bc(den[:], full), ALU.mult))
                link(vec.tensor_tensor(sc[:], sc[:], bc(gate_view[:], full), ALU.add))
                link(vec.tensor_copy(scn[:], sc[:, :, :, 0:BS]))
                vec.transpose(sct[:].rearrange("p h b c -> p (h b c)"), scn[:].rearrange("p h b c -> p (h b c)")).then_inc(S["combined"], 1)
                dve.wait_ge(S["valued"], 2 * t + 1)
                weight = sc[:, :, :, BS:KEYS].rearrange("p h b c -> p b h c")
                vec.tensor_tensor(node[:], ps[:, 1, 0:256].rearrange("p (b h c) -> p b h c", b=GROUP, h=HEADS),
                                  bc(weight, [P, GROUP, HEADS, HD]), ALU.mult).then_inc(S["noded"], 1)
                dve.wait_ge(S["noded"], t + 1)
                dve.wait_ge(S["valued"], 2 * t + 2)
                vec.tensor_tensor(mixed[:, :, 0:D], ps[:, 2, 0:256].rearrange("p (b d) -> p b d", b=GROUP),
                                  node[:].rearrange("p b h c -> p b (h c)"), ALU.add).then_inc(S["mixed_ready"], 1)
                dve.wait_ge(S["outed"], t + 1)
                g = bass.ds(GROUP * t, GROUP)
                link(vec.tensor_tensor(k.h[:, g, :], k.h[:, g, :], ps[:, 3, 0:256].rearrange("p (b d) -> p b d", b=GROUP), ALU.add))
                link.close()

        @block.scalar
        def _(act):
            with act.Fori(0, GROUPS) as t:
                act.wait_ge(S["xt_made"], t + 1)
                nc.scalar.copy(xkv[:, 0:TOK], ps[0:A1, 0, :]).then_inc(S["xt_ready"], 1)
                act.wait_ge(S["projected"], 4 * t + 1)
                nc.scalar.copy(q[:].rearrange("p n c -> p (n c)"), ps[:, 1, :]).then_inc(S["q_ready"], 1)
                act.wait_ge(S["projected"], 4 * t + 4)
                nc.scalar.copy(v[:], ps[:, 0, 0:256].rearrange("p (b d) -> p b d", b=GROUP)).then_inc(S["v_ready"], 1)
                act.wait_ge(S["shifted"], t + 1)
                nc.scalar.activation(sc[:], sc[:], ACT.Exp).then_inc(S["exped"], 1)
                act.wait_ge(S["mt_made"], t + 1)
                nc.scalar.copy(mt[:], ps[0:A1, 0, :]).then_inc(S["mt_ready"], 1)

        @block.tensor
        def _(pe):
            mm = nc.tensor.matmul
            pe.wait_ge(S["loaded"], 16 * 6)
            for n in range(4):
                ins = nc.tensor.transpose(ps[0:A1, 0, n * D:(n + 1) * D], wnat[:, n, :], k.ident[0:D, 0:D])
            ins.then_inc(S["wturned"], 1)
            pe.wait_ge(S["wready"], 1)
            with pe.Fori(0, GROUPS) as t:
                pe.wait_ge(S["normed"], t + 1)
                for b in range(GROUP):
                    ins = nc.tensor.transpose(ps[0:A1, 0, b * N:(b + 1) * N], xs[:, b, :], k.ident[:])
                ins.then_inc(S["xt_made"], 1)
                pe.wait_ge(S["xt_ready"], t + 1)
                mm(ps[:, 1, :], wq[:].rearrange("p h c -> p (h c)"), xkv[:, 0:TOK], start=True, stop=True).then_inc(S["projected"], 1)
                pe.wait_ge(S["mean_ready"], t + 1)
                mm(ps[:, 2, :], wk[:].rearrange("p h c -> p (h c)"), xkv[:, 0:TOK], start=True, stop=True).then_inc(S["projected"], 1)
                mm(ps[:, 3, 0:GROUP * NB], wk[:].rearrange("p h c -> p (h c)"), xkv[:, TOK:], start=True, stop=True).then_inc(S["projected"], 1)
                for b in range(GROUP):
                    ins = mm(ps[:, 0, b * D:(b + 1) * D], xkv[:, b * N:(b + 1) * N], wv[:], start=True, stop=True)
                ins.then_inc(S["projected"], 1)
                pe.wait_ge(S["q_ready"], t + 1)
                pe.wait_ge(S["k_ready"], 2 * t + 2)
                nc.tensor.sem_inc(S["apart"], 1)
                for b in range(GROUP):
                    for n in range(NB):
                        for h in range(HEADS):
                            ins = mm(ps[n * BS:(n + 1) * BS, 4 + h, b * KEYS:(b + 1) * KEYS],
                                     q[32 * h:32 * h + 32, b * NB + n, :], kk[32 * h:32 * h + 32, b * NB + n, :],
                                     start=True, stop=True, tile_position=(32 * h, n * BS))
                ins.then_inc(S["scored"], 1)
                pe.wait_ge(S["v_ready"], t + 1)
                mm(ps[:, 1, 0:256], blockmean[:], v[:].rearrange("p b d -> p (b d)"), start=True, stop=True).then_inc(S["valued"], 1)
                pe.wait_ge(S["combined"], t + 1)
                nc.tensor.sem_inc(S["apart"], 1)
                for b in range(GROUP):
                    for h in range(HEADS):
                        for n in range(NB):
                            r = slice(n * BS, (n + 1) * BS)
                            ins = mm(ps[r, 2, b * D + h * HD:b * D + (h + 1) * HD], sct[r, h, b, :], v[r, b, h * HD:(h + 1) * HD],
                                     start=True, stop=True, tile_position=(n * BS, n * BS))
                ins.then_inc(S["valued"], 1)
                pe.wait_ge(S["mixed_ready"], t + 1)
                for b in range(GROUP):
                    ins = nc.tensor.transpose(ps[0:A1, 0, b * N:(b + 1) * N], mixed[:, b, :], k.ident[:])
                ins.then_inc(S["mt_made"], 1)
                pe.wait_ge(S["mt_ready"], t + 1)
                for b in range(GROUP):
                    ins = mm(ps[:, 3, b * D:(b + 1) * D], mt[:, b * N:(b + 1) * N], wo[:], start=True, stop=True)
                ins.then_inc(S["outed"], 1)


def stage_l1_ffn(k):
    nc, w = k.nc, k.w
    HEADS, SETS, HD, HP = 4, 4, 16, 32
    UNITS = GROUP * SETS
    OC = HEADS * (HD + 1)
    BC = OC + HEADS * SETS
    with Scope(nc, "l1f") as s:
        wq = s.sb("wq", [P, SETS, HEADS, HP])
        wk = s.sb("wk", [P, HEADS, HP])
        wsx = s.sb("wsx", [P, HEADS, HP])
        wv = s.sb("wv", [P, D])
        fc1 = s.sb("fc1", [P, D])
        fc2 = s.sb("fc2", [P, D])
        pick = s.sb("pick", [P, SETS, BC])
        fgate_w = s.sb("fgate_w", [P, HEADS])
        gate_b = s.sb("gate_b", [P, 1, HEADS * SETS])
        norms = s.sb("norms", [P, 4, 1, D])
        causal = s.sb("causal", [P, 4, N], BF16)
        identb = s.sb("identb", [P, P], BF16)
        resid = s.sb("resid", [P, HEADS, HD])
        nhalf = s.sb("nhalf", [P, GROUP * HEADS, 1])
        fold_l1_ffn(k, wq, wk, wsx, wv, fc1, fc2, pick, fgate_w, gate_b, norms, causal, identb, resid, nhalf)
        xs = s.sb("xs", [P, GROUP, P])
        xt = s.sb("xt", [P, TOK])
        q = s.sb("q", [P, 2, SETS, TOK])
        keys = s.sb("keys", [P, 2, GROUP, HEADS, N])
        live = s.sb("live", [P, 2, GROUP, 1, N])
        v = s.sb("v", [P, 2, GROUP, HEADS, HP])
        top = s.sb("top", [P, 4, 4])
        probs = s.sb("probs", [P, 4, 4, N])
        probs_t = s.sb("probs_t", [P, 2, 4, N])
        ot = s.sb("ot", [P, SETS, N])
        rden = s.sb("rden", [P, GROUP, HEADS, 1, SETS])
        out = s.sb("out", [P, GROUP, HEADS, SETS, HD])
        gate = s.sb("gate", [P, GROUP, HEADS, SETS, SETS])
        gs = s.sb("gs", [P, GROUP * HEADS, SETS, 1])
        gtop = s.sb("gtop", [P, GROUP * HEADS, 1])
        fx = s.sb("fx", [P, GROUP, P])
        fh = s.sb("fh", [P, GROUP * HEADS, HD])
        sq = s.sb("sq", [P, GROUP * HEADS, HD])
        mom = s.sb("mom", [P, GROUP * HEADS, 1])
        var = s.sb("var", [P, GROUP * HEADS, 1])
        rstd = s.sb("rstd", [P, GROUP * HEADS, 1])
        nz = s.sb("nz", [P, GROUP, D])
        fx_t = s.sb("fx_t", [P, TOK])
        nz_t = s.sb("nz_t", [D, TOK])
        h1_t = s.sb("h1_t", [P, TOK])
        fo_t = s.sb("fo_t", [P, TOK])
        fg = s.sb("fg", [P, GROUP, HEADS, 1])
        ftop = s.sb("ftop", [P, GROUP, 1])
        ps = s.ps("ps", [P, 8, 512])
        SC, TU, OT, BACK, X, Y = 0, 2, 4, 5, 6, 7
        names = ("step ready normed xt_made xt_ready projected q_ready k_ready live_ready v_ready scored topped exped turned "
                 "turned_ready valued ot_ready back out_ready gs_shifted gs_exped var_ready rooted fx_ready fx_made fx_t_ready "
                 "h1_made h1_ready h2_made fo_ready fo_made fo_t_ready fg_made fg_shifted fg_exped added apart").split()
        S = {n: s.sem(n) for n in names}
        block = s.block()

        def heads(flat):
            return flat.rearrange("p (h n) -> p h n", h=4)

        def seqs(flat):
            return flat.rearrange("p (b n) -> p b n", b=GROUP)

        def started(t, u, back):
            return not (isinstance(t, int) and t == 0 and u < back)

        @block.gpsimd
        def _(pool):
            nc.gpsimd.memset(v[:], 0.0).then_inc(S["v_ready"], 1)
            pool.wait_ge(S["v_ready"], 1)
            nc.gpsimd.memset(v[:, :, :, :, HD:HD + 1], 1.0).then_inc(S["v_ready"], 1)
            with pool.Fori(0, GROUPS) as t:
                for j in range(2):
                    pool.wait_ge(S["var_ready"], 2 * t + j + 1)
                    nc.gpsimd.tensor_tensor(rstd[:], var[:], nhalf[:], ALU.pow).then_inc(S["rooted"], 1)

        @block.vector
        def _(dve):
            vec = nc.vector
            start = Link(dve, S["step"])
            vec.memset(xs[:], 0.0)
            vec.memset(fx[:], 0.0)
            vec.memset(h1_t[:], 0.0)
            start(vec.memset(keys[:], 0.0))
            vec.memset(xs[:, :, D:D + 1], 1.0)
            vec.memset(fx[:, :, D:D + 1], 1.0)
            start(vec.memset(h1_t[D:D + 1, :], 1.0))
            vec.sem_inc(S["ready"], 1)
            PER = 40
            f4 = fh[:].rearrange("p (b h) c -> p b (h c)", b=GROUP)
            wide = [P, GROUP, D]
            full = [P, GROUP * HEADS, HD]

            def keep_keys(t, par):
                dve.wait_ge(S["projected"], 7 * t + 5)
                for h in range(2):
                    r = slice(HP * h, HP * h + HD)
                    ins = vec.tensor_copy(keys[r, par, :, h, :], seqs(ps[r, X, :]))
                ins.then_inc(S["k_ready"], 1)

            def keep_live(t, par):
                dve.wait_ge(S["projected"], 7 * t + 6)
                vec.tensor_scalar(live[:, par].rearrange("p b o n -> p (b o n)"), ps[:, X, :], 0.0, None, ALU.not_equal).then_inc(S["live_ready"], 1)

            def prelude():
                front_dve(k, dve, xs[:], 0, S["normed"])
                keep_keys(0, 0)
                keep_live(0, 0)

            def maximum(t, u):
                dve.wait_ge(S["scored"], UNITS * t + u + 1)
                vec.tensor_reduce(top[:, u % 4], heads(ps[:, SC + u % 2, :]), AX, ALU.max, negate=True).then_inc(S["topped"], 1)

            def keep_turned(t, u):
                dve.wait_ge(S["turned"], UNITS * t + u + 1)
                if started(t, u, 2):
                    dve.wait_ge(S["valued"], UNITS * t + u - 1)
                vec.tensor_copy(probs_t[:, u % 2], heads(ps[:, TU + u % 2, :])).then_inc(S["turned_ready"], 1)

            def keep_output(t, par, b):
                dve.wait_ge(S["valued"], UNITS * t + SETS * (b + 1))
                if started(t, b, 1):
                    dve.wait_ge(S["back"], GROUP * t + b)
                dve.wait_ge(S["live_ready"], t + 1)
                vec.tensor_tensor(ot[:], ps[:, OT, :].rearrange("p (e n) -> p e n", e=SETS), bc(live[:, par, b], [P, SETS, N]),
                                  ALU.mult).then_inc(S["ot_ready"], 1)

            def normalize(t, b, link):
                dve.wait_ge(S["back"], GROUP * t + b + 1)
                o = ps[:, BACK, 0:SETS * BC].rearrange("p (e c) -> p e c", e=SETS)
                chans = o[:, :, 0:OC].rearrange("p e (h c) -> p h e c", h=HEADS)
                link(vec.reciprocal(rden[:, b, :, 0, :], chans[:, :, :, HD]))
                vec.tensor_tensor(out[:, b], chans[:, :, :, 0:HD],
                                  bc(rden[:, b].rearrange("p h o e -> p h e o"), [P, HEADS, SETS, HD]), ALU.mult)
                link(vec.tensor_tensor(gate[:, b], o[:, :, OC:BC].rearrange("p e (h g) -> p h g e", h=HEADS),
                                       bc(rden[:, b], [P, HEADS, SETS, SETS]), ALU.mult))
                vec.sem_inc(S["out_ready"], 1)

            def gate_shift(t, link):
                gflat = gs[:].rearrange("p m e o -> p (m e o)")
                link(vec.tensor_reduce(gflat, gate[:].rearrange("p b h g e -> p (b h g) e"), AX, ALU.add))
                g3 = gflat.rearrange("p (b g) -> p b g", b=GROUP)
                link(vec.tensor_tensor(g3, g3, bc(gate_b[:], [P, GROUP, HEADS * SETS]), ALU.add))
                link(vec.tensor_reduce(gtop[:, :, 0], gs[:, :, :, 0], AX, ALU.max))
                vec.tensor_tensor(gs[:, :, :, 0], gs[:, :, :, 0], bc(gtop[:], [P, 16, SETS]), ALU.subtract).then_inc(S["gs_shifted"], 1)

            def moments(j, t, link):
                link(vec.tensor_reduce(mom[:, :, 0], fh[:], AX, ALU.add))
                link(vec.tensor_scalar(mom[:], mom[:], 1.0 / HD, None, ALU.mult))
                link(vec.tensor_tensor(fh[:], fh[:], bc(mom[:], full), ALU.subtract))
                link(vec.tensor_tensor(sq[:], fh[:], fh[:], ALU.mult))
                link(vec.tensor_reduce(var[:, :, 0], sq[:], AX, ALU.add))
                vec.tensor_scalar(var[:], var[:], 1.0 / HD, 1e-8, ALU.mult, ALU.add).then_inc(S["var_ready"], 1)

            def scale(j, t, dst, link):
                dve.wait_ge(S["rooted"], 2 * t + j + 1)
                link(vec.tensor_tensor(fh[:], fh[:], bc(rstd[:], full), ALU.mult))
                link(vec.tensor_tensor(f4, f4, bc(norms[:, 2 * j], wide), ALU.mult))
                return vec.tensor_tensor(dst, f4, bc(norms[:, 2 * j + 1], wide), ALU.add)

            def mix(t, link):
                dve.wait_ge(S["gs_exped"], t + 1)
                link(vec.tensor_reduce(gtop[:, :, 0], gs[:, :, :, 0], AX, ALU.add))
                link(vec.reciprocal(gtop[:], gtop[:]))
                link(vec.tensor_tensor(gs[:, :, :, 0], gs[:, :, :, 0], bc(gtop[:], [P, 16, SETS]), ALU.mult))
                om = out[:].rearrange("p b h e c -> p (b h) e c")
                link(vec.tensor_tensor(om, om, bc(gs[:], [P, 16, SETS, HD]), ALU.mult))
                link(vec.tensor_reduce(fh[:], om.rearrange("p m e c -> p m c e"), AX, ALU.add))
                link(vec.tensor_tensor(f4, f4, bc(resid[:].rearrange("p (o h) c -> p o (h c)", o=1), wide), ALU.add))

            def relu(t, link):
                link(vec.tensor_scalar(nz[:], fx[:, :, 0:D], 0.0, None, ALU.not_equal))
                dve.wait_ge(S["fx_t_ready"], t + 1)
                link(vec.tensor_scalar(nz_t[:], fx_t[0:D, :], 0.0, None, ALU.not_equal))
                dve.wait_ge(S["h1_made"], t + 1)
                vec.scalar_tensor_tensor(out=h1_t[0:D, :], in0=ps[0:D, Y, :], scalar=0.0, in1=nz_t[:],
                                         op0=ALU.max, op1=ALU.mult).then_inc(S["h1_ready"], 1)

            def add_mlp(t, link):
                dve.wait_ge(S["h2_made"], t + 1)
                link(vec.tensor_tensor(f4, seqs(ps[:, Y, 0:GROUP * D]), nz[:], ALU.mult))
                link(vec.tensor_tensor(f4, f4, fx[:, :, 0:D], ALU.add))

            def head_shift(t, link):
                dve.wait_ge(S["fg_made"], t + 1)
                scores = seqs(ps[:, Y, 0:GROUP * HEADS])
                link(vec.tensor_reduce(ftop[:, :, 0], scores, AX, ALU.max))
                vec.tensor_tensor(fg[:, :, :, 0], scores, bc(ftop[:], [P, GROUP, HEADS]), ALU.subtract).then_inc(S["fg_shifted"], 1)

            def add(t, link):
                dve.wait_ge(S["fg_exped"], t + 1)
                link(vec.tensor_reduce(ftop[:, :, 0], fg[:, :, :, 0], AX, ALU.add))
                link(vec.reciprocal(ftop[:], ftop[:]))
                link(vec.tensor_tensor(fg[:, :, :, 0], fg[:, :, :, 0], bc(ftop[:], [P, GROUP, HEADS]), ALU.mult))
                link(vec.tensor_tensor(sq[:].rearrange("p (b h) c -> p b h c", b=GROUP), fx[:, :, 0:D].rearrange("p b (h c) -> p b h c", h=HEADS), bc(fg[:], [P, GROUP, HEADS, HD]), ALU.mult))
                g = bass.ds(GROUP * t, GROUP)
                vec.tensor_tensor(k.h[:, g, :], k.h[:, g, :], sq[:].rearrange("p (b h) c -> p b (h c)", b=GROUP), ALU.add).then_inc(S["added"], 1)

            def body(t, par, cur, prev, nxt):
                own = Link(dve, S["step"], 2 + PER * t)
                for u in range(UNITS):
                    if cur:
                        maximum(t, u)
                    if u >= 2 and cur:
                        keep_turned(t, u - 2)
                    if u < 2 and prev:
                        keep_turned(t - 1, UNITS + u - 2)
                    if u == 0 and nxt:
                        front_dve(k, dve, xs[:], t + 1, S["normed"])
                    if u == 6 and nxt:
                        keep_keys(t + 1, 1 - par)
                    if u == 7 and nxt:
                        keep_live(t + 1, 1 - par)
                    if u in (6, 10, 14) and cur:
                        keep_output(t, par, u // 4 - 1)
                    if u == 2 and prev:
                        keep_output(t - 1, 1 - par, GROUP - 1)
                    if u in (8, 12) and cur:
                        normalize(t, u // 4 - 2, own)
                    if u == 0 and prev:
                        normalize(t - 1, GROUP - 2, own)
                    if u == 4 and prev:
                        normalize(t - 1, GROUP - 1, own)
                        gate_shift(t - 1, own)
                    if u == 5 and prev:
                        mix(t - 1, own)
                        moments(0, t - 1, own)
                    if u == 7 and prev:
                        scale(0, t - 1, fx[:, :, 0:D], own).then_inc(S["fx_ready"], 1)
                        dve.wait_ge(S["fx_ready"], t)
                    if u == 9 and prev:
                        relu(t - 1, own)
                    if u == 10 and prev:
                        add_mlp(t - 1, own)
                        moments(1, t - 1, own)
                    if u == 12 and prev:
                        scale(1, t - 1, fx[:, :, 0:D], own).then_inc(S["fo_ready"], 1)
                        dve.wait_ge(S["fo_ready"], t)
                    if u == 14 and prev:
                        head_shift(t - 1, own)
                    if u == 15 and prev:
                        add(t - 1, own)
                if isinstance(t, int) and t == 0:
                    for _ in range(PER - own.n):
                        vec.sem_inc(S["step"], 1)
                elif cur:
                    assert own.n == PER, own.n

            in_turn(dve, prelude, body)

        @block.scalar
        def _(act):
            act.wait_ge(S["v_ready"], 2)
            act.wait_ge(S["ready"], 1)

            def keep_x(t):
                act.wait_ge(S["xt_made"], t + 1)
                nc.scalar.copy(xt[:], ps[:, X, :]).then_inc(S["xt_ready"], 1)

            def keep_q(t, par, e):
                act.wait_ge(S["projected"], 7 * t + e + 1)
                nc.scalar.copy(q[:, par, e, :], ps[:, X, :]).then_inc(S["q_ready"], 1)

            def keep_keys(t, par):
                act.wait_ge(S["projected"], 7 * t + 5)
                for h in range(2, 4):
                    r = slice(HP * h, HP * h + HD)
                    ins = nc.scalar.copy(keys[r, par, :, h, :], seqs(ps[r, X, :]))
                ins.then_inc(S["k_ready"], 1)

            def keep_v(t, par):
                act.wait_ge(S["projected"], 7 * t + 7)
                nc.scalar.copy(v[:, par, :, :, 0:HD], ps[:, X, 0:GROUP * D].rearrange("p (b h c) -> p b h c", b=GROUP, c=HD)).then_inc(S["v_ready"], 1)

            def prelude():
                keep_x(0)
                for e in range(SETS):
                    keep_q(0, 0, e)
                keep_keys(0, 0)
                keep_v(0, 0)

            def exponential(t, u):
                act.wait_ge(S["topped"], UNITS * t + u + 1)
                if started(t, u, 4):
                    act.wait_ge(S["turned"], UNITS * t + u - 3)
                for h in range(4):
                    ins = nc.scalar.activation(probs[:, u % 4, h], ps[:, SC + u % 2, h * N:(h + 1) * N], ACT.Exp, bias=top[:, u % 4, h:h + 1])
                ins.then_inc(S["exped"], 1)

            def body(t, par, cur, prev, nxt):
                for u in range(UNITS):
                    if u == 5 and prev:
                        act.wait_ge(S["gs_shifted"], t)
                        nc.scalar.activation(gs[:], gs[:], ACT.Exp).then_inc(S["gs_exped"], 1)
                    if u == 15 and prev:
                        act.wait_ge(S["fg_shifted"], t)
                        nc.scalar.activation(fg[:], fg[:], ACT.Exp).then_inc(S["fg_exped"], 1)
                    if cur:
                        exponential(t, u)
                    if u == 1 and nxt:
                        keep_x(t + 1)
                    if 2 <= u <= 5 and nxt:
                        keep_q(t + 1, 1 - par, u - 2)
                    if u == 6 and nxt:
                        keep_keys(t + 1, 1 - par)
                    if u == 8 and nxt:
                        keep_v(t + 1, 1 - par)
                    if u == 8 and prev:
                        act.wait_ge(S["fx_made"], t)
                        nc.scalar.copy(fx_t[:], ps[:, Y, :]).then_inc(S["fx_t_ready"], 1)
                    if u == 13 and prev:
                        act.wait_ge(S["fo_made"], t)
                        nc.scalar.copy(fo_t[:], ps[:, Y, :]).then_inc(S["fo_t_ready"], 1)

            in_turn(act, prelude, body)

        @block.tensor
        def _(pe):
            mm = nc.tensor.matmul

            def turn_x(t):
                pe.wait_ge(S["normed"], t + 1)
                if started(t, 0, 1):
                    pe.wait_ge(S["v_ready"], t + 2)
                for b in range(GROUP):
                    ins = nc.tensor.transpose(ps[:, X, b * N:(b + 1) * N], xs[:, b, :], k.ident[:])
                ins.then_inc(S["xt_made"], 1)

            def project(t, n):
                if n == 0:
                    pe.wait_ge(S["xt_ready"], t + 1)
                elif n <= 4:
                    pe.wait_ge(S["q_ready"], 4 * t + n)
                elif n == 5:
                    pe.wait_ge(S["k_ready"], 2 * t + 2)
                else:
                    pe.wait_ge(S["live_ready"], t + 1)
                if n < 6:
                    wt = wq[:, n] if n < 4 else (wk, wsx)[n - 4][:]
                    ins = mm(ps[:, X, :], wt.rearrange("p h c -> p (h c)"), xt[:], start=True, stop=True)
                else:
                    for b in range(GROUP):
                        ins = mm(ps[:, X, b * D:(b + 1) * D], xt[:, b * N:(b + 1) * N], wv[:], start=True, stop=True)
                ins.then_inc(S["projected"], 1)

            def prelude():
                pe.wait_ge(S["ready"], 1)
                turn_x(0)
                for n in range(7):
                    project(0, n)

            def scores(t, par, u):
                b, e = u // SETS, u % SETS
                if u == 0:
                    pe.wait_ge(S["q_ready"], 4 * t + 4)
                    pe.wait_ge(S["k_ready"], 2 * t + 2)
                if started(t, u, 2):
                    pe.wait_ge(S["exped"], UNITS * t + u - 1)
                mm(ps[:, SC + u % 2, :], identb[:], causal[:].rearrange("p h n -> p (h n)"), start=True, stop=False)
                mm(ps[:, SC + u % 2, :], q[:, par, e, b * N:(b + 1) * N], keys[:, par, b].rearrange("p h n -> p (h n)"),
                   start=False, stop=True).then_inc(S["scored"], 1)

            def turn(t, u):
                pe.wait_ge(S["exped"], UNITS * t + u + 1)
                if started(t, u, 2):
                    pe.wait_ge(S["turned_ready"], UNITS * t + u - 1)
                for h in range(4):
                    ins = nc.tensor.transpose(ps[:, TU + u % 2, h * N:(h + 1) * N], probs[:, u % 4, h], k.ident[:])
                ins.then_inc(S["turned"], 1)

            def values(t, par, u):
                b, e = u // SETS, u % SETS
                pe.wait_ge(S["turned_ready"], UNITS * t + u + 1)
                if u == 0:
                    pe.wait_ge(S["v_ready"], t + 3)
                if e == 0 and started(t, b, 1):
                    pe.wait_ge(S["ot_ready"], GROUP * t + b)
                nc.tensor.sem_inc(S["apart"], 1)
                for h in range(4):
                    ins = mm(ps[HP * h:HP * h + HP, OT, e * N:(e + 1) * N], v[:, par, b, h, :], probs_t[:, u % 2, h],
                             start=True, stop=True, tile_position=(0, HP * h))
                ins.then_inc(S["valued"], 1)

            def turn_back(t, b):
                pe.wait_ge(S["ot_ready"], GROUP * t + b + 1)
                if started(t, b, 1):
                    pe.wait_ge(S["out_ready"], GROUP * t + b)
                for e in range(SETS):
                    ins = mm(ps[:, BACK, e * BC:(e + 1) * BC], ot[:, e], pick[:, e], start=True, stop=True)
                ins.then_inc(S["back"], 1)

            def turn_rows(t, made, ready):
                pe.wait_ge(S[ready], t + 1)
                for b in range(GROUP):
                    ins = nc.tensor.transpose(ps[:, Y, b * N:(b + 1) * N], fx[:, b, :], k.ident[:])
                ins.then_inc(S[made], 1)

            def body(t, par, cur, prev, nxt):
                for u in range(UNITS):
                    if cur:
                        scores(t, par, u)
                    if u >= 2 and cur:
                        turn(t, u - 2)
                    if u < 2 and prev:
                        turn(t - 1, UNITS + u - 2)
                    if u >= 3 and cur:
                        values(t, par, u - 3)
                    if u < 3 and prev:
                        values(t - 1, 1 - par, UNITS + u - 3)
                    if u == 1 and nxt:
                        turn_x(t + 1)
                    if 2 <= u <= 8 and nxt:
                        project(t + 1, u - 2)
                    if u in (7, 11, 15) and cur:
                        turn_back(t, u // 4 - 1)
                    if u == 3 and prev:
                        turn_back(t - 1, GROUP - 1)
                    if u == 8 and prev:
                        turn_rows(t - 1, "fx_made", "fx_ready")
                    if u == 9 and prev:
                        pe.wait_ge(S["fx_t_ready"], t)
                        mm(ps[0:D, Y, :], fc1[:], fx_t[:], start=True, stop=True).then_inc(S["h1_made"], 1)
                    if u == 10 and prev:
                        pe.wait_ge(S["h1_ready"], t)
                        for b in range(GROUP):
                            ins = mm(ps[:, Y, b * D:(b + 1) * D], h1_t[:, b * N:(b + 1) * N], fc2[:], start=True, stop=True)
                        ins.then_inc(S["h2_made"], 1)
                    if u == 13 and prev:
                        turn_rows(t - 1, "fo_made", "fo_ready")
                    if u == 14 and prev:
                        pe.wait_ge(S["fo_t_ready"], t)
                        for b in range(GROUP):
                            ins = mm(ps[:, Y, b * HEADS:(b + 1) * HEADS], fo_t[:, b * N:(b + 1) * N], fgate_w[:], start=True, stop=True)
                        ins.then_inc(S["fg_made"], 1)

            in_turn(pe, prelude, body)


def fold_l1_ffn(k, wq, wk, wsx, wv, fc1, fc2, pick, fgate_w, gate_b, norms, causal, identb, resid, nhalf):
    nc, w = k.nc, k.w
    HEADS, SETS, HD, HP, A1 = 4, 4, 16, 32, D + 1
    OC = HEADS * (HD + 1)
    with Scope(nc, "l1fold") as s:
        hl = s.sb("hl", [D, A1])
        nat = s.sb("nat", [D, 8, D])
        turned = s.sb("turned", [D, 8, D])
        fgnat = s.sb("fgnat", [HEADS, D])
        gnat = s.sb("gnat", [HEADS * SETS, SETS, P])
        xs = s.sb("xs", [P, HEADS, A1])
        xt = s.sb("xt", [A1, TOK])
        sx = s.sb("sx", [A1, D])
        maskf = s.sb("maskf", [P, 4, N])
        ps = s.ps("ps", [P, 8, 512])
        zeroed, loaded, step, made, ready, masked = (s.sem(n) for n in "zeroed loaded step made ready masked".split())
        block = s.block()
        LOADS = 2 + HEADS * (SETS + 7 + 4) + 2

        @block.sync
        def _(sp):
            sent = [0]

            def load(dst, src):
                sp.dma_start(dst, src).then_inc(loaded, 16)
                sent[0] += 1

            sp.wait_ge(zeroed, 1)
            load(hl[:, 0:D], w["L1_ffn_hl_w"].rearrange("n d i -> (n d) i"))
            load(hl[:, D:A1], w["L1_ffn_hl_b"].rearrange("n (d u) -> (n d) u", u=1))
            for n in range(HEADS):
                r = slice(n * HD, (n + 1) * HD)
                for e in range(SETS):
                    load(nat[r, e, r], w["L1_ffn_wq"][n, e])
                load(nat[r, 4, r], w["L1_ffn_wk"][n])
                load(nat[r, 5, r], w["L1_ffn_wv"][n])
                load(nat[r, 6, r], w["L1_ffn_fc1_w"])
                load(nat[r, 7, r], w["L1_ffn_fc2_w"])
                load(gnat[n * SETS:(n + 1) * SETS, :, n * HP:n * HP + HD], w["L1_ffn_gate_w"][n].rearrange("g (e c) -> g e c", e=SETS))
                load(fc1[D:A1, r], w["L1_ffn_fc1_b"].rearrange("(o d) -> o d", o=1))
                load(fc2[D:A1, r], w["L1_ffn_fc2_b"].rearrange("(o d) -> o d", o=1))
                for m, name in enumerate(("ln_g", "ln_b", "fnorm_g", "fnorm_b")):
                    load(norms[:, m, 0, r], w[f"L1_ffn_{name}"].partition_broadcast(P))
            load(fgnat[:], w["L1_ffn_fgate_w"])
            load(gate_b[:, 0, :], w["L1_ffn_gate_b"].rearrange("n e -> (n e)").partition_broadcast(P))
            assert sent[0] == LOADS, (sent, LOADS)

        @block.gpsimd
        def _(pool):
            link = Link(pool, masked)
            link(nc.gpsimd.memset(maskf[:], 0.0))
            link(nc.gpsimd.affine_select(out=maskf[:], in_=maskf[:], compare_op=ALU.is_ge, fill=MASKED, base=0,
                                         pattern=[[0, 4], [-1, N]], channel_multiplier=1))

        @block.vector
        def _(dve):
            vec = nc.vector
            link = Link(dve, step)
            for buf in (nat, gnat, pick, fc1, fc2, wq, wk, wsx, wv, fgate_w):
                ins = vec.memset(buf[:], 0.0)
            link(ins)
            vec.sem_inc(zeroed, 1)
            for e in range(SETS):
                vec.tensor_copy(pick[:, e, 0:OC].rearrange("p (h c) -> p h c", h=HEADS), k.ident[:].rearrange("p (h c) -> p h c", h=HEADS)[:, :, 0:HD + 1])
            link(vec.memset(nhalf[:], -0.5))
            link(vec.tensor_copy(identb[:], k.ident[:]))
            link(vec.memset(xs[:, :, D:A1], 1.0))
            link(vec.tensor_tensor(xs[:, :, 0:D], k.xc[:, 0:HEADS, :], bc(k.rstd[:, 0:HEADS, :], [P, HEADS, D]), ALU.mult))
            vec.sem_inc(ready, 1)
            dve.wait_ge(masked, 2)
            link(vec.tensor_copy(causal[:], maskf[:]))
            dve.wait_ge(made, 1)
            link(vec.tensor_copy(turned[:], ps[0:D, 0, :].rearrange("p (n c) -> p n c", n=8)))
            link(vec.tensor_copy(fc1[0:D, :], ps[0:D, 0, 6 * D:7 * D]))
            link(vec.tensor_copy(fc2[0:D, :], ps[0:D, 0, 7 * D:8 * D]))
            link(vec.tensor_copy(sx[:], ps[0:A1, 1, 0:D]))
            link(vec.tensor_copy(wsx[0:A1, :, 0:HD], ps[0:A1, 1, 0:D].rearrange("p (h c) -> p h c", h=HEADS)))
            link(vec.memset(wsx[D:A1, :, HD:HD + 1], 1.0))
            link(vec.tensor_copy(fgate_w[0:D, :], ps[0:D, 3, 0:HEADS]))
            link(vec.tensor_copy(pick[:, :, OC:], ps[:, 2, 0:4 * HEADS * SETS].rearrange("p (e m) -> p e m", e=SETS)))
            link(vec.tensor_copy(xt[:], ps[0:A1, 4, :]))
            vec.sem_inc(ready, 1)
            dve.wait_ge(made, 2)
            f = ps[0:A1, 5, 0:6 * D].rearrange("p (n h c) -> p n h c", n=6, h=HEADS)
            link(vec.tensor_scalar(wq[0:A1, :, :, 0:HD], f[:, 0:4], HD ** 0.5, None, ALU.mult))
            link(vec.tensor_copy(wk[0:A1, :, 0:HD], f[:, 4]))
            link(vec.tensor_copy(wv[0:A1, :], ps[0:A1, 5, 5 * D:6 * D]))
            for n in range(HEADS):
                link(vec.tensor_copy(resid[:, n, :], ps[:, 6, n * D + n * HD:n * D + (n + 1) * HD]))

        @block.tensor
        def _(pe):
            mm = nc.tensor.matmul
            pe.wait_ge(loaded, 16 * LOADS)
            pe.wait_ge(ready, 1)
            for n in range(8):
                nc.tensor.transpose(ps[0:D, 0, n * D:(n + 1) * D], nat[:, n, :], k.ident[0:D, 0:D])
            nc.tensor.transpose(ps[0:A1, 1, 0:D], hl[:], k.ident[0:D, 0:D])
            nc.tensor.transpose(ps[0:D, 3, 0:HEADS], fgnat[:], k.ident[0:HEADS, 0:HEADS])
            for e in range(SETS):
                nc.tensor.transpose(ps[:, 2, 16 * e:16 * e + 16], gnat[:, e, :], k.ident[0:16, 0:16])
            for b in range(HEADS):
                ins = nc.tensor.transpose(ps[0:A1, 4, b * N:(b + 1) * N], xs[:, b, :], k.ident[:])
            ins.then_inc(made, 1)
            pe.wait_ge(ready, 2)
            mm(ps[0:A1, 5, 0:6 * D], hl[:], turned[:, 0:6].rearrange("p n c -> p (n c)"), start=True, stop=True)
            for b in range(HEADS):
                ins = mm(ps[:, 6, b * D:(b + 1) * D], xt[:, b * N:(b + 1) * N], sx[:], start=True, stop=True)
            ins.then_inc(made, 1)


def stage_l2_attn(k):
    nc, w = k.nc, k.w
    HEADS, HD = 8, 64
    PAIRS = HEADS // 2
    UNITS = GROUP * 2
    with Scope(nc, "l2a") as s:
        pair_map = s.sb("pair_map", [P, HEADS, HD])
        value_map = s.sb("value_map", [P, HEADS, D])
        with Scope(nc, "l2fold") as s1:
            nat = s1.sb("nat", [D, 4, HEADS, HD])
            turned = s1.sb("turned", [D, 4, HEADS, HD])
            ps = s1.ps("ps", [P, 8, 512])
            loaded, step, made, ready = (s1.sem(n) for n in "loaded step made ready".split())
            block = s1.block()

            @block.sync
            def _(sp):
                for n, name in enumerate(("q", "k", "v", "out")):
                    sp.dma_start(nat[:, n], w[f"L2_attn_weight_{name}"]).then_inc(loaded, 16)

            @block.tensor
            def _(pe):
                pe.wait_ge(loaded, 64)
                for n in range(4):
                    for h in range(HEADS):
                        ins = nc.tensor.transpose(ps[0:D, n, h * HD:(h + 1) * HD], nat[:, n, h], k.ident[0:D, 0:D])
                ins.then_inc(made, 1)
                pe.wait_ge(ready, 1)
                for h in range(HEADS):
                    nc.tensor.matmul(ps[0:D, 4, h * HD:(h + 1) * HD], turned[:, 0, h], turned[:, 1, h], start=True, stop=True)
                    ins = nc.tensor.matmul(ps[0:D, 5, h * HD:(h + 1) * HD], turned[:, 2, h], turned[:, 3, h], start=True, stop=True)
                ins.then_inc(made, 1)

            @block.vector
            def _(dve):
                link = Link(dve, step)
                nc.vector.memset(pair_map[D:P], 0.0)
                link(nc.vector.memset(value_map[D:P], 0.0))
                dve.wait_ge(made, 1)
                for n in range(4):
                    link(nc.vector.tensor_copy(turned[:, n], ps[0:D, n, :].rearrange("p (h c) -> p h c", h=HEADS)))
                nc.vector.sem_inc(ready, 1)
                dve.wait_ge(made, 2)
                link(nc.vector.tensor_scalar(pair_map[0:D], ps[0:D, 4, :].rearrange("p (h c) -> p h c", h=HEADS), HD ** -0.5, None, ALU.mult))
                link(nc.vector.tensor_copy(value_map[0:D], ps[0:D, 5, :].rearrange("p (h c) -> p h c", h=HEADS)))

        xs = s.sb("xs", [P, GROUP, 2, D])
        xh = s.sb("xh", [P, 2, 2, TOK])
        xm = s.sb("xm", [P, 2, PAIRS, TOK])
        top = s.sb("top", [P, 4, 4])
        probs = s.sb("probs", [P, 4, 4, N])
        total = s.sb("total", [P, 4, 4])
        rtotal = s.sb("rtotal", [P, 4, 4])
        weight = s.sb("weight", [P, 2, HEADS, 1])
        part = s.sb("part", [P, 2, HEADS, D])
        summed = s.sb("summed", [P, 2, D])
        ps = s.ps("ps", [P, 8, 512])
        SC, XV, WT, X, Y = 0, 2, 4, 6, 7
        names = "step zeroed normed xt_made xt_ready projected xm_ready scored topped exped inverted weighed taken xv_made".split()
        S = {n: s.sem(n) for n in names}
        block = s.block()

        def started(t, u, back):
            return not (isinstance(t, int) and t == 0 and u < back)

        @block.vector
        def _(dve):
            vec = nc.vector
            vec.memset(xh[:], 0.0).then_inc(S["zeroed"], 1)
            PER = 4 * GROUP

            def front(t):
                g = bass.ds(GROUP * t, GROUP)
                for half in range(2):
                    vec.tensor_tensor(xs[:, :, half, :], k.xc[:, g, :], bc(k.rstd[:, g, :], [P, GROUP, D]), ALU.mult).then_inc(S["normed"], 1)

            def prelude():
                front(0)

            def maximum(t, u):
                dve.wait_ge(S["scored"], UNITS * t + u + 1)
                vec.tensor_reduce(top[:, u % 4], ps[:, SC + u % 2, :].rearrange("p (a n) -> p a n", a=4), AX, ALU.max,
                                  negate=True).then_inc(S["topped"], 1)

            def invert(t, u):
                dve.wait_ge(S["exped"], UNITS * t + u + 1)
                if started(t, u, 4):
                    dve.wait_ge(S["weighed"], UNITS * t + u - 3)
                vec.reciprocal(rtotal[:, u % 4], total[:, u % 4]).then_inc(S["inverted"], 1)

            def combine(t, b, link):
                dve.wait_ge(S["weighed"], UNITS * t + 2 * b + 2)
                dve.wait_ge(S["xv_made"], GROUP * t + b + 1)
                link(vec.tensor_copy(weight[:, b % 2].rearrange("p h o -> p (h o)"), ps[:, WT + b % 2, 0:HEADS]))
                link(vec.tensor_tensor(part[:, b % 2], ps[:, XV + b % 2, :].rearrange("p (h d) -> p h d", h=HEADS),
                                       bc(weight[:, b % 2], [P, HEADS, D]), ALU.mult))
                vec.sem_inc(S["taken"], 1)
                link(vec.tensor_reduce(summed[:, b % 2], part[:, b % 2].rearrange("p h d -> p d h"), AX, ALU.add))
                one = bass.ds(GROUP * t + b, 1)
                link(vec.tensor_tensor(k.h[:, one, :], k.h[:, one, :], summed[:, b % 2:b % 2 + 1, :], ALU.add))

            def body(t, par, cur, prev, nxt):
                link = Link(dve, S["step"], PER * t - PER // 2 if prev else 0)
                for u in range(UNITS):
                    if cur:
                        maximum(t, u)
                    if u >= 1 and cur:
                        invert(t, u - 1)
                    if u == 0 and prev:
                        invert(t - 1, UNITS - 1)
                    if u == 0 and nxt:
                        front(t + 1)
                    if u in (0, 2) and prev:
                        combine(t - 1, 2 + u // 2, link)
                    if u in (4, 6) and cur:
                        combine(t, u // 2 - 2, link)

            in_turn(dve, prelude, body)

        @block.scalar
        def _(act):
            act.wait_ge(S["zeroed"], 1)

            def keep_x(t, par):
                act.wait_ge(S["xt_made"], t + 1)
                for half in range(2):
                    r = slice(D * half, D * half + D)
                    ins = nc.scalar.copy(xh[r, par, half, :], ps[r, X, :])
                ins.then_inc(S["xt_ready"], 1)

            def keep_projected(t, par, p):
                act.wait_ge(S["projected"], PAIRS * t + p + 1)
                nc.scalar.copy(xm[:, par, p, :], ps[:, (Y, X)[p % 2], :]).then_inc(S["xm_ready"], 1)

            def prelude():
                keep_x(0, 0)
                for p in range(PAIRS):
                    keep_projected(0, 0, p)

            def exponential(t, u):
                act.wait_ge(S["topped"], UNITS * t + u + 1)
                if started(t, u, 4):
                    act.wait_ge(S["weighed"], UNITS * t + u - 3)
                    act.wait_ge(S["inverted"], UNITS * t + u - 3)
                for a in range(4):
                    ins = nc.scalar.activation(probs[:, u % 4, a], ps[:, SC + u % 2, a * N:(a + 1) * N], ACT.Exp, bias=top[:, u % 4, a:a + 1],
                                               accum_out=total[:, u % 4, a:a + 1])
                ins.then_inc(S["exped"], 1)

            def body(t, par, cur, prev, nxt):
                for u in range(UNITS):
                    if cur:
                        exponential(t, u)
                    if u == 1 and nxt:
                        keep_x(t + 1, 1 - par)
                    if 2 <= u <= 5 and nxt:
                        keep_projected(t + 1, 1 - par, u - 2)

            in_turn(act, prelude, body)

        @block.tensor
        def _(pe):
            mm = nc.tensor.matmul

            def turn_x(t):
                pe.wait_ge(S["normed"], 2 * t + 2)
                if started(t, 0, 1):
                    pe.wait_ge(S["xm_ready"], PAIRS * t)
                for b in range(GROUP):
                    ins = nc.tensor.transpose(ps[:, X, b * N:(b + 1) * N], xs[:, b].rearrange("p z d -> p (z d)"), k.ident[:])
                ins.then_inc(S["xt_made"], 1)

            def project(t, par, p):
                pe.wait_ge(S["xt_ready"], t + 1)
                if p >= 2:
                    pe.wait_ge(S["xm_ready"], PAIRS * t + p - 1)
                mm(ps[:, (Y, X)[p % 2], :], pair_map[:, 2 * p:2 * p + 2].rearrange("c h d -> c (h d)"), xh[:, par, 0, :],
                   start=True, stop=True).then_inc(S["projected"], 1)

            def prelude():
                turn_x(0)
                for p in range(PAIRS):
                    project(0, 0, p)

            def scores(t, par, u):
                b, half = u // 2, u % 2
                if u == 0:
                    pe.wait_ge(S["xm_ready"], PAIRS * t + PAIRS)
                if started(t, u, 2):
                    pe.wait_ge(S["exped"], UNITS * t + u - 1)
                mm(ps[:, SC + u % 2, :], xh[:, par, half, b * N:(b + 1) * N], xm[:, par, :, b * N:(b + 1) * N],
                   start=True, stop=True).then_inc(S["scored"], 1)

            def weigh(t, par, u):
                b = u // 2
                if u % 2 == 0 and started(t, b, 2):
                    pe.wait_ge(S["taken"], GROUP * t + b - 1)
                pe.wait_ge(S["inverted"], UNITS * t + u + 1)
                for a in range(4):
                    ins = mm(ps[:, WT + b % 2, 2 * a + u % 2:2 * a + u % 2 + 1], probs[:, u % 4, a, :], rtotal[:, u % 4, a:a + 1],
                             start=True, stop=True)
                ins.then_inc(S["weighed"], 1)
                if u % 2:
                    mm(ps[:, XV + b % 2, :], xh[:, par, 0, b * N:(b + 1) * N], value_map[:].rearrange("c h o -> c (h o)"),
                       start=True, stop=True).then_inc(S["xv_made"], 1)

            def body(t, par, cur, prev, nxt):
                for u in range(UNITS):
                    if cur:
                        scores(t, par, u)
                    if u >= 2 and cur:
                        weigh(t, par, u - 2)
                    if u < 2 and prev:
                        weigh(t - 1, 1 - par, UNITS + u - 2)
                    if u == 1 and nxt:
                        turn_x(t + 1)
                    if 2 <= u <= 5 and nxt:
                        project(t + 1, 1 - par, u - 2)

            in_turn(pe, prelude, body)


def turn_all(k, tag, xt, router=None, logits=None, by_token=False):
    nc = k.nc
    rows = xt.shape[0]
    with Scope(nc, f"turn{tag}") as s:
        xs = s.sb("xs", [P, 2, GROUP, P])
        xg = s.sb("xg", [P, 2, TOK])
        ps = s.ps("ps", [P, 4, 512])
        names = "step normed made ready kept routed taken".split()
        S = {n: s.sem(n) for n in names}
        block = s.block()
        E = router.shape[1] if router is not None else 0

        @block.vector
        def _(dve):
            link = Link(dve, S["step"])
            link(nc.vector.memset(xs[:], 0.0))
            link(nc.vector.memset(xs[:, :, :, D:D + 1], 1.0))
            with dve.Fori(0, GROUPS // 2) as i:
                for j in range(2):
                    dve.wait_ge(S["taken"], 2 * i + j + 1)
                    front_dve(k, dve, xs[:, j], 2 * i + j, S["normed"])
                for j in range(2):
                    t = 2 * i + j
                    g = bass.ds(GROUP * t, GROUP)
                    dve.wait_ge(S["ready"], t + 1)
                    src = xg[:, j].rearrange("p (b n) -> p b n", b=GROUP)
                    dst = xt[:, :, g].rearrange("p n b -> p b n") if by_token else xt[:, g, :]
                    nc.vector.tensor_copy(dst, src[0:rows]).then_inc(S["kept"], 1)
                    if E:
                        dve.wait_ge(S["routed"], t + 1)
                        nc.vector.tensor_copy(logits[:, g, :], ps[:, 2 + j, 0:GROUP * E].rearrange("p (b e) -> p b e", b=GROUP)).then_inc(S["kept"], 1)

        @block.scalar
        def _(act):
            with act.Fori(0, GROUPS // 2) as i:
                for j in range(2):
                    t = 2 * i + j
                    act.wait_ge(S["made"], t + 1)
                    nc.scalar.copy(xg[:, j], ps[:, j, :]).then_inc(S["ready"], 1)

        @block.tensor
        def _(pe):
            nc.tensor.sem_inc(S["taken"], 2)
            with pe.Fori(0, GROUPS // 2) as i:
                for j in range(2):
                    t = 2 * i + j
                    pe.wait_ge(S["normed"], t + 1)
                    for b in range(GROUP):
                        ins = nc.tensor.transpose(ps[:, j, b * N:(b + 1) * N], xs[:, j, b, :], k.ident[:])
                    ins.then_inc(S["made"], 1)
                for j in range(2):
                    t = 2 * i + j
                    pe.wait_ge(S["ready"], t + 1)
                    if E:
                        for b in range(GROUP):
                            ins = nc.tensor.matmul(ps[:, 2 + j, b * E:(b + 1) * E], xg[:, j, b * N:(b + 1) * N], router[:], start=True, stop=True)
                        ins.then_inc(S["routed"], 1)
                    nc.tensor.sem_inc(S["taken"], 1)


def route(k, tag, logits, share):
    nc = k.nc
    E = logits.shape[2]
    with Scope(nc, f"route{tag}") as s:
        shape = [P, SEQS, E]
        top = s.sb("top", [P, SEQS, 1])
        prob = s.sb("prob", [P, SEQS * E, 1])
        before = s.sb("before", [P, SEQS, E, E])
        tie = s.sb("tie", [P, SEQS, E, E])
        lower_f = s.sb("lower_f", [P, E, E])
        rank = s.sb("rank", shape)
        step, shifted, exped, made = (s.sem(n) for n in "step shifted exped made".split())
        block = s.block()
        p3 = prob[:].rearrange("p (s e) o -> p s (e o)", e=E)

        @block.gpsimd
        def _(pool):
            link = Link(pool, made)
            link(nc.gpsimd.memset(lower_f[:], 1.0))
            link(nc.gpsimd.affine_select(out=lower_f[:], in_=lower_f[:], compare_op=ALU.is_gt, fill=0.0, base=0,
                                         pattern=[[1, E], [-1, E]], channel_multiplier=0))

        @block.scalar
        def _(act):
            act.wait_ge(shifted, 1)
            nc.scalar.activation(p3, p3, ACT.Exp).then_inc(exped, 1)

        @block.vector
        def _(dve):
            vec = nc.vector
            link = Link(dve, step)
            link(vec.tensor_reduce(top[:, :, 0], logits[:], AX, ALU.max))
            vec.tensor_tensor(p3, logits[:], bc(top[:], shape), ALU.subtract).then_inc(shifted, 1)
            dve.wait_ge(exped, 1)
            dve.wait_ge(made, 2)
            for e in range(E):
                mine = bc(p3[:, :, e:e + 1], shape)
                vec.tensor_tensor(before[:, :, e, :], p3, mine, ALU.is_gt)
                ins = vec.tensor_tensor(tie[:, :, e, :], p3, mine, ALU.is_equal)
            link(ins)
            flat = [P, SEQS, E * E]
            t3 = tie[:].rearrange("p s e f -> p s (e f)")
            link(vec.tensor_tensor(t3, t3, bc(lower_f[:].rearrange("p (o e) f -> p o (e f)", o=1), flat), ALU.mult))
            link(vec.tensor_tensor(before[:], before[:], tie[:], ALU.add))
            link(vec.tensor_reduce(rank[:], before[:], AX, ALU.add))
            link(vec.tensor_scalar(rank[:], rank[:], 1.5, None, ALU.is_lt))
            link(vec.tensor_tensor(rank[:], rank[:], p3, ALU.mult))
            link(vec.tensor_reduce(top[:, :, 0], rank[:], AX, ALU.add))
            link(vec.reciprocal(top[:], top[:]))
            link(vec.tensor_tensor(share[:], rank[:], bc(top[:], shape), ALU.mult))


def split_shares(k, tag, share, parts_t):
    nc = k.nc
    E = share.shape[2]
    PARTS = 3
    with Scope(nc, f"split{tag}") as s:
        parts = s.sb("parts", [P, SEQS, PARTS * E], BF16)
        rest = s.sb("rest", [P, SEQS, E])
        now = s.sb("now", [P, 2, GROUP, PARTS * E], BF16)
        identb = s.sb("identb", [P, P], BF16)
        ps = s.ps("ps", [PARTS * E, 2, 2 * BANK], BF16)
        step, ready, taken, kept, apart = (s.sem(n) for n in "step ready taken kept apart".split())
        block = s.block()

        @block.vector
        def _(dve):
            vec = nc.vector
            link = Link(dve, step)
            link(vec.tensor_copy(identb[:], k.ident[:]))
            link(vec.memset(parts_t[:], 0.0))
            link(vec.tensor_copy(parts[:, :, 0:E], share[:]))
            link(vec.tensor_tensor(rest[:], share[:], parts[:, :, 0:E], ALU.subtract))
            link(vec.tensor_copy(parts[:, :, E:2 * E], rest[:]))
            link(vec.tensor_tensor(rest[:], rest[:], parts[:, :, E:2 * E], ALU.subtract))
            link(vec.tensor_copy(parts[:, :, 2 * E:3 * E], rest[:]))
            with dve.Fori(0, GROUPS // 2) as i:
                for j in range(2):
                    t = 2 * i + j
                    dve.wait_ge(taken, t + 1)
                    vec.tensor_copy(now[:, j], parts[:, bass.ds(GROUP * t, GROUP), :]).then_inc(ready, 1)

        @block.tensor
        def _(pe):
            nc.tensor.sem_inc(taken, 2)
            nc.tensor.sem_inc(kept, 2)
            with pe.Fori(0, GROUPS // 2) as i:
                for j in range(2):
                    pe.wait_ge(ready, 2 * i + j + 1)
                    pe.wait_ge(kept, 2 * i + j + 1)
                    nc.tensor.sem_inc(apart, 1)
                    for b in range(GROUP):
                        ins = nc.tensor.transpose(ps[:, j, b * N:(b + 1) * N], now[:, j, b, :], identb[:])
                    ins.then_inc(taken, 1)

        @block.scalar
        def _(act):
            with act.Fori(0, GROUPS // 2) as i:
                for j in range(2):
                    act.wait_ge(taken, 2 * i + j + 3)
                    nc.scalar.copy(parts_t[0:PARTS * E, bass.ds(GROUP * (2 * i + j), GROUP), :],
                                   ps[:, j, 0:TOK].rearrange("p (b n) -> p b n", b=GROUP)).then_inc(kept, 1)


def mix_experts(k, tag, xt, share, w1, w2, b2, shared):
    nc = k.nc
    HC, E, PARTS = 2, 8, 3
    ALL = E + (1 if shared else 0)
    with Scope(nc, f"mix{tag}") as s:
        parts_t = s.sb("parts_t", [P, SEQS, N], BF16)
        split_shares(k, tag, share, parts_t)
        pick_f = s.sb("pick_f", [P, E, P])
        pick = s.sb("pick", [P, E, P], BF16)
        b2x = s.sb("b2x", [P, D])
        b2rest = s.sb("b2rest", [P, D])
        b2_parts = s.sb("b2_parts", [P, PARTS, D], BF16)
        halves = s.sb("halves", [P, D])
        act_t = s.sb("act_t", [P, 3, HC, TOK])
        scaled = s.sb("scaled", [P, 2, HC, TOK])
        y_t = s.sb("y_t", [P, TOK])
        ps = s.ps("ps", [P, 8, 512])
        names = "step picked loaded ready hidden active spread scaled output y_ready back added apart".split()
        S = {n: s.sem(n) for n in names}
        block = s.block()
        NH = ALL * HC
        HIDDEN, SPREAD, Y, BACK = 0, 3, 5, 6
        HB = 3 if NH % 3 == 0 else 2

        @block.sync
        def _(sp):
            sp.wait_ge(S["ready"], 1)
            for n in range(PARTS):
                sp.dma_start(b2x[n * E:(n + 1) * E, :], b2).then_inc(S["loaded"], 16)

        @block.gpsimd
        def _(pool):
            link = Link(pool, S["picked"])
            link(nc.gpsimd.memset(pick_f[:], 0.0))
            for n in range(PARTS):
                link(nc.gpsimd.affine_select(out=pick_f[:], in_=pick_f[:], compare_op=ALU.not_equal, fill=1.0,
                                             base=-n * E, pattern=[[-1, E], [0, P]], channel_multiplier=1))

        @block.vector
        def _(dve):
            vec = nc.vector
            link = Link(dve, S["step"])
            link(vec.memset(b2x[:], 0.0))
            vec.sem_inc(S["ready"], 1)
            for n in range(2):
                link(vec.tensor_copy(halves[n * D:(n + 1) * D, :], k.ident[n * D:(n + 1) * D, n * D:(n + 1) * D]))
            dve.wait_ge(S["loaded"], 16 * PARTS)
            link(vec.tensor_copy(b2_parts[:, 0], b2x[:]))
            link(vec.tensor_tensor(b2rest[:], b2x[:], b2_parts[:, 0], ALU.subtract))
            link(vec.tensor_copy(b2_parts[:, 1], b2rest[:]))
            link(vec.tensor_tensor(b2rest[:], b2rest[:], b2_parts[:, 1], ALU.subtract))
            link(vec.tensor_copy(b2_parts[:, 2], b2rest[:]))
            dve.wait_ge(S["picked"], 1 + PARTS)
            link(vec.tensor_copy(pick[:], pick_f[:]))
            vec.sem_inc(S["ready"], 1)

            def keep(t):
                g = bass.ds(GROUP * t, GROUP)
                dve.wait_ge(S["back"], t + 1)
                vec.tensor_tensor(k.h[:, g, :], k.h[:, g, :], ps[:, BACK, 0:GROUP * D].rearrange("p (b d) -> p b d", b=GROUP), ALU.add).then_inc(S["added"], 1)

            def group(t, first):
                for e in range(E):
                    if e == 1 and not first:
                        keep(t - 1)
                    dve.wait_ge(S["spread"], E * t + e + 1)
                    dve.wait_ge(S["active"], NH * t + HC * e + HC)
                    if e >= 2:
                        dve.wait_ge(S["output"], ALL * t + e - 1)
                    vec.tensor_tensor(scaled[:, e % 2], act_t[:, e % 3],
                                      bc(ps[:, SPREAD + e % 2, :].rearrange("p (o n) -> p o n", o=1), [P, HC, TOK]), ALU.mult).then_inc(S["scaled"], 1)
                dve.wait_ge(S["output"], ALL * t + ALL)
                if not first:
                    dve.wait_ge(S["back"], t)
                vec.tensor_copy(y_t[:], ps[:, Y, :]).then_inc(S["y_ready"], 1)

            group(0, True)
            with dve.Fori(1, GROUPS) as t:
                group(t, False)
            keep(GROUPS - 1)

        @block.scalar
        def _(act):
            with act.Fori(0, GROUPS) as t:
                for n in range(NH):
                    e, c = n // HC, n % HC
                    act.wait_ge(S["hidden"], NH * t + n + 1)
                    if n >= 3 * HC and c == 0:
                        act.wait_ge(S["scaled"], E * t + e - 2)
                    nc.scalar.activation(act_t[:, e % 3, c, :], ps[:, HIDDEN + n % HB, :], ACT.Gelu).then_inc(S["active"], 1)

        @block.tensor
        def _(pe):
            mm = nc.tensor.matmul
            pe.wait_ge(S["ready"], 2)

            def back(t):
                pe.wait_ge(S["y_ready"], t + 1)
                for b in range(GROUP):
                    ins = mm(ps[:, BACK, b * D:(b + 1) * D], y_t[:, b * N:(b + 1) * N], halves[:], start=True, stop=True)
                ins.then_inc(S["back"], 1)

            def group(t, first):
                g = bass.ds(GROUP * t, GROUP)
                x = xt[:, g, :].rearrange("p b n -> p (b n)")
                parts = parts_t[:, g, :].rearrange("p b n -> p (b n)")

                def hidden(e):
                    for c in range(HC):
                        n = HC * e + c
                        if n >= HB:
                            pe.wait_ge(S["active"], NH * t + n - HB + 1)
                        mm(ps[:, HIDDEN + n % HB, :], w1[:, e, c * P:(c + 1) * P], x, start=True, stop=True).then_inc(S["hidden"], 1)

                def spread(e):
                    if e >= 2:
                        pe.wait_ge(S["scaled"], E * t + e - 1)
                    mm(ps[:, SPREAD + e % 2, :], pick[:, e, :], parts, start=True, stop=True).then_inc(S["spread"], 1)

                def output(e):
                    src = scaled[:, e % 2] if e < E else act_t[:, e % 3]
                    if e < E:
                        pe.wait_ge(S["scaled"], E * t + e + 1)
                    else:
                        pe.wait_ge(S["active"], NH * t + NH)
                    for c in range(HC):
                        ins = mm(ps[c * D:(c + 1) * D, Y, :], w2[:, e, c, :], src[:, c, :], start=(e == 0 and c == 1), stop=(e == ALL - 1),
                                 skip_group_check=True, tile_position=(0, c * D))
                    return ins.then_inc(S["output"], 1)

                spread(0)
                hidden(0)
                if not first:
                    back(t - 1)
                for n in range(PARTS):
                    mm(ps[0:D, Y, :], b2_parts[:, n, :], parts, start=(n == 0), stop=False, skip_group_check=True, tile_position=(0, 0))
                for e in range(1, ALL):
                    hidden(e)
                    if e < E:
                        spread(e)
                    output(e - 1)
                output(ALL - 1)

            group(0, True)
            with pe.Fori(1, GROUPS) as t:
                group(t, False)
            back(GROUPS - 1)


def stage_l2_ffn(k):
    nc, w = k.nc, k.w
    E, F, A1 = 8, 256, D + 1
    with Scope(nc, "l2f") as s:
        share = s.sb("share", [P, SEQS, E])
        xt = s.sb("xt", [P, SEQS, N])
        w1 = s.sb("w1", [P, E + 1, F])
        w2 = s.sb("w2", [P, E + 1, 2, D])
        with Scope(nc, "l2froute") as s1:
            wr = s1.sb("wr", [P, E])
            bshared = s1.sb("bshared", [P, 1, D])
            logits = s1.sb("logits", [P, SEQS, E])
            with Scope(nc, "l2fload") as s2:
                loaded, zeroed, added = s2.sem("loaded"), s2.sem("zeroed"), s2.sem("added")
                block = s2.block()

                @block.sync
                def _(sp):
                    sp.wait_ge(zeroed, 1)
                    sp.dma_start(w1[0:D, 0:E], w["L2_ffn_W1p"].rearrange("e d f -> d e f")).then_inc(loaded, 16)
                    sp.dma_start(w1[0:D, E], w["L2_ffn_W1s"]).then_inc(loaded, 16)
                    sp.dma_start(w1[D:A1, 0:E], w["L2_ffn_b1p"].rearrange("(o e) f -> o e f", o=1)).then_inc(loaded, 16)
                    sp.dma_start(w1[D:A1, E], w["L2_ffn_b1s"].rearrange("(o f) -> o f", o=1)).then_inc(loaded, 16)
                    for c in range(2):
                        sp.dma_start(w2[:, 0:E, c], w["L2_ffn_W2p"].rearrange("e (c f) d -> c f e d", c=2)[c]).then_inc(loaded, 16)
                    sp.dma_start(w2[:, E], w["L2_ffn_W2s"].rearrange("(c f) d -> f c d", c=2)).then_inc(loaded, 16)
                    sp.dma_start(bshared[:, 0, :], w["L2_ffn_b2s"].partition_broadcast(P)).then_inc(loaded, 16)
                    sp.dma_start(wr[0:D, :], w["L2_ffn_Wr"]).then_inc(loaded, 16)

                @block.vector
                def _(dve):
                    nc.vector.memset(wr[D:P, :], 0.0)
                    nc.vector.memset(w1[D:P], 0.0).then_inc(zeroed, 1)
                    dve.wait_ge(loaded, 144)
                    nc.vector.tensor_tensor(k.h[:], k.h[:], bc(bshared[:], [P, SEQS, D]), ALU.add).then_inc(added, 1)
                    dve.wait_ge(added, 1)
            turn_all(k, "l2f", xt, wr, logits)
            route(k, "l2f", logits, share)
        mix_experts(k, "l2f", xt, share, w1, w2, w["L2_ffn_b2p"], True)


def stage_neighbours(k, xt, mask):
    nc, w = k.nc, k.w
    A1, NEAR = D + 1, 17
    with Scope(nc, "knn") as s:
        wr = s.sb("wr", [A1, D])
        mean_t = s.sb("mean_t", [A1, SEQS])
        reprs = s.sb("reprs", [SEQS, D])
        sq = s.sb("sq", [SEQS, D])
        norm = s.sb("norm", [SEQS, 1])
        unit_t = s.sb("unit_t", [D, SEQS])
        sim = s.sb("sim", [SEQS, 1, SEQS])
        before = s.sb("before", [SEQS, SEQS, SEQS])
        tie = s.sb("tie", [SEQS, SEQS, SEQS])
        lower = s.sb("lower", [SEQS, SEQS, SEQS])
        rank = s.sb("rank", [SEQS, SEQS])
        ps = s.ps("ps", [SEQS, 4, 512])
        loaded, step, meaned, made, squared, rooted, united, lowered = (s.sem(n) for n in "loaded step meaned made squared rooted united lowered".split())
        block = s.block()

        @block.sync
        def _(sp):
            sp.dma_start(wr[0:D, :], w["L3_attn_W_repr"]).then_inc(loaded, 16)
            sp.dma_start(wr[D:A1, :], w["L3_attn_b_repr"].rearrange("(o d) -> o d", o=1)).then_inc(loaded, 16)

        @block.gpsimd
        def _(pool):
            link = Link(pool, lowered)
            link(nc.gpsimd.memset(lower[:], 1.0))
            link(nc.gpsimd.affine_select(out=lower[:], in_=lower[:], compare_op=ALU.is_gt, fill=0.0, base=0,
                                         pattern=[[1, SEQS], [-1, SEQS]], channel_multiplier=0))

        @block.scalar
        def _(act):
            act.wait_ge(squared, 1)
            nc.scalar.activation(norm[:], norm[:], ACT.Sqrt).then_inc(rooted, 1)

        @block.tensor
        def _(pe):
            pe.wait_ge(loaded, 32)
            pe.wait_ge(meaned, 1)
            nc.tensor.matmul(ps[:, 0, 0:D], mean_t[:], wr[:], start=True, stop=True).then_inc(made, 1)
            pe.wait_ge(united, 1)
            nc.tensor.transpose(ps[:, 1, 0:SEQS], reprs[:], k.ident[0:SEQS, 0:SEQS]).then_inc(made, 1)
            pe.wait_ge(united, 2)
            nc.tensor.matmul(ps[:, 2, 0:SEQS], unit_t[:], unit_t[:], start=True, stop=True).then_inc(made, 1)

        @block.vector
        def _(dve):
            vec = nc.vector
            link = Link(dve, step)
            link(vec.memset(mean_t[D:A1, :], 1.0))
            link(vec.tensor_reduce(mean_t[0:D, :], xt[0:D].rearrange("d n b -> d b n"), AX, ALU.add))
            link(vec.tensor_scalar(mean_t[0:D, :], mean_t[0:D, :], 1.0 / N, None, ALU.mult))
            vec.sem_inc(meaned, 1)
            dve.wait_ge(made, 1)
            link(vec.tensor_copy(reprs[:], ps[:, 0, 0:D]))
            link(vec.tensor_tensor(sq[:], reprs[:], reprs[:], ALU.mult))
            vec.tensor_reduce(norm[:], sq[:], AX, ALU.add).then_inc(squared, 1)
            dve.wait_ge(rooted, 1)
            link(vec.reciprocal(norm[:], norm[:]))
            vec.tensor_scalar(reprs[:], reprs[:], norm[:, 0:1], None, ALU.mult).then_inc(united, 1)
            dve.wait_ge(made, 2)
            vec.tensor_copy(unit_t[:], ps[:, 1, 0:SEQS]).then_inc(united, 1)
            dve.wait_ge(made, 3)
            link(vec.tensor_copy(sim[:, 0, :], ps[:, 2, 0:SEQS]))
            cube = [SEQS, SEQS, SEQS]
            mine = bc(sim[:, 0, :].rearrange("p (b o) -> p b o", o=1), cube)
            vec.tensor_tensor(before[:], bc(sim[:], cube), mine, ALU.is_gt)
            link(vec.tensor_tensor(tie[:], bc(sim[:], cube), mine, ALU.is_equal))
            dve.wait_ge(lowered, 2)
            link(vec.tensor_tensor(tie[:], tie[:], lower[:], ALU.mult))
            link(vec.tensor_tensor(before[:], before[:], tie[:], ALU.add))
            link(vec.tensor_reduce(rank[:], before[:], AX, ALU.add))
            link(vec.tensor_scalar(rank[:], rank[:], NEAR - 0.5, MASKED, ALU.is_gt, ALU.mult))
            link(vec.memset(mask[SEQS:P], 0.0))
            link(vec.tensor_copy(mask[0:SEQS], bc(rank[:].rearrange("p (o b) -> p o b", o=1), [SEQS, 8, SEQS])))


def stage_l3_attn(k):
    with Scope(k.nc, "l3") as s:
        xt = s.sb("xt", [P, N, SEQS])
        yt = s.sb("yt", [D, SEQS, N])
        mask = s.sb("mask", [P, 8, SEQS], BF16)
        turn_all(k, "l3a", xt, by_token=True)
        stage_neighbours(k, xt, mask)
        attend_sequences(k, xt, yt, mask)
        add_turned_back(k, "l3a", yt)


def attend_sequences(k, xt, yt, mask):
    nc, w = k.nc, k.w
    HEADS, HD = 8, 32
    NG = 8
    assert N // NG == GROUPS
    COLS = NG * SEQS
    UNITS = NG // 2
    PROJ = 6
    with Scope(nc, "l3a") as s:
        twice = s.sb("twice", [P, 2, SEQS], BF16)
        wqk = s.sb("wqk", [P, 2, 2, P])
        wv = s.sb("wv", [P, 2, 4, HD])
        wo = s.sb("wo", [P, 2, D])
        bo = s.sb("bo", [D, 1])
        xg = s.sb("xg", [P, COLS])
        q = s.sb("q", [P, 2, 2, COLS])
        keys = s.sb("keys", [P, 2, 2, NG, 4, SEQS])
        v = s.sb("v", [P, 2, NG, 4, 2, HD + 1])
        top = s.sb("top", [P, 2, HEADS, 1])
        probs = s.sb("probs", [P, 2, HEADS, SEQS])
        probs_t = s.sb("probs_t", [P, 2, 4, P])
        rden = s.sb("rden", [P, 2, HEADS, 1])
        mixed = s.sb("mixed", [P, 2, UNITS, HEADS, HD])
        mt = s.sb("mt", [P, 2, COLS])
        ps = s.ps("ps", [P, 8, 512])
        SC, TU, OUT, X, Y = 0, 2, 4, 5, 7
        names = ("loaded step zeroed v_laid x_in projected q_ready kv_ready topped scored shifted exped turned turned_ready valued inverted mixed_ready "
                 "mt_made mt_ready y_made y_kept apart").split()
        S = {n: s.sem(n) for n in names}
        block = s.block()

        def started(t, u, back):
            return not (isinstance(t, int) and t == 0 and u < back)

        @block.sync
        def _(sp):
            sp.wait_ge(S["zeroed"], 1)
            sp.dma_start(wqk[0:D], w["L3_attn_W_qkv"][:, 0:4 * P].rearrange("d (z g c) -> d z g c", z=2, g=2)).then_inc(S["loaded"], 16)
            for z in range(2):
                sp.dma_start(wv[0:D, z], w["L3_attn_W_qkv"][:, 4 * P:6 * P].rearrange("d (a z c) -> z d a c", z=2, c=HD)[z]).then_inc(S["loaded"], 16)
            sp.dma_start(wo[:], w["L3_attn_W_out"].rearrange("(g c) o -> c g o", g=2)).then_inc(S["loaded"], 16)
            sp.dma_start(bo[:], w["L3_attn_b_out"].rearrange("(o u) -> o u", u=1)).then_inc(S["loaded"], 16)

        @block.gpsimd
        def _(pool):
            nc.gpsimd.memset(v[:], 0.0).then_inc(S["v_laid"], 1)
            pool.wait_ge(S["v_laid"], 1)
            for z in range(2):
                nc.gpsimd.memset(v[D * z:D * z + D, :, :, :, z, HD:HD + 1], 1.0).then_inc(S["v_laid"], 1)

        @block.vector
        def _(dve):
            vec = nc.vector
            link = Link(dve, S["step"])
            vec.memset(wqk[:], 0.0)
            vec.memset(wv[:], 0.0)
            vec.memset(twice[:], 0.0)
            link(vec.memset(keys[:], 0.0))
            vec.sem_inc(S["zeroed"], 1)
            dve.wait_ge(S["v_laid"], 3)
            for z in range(2):
                link(vec.tensor_copy(twice[0:SEQS, z, :], k.ident[0:SEQS, 0:SEQS]))
            dve.wait_ge(S["loaded"], 16 * 5)
            link(vec.tensor_scalar(wqk[:, 0], wqk[:, 0], HD ** -0.5, None, ALU.mult))
            vec.sem_inc(S["step"], 1)

            def fetch(t):
                if started(t, 0, 1):
                    dve.wait_ge(S["projected"], PROJ * t)
                vec.tensor_copy(xg[:], xt[:, bass.ds(NG * t, NG), :].rearrange("p n b -> p (n b)")).then_inc(S["x_in"], 1)

            def keep_keys(t, par, g):
                dve.wait_ge(S["projected"], PROJ * t + 3 + g)
                for h in range(2):
                    r = slice(HD * h, HD * h + HD)
                    ins = vec.tensor_copy(keys[r, par, g, :, h, :], ps[r, X + g, :].rearrange("p (n b) -> p n b", n=NG))
                ins.then_inc(S["kv_ready"], 1)

            def keep_values(t, par, j):
                dve.wait_ge(S["projected"], PROJ * t + 5 + j)
                vec.tensor_copy(v[0:D, par, 4 * j:4 * j + 4, :, 0, 0:HD],
                                ps[0:D, X + j, :].rearrange("p (n a c) -> p n a c", n=4, c=HD)).then_inc(S["kv_ready"], 1)

            def prelude():
                fetch(0)
                for n in range(2):
                    keep_keys(0, 0, n)
                for n in range(2):
                    keep_values(0, 0, n)

            def shift(t, u):
                dve.wait_ge(S["scored"], UNITS * t + u + 1)
                bank = ps[:, SC + u % 2, :].rearrange("p (h b) -> p h b", h=HEADS)
                vec.tensor_reduce(top[:, u % 2, :, 0], bank, AX, ALU.max).then_inc(S["topped"], 1)
                dve.wait_ge(S["topped"], UNITS * t + u + 1)
                if started(t, u, 2):
                    dve.wait_ge(S["turned"], UNITS * t + u - 1)
                vec.tensor_tensor(probs[:, u % 2], bank, bc(top[:, u % 2], [P, HEADS, SEQS]), ALU.subtract).then_inc(S["shifted"], 1)

            def normalize(t, par, u):
                dve.wait_ge(S["valued"], UNITS * t + u + 1)
                o = ps[:, OUT, 0:HEADS * (HD + 1)].rearrange("p (h c) -> p h c", h=HEADS)
                vec.reciprocal(rden[:, u % 2], o[:, :, HD:HD + 1]).then_inc(S["inverted"], 1)
                dve.wait_ge(S["inverted"], UNITS * t + u + 1)
                vec.tensor_tensor(mixed[:, par, u], o[:, :, 0:HD], bc(rden[:, u % 2], [P, HEADS, HD]), ALU.mult).then_inc(S["mixed_ready"], 1)

            def keep_y(t):
                dve.wait_ge(S["y_made"], t + 1)
                vec.tensor_scalar(yt[:, :, bass.ds(NG * t, NG)].rearrange("p b n -> p n b"), ps[0:D, Y, :].rearrange("p (n b) -> p n b", n=NG),
                                  bo[:, 0:1], None, ALU.add).then_inc(S["y_kept"], 1)

            def body(t, par, cur, prev, nxt):
                for u in range(UNITS):
                    if cur:
                        shift(t, u)
                    if u == 0 and nxt:
                        fetch(t + 1)
                    if u == 1 and nxt:
                        keep_keys(t + 1, 1 - par, 0)
                        keep_keys(t + 1, 1 - par, 1)
                    if u >= 2 and nxt:
                        keep_values(t + 1, 1 - par, u - 2)
                    if u >= 2 and cur:
                        normalize(t, par, u - 2)
                    if u < 2 and prev:
                        normalize(t - 1, 1 - par, UNITS + u - 2)
                    if u == 3 and prev:
                        keep_y(t - 1)

            in_turn(dve, prelude, body)

        @block.scalar
        def _(act):
            act.wait_ge(S["zeroed"], 1)
            act.wait_ge(S["v_laid"], 3)

            def keep_q(t, par, g):
                act.wait_ge(S["projected"], PROJ * t + g + 1)
                nc.scalar.copy(q[:, par, g, :], ps[:, X + g, :]).then_inc(S["q_ready"], 1)

            def keep_keys(t, par, g):
                act.wait_ge(S["projected"], PROJ * t + 3 + g)
                for h in range(2, 4):
                    r = slice(HD * h, HD * h + HD)
                    ins = nc.scalar.copy(keys[r, par, g, :, h, :], ps[r, X + g, :].rearrange("p (n b) -> p n b", n=NG))
                ins.then_inc(S["kv_ready"], 1)

            def keep_values(t, par, j):
                act.wait_ge(S["projected"], PROJ * t + 5 + j)
                nc.scalar.copy(v[D:P, par, 4 * j:4 * j + 4, :, 1, 0:HD],
                               ps[D:P, X + j, :].rearrange("p (n a c) -> p n a c", n=4, c=HD)).then_inc(S["kv_ready"], 1)

            def prelude():
                for n in range(2):
                    keep_q(0, 0, n)
                for n in range(2):
                    keep_keys(0, 0, n)
                for n in range(2):
                    keep_values(0, 0, n)

            def exponential(t, u):
                act.wait_ge(S["shifted"], UNITS * t + u + 1)
                nc.scalar.activation(probs[:, u % 2], probs[:, u % 2], ACT.Exp).then_inc(S["exped"], 1)

            def keep_turned(t, u):
                act.wait_ge(S["turned"], UNITS * t + u + 1)
                if started(t, u, 2):
                    act.wait_ge(S["valued"], UNITS * t + u - 1)
                nc.scalar.copy(probs_t[:, u % 2], ps[:, TU + u % 2, :].rearrange("p (a c) -> p a c", a=4)).then_inc(S["turned_ready"], 1)

            def keep_mixed(t, g):
                act.wait_ge(S["mt_made"], 2 * t + g + 1)
                nc.scalar.copy(mt[:, g], ps[:, Y, :]).then_inc(S["mt_ready"], 1)

            def body(t, par, cur, prev, nxt):
                for u in range(UNITS):
                    if u == 0 and nxt:
                        keep_q(t + 1, 1 - par, 0)
                        keep_q(t + 1, 1 - par, 1)
                    if u >= 1 and cur:
                        keep_turned(t, u - 1)
                    if u == 0 and prev:
                        keep_turned(t - 1, UNITS - 1)
                    if cur:
                        exponential(t, u)
                    if u == 1 and nxt:
                        keep_keys(t + 1, 1 - par, 0)
                        keep_keys(t + 1, 1 - par, 1)
                    if u >= 2 and nxt:
                        keep_values(t + 1, 1 - par, u - 2)
                    if u >= 2 and prev:
                        keep_mixed(t - 1, u - 2)

            in_turn(act, prelude, body)

        @block.tensor
        def _(pe):
            mm = nc.tensor.matmul
            pe.wait_ge(S["step"], 5)

            def project(t, n):
                if n >= 4:
                    pe.wait_ge(S["x_in"], t + 1)
                if n < 2:
                    if started(t, 0, 1):
                        pe.wait_ge(S["kv_ready"], 8 * t)
                elif n < 4:
                    pe.wait_ge(S["q_ready"], 2 * t + n - 1)
                else:
                    pe.wait_ge(S["kv_ready"], 8 * t + 4)
                if n < 4:
                    x = xt[:, bass.ds(NG * t, NG), :].rearrange("p n b -> p (n b)")
                    ins = mm(ps[:, X + n % 2, :], wqk[:, n // 2, n % 2, :], x, start=True, stop=True)
                else:
                    for p in range(4 * (n - 4), 4 * (n - 4) + 4):
                        for z in range(2):
                            ins = mm(ps[D * z:D * z + D, X + n % 2, (p % 4) * P:(p % 4 + 1) * P], xg[:, p * SEQS:(p + 1) * SEQS],
                                     wv[:, z].rearrange("p a c -> p (a c)"), start=True, stop=True, tile_position=(0, D * z))
                ins.then_inc(S["projected"], 1)

            def prelude():
                for n in range(PROJ):
                    project(0, n)

            def scores(t, par, u):
                if u == 0:
                    pe.wait_ge(S["q_ready"], 2 * t + 2)
                    pe.wait_ge(S["kv_ready"], 8 * t + 8)
                if started(t, u, 2):
                    pe.wait_ge(S["shifted"], UNITS * t + u - 1)
                bank = ps[:, SC + u % 2, :]
                mm(bank, twice[:].rearrange("p z b -> p (z b)"), mask[:].rearrange("p s b -> p (s b)"), start=True, stop=False)
                for g in range(2):
                    for z in range(2):
                        n = 2 * u + z
                        ins = mm(bank[D * z:D * z + D, g * 256:(g + 1) * 256], q[:, par, g, n * SEQS:(n + 1) * SEQS],
                                 keys[:, par, g, n].rearrange("p h b -> p (h b)"), start=False, stop=(g == 1), tile_position=(0, D * z))
                ins.then_inc(S["scored"], 1)

            def turn(t, u):
                pe.wait_ge(S["exped"], UNITS * t + u + 1)
                if started(t, u, 2):
                    pe.wait_ge(S["turned_ready"], UNITS * t + u - 1)
                for a in range(4):
                    ins = nc.tensor.transpose(ps[:, TU + u % 2, a * P:(a + 1) * P], probs[:, u % 2, 2 * a:2 * a + 2].rearrange("p s b -> p (s b)"), k.ident[:])
                ins.then_inc(S["turned"], 1)

            def values(t, par, u):
                pe.wait_ge(S["turned_ready"], UNITS * t + u + 1)
                if started(t, u, 1):
                    pe.wait_ge(S["mixed_ready"], UNITS * t + u)
                nc.tensor.sem_inc(S["apart"], 1)
                W = 2 * (HD + 1)
                for a in range(4):
                    for z in range(2):
                        ins = mm(ps[D * z:D * z + D, OUT, a * W:(a + 1) * W], probs_t[:, u % 2, a, D * z:D * z + D],
                                 v[:, par, 2 * u + z, a].rearrange("p z c -> p (z c)"), start=True, stop=True, tile_position=(0, D * z))
                ins.then_inc(S["valued"], 1)

            def turn_mixed(t, par, g):
                pe.wait_ge(S["mixed_ready"], UNITS * t + UNITS)
                if g == 1:
                    pe.wait_ge(S["mt_ready"], 2 * t + 1)
                elif started(t, 0, 1):
                    pe.wait_ge(S["y_kept"], t)
                for u in range(UNITS):
                    ins = nc.tensor.transpose(ps[:, Y, u * P:(u + 1) * P], mixed[:, par, u, 4 * g:4 * g + 4].rearrange("p h c -> p (h c)"), k.ident[:])
                ins.then_inc(S["mt_made"], 1)

            def outputs(t):
                pe.wait_ge(S["mt_ready"], 2 * t + 2)
                for g in range(2):
                    ins = mm(ps[0:D, Y, :], wo[:, g, :], mt[:, g], start=(g == 0), stop=(g == 1))
                ins.then_inc(S["y_made"], 1)

            def body(t, par, cur, prev, nxt):
                for u in range(UNITS):
                    if cur:
                        scores(t, par, u)
                    if nxt:
                        project(t + 1, (0, 2, 4, 5)[u])
                    if u >= 1 and cur:
                        turn(t, u - 1)
                    if u == 0 and prev:
                        turn(t - 1, UNITS - 1)
                    if u < 2 and nxt:
                        project(t + 1, (1, 3)[u])
                    if u >= 2 and prev:
                        turn_mixed(t - 1, 1 - par, u - 2)
                    if u >= 2 and cur:
                        values(t, par, u - 2)
                    if u < 2 and prev:
                        values(t - 1, 1 - par, UNITS + u - 2)
                    if u == 3 and prev:
                        outputs(t - 1)

            in_turn(pe, prelude, body)


def add_turned_back(k, tag, yt):
    nc = k.nc
    with Scope(nc, f"back{tag}") as s:
        yg = s.sb("yg", [D, 2, TOK])
        ps = s.ps("ps", [P, 2, 512])
        ready, made, added, apart, free = (s.sem(n) for n in "ready made added apart free".split())
        block = s.block()

        @block.vector
        def _(dve):
            nc.vector.sem_inc(added, 2)
            with dve.Fori(0, GROUPS // 2) as i:
                for j in range(2):
                    t = 2 * i + j
                    g = bass.ds(GROUP * t, GROUP)
                    dve.wait_ge(made, t + 1)
                    nc.vector.tensor_tensor(k.h[:, g, :], k.h[:, g, :], ps[:, j, 0:GROUP * D].rearrange("p (b d) -> p b d", b=GROUP), ALU.add).then_inc(added, 1)

        @block.scalar
        def _(act):
            with act.Fori(0, GROUPS // 2) as i:
                for j in range(2):
                    t = 2 * i + j
                    act.wait_ge(free, t + 1)
                    nc.scalar.copy(yg[:, j], yt[:, bass.ds(GROUP * t, GROUP), :].rearrange("p b n -> p (b n)")).then_inc(ready, 1)

        @block.tensor
        def _(pe):
            nc.tensor.sem_inc(free, 2)
            with pe.Fori(0, GROUPS // 2) as i:
                for j in range(2):
                    t = 2 * i + j
                    pe.wait_ge(ready, t + 1)
                    pe.wait_ge(added, t + 1)
                    nc.tensor.sem_inc(apart, 1)
                    for b in range(GROUP):
                        ins = nc.tensor.transpose(ps[:, j, b * D:(b + 1) * D], yg[:, j, b * N:(b + 1) * N], k.ident[0:D, 0:D])
                    ins.then_inc(made, 1)
                    pe.wait_ge(made, t + 1)
                    nc.tensor.sem_inc(free, 1)


def stage_l3_ffn(k):
    nc, w = k.nc, k.w
    E, F, A1 = 8, 256, D + 1
    with Scope(nc, "l3f") as s:
        share = s.sb("share", [P, SEQS, E])
        xt = s.sb("xt", [P, SEQS, N])
        w1 = s.sb("w1", [P, E, F])
        w2 = s.sb("w2", [P, E, 2, D])
        with Scope(nc, "l3froute") as s1:
            wr = s1.sb("wr", [P, E])
            logits = s1.sb("logits", [P, SEQS, E])
            with Scope(nc, "l3fload") as s2:
                gain = s2.sb("gain", [E, 2, D])
                gain_t = s2.sb("gain_t", [D, E])
                shift_t = s2.sb("shift_t", [D, E, A1])
                ps = s2.ps("ps", [P, 6, 512])
                loaded, step, made, ready, zeroed = (s2.sem(n) for n in "loaded step made ready zeroed".split())
                block = s2.block()

                @block.sync
                def _(sp):
                    sp.wait_ge(zeroed, 1)
                    sp.dma_start(w1[0:D], w["L3_ffn_W1"].rearrange("e d f -> d e f")).then_inc(loaded, 16)
                    sp.dma_start(w1[D:A1], w["L3_ffn_b1"].rearrange("(o e) f -> o e f", o=1)).then_inc(loaded, 16)
                    for c in range(2):
                        sp.dma_start(w2[:, :, c], w["L3_ffn_W2"].rearrange("e (c f) d -> c f e d", c=2)[c]).then_inc(loaded, 16)
                    sp.dma_start(wr[0:D, :], w["L3_ffn_Wr"]).then_inc(loaded, 16)
                    sp.dma_start(wr[D:A1, :], w["L3_ffn_br"].rearrange("(o e) -> o e", o=1)).then_inc(loaded, 16)
                    sp.dma_start(gain[:, 0, :], w["L3_ffn_ln_g"]).then_inc(loaded, 16)
                    sp.dma_start(gain[:, 1, :], w["L3_ffn_ln_b"]).then_inc(loaded, 16)

                @block.tensor
                def _(pe):
                    pe.wait_ge(loaded, 16 * 8)
                    for n in range(2):
                        ins = nc.tensor.transpose(ps[0:D, 0, E * n:E * n + E], gain[:, n, :], k.ident[0:E, 0:E])
                    ins.then_inc(made, 1)
                    pe.wait_ge(ready, 1)
                    for e in range(E):
                        ins = nc.tensor.matmul(ps[0:A1, 1 + e // 2, (e % 2) * F:(e % 2 + 1) * F], shift_t[:, e, :], w1[0:D, e, :], start=True, stop=True)
                    ins.then_inc(made, 1)

                @block.vector
                def _(dve):
                    vec = nc.vector
                    link = Link(dve, step)
                    link(vec.memset(wr[D:P, :], 0.0))
                    link(vec.memset(w1[D:P], 0.0))
                    vec.sem_inc(zeroed, 1)
                    link(vec.memset(shift_t[:], 0.0))
                    dve.wait_ge(made, 1)
                    link(vec.tensor_copy(gain_t[:], ps[0:D, 0, 0:E]))
                    link(vec.tensor_copy(shift_t[:, :, D], ps[0:D, 0, E:2 * E]))
                    vec.sem_inc(ready, 1)
                    dve.wait_ge(made, 2)
                    row = w1[D:A1].rearrange("p (a z) f -> p a z f", z=2)
                    link(vec.tensor_tensor(row, row, ps[D:A1, 1:5, :].rearrange("p a (z f) -> p a z f", z=2), ALU.add))
                    for e in range(E):
                        link(vec.tensor_scalar(w1[0:D, e, :], w1[0:D, e, :], gain_t[:, e:e + 1], None, ALU.mult))
            turn_all(k, "l3fr", xt, wr, logits)
            route(k, "l3f", logits, share)
        inner_center(k)
        turn_all(k, "l3fx", xt)
        mix_experts(k, "l3f", xt, share, w1, w2, w["L3_ffn_b2"], False)


def inner_center(k):
    nc = k.nc
    with Scope(nc, "inner") as s:
        sq = s.sb("sq", [P, SEQS, D])
        mean = s.sb("mean", [P, SEQS, 1])
        std = s.sb("std", [P, SEQS, 1])
        eps = s.sb("eps", [P, 1])
        step, summed, rooted = s.sem("step"), s.sem("summed"), s.sem("rooted")
        block = s.block()

        @block.scalar
        def _(act):
            act.wait_ge(summed, 1)
            nc.scalar.activation(std[:], mean[:], ACT.Sqrt, bias=eps[:, 0:1], scale=1.0 / D).then_inc(rooted, 1)

        @block.vector
        def _(dve):
            vec = nc.vector
            link = Link(dve, step)
            full = [P, SEQS, D]
            link(vec.memset(eps[:], LN_EPS))
            link(vec.tensor_tensor(k.xc[:], k.xc[:], bc(k.rstd[:], full), ALU.mult))
            link(vec.tensor_reduce(mean[:, :, 0], k.xc[:], AX, ALU.add))
            link(vec.tensor_scalar(mean[:], mean[:], 1.0 / D, None, ALU.mult))
            link(vec.tensor_tensor(k.xc[:], k.xc[:], bc(mean[:], full), ALU.subtract))
            link(vec.tensor_tensor(sq[:], k.xc[:], k.xc[:], ALU.mult))
            vec.tensor_reduce(mean[:, :, 0], sq[:], AX, ALU.add).then_inc(summed, 1)
            dve.wait_ge(rooted, 1)
            link(vec.reciprocal(k.rstd[:], std[:]))


def stage_store(k):
    nc = k.nc
    with Scope(nc, "store") as s:
        stored = s.sem("stored")
        block = s.block()

        @block.sync
        def _(sp):
            sp.dma_start(k.out.rearrange("b n d -> n b d"), k.h[:]).then_inc(stored, 16)
            sp.wait_ge(stored, 16)


def build(nc, w, out):
    k = Core(nc, w, out)
    with ExitStack() as ctx:
        k.h = ctx.enter_context(nc.sbuf_tensor("h", [P, SEQS, D], F32))
        k.xc = ctx.enter_context(nc.sbuf_tensor("xc", [P, SEQS, D], F32))
        k.rstd = ctx.enter_context(nc.sbuf_tensor("rstd", [P, SEQS, 1], F32))
        k.ident = ctx.enter_context(nc.sbuf_tensor("ident", [P, P], F32))
        k.rows_landed = [ctx.enter_context(nc.semaphore(f"rows_landed{n}")) for n in range(3)]
        k.attr_fetched = ctx.enter_context(nc.semaphore("attr_fetched"))
        k.chunks_fetched = ctx.enter_context(nc.semaphore("chunks_fetched"))
        Scope.psum = ctx.enter_context(nc.psum_tensor("psum", [P, 8 * BANK], F32))
        stage_constants(k)
        for name, run, normed in TOWER:
            if normed:
                stage_center(k, name)
            run(k)
        stage_store(k)


TOWER = [("tok", stage_tokens, False), ("L0a", stage_l0_attn, True), ("L0f", stage_l0_ffn, True), ("L1a", stage_l1_attn, True), ("L1f", stage_l1_ffn, True), ("L2a", stage_l2_attn, True), ("L2f", stage_l2_ffn, True), ("L3a", stage_l3_attn, True), ("L3f", stage_l3_ffn, True)]


def kernel(**inputs):
    import numpy as _np
    import concourse.bacc as _bacc
    from concourse import mybir as _mybir
    from concourse.bass_utils import run_bass_kernel_spmd as _run

    nc = _bacc.Bacc("TRN2", target_bir_lowering=False, num_devices=1)
    arrays, w = {}, {}
    for name, value in inputs.items():
        a = _np.ascontiguousarray(value)
        arrays[f"in_{name}"] = a
        w[name] = nc.dram_tensor(f"in_{name}", a.shape, _mybir.dt.from_np(a.dtype), kind="ExternalInput").ap()
    out = nc.dram_tensor("out", (SEQS, N, D), F32, kind="ExternalOutput").ap()
    build(nc, w, out)
    r = _run(nc, [arrays], core_ids=[0])
    return r.results[0]["out"]
```

```python
from contextlib import ExitStack

import concourse.bass as bass
from concourse import mybir

F32 = mybir.dt.float32
BF16 = mybir.dt.bfloat16
I32 = mybir.dt.int32
U32 = mybir.dt.uint32
ALU = mybir.AluOpType
ACT = mybir.ActivationFunctionType
AX = mybir.AxisListType.X

P = 128
SEQS = 64
N = 128
D = 64
GROUP = 4
GROUPS = SEQS // GROUP
TOK = GROUP * N
LN_EPS = 1e-5
BANK = 512
MASKED = -1e30


class Core:

    def __init__(self, nc, w, out):
        self.nc, self.w, self.out = nc, w, out


class Scope:

    psum = None
    next_bank = 0

    def __init__(self, nc, stage):
        self.nc, self.stage, self.ctx = nc, stage, ExitStack()
        self.first_bank, self.sems = Scope.next_bank, []

    def __enter__(self):
        return self

    def __exit__(self, *a):
        Scope.next_bank = self.first_bank
        self.ctx.close()
        if self.sems:
            self.nc.clear_and_free_semaphores(self.sems)
            self.nc.all_engine_barrier()

    def sb(self, name, shape, dt=F32):
        return self.ctx.enter_context(self.nc.sbuf_tensor(f"{self.stage}_{name}", shape, dt))

    def ps(self, name, shape, dt=F32):
        size = 1
        for n in shape[1:]:
            size *= n
        words = size if dt == F32 else size // 2
        start = Scope.next_bank * BANK
        Scope.next_bank += -(-words // BANK)
        assert Scope.next_bank <= 8, name
        flat = Scope.psum[0:shape[0], start:start + words]
        if dt != F32:
            flat = flat.bitcast(dt)
        axes = "abcd"[:len(shape) - 1]
        return flat.rearrange(f"p ({' '.join(axes)}) -> p {' '.join(axes)}", **dict(zip(axes, shape[1:])))

    def sem(self, name):
        self.sems.append(self.nc.alloc_semaphore(name=f"{self.stage}_{name}"))
        return self.sems[-1]

    def block(self):
        return self.ctx.enter_context(self.nc.Block())


class Link:

    def __init__(self, eng, sem, base=0, per=None):
        self.eng, self.sem, self.base, self.n, self.per = eng, sem, base, 0, per

    def __call__(self, ins):
        ins.then_inc(self.sem, 1)
        self.n += 1
        self.eng.wait_ge(self.sem, self.base + self.n)

    def close(self):
        assert self.per is None or self.n == self.per, (self.n, self.per)


def bc(ap, shape):
    return ap.to_broadcast(shape)


def stage_constants(k):
    nc = k.nc
    with Scope(nc, "const") as s:
        made = s.sem("ident_step")
        block = s.block()

        @block.gpsimd
        def _(pool):
            link = Link(pool, made)
            link(nc.gpsimd.memset(k.ident[:], 0.0))
            link(nc.gpsimd.affine_select(out=k.ident[:], in_=k.ident[:], compare_op=ALU.not_equal, fill=1.0,
                                         base=0, pattern=[[-1, P]], channel_multiplier=1))


def stage_tokens(k):
    nc = k.nc
    with Scope(nc, "tok") as s:
        index = s.sb("index", [P, 3, SEQS], U32)
        rows = [s.sb(f"rows{n}", [P, SEQS, D]) for n in range(2)]
        keep = s.sb("keep", [P, 3])
        dest = [k.h, rows[0], rows[1]]
        hash_tokens(k, index, keep)

        def gather():
            for g in range(3):
                for b in range(SEQS):
                    nc.gpsimd.indirect_dma_start(
                        dest[g][:, b, :], None, k.w[f"L0_tok_emb_{g + 2}"],
                        bass.IndirectOffsetOnAxis(index[:, g, b:b + 1], 0)).then_inc(k.rows_landed[g], 16)

        stage_edge_cells(k, gather)
        step = s.sem("step")
        block = s.block()

        @block.vector
        def _(dve):
            link = Link(dve, step)
            for g in range(3):
                dve.wait_ge(k.rows_landed[g], 16 * SEQS)
                if g == 0:
                    link(nc.vector.tensor_scalar(k.h[:], k.h[:], keep[:, 0:1], None, ALU.mult))
                else:
                    link(nc.vector.scalar_tensor_tensor(out=k.h[:], in0=dest[g][:], scalar=keep[:, g:g + 1],
                                                        in1=k.h[:], op0=ALU.mult, op1=ALU.add))


def hash_tokens(k, index, keep):
    nc, w = k.nc, k.w
    PRIME, VOCAB = 31, 125000
    with Scope(nc, "hash") as s:
        ids_i = s.sb("ids_i", [SEQS, N], I32)
        ids = s.sb("ids", [SEQS, N + 3])
        acc = s.sb("acc", [SEQS, 3, N])
        over = s.sb("over", [SEQS, 3, N])
        ones = s.sb("ones", [P, 3])
        turned = s.ps("turned", [P, 3, SEQS])
        loaded, step, hashed, transposed, one = (s.sem(n) for n in "loaded step hashed transposed one".split())
        block = s.block()

        @block.sync
        def _(sp):
            sp.dma_start(ids_i[:], w["x"]).then_inc(loaded, 16)

        @block.gpsimd
        def _(pool):
            link = Link(pool, one)
            link(nc.gpsimd.memset(ones[:], 0.25))
            link(nc.gpsimd.affine_select(out=keep[:], in_=ones[:], compare_op=ALU.is_ge, fill=0.0, base=-1,
                                         pattern=[[-1, 3]], channel_multiplier=1))

        @block.vector
        def _(dve):
            link = Link(dve, step)
            link(nc.vector.memset(ids[:], 0.0))
            dve.wait_ge(loaded, 16)
            link(nc.vector.tensor_copy(ids[:, 3:], ids_i[:]))
            for g in range(3):
                link(nc.vector.tensor_copy(acc[:, g, :], ids[:, 3:]))
                for j in range(1, g + 2):
                    link(nc.vector.scalar_tensor_tensor(out=acc[:, g, :], in0=ids[:, 3 - j:3 - j + N],
                                                        scalar=float(PRIME ** j % VOCAB), in1=acc[:, g, :],
                                                        op0=ALU.mult, op1=ALU.add))
            for bit in range(7, -1, -1):
                m = float(VOCAB << bit)
                link(nc.vector.tensor_scalar(over[:], acc[:], m, m, ALU.is_ge, ALU.mult))
                link(nc.vector.tensor_tensor(acc[:], acc[:], over[:], ALU.subtract))
            nc.vector.sem_inc(hashed, 1)
            dve.wait_ge(transposed, 1)
            link(nc.vector.tensor_copy(index[:], turned[:]))

        @block.tensor
        def _(pe):
            pe.wait_ge(hashed, 1)
            for g in range(3):
                ins = nc.tensor.transpose(turned[:, g, :], acc[:, g, :], k.ident[0:SEQS, 0:SEQS])
            ins.then_inc(transposed, 1)


def center_parts(k, s):
    nc = k.nc
    sq = s.sb("sq", [P, SEQS, D])
    mean = s.sb("mean", [P, SEQS, 1])
    std = s.sb("std", [P, SEQS, 1])
    eps = s.sb("eps", [P, 1])
    step, summed, rooted = s.sem("center_step"), s.sem("summed"), s.sem("rooted")
    centered, squared = s.sem("centered"), s.sem("squared")
    HALF = SEQS // 2

    def on_vector(dve):
        link = Link(dve, step)
        link(nc.vector.memset(eps[:], LN_EPS))
        link(nc.vector.tensor_reduce(mean[:, :, 0], k.h[:], AX, ALU.add))
        link(nc.vector.tensor_scalar(mean[:], mean[:], 1.0 / D, None, ALU.mult))
        for n in range(2):
            r = slice(HALF * n, HALF * n + HALF)
            nc.vector.tensor_tensor(k.xc[:, r], k.h[:, r], bc(mean[:, r], [P, HALF, D]), ALU.subtract).then_inc(centered, 1)
        for n in range(2):
            r = slice(HALF * n, HALF * n + HALF)
            dve.wait_ge(squared, n + 1)
            ins = nc.vector.tensor_reduce(mean[:, r, 0], sq[:, r], AX, ALU.add)
        ins.then_inc(summed, 1)
        dve.wait_ge(rooted, 1)
        link(nc.vector.reciprocal(k.rstd[:], std[:]))

    def on_scalar(act):
        for n in range(2):
            r = slice(HALF * n, HALF * n + HALF)
            act.wait_ge(centered, n + 1)
            nc.scalar.activation(sq[:, r], k.xc[:, r], ACT.Square).then_inc(squared, 1)
        act.wait_ge(summed, 1)
        nc.scalar.activation(std[:], mean[:], ACT.Sqrt, bias=eps[:, 0:1], scale=1.0 / D).then_inc(rooted, 1)

    return on_vector, on_scalar


def stage_center(k, tag):
    with Scope(k.nc, f"ln{tag}") as s:
        on_vector, on_scalar = center_parts(k, s)
        block = s.block()

        @block.scalar
        def _(act):
            on_scalar(act)

        @block.vector
        def _(dve):
            on_vector(dve)


def front_dve(k, dve, xs, t, normed):
    g = bass.ds(GROUP * t, GROUP)
    return k.nc.vector.tensor_tensor(xs[:, :, 0:D], k.xc[:, g, :], bc(k.rstd[:, g, :], [P, GROUP, D]), ALU.mult).then_inc(normed, 1)


def last_edge_parts(k, s):
    nc, w = k.nc, k.w
    F = w["L0_attn_edge_index"].shape[1] // P
    CH = 32
    assert F <= 256 and N <= 255
    tgt_i = s.sb("tgt_i", [P, F], I32)
    tgt = s.sb("tgt", [P, F])
    tgt_c = s.sb("tgt_c", [P, 2, 1, F], BF16)
    place_f = s.sb("place_f", [P, F])
    place = s.sb("edge_place", [P, 1, F], BF16)
    token_f = s.sb("token_f", [P, CH, 1])
    token = s.sb("token", [P, CH, F], BF16)
    hit = s.sb("hit", [P, CH, F], BF16)
    base = s.sb("base", [P, 1])
    before = s.sb("before", [P, N])
    loaded, counted, step = s.sem("target_loaded"), s.sem("target_counted"), s.sem("target_step")

    def on_sync(sp):
        sp.dma_start(tgt_i[:], w["L0_attn_edge_index"][1].rearrange("(p f) -> p f", p=P)).then_inc(loaded, 16)

    def on_gpsimd(pool):
        imp = dict(allow_small_or_imprecise_dtypes=True)
        nc.gpsimd.iota(place_f[:], [[1, F]], 1, 0, **imp).then_inc(counted, 1)
        nc.gpsimd.iota(token_f[:, :, 0], [[1, CH]], 0, 0, **imp).then_inc(counted, 1)
        nc.gpsimd.iota(base[:], [[0, 1]], 0, F, **imp).then_inc(counted, 1)

    def on_vector(dve):
        vec = nc.vector
        link = Link(dve, step)
        dve.wait_ge(loaded, 16)
        dve.wait_ge(counted, 3)
        link(vec.tensor_copy(tgt[:], tgt_i[:]))
        link(vec.tensor_scalar(tgt[:], tgt[:], 255.0, None, ALU.min))
        link(vec.tensor_copy(place[:, 0], place_f[:]))
        link(vec.tensor_copy(token[:], bc(token_f[:], [P, CH, F])))
        for n, c in enumerate(range(0, N, CH)):
            link(vec.tensor_scalar(tgt_c[:, n % 2, 0], tgt[:], float(-c), None, ALU.add))
            link(vec.tensor_tensor(hit[:], bc(tgt_c[:, n % 2], [P, CH, F]), token[:], ALU.is_equal))
            link(vec.tensor_tensor(hit[:], hit[:], bc(place[:], [P, CH, F]), ALU.mult))
            link(vec.tensor_reduce(k.last_edge[:, c:c + CH], hit[:], AX, ALU.max))
        link(vec.tensor_scalar(before[:], k.last_edge[:], 1.0, base[:, 0:1], ALU.min, ALU.mult))
        link(vec.tensor_tensor(k.last_edge[:], k.last_edge[:], before[:], ALU.add))

    return on_sync, on_gpsimd, on_vector


def stage_edge_bias(k):
    nc, w = k.nc, k.w
    HEADS = 8
    with Scope(nc, "ebias") as s:
        last = s.sb("last", [P, 1])
        found = s.sb("found", [P, 1])
        row = s.sb("row", [P, 1])
        row_u = s.sb("row_u", [P, 1], U32)
        attr = s.sb("attr", [P, 3])
        we = s.sb("we", [P, 3, HEADS])
        be = s.sb("be", [P, HEADS])
        eb = s.sb("eb", [P, HEADS])
        spread = s.sb("spread", [P, 2, 4, 32])
        turned = s.ps("turned", [P, N])
        placed = s.ps("placed", [P, 2, N])
        loaded, step = s.sem("loaded"), s.sem("step")
        transposed, rowed, fetched, spreaded = s.sem("transposed"), s.sem("rowed"), k.attr_fetched, s.sem("spreaded")
        center_vector, center_scalar = center_parts(k, s)
        block = s.block()

        @block.scalar
        def _(act):
            center_scalar(act)

        @block.sync
        def _(sp):
            sp.dma_start(we[:], w["L0_attn_We"].partition_broadcast(P)).then_inc(loaded, 16)
            sp.dma_start(be[:], w["L0_attn_be"].partition_broadcast(P)).then_inc(loaded, 16)

        @block.gpsimd
        def _(pool):
            pool.wait_ge(rowed, 1)
            nc.gpsimd.indirect_dma_start(attr[:], None, w["L0_attn_edge_attr"],
                                         bass.IndirectOffsetOnAxis(row_u[:, 0:1], 0)).then_inc(fetched, 16)

        @block.vector
        def _(dve):
            center_vector(dve)
            link = Link(dve, step)
            link(nc.vector.memset(spread[:], 0.0))
            dve.wait_ge(loaded, 32)
            dve.wait_ge(transposed, 1)
            link(nc.vector.tensor_reduce(last[:], turned[:], AX, ALU.max))
            link(nc.vector.tensor_scalar(found[:], last[:], 1.0, None, ALU.is_ge))
            link(nc.vector.tensor_tensor(row[:], last[:], found[:], ALU.subtract))
            nc.vector.tensor_copy(row_u[:], row[:]).then_inc(rowed, 1)
            dve.wait_ge(fetched, 16)
            link(nc.vector.tensor_copy(eb[:], be[:]))
            for j in range(3):
                link(nc.vector.scalar_tensor_tensor(out=eb[:], in0=we[:, j, :], scalar=attr[:, j:j + 1], in1=eb[:],
                                                    op0=ALU.mult, op1=ALU.add))
            nc.vector.tensor_scalar(spread[:, :, :, 8], eb[:].rearrange("p (g h) -> p g h", g=2), found[:, 0:1], None,
                                    ALU.mult).then_inc(spreaded, 1)
            dve.wait_ge(transposed, 2)
            link(nc.vector.tensor_copy(k.colbias[:], placed[:]))

        @block.tensor
        def _(pe):
            nc.tensor.transpose(turned[:], k.last_edge[:], k.ident[:]).then_inc(transposed, 1)
            pe.wait_ge(spreaded, 1)
            for g in range(2):
                ins = nc.tensor.transpose(placed[:, g, :], spread[:, g].rearrange("p h c -> p (h c)"), k.ident[:])
            ins.then_inc(transposed, 1)


def in_turn(eng, prelude, body, older=False):
    more = (lambda there: (there,)) if older else (lambda there: ())
    prelude()
    body(0, 0, True, False, True, *more(False))
    if older:
        body(1, 1, True, True, True, False)
        with eng.Fori(1, (GROUPS - 2) // 2) as i:
            body(2 * i, 0, True, True, True, True)
            body(2 * i + 1, 1, True, True, True, True)
        body(GROUPS - 2, 0, True, True, True, True)
    else:
        with eng.Fori(0, (GROUPS - 2) // 2) as i:
            body(2 * i + 1, 1, True, True, True)
            body(2 * i + 2, 0, True, True, True)
    body(GROUPS - 1, 1, True, True, False, *more(True))
    body(GROUPS, 0, False, True, False, *more(True))
    if older:
        body(GROUPS + 1, 1, False, False, False, True)


def stage_l0_attn(k):
    nc, w = k.nc, k.w
    HEADS, HD, HP = 8, 8, 32
    UNITS = GROUP * 2
    with Scope(nc, "l0a") as s:
        wq = s.sb("wq", [P, 2, 4, HP])
        wk = s.sb("wk", [P, 2, 4, HP])
        wv = s.sb("wv", [P, D])
        wo = s.sb("wo", [P, D])
        k.colbias = s.sb("colbias", [P, 2, N])
        stage_edge_bias(k)
        compact = s.sb("compact", [P, 4, HD + 1])
        xs = s.sb("xs", [P, GROUP, P])
        xt = s.sb("xt", [P, TOK])
        q = s.sb("q", [P, 2, 2, TOK])
        keys = s.sb("keys", [P, 2, 2, GROUP, 4, N])
        v = s.sb("v", [P, 2, GROUP, HEADS, HP])
        top = s.sb("top", [P, 4, 4])
        probs = s.sb("probs", [P, 4, 4, N])
        probs_t = s.sb("probs_t", [P, 2, 4, N])
        ot = s.sb("ot", [P, 2, TOK])
        rden = s.sb("rden", [P, GROUP, HEADS, 1])
        mixed = s.sb("mixed", [P, GROUP, P])
        mt = s.sb("mt", [P, TOK])
        ps = s.ps("ps", [P, 8, 512])
        SC, TU, OT, X, Y = 0, 2, 4, 6, 7
        names = ("loaded step ready normed xt_made xt_ready projected q_ready k_ready v_ready scored topped exped turned "
                 "turned_ready valued ot_ready back inverted mixed_ready mt_made mt_ready outed added apart").split()
        S = {n: s.sem(n) for n in names}
        loaded, step, ready = S["loaded"], S["step"], S["ready"]
        block = s.block()

        def heads(flat):
            return flat.rearrange("p (h n) -> p h n", h=4)

        def seqs(flat):
            return flat.rearrange("p (b n) -> p b n", b=GROUP)

        @block.sync
        def _(sp):
            sp.wait_ge(ready, 1)
            for g in range(2):
                for wt, n in ((wq, "q"), (wk, "k")):
                    sp.dma_start(wt[0:D, g, :, 0:HD],
                                 w[f"L0_attn_W{n}"].rearrange("i (g h c) -> g i h c", g=2, c=HD)[g]).then_inc(loaded, 16)
                    sp.dma_start(wt[D:D + 1, g, :, 0:HD],
                                 w[f"L0_attn_b{n}"].rearrange("(o g h c) -> g o h c", o=1, g=2, c=HD)[g]).then_inc(loaded, 16)
            for wt, n in ((wv, "v"), (wo, "o")):
                sp.dma_start(wt[0:D, :], w[f"L0_attn_W{n}"]).then_inc(loaded, 16)
                sp.dma_start(wt[D:D + 1, :], w[f"L0_attn_b{n}"].rearrange("(o d) -> o d", o=1)).then_inc(loaded, 16)

        LOADED = 16 * 12

        @block.gpsimd
        def _(pool):
            nc.gpsimd.memset(v[:], 0.0).then_inc(S["v_ready"], 1)
            pool.wait_ge(S["v_ready"], 1)
            nc.gpsimd.memset(v[:, :, :, :, HD:HD + 1], 1.0).then_inc(S["v_ready"], 1)

        @block.vector
        def _(dve):
            vec = nc.vector
            link = Link(dve, step)
            vec.memset(wo[:], 0.0)
            vec.memset(wv[:], 0.0)
            vec.memset(wq[:], 0.0)
            link(vec.memset(wk[:], 0.0))
            vec.sem_inc(ready, 1)
            vec.memset(xs[:], 0.0)
            vec.memset(mixed[:], 0.0)
            link(vec.memset(keys[:], 0.0))
            link(vec.memset(xs[:, :, D:D + 1], 1.0))
            link(vec.memset(mixed[:, :, D:D + 1], 1.0))
            for h in range(4):
                r = slice(HP * h, HP * h + HP)
                for par in range(2):
                    for g in range(2):
                        ins = vec.tensor_copy(keys[r, par, g, :, h, :], bc(k.colbias[r, g:g + 1, :], [HP, GROUP, N]))
            link(vec.tensor_copy(compact[:], k.ident[:].rearrange("p (h c) -> p h c", h=4)[:, :, 0:HD + 1]))
            dve.wait_ge(loaded, LOADED)
            link(vec.tensor_scalar(wq[:], wq[:], HD ** -0.5, None, ALU.mult))
            link(vec.memset(wq[D:D + 1, :, :, HD:HD + 1], 1.0))
            vec.sem_inc(ready, 1)

            def front(t):
                front_dve(k, dve, xs[:], t, S["normed"])

            def keep_keys(t, par, g):
                dve.wait_ge(S["projected"], 5 * t + 3 + g)
                for h in range(2):
                    r = slice(HP * h, HP * h + HD)
                    ins = vec.tensor_copy(keys[r, par, g, :, h, :], seqs(ps[r, X, :]))
                ins.then_inc(S["k_ready"], 1)

            def prelude():
                front(0)
                keep_keys(0, 0, 0)
                keep_keys(0, 0, 1)

            def maximum(t, u):
                dve.wait_ge(S["scored"], UNITS * t + u + 1)
                vec.tensor_reduce(top[:, u % 4], heads(ps[:, SC + u % 2, :]), AX, ALU.max, negate=True).then_inc(S["topped"], 1)

            def keep_turned(t, u):
                dve.wait_ge(S["turned"], UNITS * t + u + 1)
                if not (isinstance(t, int) and t == 0 and u < 2):
                    dve.wait_ge(S["valued"], UNITS * t + u - 1)
                vec.tensor_copy(probs_t[:, u % 2], heads(ps[:, TU + u % 2, :])).then_inc(S["turned_ready"], 1)

            def normalize(t):
                dve.wait_ge(S["back"], t + 1)
                o = ps[:, Y, 0:GROUP * HEADS * (HD + 1)].rearrange("p (b h c) -> p b h c", b=GROUP, h=HEADS)
                vec.reciprocal(rden[:], o[:, :, :, HD:HD + 1]).then_inc(S["inverted"], 1)
                dve.wait_ge(S["inverted"], t + 1)
                vec.tensor_tensor(mixed[:, :, 0:D].rearrange("p b (h c) -> p b h c", h=HEADS), o[:, :, :, 0:HD],
                                  bc(rden[:], [P, GROUP, HEADS, HD]), ALU.mult).then_inc(S["mixed_ready"], 1)

            def add(t):
                dve.wait_ge(S["outed"], t + 1)
                g = bass.ds(GROUP * t, GROUP)
                vec.tensor_tensor(k.h[:, g, :], k.h[:, g, :], ps[:, Y, 0:GROUP * D].rearrange("p (b d) -> p b d", b=GROUP),
                                  ALU.add).then_inc(S["added"], 1)

            def body(t, par, cur, prev, nxt):
                for u in range(UNITS):
                    if cur:
                        maximum(t, u)
                    if u >= 2 and cur:
                        keep_turned(t, u - 2)
                    if u < 2 and prev:
                        keep_turned(t - 1, UNITS + u - 2)
                    if u == 0 and nxt:
                        front(t + 1)
                    if u in (4, 5) and nxt:
                        keep_keys(t + 1, 1 - par, u - 4)
                    if u == 3 and prev:
                        normalize(t - 1)
                    if u == 7 and prev:
                        add(t - 1)

            in_turn(dve, prelude, body)

        @block.scalar
        def _(act):
            act.wait_ge(S["v_ready"], 2)

            def keep_x(t):
                act.wait_ge(S["xt_made"], t + 1)
                nc.scalar.copy(xt[:], ps[:, X, :]).then_inc(S["xt_ready"], 1)

            def keep_q(t, par, g):
                act.wait_ge(S["projected"], 5 * t + g + 1)
                nc.scalar.copy(q[:, par, g, :], ps[:, X, :]).then_inc(S["q_ready"], 1)

            def keep_keys(t, par, g):
                act.wait_ge(S["projected"], 5 * t + 3 + g)
                for h in range(2, 4):
                    r = slice(HP * h, HP * h + HD)
                    ins = nc.scalar.copy(keys[r, par, g, :, h, :], seqs(ps[r, X, :]))
                ins.then_inc(S["k_ready"], 1)

            def keep_v(t, par):
                act.wait_ge(S["projected"], 5 * t + 5)
                nc.scalar.copy(v[:, par, :, :, 0:HD], ps[:, X, 0:GROUP * D].rearrange("p (b h c) -> p b h c", b=GROUP, c=HD)).then_inc(S["v_ready"], 1)

            def prelude():
                keep_x(0)
                keep_q(0, 0, 0)
                keep_q(0, 0, 1)
                keep_keys(0, 0, 0)
                keep_keys(0, 0, 1)
                keep_v(0, 0)

            def exponential(t, u):
                act.wait_ge(S["topped"], UNITS * t + u + 1)
                if not (isinstance(t, int) and t == 0 and u < 4):
                    act.wait_ge(S["turned"], UNITS * t + u - 3)
                for h in range(4):
                    ins = nc.scalar.activation(probs[:, u % 4, h], ps[:, SC + u % 2, h * N:(h + 1) * N], ACT.Exp, bias=top[:, u % 4, h:h + 1])
                ins.then_inc(S["exped"], 1)

            def keep_output(t, g):
                act.wait_ge(S["valued"], UNITS * t + 4 * g + 4)
                nc.scalar.copy(ot[:, g], ps[:, OT + g, :]).then_inc(S["ot_ready"], 1)

            def body(t, par, cur, prev, nxt):
                for u in range(UNITS):
                    if cur:
                        exponential(t, u)
                    if u == 1 and nxt:
                        keep_x(t + 1)
                    if u in (2, 3) and nxt:
                        keep_q(t + 1, 1 - par, u - 2)
                    if u == 2 and prev:
                        keep_output(t - 1, 1)
                    if u in (4, 5) and nxt:
                        keep_keys(t + 1, 1 - par, u - 4)
                    if u == 6 and nxt:
                        keep_v(t + 1, 1 - par)
                    if u == 6 and cur:
                        keep_output(t, 0)
                    if u == 5 and prev:
                        act.wait_ge(S["mt_made"], t)
                        nc.scalar.copy(mt[:], ps[:, Y, :]).then_inc(S["mt_ready"], 1)

            in_turn(act, prelude, body)

        @block.tensor
        def _(pe):
            mm = nc.tensor.matmul

            def turn_x(t):
                pe.wait_ge(S["normed"], t + 1)
                if not (isinstance(t, int) and t == 0):
                    pe.wait_ge(S["v_ready"], t + 2)
                for b in range(GROUP):
                    ins = nc.tensor.transpose(ps[:, X, b * N:(b + 1) * N], xs[:, b, :], k.ident[:])
                ins.then_inc(S["xt_made"], 1)

            def project(t, n):
                if n == 0:
                    pe.wait_ge(S["xt_ready"], t + 1)
                elif n <= 2:
                    pe.wait_ge(S["q_ready"], 2 * t + n)
                else:
                    pe.wait_ge(S["k_ready"], 4 * t + 2 * (n - 2))
                if n < 4:
                    wt = (wq, wk)[n // 2][:, n % 2].rearrange("p h c -> p (h c)")
                    ins = mm(ps[:, X, :], wt, xt[:], start=True, stop=True)
                else:
                    for b in range(GROUP):
                        ins = mm(ps[:, X, b * D:(b + 1) * D], xt[:, b * N:(b + 1) * N], wv[:], start=True, stop=True)
                ins.then_inc(S["projected"], 1)

            def prelude():
                pe.wait_ge(ready, 2)
                turn_x(0)
                for n in range(5):
                    project(0, n)

            def scores(t, par, u):
                g, b = u // 4, u % 4
                if u == 0:
                    pe.wait_ge(S["q_ready"], 2 * t + 2)
                    pe.wait_ge(S["k_ready"], 4 * t + 4)
                if not (isinstance(t, int) and t == 0 and u < 2):
                    pe.wait_ge(S["exped"], UNITS * t + u - 1)
                mm(ps[:, SC + u % 2, :], q[:, par, g, b * N:(b + 1) * N], keys[:, par, g, b].rearrange("p h n -> p (h n)"),
                   start=True, stop=True).then_inc(S["scored"], 1)

            def turn(t, u):
                pe.wait_ge(S["exped"], UNITS * t + u + 1)
                if not (isinstance(t, int) and t == 0 and u < 2):
                    pe.wait_ge(S["turned_ready"], UNITS * t + u - 1)
                for h in range(4):
                    ins = nc.tensor.transpose(ps[:, TU + u % 2, h * N:(h + 1) * N], probs[:, u % 4, h], k.ident[:])
                ins.then_inc(S["turned"], 1)

            def values(t, par, u):
                g, b = u // 4, u % 4
                pe.wait_ge(S["turned_ready"], UNITS * t + u + 1)
                if u == 0:
                    pe.wait_ge(S["v_ready"], t + 3)
                if b == 0 and not (isinstance(t, int) and t == 0):
                    pe.wait_ge(S["ot_ready"], 2 * t + g - 1)
                nc.tensor.sem_inc(S["apart"], 1)
                for h in range(4):
                    ins = mm(ps[HP * h:HP * h + HP, OT + g, b * N:(b + 1) * N], v[:, par, b, 4 * g + h, :], probs_t[:, u % 2, h],
                             start=True, stop=True, tile_position=(0, HP * h))
                ins.then_inc(S["valued"], 1)

            def turn_back(t):
                pe.wait_ge(S["ot_ready"], 2 * t + 2)
                if not (isinstance(t, int) and t == 0):
                    pe.wait_ge(S["added"], t)
                for b in range(GROUP):
                    for g in range(2):
                        c = (2 * b + g) * 4 * (HD + 1)
                        ins = mm(ps[:, Y, c:c + 4 * (HD + 1)], ot[:, g, b * N:(b + 1) * N], compact[:].rearrange("p h c -> p (h c)"),
                                 start=True, stop=True)
                ins.then_inc(S["back"], 1)

            def turn_mixed(t):
                pe.wait_ge(S["mixed_ready"], t + 1)
                for b in range(GROUP):
                    ins = nc.tensor.transpose(ps[:, Y, b * N:(b + 1) * N], mixed[:, b, :], k.ident[:])
                ins.then_inc(S["mt_made"], 1)

            def outputs(t):
                pe.wait_ge(S["mt_ready"], t + 1)
                for b in range(GROUP):
                    ins = mm(ps[:, Y, b * D:(b + 1) * D], mt[:, b * N:(b + 1) * N], wo[:], start=True, stop=True)
                ins.then_inc(S["outed"], 1)

            def body(t, par, cur, prev, nxt):
                for u in range(UNITS):
                    if cur:
                        scores(t, par, u)
                    if u >= 2 and cur:
                        turn(t, u - 2)
                    if u < 2 and prev:
                        turn(t - 1, UNITS + u - 2)
                    if u >= 3 and cur:
                        values(t, par, u - 3)
                    if u < 3 and prev:
                        values(t - 1, 1 - par, UNITS + u - 3)
                    if u == 1 and nxt:
                        turn_x(t + 1)
                    if 2 <= u <= 6 and nxt:
                        project(t + 1, u - 2)
                    if u == 3 and prev:
                        turn_back(t - 1)
                    if u == 5 and prev:
                        turn_mixed(t - 1)
                    if u == 7 and prev:
                        outputs(t - 1)

            in_turn(pe, prelude, body)


def stage_l0_ffn(k):
    nc, w = k.nc, k.w
    H, G, A1 = 8, 64, D + 1
    PAIRS = H // 2
    with Scope(nc, "l0f") as s:
        slice_map = s.sb("slice_map", [P, H, G])
        pair_map = s.sb("pair_map", [P, H, P])
        value_map = s.sb("value_map", [P, H, D])
        fold_l0_ffn(k, slice_map, pair_map, value_map)
        xs = s.sb("xs", [P, 2, GROUP, P])
        xt = s.sb("xt", [P, 2, TOK])
        sw = s.sb("sw", [P, GROUP, H, G])
        sw_t = s.sb("sw_t", [P, 2 * GROUP, PAIRS, N])
        top = s.sb("top", [P, GROUP, H, 1])
        den = s.sb("den", [P, GROUP, H, 1])
        rden = s.sb("rden", [P, GROUP, H, 1])
        znorm = s.sb("znorm", [P, GROUP, PAIRS, 1])
        z = s.sb("z", [P, GROUP, PAIRS, P])
        z_t = s.sb("z_t", [P, GROUP, H, G])
        za = s.sb("za", [P, GROUP, H, G])
        vals = s.sb("vals", [P, GROUP, 2, 2, D])
        att = s.sb("att", [P, GROUP, PAIRS, G])
        atop = s.sb("atop", [P, GROUP, PAIRS, 1])
        aden = s.sb("aden", [P, GROUP, PAIRS, 1])
        att_t = s.sb("att_t", [P, GROUP, 2, P])
        y = s.sb("y", [P, GROUP, PAIRS, D])
        ps = s.ps("ps", [P, 8, 512])
        names = ("step normed xt_made xt_ready logit shifted exped weighted swt_made swt_ready z_made z_ready zt_made zt_ready "
                 "za_made za_ready val_made val_ready sc_made sc_topped sc_exped att_made att_t_ready y_made y_ready outed added apart").split()
        S = {n: s.sem(n) for n in names}
        block = s.block()

        LOG, SWT, Z, ZT, ZA, VAL, SC, AT = range(8)
        XT, Y, OUT = SWT, (Z, ZT), VAL

        def view(bank, cols, *dims):
            a = ps[:, bank, 0:cols]
            if len(dims) == 1:
                return a.rearrange("p (a b) -> p a b", b=dims[0])
            return a.rearrange("p (a b c) -> p a b c", b=dims[0], c=dims[1])

        def alive(t, b, lag):
            return not isinstance(t, int) or 0 <= GROUP * t + b - lag < SEQS

        def run(eng, slot, prelude):
            def group(t, par):
                for b in range(GROUP):
                    slot(t, par, b)
            prelude()
            group(0, 0)
            group(1, 1)
            with eng.Fori(1, GROUPS // 2 - 1) as i:
                group(2 * i, 0)
                group(2 * i + 1, 1)
            for t in range(GROUPS - 2, GROUPS + 2):
                group(t, t % 2)

        @block.vector
        def _(dve):
            vec = nc.vector
            start = Link(dve, S["step"])
            vec.memset(z[:], 0.0)
            start(vec.memset(xs[:], 0.0))
            start(vec.memset(xs[:, :, :, D:A1], 1.0))
            PER = 6
            BASE = 2

            def prelude():
                front_dve(k, dve, xs[:, 0], 0, S["normed"])

            def slot(t, par, b):
                link = Link(dve, S["step"], BASE + PER * (GROUP * t + b), PER)

                def wait(sem, lag):
                    dve.wait_ge(S[sem], GROUP * t + b - lag + 1)

                def skip(n):
                    vec.sem_inc(S["step"], n)
                    link.n += n

                c = (b - 1) % GROUP
                if alive(t, b, 1):
                    wait("exped", 1)
                    link(vec.tensor_reduce(den[:, c, :, 0], sw[:, c], AX, ALU.add))
                    link(vec.reciprocal(rden[:, c], den[:, c]))
                else:
                    skip(2)
                if alive(t, b, 0):
                    wait("logit", 0)
                    lg = view(LOG, 512, G)
                    link(vec.tensor_reduce(top[:, b, :, 0], lg, AX, ALU.max))
                    vec.tensor_tensor(sw[:, b], lg, bc(top[:, b], [P, H, G]), ALU.subtract).then_inc(S["shifted"], 1)
                else:
                    skip(1)
                if alive(t, b, 1):
                    vec.tensor_tensor(sw[:, c], sw[:, c], bc(rden[:, c], [P, H, G]), ALU.mult).then_inc(S["weighted"], 1)
                c = (b - 2) % GROUP
                if alive(t, b, 2):
                    wait("z_made", 2)
                    zz = view(Z, PAIRS * A1, A1)
                    link(vec.tensor_scalar(znorm[:, c], zz[:, :, D:A1], 1e-5, None, ALU.add))
                    link(vec.reciprocal(znorm[:, c], znorm[:, c]))
                    vec.tensor_tensor(z[:, c, :, 0:A1], zz, bc(znorm[:, c], [P, PAIRS, A1]), ALU.mult).then_inc(S["z_ready"], 1)
                else:
                    skip(2)
                if b == 1 and alive(t + 1, 0, 0):
                    front_dve(k, dve, xs[:, 1 - par], t + 1, S["normed"])
                c = (b - 5) % GROUP
                if alive(t, b, 5):
                    wait("sc_made", 5)
                    sc = view(SC, 256, G)
                    vec.tensor_reduce(atop[:, c, :, 0], sc, AX, ALU.max, negate=True).then_inc(S["sc_topped"], 1)
                c = (b - 6) % GROUP
                if alive(t, b, 6):
                    wait("sc_exped", 6)
                    link(vec.reciprocal(aden[:, c], aden[:, c]))
                else:
                    skip(1)
                c = (b - 7) % GROUP
                if alive(t, b, 7):
                    wait("y_made", 7)
                    for q in range(2):
                        ins = vec.tensor_tensor(y[:, c].rearrange("p (j q) o -> p q j o", q=2)[:, q], view(Y[q], 128, D),
                                                bc(aden[:, c].rearrange("p (j q) o -> p q j o", q=2)[:, q], [P, 2, D]), ALU.mult)
                    ins.then_inc(S["y_ready"], 1)
                if alive(t, b, 8):
                    wait("outed", 8)
                    one = bass.ds(GROUP * t + b - 8, 1)
                    vec.tensor_tensor(k.h[:, one, :], k.h[:, one, :], view(OUT, D, D), ALU.add).then_inc(S["added"], 1)
                link.close()

            run(dve, slot, prelude)

        @block.scalar
        def _(act):
            def keep_x(t, par):
                act.wait_ge(S["xt_made"], t + 1)
                nc.scalar.copy(xt[:, par], ps[:, XT, :]).then_inc(S["xt_ready"], 1)

            def slot(t, par, b):
                def wait(sem, lag):
                    act.wait_ge(S[sem], GROUP * t + b - lag + 1)

                if alive(t, b, 0):
                    wait("shifted", 0)
                    nc.scalar.activation(sw[:, b], sw[:, b], ACT.Exp).then_inc(S["exped"], 1)
                if alive(t, b, 2):
                    wait("swt_made", 2)
                    nc.scalar.copy(sw_t[:, (GROUP * par + b - 2) % 8], view(SWT, 512, N)).then_inc(S["swt_ready"], 1)
                if alive(t, b, 3):
                    wait("zt_made", 3)
                    nc.scalar.copy(z_t[:, (b - 3) % GROUP], view(ZT, 512, G)).then_inc(S["zt_ready"], 1)
                if alive(t, b, 4):
                    wait("za_made", 4)
                    nc.scalar.copy(za[:, (b - 4) % GROUP], view(ZA, 512, G)).then_inc(S["za_ready"], 1)
                if alive(t, b, 4):
                    wait("val_made", 4)
                    nc.scalar.copy(vals[:, (b - 4) % GROUP], view(VAL, 256, 2, D)).then_inc(S["val_ready"], 1)
                if b == 2 and alive(t + 1, 0, 0):
                    keep_x(t + 1, 1 - par)
                if alive(t, b, 5):
                    wait("sc_topped", 5)
                    c = (b - 5) % GROUP
                    for q in range(PAIRS):
                        ins = nc.scalar.activation(att[:, c, q], view(SC, 256, G)[:, q], ACT.Exp, bias=atop[:, c, q], accum_out=aden[:, c, q])
                    ins.then_inc(S["sc_exped"], 1)
                if alive(t, b, 6):
                    wait("att_made", 6)
                    nc.scalar.copy(att_t[:, (b - 6) % GROUP], view(AT, 256, P)).then_inc(S["att_t_ready"], 1)

            run(act, slot, lambda: keep_x(0, 0))

        @block.tensor
        def _(pe):
            mm = nc.tensor.matmul

            def turn_x(t, par):
                pe.wait_ge(S["normed"], t + 1)
                for b in range(GROUP):
                    ins = nc.tensor.transpose(ps[:, XT, b * N:(b + 1) * N], xs[:, par, b, :], k.ident[:])
                ins.then_inc(S["xt_made"], 1)

            def slot(t, par, b):
                def wait(sem, lag):
                    if alive(t, b, lag):
                        pe.wait_ge(S[sem], GROUP * t + b - lag + 1)

                if alive(t, b, 0):
                    if b == 0:
                        pe.wait_ge(S["xt_ready"], t + 1)
                    wait("shifted", 1)
                    mm(ps[:, LOG, :], xt[:, par, b * N:(b + 1) * N], slice_map[:].rearrange("p h g -> p (h g)"),
                       start=True, stop=True).then_inc(S["logit"], 1)
                if alive(t, b, 2):
                    c = (b - 2) % GROUP
                    wait("weighted", 2)
                    if b == 3:
                        if alive(t + 1, 0, 0):
                            pe.wait_ge(S["xt_ready"], t + 2)
                    wait("swt_ready", 3)
                    for q in range(PAIRS):
                        ins = nc.tensor.transpose(view(SWT, 512, N)[:, q], sw[:, c, 2 * q:2 * q + 2].rearrange("p h g -> p (h g)"), k.ident[:])
                    ins.then_inc(S["swt_made"], 1)
                    wait("z_ready", 3)
                    wait("y_ready", 8)
                    rows = xs[:, par if b >= 2 else 1 - par, c, 0:A1]
                    for q in range(PAIRS):
                        ins = mm(view(Z, PAIRS * A1, A1)[:, q], sw[:, c, 2 * q:2 * q + 2].rearrange("p h g -> p (h g)"), rows, start=True, stop=True)
                    ins.then_inc(S["z_made"], 1)
                if alive(t, b, 3):
                    wait("z_ready", 3)
                    wait("zt_ready", 4)
                    wait("y_ready", 8)
                    for q in range(PAIRS):
                        ins = nc.tensor.transpose(view(ZT, 512, N)[:, q], z[:, (b - 3) % GROUP, q], k.ident[:])
                    ins.then_inc(S["zt_made"], 1)
                if alive(t, b, 4):
                    c = (b - 4) % GROUP
                    wait("zt_ready", 4)
                    wait("za_ready", 5)
                    for h in range(H):
                        ins = mm(view(ZA, 512, G)[:, h], pair_map[:, h], z_t[:, c, h], start=True, stop=True)
                    ins.then_inc(S["za_made"], 1)
                    wait("shifted", 0)
                    if not alive(t, b, 0):
                        wait("added", 9)
                    wait("val_ready", 5)
                    for h in range(H):
                        pr, sub = h // 2, h % 2
                        r = 64 * (pr % 2)
                        ins = mm(view(VAL, 256, 2, D)[r:r + 64, pr // 2, sub], z_t[:, c, h], value_map[:, h], start=True, stop=True)
                    ins.then_inc(S["val_made"], 1)
                if alive(t, b, 5):
                    c = (b - 5) % GROUP
                    wait("za_ready", 5)
                    wait("sc_exped", 6)
                    for h in range(H):
                        r = 64 * (h % 2)
                        ins = mm(view(SC, 256, G)[r:r + 64, h // 2], za[:, c, h], z_t[:, c, h], start=True, stop=True)
                    ins.then_inc(S["sc_made"], 1)
                if alive(t, b, 6):
                    c = (b - 6) % GROUP
                    wait("sc_exped", 6)
                    wait("att_t_ready", 7)
                    for j in range(2):
                        ins = nc.tensor.transpose(view(AT, 256, P)[:, j], att[:, c, 2 * j:2 * j + 2].rearrange("p a g -> p (a g)"), k.ident[:])
                    ins.then_inc(S["att_made"], 1)
                if b == 2 and alive(t + 1, 0, 0):
                    wait("swt_ready", 2)
                    turn_x(t + 1, 1 - par)
                if alive(t, b, 7):
                    c = (b - 7) % GROUP
                    wait("att_t_ready", 7)
                    wait("val_ready", 7)
                    wait("z_ready", 2)
                    if not alive(t, b, 2):
                        wait("y_ready", 8)
                    wait("zt_ready", 3)
                    nc.tensor.sem_inc(S["apart"], 1)
                    for h in range(H):
                        pr, sub = h // 2, h % 2
                        r, o = 64 * (pr % 2), 64 * sub
                        ins = mm(view(Y[pr % 2], 128, D)[o:o + 64, pr // 2], att_t[r:r + 64, c, pr // 2, o:o + 64],
                                 vals[r:r + 64, c, pr // 2, sub], start=True, stop=True, tile_position=(r, o))
                    ins.then_inc(S["y_made"], 1)
                if alive(t, b, 8):
                    wait("y_ready", 8)
                    wait("val_ready", 4)
                    if not alive(t, b, 4):
                        wait("added", 9)
                    for q in range(PAIRS):
                        ins = mm(ps[:, OUT, 0:D], sw_t[:, (GROUP * par + b - 8) % 8, q], y[:, b, q], start=(q == 0), stop=(q == PAIRS - 1))
                    ins.then_inc(S["outed"], 1)

            run(pe, slot, lambda: turn_x(0, 0))


def fold_l0_ffn(k, slice_map, pair_map, value_map):
    nc, w = k.nc, k.w
    H, G, A1 = 8, 64, D + 1
    with Scope(nc, "l0fold") as s:
        fx = s.sb("fx", [A1, H, D])
        wx = s.sb("wx", [A1, H, D])
        fx_t = s.sb("fx_t", [D, H, A1])
        wx_t = s.sb("wx_t", [D, H, A1])
        wsl, wq, wk, wv = (s.sb(n, [D, D]) for n in ("wsl", "wq", "wk", "wv"))
        wout = s.sb("wout", [D, H, D])
        bsl = s.sb("bsl", [A1, G])
        temp = s.sb("temp", [A1, H, 1])
        bout = s.sb("bout", [P, 1, D])
        proj = s.sb("proj", [D, 3, H, A1])
        ps = s.ps("ps", [P, 8, 512])
        loaded, step, made, ready = s.sem("loaded"), s.sem("step"), s.sem("made"), s.sem("ready")
        center_vector, center_scalar = center_parts(k, s)
        block = s.block()

        @block.scalar
        def _(act):
            center_scalar(act)

        def maps(first):
            return [ps[0:D, first + j, 0:4 * A1].rearrange("p (h c) -> p h c", c=A1) for j in range(2)]

        @block.sync
        def _(sp):
            n = 0
            for dst, src in ((fx, "fx"), (wx, "x")):
                sp.dma_start(dst[0:D], w[f"L0_ffn_W_{src}"].rearrange("i (h d) -> i h d", d=D)).then_inc(loaded, 16)
                sp.dma_start(dst[D:A1], w[f"L0_ffn_b_{src}"].rearrange("(o h d) -> o h d", o=1, d=D)).then_inc(loaded, 16)
            for dst, src in ((wsl, "W_slice"), (wq, "W_q"), (wk, "W_k"), (wv, "W_v")):
                sp.dma_start(dst[:], w[f"L0_ffn_{src}"]).then_inc(loaded, 16)
            sp.dma_start(wout[:], w["L0_ffn_W_out"].rearrange("(h d) o -> d h o", d=D)).then_inc(loaded, 16)
            sp.dma_start(bsl[D:A1, :], w["L0_ffn_b_slice"].rearrange("(o g) -> o g", o=1)).then_inc(loaded, 16)
            sp.dma_start(temp[:, :, 0], w["L0_ffn_temperature"].rearrange("a h b c -> (a h b c)").partition_broadcast(A1)).then_inc(loaded, 16)
            sp.dma_start(bout[:, 0, :], w["L0_ffn_b_out"].partition_broadcast(P)).then_inc(loaded, 16)

        LOADED = 16 * 12

        @block.vector
        def _(dve):
            link = Link(dve, step)
            for buf in (slice_map, pair_map, value_map):
                ins = nc.vector.memset(buf[:], 0.0)
            link(ins)
            center_vector(dve)
            dve.wait_ge(loaded, LOADED)
            link(nc.vector.tensor_tensor(k.h[:], k.h[:], bc(bout[:], [P, SEQS, D]), ALU.add))
            link(nc.vector.tensor_scalar(temp[:], temp[:], 0.1, 5.0, ALU.max, ALU.min))
            link(nc.vector.reciprocal(temp[:], temp[:]))
            dve.wait_ge(made, 1)
            for j in range(2):
                link(nc.vector.tensor_copy(fx_t[:, 4 * j:4 * j + 4], maps(0)[j]))
                link(nc.vector.tensor_copy(wx_t[:, 4 * j:4 * j + 4], maps(2)[j]))
            nc.vector.sem_inc(ready, 1)
            dve.wait_ge(made, 2)
            for n in range(3):
                for j in range(2):
                    src = maps(2 * n)[j]
                    if n == 0:
                        link(nc.vector.tensor_scalar(proj[:, n, 4 * j:4 * j + 4], src, D ** -0.5, None, ALU.mult))
                    else:
                        link(nc.vector.tensor_copy(proj[:, n, 4 * j:4 * j + 4], src))
            sl = ps[0:A1, 6, :].rearrange("p (h g) -> p h g", g=G)
            link(nc.vector.tensor_copy(slice_map[0:A1], sl))
            link(nc.vector.tensor_tensor(slice_map[D:A1], slice_map[D:A1],
                                         bc(bsl[D:A1, :].rearrange("p (o g) -> p o g", o=1), [1, H, G]), ALU.add))
            link(nc.vector.tensor_tensor(slice_map[0:A1], slice_map[0:A1], bc(temp[:], [A1, H, G]), ALU.mult))
            nc.vector.sem_inc(ready, 1)
            dve.wait_ge(made, 3)
            for j in range(2):
                link(nc.vector.tensor_copy(pair_map[0:A1, 4 * j:4 * j + 4, 0:A1], ps[0:A1, j, 0:4 * A1].rearrange("p (h c) -> p h c", c=A1)))
            link(nc.vector.tensor_copy(value_map[0:A1], ps[0:A1, 2, :].rearrange("p (h o) -> p h o", o=D)))

        @block.tensor
        def _(pe):
            mm = nc.tensor.matmul
            pe.wait_ge(loaded, LOADED)
            for h in range(H):
                nc.tensor.transpose(maps(0)[h // 4][:, h % 4], fx[:, h], k.ident[0:A1, 0:A1])
                ins = nc.tensor.transpose(maps(2)[h // 4][:, h % 4], wx[:, h], k.ident[0:A1, 0:A1])
            ins.then_inc(made, 1)
            pe.wait_ge(ready, 1)
            for n, wt in enumerate((wq, wk, wv)):
                for j in range(2):
                    mm(maps(2 * n)[j], wt[:], fx_t[:, 4 * j:4 * j + 4], start=True, stop=True)
            for h in range(H):
                ins = mm(ps[0:A1, 6, h * G:(h + 1) * G], wx_t[:, h], wsl[:], start=True, stop=True)
            ins.then_inc(made, 1)
            pe.wait_ge(ready, 2)
            for h in range(H):
                mm(ps[0:A1, h // 4, (h % 4) * A1:(h % 4 + 1) * A1], proj[:, 0, h], proj[:, 1, h], start=True, stop=True)
                ins = mm(ps[0:A1, 2, h * D:(h + 1) * D], proj[:, 2, h], wout[:, h], start=True, stop=True)
            ins.then_inc(made, 1)


def stage_edge_cells(k, meanwhile=None):
    nc, w = k.nc, k.w
    E = w["L1_attn_edge_index"].shape[1]
    BS = 32
    LANE = E // P
    CPL = LANE // P
    UN = 4
    CB = UN * CPL
    STEPS = P // (2 * UN)
    HEADS = 4
    assert CPL == 16
    keys_dram = nc.dram_tensor("edge_keys", (E // P, P), F32).ap()
    with Scope(nc, "cells") as s:
        r_t = s.sb("r_t", [P, P, CPL, 1], BF16)
        c_t = s.sb("c_t", [P, P, CPL, 1], BF16)
        stored = s.sem("stored")
        with Scope(nc, "cellkeys") as s1:
            rows = s1.sb("rows", [P, LANE], I32)
            cols = s1.sb("cols", [P, LANE], I32)
            away = s1.sb("away", [P, LANE], I32)
            key = s1.sb("key", [P, LANE])
            rf = s1.sb("rf", [P, LANE])
            rb = s1.sb("rb", [P, CPL, P], BF16)
            cb = s1.sb("cb", [P, CPL, P], BF16)
            identb = s1.sb("identb", [P, P], BF16)
            ps = s1.ps("ps", [P, 4, 8, P], BF16)
            loaded, step, keyed, turned, copied = (s1.sem(n) for n in "loaded step keyed turned copied".split())
            block = s1.block()

            @block.sync
            def _(sp):
                sp.dma_start(rows[:], w["L1_attn_edge_index"][0].rearrange("(p f) -> p f", p=P)).then_inc(loaded, 16)
                sp.dma_start(cols[:], w["L1_attn_edge_index"][1].rearrange("(p f) -> p f", p=P)).then_inc(loaded, 16)
                sp.wait_ge(keyed, 1)
                sp.dma_start(keys_dram.rearrange("(p c) f -> p (c f)", p=P), key[:]).then_inc(stored, 16)
                sp.wait_ge(stored, 16)

            @block.vector
            def _(dve):
                link = Link(dve, step)
                link(nc.vector.tensor_copy(identb[:], k.ident[:]))
                dve.wait_ge(loaded, 32)
                link(nc.vector.tensor_tensor(away[:], rows[:], cols[:], ALU.bitwise_xor))
                link(nc.vector.tensor_scalar(away[:], away[:], 5, None, ALU.logical_shift_right))
                link(nc.vector.tensor_scalar(cols[:], cols[:], BS - 1, None, ALU.bitwise_and))
                link(nc.vector.tensor_scalar(rf[:], away[:], 1.0, 128.0, ALU.min, ALU.mult))
                link(nc.vector.tensor_tensor(rf[:], rf[:], rows[:], ALU.add))
                link(nc.vector.tensor_scalar(rf[:], rf[:], 128.0, None, ALU.min))
                link(nc.vector.scalar_tensor_tensor(out=key[:], in0=rf[:], scalar=float(BS), in1=cols[:], op0=ALU.mult, op1=ALU.add))
                nc.vector.tensor_copy(rb[:].rearrange("p c f -> p (c f)"), rf[:]).then_inc(keyed, 1)
                nc.vector.tensor_copy(cb[:].rearrange("p c f -> p (c f)"), cols[:]).then_inc(keyed, 1)
                for n in range(4):
                    dst = (r_t, c_t)[n // 2]
                    dve.wait_ge(turned, n + 1)
                    nc.vector.tensor_copy(dst[:, :, 8 * (n % 2):8 * (n % 2) + 8, 0].rearrange("f p c -> f c p"), ps[:, n]).then_inc(copied, 1)
                dve.wait_ge(copied, 4)

            @block.tensor
            def _(pe):
                pe.wait_ge(keyed, 2)
                for n in range(4):
                    src = (rb, cb)[n // 2]
                    for j in range(8):
                        ins = nc.tensor.transpose(ps[:, n, j], src[:, 8 * (n % 2) + j], identb[:])
                    ins.then_inc(turned, 1)

        with Scope(nc, "cellhits") as s2:
            hits = s2.sb("hits", [P, P, BS])
            with Scope(nc, "cellcount") as s3:
                tok_i = s3.sb("tok_i", [P, 1, P])
                tok = s3.sb("tok", [P, P, CB], BF16)
                power = s3.sb("power", [P, 1, UN, CPL], BF16)
                rhot = s3.sb("rhot", [P, 2, P, CB], BF16)
                chot = s3.sb("chot", [P, 2, BS, CB], BF16)
                ps = s3.ps("ps", [P, 2, 512])
                step, iotad, hot, counted, taken = (s3.sem(n) for n in "step iotad hot counted taken".split())
                block = s3.block()

                @block.gpsimd
                def _(pool):
                    nc.gpsimd.iota(tok_i[:, 0, :], [[1, P]], 0, 0, allow_small_or_imprecise_dtypes=True).then_inc(iotad, 1)
                    if meanwhile is not None:
                        meanwhile()

                @block.vector
                def _(dve):
                    link = Link(dve, step)
                    for b in range(CPL):
                        link(nc.vector.memset(power[:, :, :, b], 2.0 ** (8 * (b - 8))))
                    dve.wait_ge(iotad, 1)
                    link(nc.vector.tensor_copy(tok[:], bc(tok_i[:].rearrange("p o n -> p n o"), [P, P, CB])))
                    BASE = CPL + 1
                    with dve.Fori(0, STEPS) as t:
                        link = Link(dve, step, BASE + 2 * t, 2)
                        for j in range(2):
                            dve.wait_ge(counted, 2 * t + j + 1)
                            lanes = bass.ds(2 * UN * t + UN * j, UN)
                            rr = r_t[:, lanes].rearrange("p l c o -> p o (l c)")
                            cc = c_t[:, lanes].rearrange("p l c o -> p o (l c)")
                            nc.vector.tensor_tensor(rhot[:, j], bc(rr, [P, P, CB]), tok[:], ALU.is_equal).then_inc(hot, 1)
                            link(nc.vector.tensor_tensor(chot[:, j], bc(cc, [P, BS, CB]), tok[:, 0:BS], ALU.is_equal))
                            nc.vector.tensor_tensor(chot[:, j], chot[:, j], bc(power[:].rearrange("p o l c -> p o (l c)"), [P, BS, CB]), ALU.mult).then_inc(hot, 1)
                        link.close()

                @block.tensor
                def _(pe):
                    nc.tensor.sem_inc(counted, 2)
                    with pe.Fori(0, STEPS) as t:
                        for j in range(2):
                            pe.wait_ge(hot, 2 * (2 * t + j) + 2)
                            pe.wait_ge(taken, 2 * t + j + 1)
                            for l in range(UN):
                                for b in range(CPL):
                                    ins = nc.tensor.matmul(ps[:, j, l * BS:(l + 1) * BS], rhot[:, j, :, l * CPL + b], chot[:, j, :, l * CPL + b],
                                                           start=(b == 0), stop=(b == CPL - 1))
                            ins.then_inc(counted, 1)

                @block.scalar
                def _(act):
                    nc.scalar.sem_inc(taken, 2)
                    with act.Fori(0, STEPS) as t:
                        for j in range(2):
                            act.wait_ge(counted, 2 * t + j + 3)
                            nc.scalar.copy(hits[:, bass.ds(2 * UN * t + UN * j, UN), :],
                                           ps[:, j, 0:UN * BS].rearrange("p (l k) -> p l k", l=UN)).then_inc(taken, 1)

            with Scope(nc, "cellfind") as s4:
                expo = s4.sb("expo", [P, P, BS], I32)
                lane = s4.sb("lane", [P, P, 1])
                last = s4.sb("last", [P, BS])
                found = s4.sb("found", [P, BS])
                number = s4.sb("number", [P, BS])
                last_i = s4.sb("last_i", [P, 2, BS], I32)
                chunk = s4.sb("chunk", [P, BS], U32)
                keys = s4.sb("keys", [P, BS, P])
                vals = s4.sb("vals", [P, BS, P])
                cell = s4.sb("cell", [P, BS, 1])
                place = s4.sb("place", [P, 1, P])
                at = s4.sb("at", [P, BS, 1])
                col = s4.sb("col", [P, BS])
                row_i = s4.sb("row_i", [P, 1], I32)
                row_f = s4.sb("row_f", [P, 1])
                diag = s4.sb("diag", [P, BS])
                off = s4.sb("off", [P, BS])
                mask = s4.sb("mask", [P, BS + 1])
                feats = s4.sb("feats", [P, 4, BS + 1])
                pos = s4.sb("pos", [P, BS, 3])
                pos_r = s4.sb("pos_r", [P, 3])
                gw = s4.sb("gw", [P, HEADS, 4])
                gb = s4.sb("gb", [P, HEADS])
                loaded, iotad, step, chunked = (s4.sem(n) for n in "loaded iotad step chunked".split())
                fetched = k.chunks_fetched
                targets_sync, targets_gpsimd, targets_vector = last_edge_parts(k, s4)
                block = s4.block()

                @block.sync
                def _(sp):
                    targets_sync(sp)
                    for n in range(P // BS):
                        sp.dma_start(pos[n * BS:(n + 1) * BS].rearrange("p c x -> p (c x)"),
                                     w["L1_attn_positions"][n * BS:(n + 1) * BS].rearrange("c x -> (c x)").partition_broadcast(BS)).then_inc(loaded, 16)
                    sp.dma_start(pos_r[:], w["L1_attn_positions"][0:P]).then_inc(loaded, 16)
                    sp.dma_start(gw[:], w["L1_attn_gate_w"].partition_broadcast(P)).then_inc(loaded, 16)
                    sp.dma_start(gb[:], w["L1_attn_gate_b"].partition_broadcast(P)).then_inc(loaded, 16)

                @block.gpsimd
                def _(pool):
                    imp = dict(allow_small_or_imprecise_dtypes=True)
                    nc.gpsimd.iota(lane[:, :, 0], [[256, P]], 0, 0, **imp).then_inc(iotad, 1)
                    nc.gpsimd.iota(cell[:, :, 0], [[1, BS]], 0, BS, **imp).then_inc(iotad, 1)
                    nc.gpsimd.iota(place[:, 0, :], [[1, P]], 1, 0, **imp).then_inc(iotad, 1)
                    nc.gpsimd.iota(col[:], [[1, BS]], 0, 0, **imp).then_inc(iotad, 1)
                    nc.gpsimd.iota(row_i[:], [[0, 1]], 0, 1).then_inc(iotad, 1)
                    targets_gpsimd(pool)
                    pool.wait_ge(chunked, 1)
                    for c in range(BS):
                        index = bass.IndirectOffsetOnAxis(chunk[:, c:c + 1], 0)
                        nc.gpsimd.indirect_dma_start(keys[:, c, :], None, keys_dram, index).then_inc(fetched, 16)
                        nc.gpsimd.indirect_dma_start(vals[:, c, :], None, w["L1_attn_edge_values"].rearrange("(c f) -> c f", f=P),
                                                     index).then_inc(fetched, 16)

                @block.vector
                def _(dve):
                    link = Link(dve, step)
                    v = nc.vector
                    full = [P, P, BS]
                    dve.wait_ge(iotad, 5)
                    link(v.tensor_scalar(expo[:], hits[:].bitcast(I32), 23, None, ALU.logical_shift_right))
                    link(v.scalar_tensor_tensor(out=hits[:], in0=expo[:], scalar=1.0, in1=bc(lane[:], full), op0=ALU.min, op1=ALU.mult))
                    link(v.tensor_tensor(hits[:], hits[:], expo[:], ALU.add))
                    link(v.tensor_reduce(last[:], hits[:].rearrange("r p c -> r c p"), AX, ALU.max))
                    link(v.tensor_scalar(found[:], last[:], 1.0, None, ALU.min))
                    link(v.tensor_copy(last_i[:, 0], last[:]))
                    link(v.tensor_scalar(last_i[:, 1], last_i[:, 0], 255, None, ALU.bitwise_and))
                    link(v.tensor_scalar(last_i[:, 0], last_i[:, 0], 8, None, ALU.logical_shift_right))
                    link(v.tensor_scalar(number[:], last_i[:, 1], -63.0, 0.0, ALU.add, ALU.max))
                    link(v.tensor_copy(last_i[:, 1], number[:]))
                    link(v.tensor_scalar(last_i[:, 1], last_i[:, 1], 3, None, ALU.logical_shift_right))
                    link(v.scalar_tensor_tensor(out=number[:], in0=last_i[:, 0], scalar=float(CPL), in1=last_i[:, 1], op0=ALU.mult, op1=ALU.add))
                    v.tensor_copy(chunk[:], number[:]).then_inc(chunked, 1)
                    link(v.tensor_scalar(row_i[:], row_i[:], BS - 1, None, ALU.bitwise_and))
                    link(v.tensor_copy(row_f[:], row_i[:]))
                    link(v.tensor_scalar(diag[:], col[:], row_f[:, 0:1], None, ALU.is_equal))
                    link(v.tensor_scalar(off[:], diag[:], -1.0, 1.0, ALU.mult, ALU.add))
                    link(v.memset(mask[:], 1.0))
                    link(v.tensor_tensor(mask[:, 0:BS], diag[:], found[:], ALU.max))
                    link(v.tensor_tensor(off[:], off[:], found[:], ALU.mult))
                    link(v.memset(feats[:], 0.0))
                    link(v.memset(feats[:, 3, BS:BS + 1], 1.0))
                    dve.wait_ge(loaded, 16 * 7)
                    for x in range(3):
                        link(v.tensor_scalar(feats[:, x, 0:BS], pos[:, :, x], pos_r[:, x:x + 1], None, ALU.subtract))
                        link(v.tensor_tensor(feats[:, x, 0:BS], feats[:, x, 0:BS], off[:], ALU.mult))
                    targets_vector(dve)
                    dve.wait_ge(fetched, 16 * 2 * BS)
                    one = [P, BS, P]
                    link(v.tensor_tensor(keys[:], keys[:], bc(cell[:], one), ALU.is_equal))
                    link(v.tensor_tensor(keys[:], keys[:], bc(place[:], one), ALU.mult))
                    link(v.tensor_reduce(at[:, :, 0], keys[:], AX, ALU.max))
                    link(v.tensor_scalar(at[:], at[:], 1.0, None, ALU.max))
                    link(v.tensor_tensor(keys[:], bc(place[:], one), bc(at[:], one), ALU.is_equal))
                    link(v.tensor_tensor(vals[:], vals[:], keys[:], ALU.mult))
                    link(v.tensor_reduce(number[:], vals[:], AX, ALU.add))
                    link(v.tensor_tensor(number[:], number[:], off[:], ALU.mult))
                    link(v.tensor_tensor(feats[:, 3, 0:BS], number[:], diag[:], ALU.add))
                    score = k.edge_score[:, 0]
                    link(v.tensor_scalar(score, mask[:], -MASKED, MASKED, ALU.mult, ALU.add))
                    link(v.tensor_tensor(score, score, feats[:, 3], ALU.add))
                    for h in range(HEADS):
                        g = k.edge_gate[:, h, 0]
                        link(v.tensor_scalar(g, feats[:, 0], gw[:, h, 0:1], gb[:, h:h + 1], ALU.mult, ALU.add))
                        for x in range(1, 4):
                            link(v.scalar_tensor_tensor(out=g, in0=feats[:, x], scalar=gw[:, h, x:x + 1], in1=g, op0=ALU.mult, op1=ALU.add))
                        link(v.tensor_tensor(g, g, mask[:], ALU.mult))


def stage_l1_attn(k):
    nc, w = k.nc, k.w
    HEADS, HD, BS, A1 = 4, 16, 32, D + 1
    NB = N // BS
    KEYS = BS + 1
    with Scope(nc, "l1a") as s:
        wnat = s.sb("wnat", [D, 4, A1])
        wq = s.sb("wq", [P, HEADS, 32])
        wk = s.sb("wk", [P, HEADS, 32])
        wv = s.sb("wv", [P, D])
        wo = s.sb("wo", [P, D])
        blockmean = s.sb("blockmean", [P, P])
        xs = s.sb("xs", [P, GROUP, P])
        xkv = s.sb("xkv", [P, TOK + GROUP * NB])
        q = s.sb("q", [P, GROUP * NB, BS])
        kk = s.sb("kk", [P, GROUP * NB, KEYS])
        v = s.sb("v", [P, 2, GROUP, D])
        sc = s.sb("sc", [P, HEADS, GROUP, KEYS])
        top = s.sb("top", [P, HEADS, GROUP, 1])
        den = s.sb("den", [P, HEADS, GROUP, 1])
        sct = s.sb("sct", [P, HEADS, GROUP, BS])
        scn = s.sb("scn", [P, HEADS, GROUP, BS])
        mixed = s.sb("mixed", [P, GROUP, P])
        node = s.sb("node", [P, GROUP, HEADS, HD])
        mt = s.sb("mt", [P, TOK])
        ps = s.ps("ps", [P, 8, 512])
        names = ("loaded step wturned wready normed xt_made xt_ready mean_ready projected q_ready k_ready v_ready "
                 "scored shifted exped combined valued added mixed_ready mt_made mt_ready outed apart").split()
        S = {n: s.sem(n) for n in names}
        block = s.block()

        @block.sync
        def _(sp):
            qkv = w["L1_attn_qkv_w"].rearrange("(n o) i -> o n i", o=D)
            sp.dma_start(wnat[:, 0:3, 0:D], qkv).then_inc(S["loaded"], 16)
            sp.dma_start(wnat[:, 3, 0:D], w["L1_attn_proj_w"]).then_inc(S["loaded"], 16)
            for n in range(3):
                sp.dma_start(wnat[:, n, D:A1], w["L1_attn_qkv_b"].rearrange("(n o u) -> n o u", o=D, u=1)[n]).then_inc(S["loaded"], 16)
            sp.dma_start(wnat[:, 3, D:A1], w["L1_attn_proj_b"].rearrange("(o u) -> o u", u=1)).then_inc(S["loaded"], 16)

        @block.vector
        def _(dve):
            vec = nc.vector
            link = Link(dve, S["step"])
            for buf in (wq, wk, wv, wo, xs, mixed):
                vec.memset(buf[:], 0.0)
            link(vec.memset(blockmean[:], 0.0))
            vec.memset(xs[:, :, D:A1], 1.0)
            link(vec.memset(mixed[:, :, D:A1], 1.0))
            for n in range(NB):
                link(vec.memset(blockmean[n * BS:(n + 1) * BS, n * BS:(n + 1) * BS], 1.0 / BS))
            dve.wait_ge(S["wturned"], 1)
            wt = ps[0:A1, 0, 0:4 * D].rearrange("p (n h c) -> p n h c", n=4, h=HEADS)
            link(vec.tensor_scalar(wq[0:A1, :, 0:HD], wt[:, 0], HD ** -0.5, None, ALU.mult))
            link(vec.tensor_copy(wk[0:A1, :, 0:HD], wt[:, 1]))
            link(vec.tensor_copy(wv[0:A1].rearrange("p (h c) -> p h c", h=HEADS), wt[:, 2]))
            link(vec.tensor_copy(wo[0:A1].rearrange("p (h c) -> p h c", h=HEADS), wt[:, 3]))
            vec.sem_inc(S["wready"], 1)
            BASE = 2 + NB + 4
            PER = 8
            full = [P, HEADS, GROUP, KEYS]

            def keep_keys(t):
                dve.wait_ge(S["xt_ready"], t + 1)
                vec.tensor_reduce(xkv[:, TOK:], xkv[:, 0:TOK].rearrange("p (n c) -> p n c", c=BS), AX, ALU.add).then_inc(S["mean_ready"], 1)
                dve.wait_ge(S["mean_ready"], 2 * t + 1)
                vec.tensor_scalar(xkv[:, TOK:], xkv[:, TOK:], 1.0 / BS, None, ALU.mult).then_inc(S["mean_ready"], 1)
                dve.wait_ge(S["projected"], 4 * t + 2)
                vec.tensor_copy(kk[:, :, 0:BS], ps[:, 0, :].rearrange("p (n c) -> p n c", c=BS)).then_inc(S["k_ready"], 1)
                dve.wait_ge(S["projected"], 4 * t + 3)
                vec.tensor_copy(kk[:, :, BS], ps[:, 1, 0:GROUP * NB]).then_inc(S["k_ready"], 1)

            def prelude():
                front_dve(k, dve, xs[:], 0, S["normed"])
                keep_keys(0)

            def add(t):
                dve.wait_ge(S["outed"], t + 1)
                g = bass.ds(GROUP * t, GROUP)
                vec.tensor_tensor(k.h[:, g, :], k.h[:, g, :], ps[:, 3, 0:256].rearrange("p (b d) -> p b d", b=GROUP), ALU.add).then_inc(S["added"], 1)

            def body(t, par, cur, prev, nxt):
                link = Link(dve, S["step"], BASE + PER * t, PER)
                if cur:
                    dve.wait_ge(S["scored"], t + 1)
                    psc = ps[:, 4:8, 0:GROUP * KEYS].rearrange("p h (b c) -> p h b c", c=KEYS)
                    for h in range(HEADS):
                        ins = vec.tensor_tensor(sc[:, h], psc[:, h], bc(k.edge_score[:], [P, GROUP, KEYS]), ALU.add)
                    link(ins)
                    link(vec.tensor_reduce(top[:, :, :, 0], sc[:], AX, ALU.max))
                    vec.tensor_tensor(sc[:], sc[:], bc(top[:], full), ALU.subtract).then_inc(S["shifted"], 1)
                if prev:
                    add(t - 1)
                if nxt:
                    front_dve(k, dve, xs[:], t + 1, S["normed"])
                if cur:
                    dve.wait_ge(S["exped"], t + 1)
                    link(vec.tensor_reduce(den[:, :, :, 0], sc[:], AX, ALU.add))
                    link(vec.reciprocal(den[:], den[:]))
                    link(vec.tensor_tensor(sc[:], sc[:], bc(den[:], full), ALU.mult))
                    link(vec.tensor_tensor(sc[:], sc[:], bc(k.edge_gate[:], full), ALU.add))
                    link(vec.tensor_copy(scn[:], sc[:, :, :, 0:BS]))
                    vec.transpose(sct[:].rearrange("p h b c -> p (h b c)"), scn[:].rearrange("p h b c -> p (h b c)")).then_inc(S["combined"], 1)
                if nxt:
                    keep_keys(t + 1)
                if cur:
                    dve.wait_ge(S["valued"], 2 * t + 1)
                    weight = sc[:, :, :, BS:KEYS].rearrange("p h b c -> p b h c")
                    link(vec.tensor_tensor(node[:], ps[:, 2, 0:256].rearrange("p (b h c) -> p b h c", b=GROUP, h=HEADS),
                                           bc(weight, [P, GROUP, HEADS, HD]), ALU.mult))
                    dve.wait_ge(S["valued"], 2 * t + 2)
                    vec.tensor_tensor(mixed[:, :, 0:D], ps[:, 3, 0:256].rearrange("p (b d) -> p b d", b=GROUP),
                                      node[:].rearrange("p b h c -> p b (h c)"), ALU.add).then_inc(S["mixed_ready"], 1)
                    link.close()

            in_turn(dve, prelude, body)

        @block.scalar
        def _(act):
            def start(t, par):
                act.wait_ge(S["xt_made"], t + 1)
                nc.scalar.copy(xkv[:, 0:TOK], ps[:, 0, :]).then_inc(S["xt_ready"], 1)
                act.wait_ge(S["projected"], 4 * t + 1)
                nc.scalar.copy(q[:].rearrange("p n c -> p (n c)"), ps[:, 1, :]).then_inc(S["q_ready"], 1)
                act.wait_ge(S["projected"], 4 * t + 4)
                nc.scalar.copy(v[:, par], ps[:, 0, 0:256].rearrange("p (b d) -> p b d", b=GROUP)).then_inc(S["v_ready"], 1)

            def body(t, par, cur, prev, nxt):
                if cur:
                    act.wait_ge(S["shifted"], t + 1)
                    nc.scalar.activation(sc[:], sc[:], ACT.Exp).then_inc(S["exped"], 1)
                if nxt:
                    start(t + 1, 1 - par)
                if cur:
                    act.wait_ge(S["mt_made"], t + 1)
                    nc.scalar.copy(mt[:], ps[:, 2, :]).then_inc(S["mt_ready"], 1)

            in_turn(act, lambda: start(0, 0), body)

        @block.tensor
        def _(pe):
            mm = nc.tensor.matmul
            pe.wait_ge(S["loaded"], 16 * 6)
            for n in range(4):
                ins = nc.tensor.transpose(ps[0:A1, 0, n * D:(n + 1) * D], wnat[:, n, :], k.ident[0:D, 0:D])
            ins.then_inc(S["wturned"], 1)
            pe.wait_ge(S["wready"], 1)

            def turn_x(t):
                pe.wait_ge(S["normed"], t + 1)
                if not (isinstance(t, int) and t == 0):
                    pe.wait_ge(S["v_ready"], t)
                for b in range(GROUP):
                    ins = nc.tensor.transpose(ps[:, 0, b * N:(b + 1) * N], xs[:, b, :], k.ident[:])
                ins.then_inc(S["xt_made"], 1)

            def project(t):
                pe.wait_ge(S["xt_ready"], t + 1)
                if not (isinstance(t, int) and t == 0):
                    pe.wait_ge(S["k_ready"], 2 * t)
                mm(ps[:, 1, :], wq[:].rearrange("p h c -> p (h c)"), xkv[:, 0:TOK], start=True, stop=True).then_inc(S["projected"], 1)
                mm(ps[:, 0, :], wk[:].rearrange("p h c -> p (h c)"), xkv[:, 0:TOK], start=True, stop=True).then_inc(S["projected"], 1)
                pe.wait_ge(S["mean_ready"], 2 * t + 2)
                pe.wait_ge(S["q_ready"], t + 1)
                mm(ps[:, 1, 0:GROUP * NB], wk[:].rearrange("p h c -> p (h c)"), xkv[:, TOK:], start=True, stop=True).then_inc(S["projected"], 1)

            def project_values(t):
                pe.wait_ge(S["k_ready"], 2 * t + 1)
                for b in range(GROUP):
                    ins = mm(ps[:, 0, b * D:(b + 1) * D], xkv[:, b * N:(b + 1) * N], wv[:], start=True, stop=True)
                ins.then_inc(S["projected"], 1)

            def scores(t, first):
                if first == 0:
                    if not (isinstance(t, int) and t == 0):
                        pe.wait_ge(S["shifted"], t)
                    pe.wait_ge(S["k_ready"], 2 * t + 2)
                    nc.tensor.sem_inc(S["apart"], 1)
                for b in range(first, first + 2):
                    for n in range(NB):
                        for h in range(HEADS):
                            ins = mm(ps[n * BS:(n + 1) * BS, 4 + h, b * KEYS:(b + 1) * KEYS],
                                     q[32 * h:32 * h + 32, b * NB + n, :], kk[32 * h:32 * h + 32, b * NB + n, :],
                                     start=True, stop=True, tile_position=(32 * h, n * BS))
                if first:
                    ins.then_inc(S["scored"], 1)

            def prelude():
                turn_x(0)
                project(0)
                project_values(0)
                scores(0, 0)
                scores(0, 2)

            def means(t, par):
                pe.wait_ge(S["v_ready"], t + 1)
                mm(ps[:, 2, 0:256], blockmean[:], v[:, par].rearrange("p b d -> p (b d)"), start=True, stop=True).then_inc(S["valued"], 1)

            def values(t, par):
                pe.wait_ge(S["combined"], t + 1)
                nc.tensor.sem_inc(S["apart"], 1)
                for b in range(GROUP):
                    for h in range(HEADS):
                        for n in range(NB):
                            r = slice(n * BS, (n + 1) * BS)
                            ins = mm(ps[r, 3, b * D + h * HD:b * D + (h + 1) * HD], sct[r, h, b, :], v[r, par, b, h * HD:(h + 1) * HD],
                                     start=True, stop=True, tile_position=(n * BS, n * BS))
                ins.then_inc(S["valued"], 1)

            def body(t, par, cur, prev, nxt):
                if cur:
                    means(t, par)
                if nxt:
                    turn_x(t + 1)
                    project(t + 1)
                if cur:
                    values(t, par)
                if nxt:
                    project_values(t + 1)
                    scores(t + 1, 0)
                if cur:
                    pe.wait_ge(S["mixed_ready"], t + 1)
                    for b in range(GROUP):
                        ins = nc.tensor.transpose(ps[:, 2, b * N:(b + 1) * N], mixed[:, b, :], k.ident[:])
                    ins.then_inc(S["mt_made"], 1)
                if nxt:
                    scores(t + 1, 2)
                if cur:
                    pe.wait_ge(S["mt_ready"], t + 1)
                    for b in range(GROUP):
                        ins = mm(ps[:, 3, b * D:(b + 1) * D], mt[:, b * N:(b + 1) * N], wo[:], start=True, stop=True)
                    ins.then_inc(S["outed"], 1)

            in_turn(pe, prelude, body)


def stage_l1_ffn(k):
    nc, w = k.nc, k.w
    HEADS, SETS, HD, HP = 4, 4, 16, 32
    UNITS = GROUP * SETS
    OC = HEADS * (HD + 1)
    BC = OC + HEADS * SETS
    with Scope(nc, "l1f") as s:
        wq = s.sb("wq", [P, SETS, HEADS, HP])
        wk = s.sb("wk", [P, HEADS, HP])
        wsx = s.sb("wsx", [P, HEADS, HP])
        wv = s.sb("wv", [P, D])
        fc1 = s.sb("fc1", [P, D])
        fc2 = s.sb("fc2", [P, D])
        pick = s.sb("pick", [P, SETS, BC])
        fgate_w = s.sb("fgate_w", [P, HEADS])
        gate_b = s.sb("gate_b", [P, 1, HEADS * SETS])
        norms = s.sb("norms", [P, 4, 1, D])
        causal = s.sb("causal", [P, 4, N], BF16)
        identb = s.sb("identb", [P, P], BF16)
        resid = s.sb("resid", [P, HEADS, HD])
        nhalf = s.sb("nhalf", [P, GROUP * HEADS, 1])
        fold_l1_ffn(k, wq, wk, wsx, wv, fc1, fc2, pick, fgate_w, gate_b, norms, causal, identb, resid, nhalf)
        xs = s.sb("xs", [P, GROUP, P])
        xt = s.sb("xt", [P, TOK])
        q = s.sb("q", [P, 2, SETS, TOK])
        keys = s.sb("keys", [P, 2, GROUP, HEADS, N])
        live = s.sb("live", [P, 2, GROUP, 1, N])
        v = s.sb("v", [P, 2, GROUP, HEADS, HP])
        top = s.sb("top", [P, 4, 4])
        probs = s.sb("probs", [P, 4, 4, N])
        probs_t = s.sb("probs_t", [P, 2, 4, N])
        ot = s.sb("ot", [P, SETS, N])
        rden = s.sb("rden", [P, GROUP, HEADS, 1, SETS])
        out = s.sb("out", [P, GROUP, HEADS, SETS, HD])
        gate = s.sb("gate", [P, GROUP, HEADS, SETS, SETS])
        gs = s.sb("gs", [P, GROUP * HEADS, SETS, 1])
        gtop = s.sb("gtop", [P, GROUP * HEADS, 1])
        fx = s.sb("fx", [P, GROUP, P])
        fh = s.sb("fh", [P, GROUP * HEADS, HD])
        sq = s.sb("sq", [P, GROUP * HEADS, HD])
        mom = s.sb("mom", [P, GROUP * HEADS, 1])
        var = s.sb("var", [P, GROUP * HEADS, 1])
        rstd = s.sb("rstd", [P, GROUP * HEADS, 1])
        nz = s.sb("nz", [P, GROUP, D])
        fx_t = s.sb("fx_t", [P, TOK])
        nz_t = s.sb("nz_t", [D, TOK])
        h1_t = s.sb("h1_t", [P, TOK])
        fo_t = s.sb("fo_t", [P, TOK])
        fg = s.sb("fg", [P, GROUP, HEADS, 1])
        ftop = s.sb("ftop", [P, GROUP, 1])
        ps = s.ps("ps", [P, 8, 512])
        SC, TU, OT, BACK, X, Y = 0, 2, 4, 5, 6, 7
        names = ("step ready normed xt_made xt_ready projected q_ready k_ready live_ready v_ready scored topped exped turned "
                 "even_ready odd_ready valued ot_ready back out_ready gs_shifted gs_exped var_ready rooted fx_ready fx_made fx_t_ready "
                 "h1_made h1_ready h2_made fo_ready fo_made fo_t_ready fg_made fg_shifted fg_exped added apart").split()
        S = {n: s.sem(n) for n in names}
        block = s.block()

        def copied(u):
            return ("even_ready", "odd_ready")[u % 2]

        def heads(flat):
            return flat.rearrange("p (h n) -> p h n", h=4)

        def seqs(flat):
            return flat.rearrange("p (b n) -> p b n", b=GROUP)

        def started(t, u, back):
            return not (isinstance(t, int) and t == 0 and u < back)

        @block.gpsimd
        def _(pool):
            nc.gpsimd.memset(v[:], 0.0).then_inc(S["v_ready"], 1)
            pool.wait_ge(S["v_ready"], 1)
            nc.gpsimd.memset(v[:, :, :, :, HD:HD + 1], 1.0).then_inc(S["v_ready"], 1)
            with pool.Fori(0, GROUPS) as t:
                for j in range(2):
                    pool.wait_ge(S["var_ready"], 2 * t + j + 1)
                    nc.gpsimd.tensor_tensor(rstd[:], var[:], nhalf[:], ALU.pow).then_inc(S["rooted"], 1)

        @block.vector
        def _(dve):
            vec = nc.vector
            start = Link(dve, S["step"])
            vec.memset(xs[:], 0.0)
            vec.memset(fx[:], 0.0)
            vec.memset(h1_t[:], 0.0)
            start(vec.memset(keys[:], 0.0))
            vec.memset(xs[:, :, D:D + 1], 1.0)
            vec.memset(fx[:, :, D:D + 1], 1.0)
            start(vec.memset(h1_t[D:D + 1, :], 1.0))
            vec.sem_inc(S["ready"], 1)
            PER = 40
            f4 = fh[:].rearrange("p (b h) c -> p b (h c)", b=GROUP)
            wide = [P, GROUP, D]
            full = [P, GROUP * HEADS, HD]

            def keep_keys(t, par):
                dve.wait_ge(S["projected"], 7 * t + 5)
                for h in range(2):
                    r = slice(HP * h, HP * h + HD)
                    ins = vec.tensor_copy(keys[r, par, :, h, :], seqs(ps[r, X, :]))
                ins.then_inc(S["k_ready"], 1)

            def keep_live(t, par):
                dve.wait_ge(S["projected"], 7 * t + 6)
                vec.tensor_scalar(live[:, par].rearrange("p b o n -> p (b o n)"), ps[:, X, :], 0.0, None, ALU.not_equal).then_inc(S["live_ready"], 1)

            def prelude():
                front_dve(k, dve, xs[:], 0, S["normed"])
                keep_keys(0, 0)
                keep_live(0, 0)

            def maximum(t, u):
                dve.wait_ge(S["scored"], UNITS * t + u + 1)
                vec.tensor_reduce(top[:, u % 4], heads(ps[:, SC + u % 2, :]), AX, ALU.max, negate=True).then_inc(S["topped"], 1)

            def keep_turned(t, u):
                dve.wait_ge(S["turned"], UNITS * t + u + 1)
                if started(t, u, 2):
                    dve.wait_ge(S["valued"], UNITS * t + u - 1)
                vec.tensor_copy(probs_t[:, u % 2], heads(ps[:, TU + u % 2, :])).then_inc(S["even_ready"], 1)

            def keep_output(t, par, b):
                dve.wait_ge(S["valued"], UNITS * t + SETS * (b + 1))
                if started(t, b, 1):
                    dve.wait_ge(S["back"], GROUP * t + b)
                dve.wait_ge(S["live_ready"], t + 1)
                vec.tensor_tensor(ot[:], ps[:, OT, :].rearrange("p (e n) -> p e n", e=SETS), bc(live[:, par, b], [P, SETS, N]),
                                  ALU.mult).then_inc(S["ot_ready"], 1)

            def normalize(t, b, link):
                dve.wait_ge(S["back"], GROUP * t + b + 1)
                o = ps[:, BACK, 0:SETS * BC].rearrange("p (e c) -> p e c", e=SETS)
                chans = o[:, :, 0:OC].rearrange("p e (h c) -> p h e c", h=HEADS)
                link(vec.reciprocal(rden[:, b, :, 0, :], chans[:, :, :, HD]))
                vec.tensor_tensor(out[:, b], chans[:, :, :, 0:HD],
                                  bc(rden[:, b].rearrange("p h o e -> p h e o"), [P, HEADS, SETS, HD]), ALU.mult)
                link(vec.tensor_tensor(gate[:, b], o[:, :, OC:BC].rearrange("p e (h g) -> p h g e", h=HEADS),
                                       bc(rden[:, b], [P, HEADS, SETS, SETS]), ALU.mult))
                vec.sem_inc(S["out_ready"], 1)

            def gate_shift(t, link):
                gflat = gs[:].rearrange("p m e o -> p (m e o)")
                link(vec.tensor_reduce(gflat, gate[:].rearrange("p b h g e -> p (b h g) e"), AX, ALU.add))
                g3 = gflat.rearrange("p (b g) -> p b g", b=GROUP)
                link(vec.tensor_tensor(g3, g3, bc(gate_b[:], [P, GROUP, HEADS * SETS]), ALU.add))
                link(vec.tensor_reduce(gtop[:, :, 0], gs[:, :, :, 0], AX, ALU.max))
                vec.tensor_tensor(gs[:, :, :, 0], gs[:, :, :, 0], bc(gtop[:], [P, 16, SETS]), ALU.subtract).then_inc(S["gs_shifted"], 1)

            def moments(j, t, link):
                link(vec.tensor_reduce(mom[:, :, 0], fh[:], AX, ALU.add))
                link(vec.tensor_scalar(mom[:], mom[:], 1.0 / HD, None, ALU.mult))
                link(vec.tensor_tensor(fh[:], fh[:], bc(mom[:], full), ALU.subtract))
                link(vec.tensor_tensor(sq[:], fh[:], fh[:], ALU.mult))
                link(vec.tensor_reduce(var[:, :, 0], sq[:], AX, ALU.add))
                vec.tensor_scalar(var[:], var[:], 1.0 / HD, 1e-8, ALU.mult, ALU.add).then_inc(S["var_ready"], 1)

            def scale(j, t, dst, link):
                dve.wait_ge(S["rooted"], 2 * t + j + 1)
                link(vec.tensor_tensor(fh[:], fh[:], bc(rstd[:], full), ALU.mult))
                link(vec.tensor_tensor(f4, f4, bc(norms[:, 2 * j], wide), ALU.mult))
                return vec.tensor_tensor(dst, f4, bc(norms[:, 2 * j + 1], wide), ALU.add)

            def weigh_sets(t, link):
                dve.wait_ge(S["gs_exped"], t + 1)
                link(vec.tensor_reduce(gtop[:, :, 0], gs[:, :, :, 0], AX, ALU.add))
                link(vec.reciprocal(gtop[:], gtop[:]))
                link(vec.tensor_tensor(gs[:, :, :, 0], gs[:, :, :, 0], bc(gtop[:], [P, 16, SETS]), ALU.mult))
                om = out[:].rearrange("p b h e c -> p (b h) e c")
                link(vec.tensor_tensor(om, om, bc(gs[:], [P, 16, SETS, HD]), ALU.mult))

            def mix(t, link):
                om = out[:].rearrange("p b h e c -> p (b h) e c")
                link(vec.tensor_reduce(fh[:], om.rearrange("p m e c -> p m c e"), AX, ALU.add))
                link(vec.tensor_tensor(f4, f4, bc(resid[:].rearrange("p (o h) c -> p o (h c)", o=1), wide), ALU.add))

            def relu(t, link):
                link(vec.tensor_scalar(nz[:], fx[:, :, 0:D], 0.0, None, ALU.not_equal))
                dve.wait_ge(S["fx_t_ready"], t + 1)
                link(vec.tensor_scalar(nz_t[:], fx_t[0:D, :], 0.0, None, ALU.not_equal))
                dve.wait_ge(S["h1_made"], t + 1)
                vec.scalar_tensor_tensor(out=h1_t[0:D, :], in0=ps[0:D, Y, :], scalar=0.0, in1=nz_t[:],
                                         op0=ALU.max, op1=ALU.mult).then_inc(S["h1_ready"], 1)

            def add_mlp(t, link):
                dve.wait_ge(S["h2_made"], t + 1)
                link(vec.tensor_tensor(f4, seqs(ps[:, Y, 0:GROUP * D]), nz[:], ALU.mult))
                link(vec.tensor_tensor(f4, f4, fx[:, :, 0:D], ALU.add))

            def head_shift(t, link):
                dve.wait_ge(S["fg_made"], t + 1)
                scores = seqs(ps[:, Y, 0:GROUP * HEADS])
                link(vec.tensor_reduce(ftop[:, :, 0], scores, AX, ALU.max))
                vec.tensor_tensor(fg[:, :, :, 0], scores, bc(ftop[:], [P, GROUP, HEADS]), ALU.subtract).then_inc(S["fg_shifted"], 1)

            def add(t, link):
                dve.wait_ge(S["fg_exped"], t + 1)
                link(vec.tensor_reduce(ftop[:, :, 0], fg[:, :, :, 0], AX, ALU.add))
                link(vec.reciprocal(ftop[:], ftop[:]))
                link(vec.tensor_tensor(fg[:, :, :, 0], fg[:, :, :, 0], bc(ftop[:], [P, GROUP, HEADS]), ALU.mult))
                link(vec.tensor_tensor(sq[:].rearrange("p (b h) c -> p b h c", b=GROUP), fx[:, :, 0:D].rearrange("p b (h c) -> p b h c", h=HEADS), bc(fg[:], [P, GROUP, HEADS, HD]), ALU.mult))
                g = bass.ds(GROUP * t, GROUP)
                vec.tensor_tensor(k.h[:, g, :], k.h[:, g, :], sq[:].rearrange("p (b h) c -> p b (h c)", b=GROUP), ALU.add).then_inc(S["added"], 1)

            def body(t, par, cur, prev, nxt, old):
                own = Link(dve, S["step"], 2 + PER * t)
                for u in range(UNITS):
                    if cur:
                        maximum(t, u)
                    if u >= 2 and u % 2 == 0 and cur:
                        keep_turned(t, u - 2)
                    if u == 0 and prev:
                        keep_turned(t - 1, UNITS - 2)
                    if u == 3 and nxt:
                        front_dve(k, dve, xs[:], t + 1, S["normed"])
                    if u == 9 and nxt:
                        keep_keys(t + 1, 1 - par)
                    if u == 10 and nxt:
                        keep_live(t + 1, 1 - par)
                    if u in (6, 10, 14) and cur:
                        keep_output(t, par, u // 4 - 1)
                    if u == 2 and prev:
                        keep_output(t - 1, 1 - par, GROUP - 1)
                    if u in (8, 12) and cur:
                        normalize(t, u // 4 - 2, own)
                    if u == 0 and prev:
                        normalize(t - 1, GROUP - 2, own)
                    if u == 4 and prev:
                        normalize(t - 1, GROUP - 1, own)
                        gate_shift(t - 1, own)
                    if u == 5 and prev:
                        weigh_sets(t - 1, own)
                    if u == 6 and prev:
                        mix(t - 1, own)
                    if u == 7 and prev:
                        moments(0, t - 1, own)
                    if u == 9 and prev:
                        scale(0, t - 1, fx[:, :, 0:D], own).then_inc(S["fx_ready"], 1)
                        dve.wait_ge(S["fx_ready"], t)
                    if u == 11 and prev:
                        relu(t - 1, own)
                    if u == 12 and prev:
                        add_mlp(t - 1, own)
                    if u == 13 and prev:
                        moments(1, t - 1, own)
                    if u == 15 and prev:
                        scale(1, t - 1, fx[:, :, 0:D], own).then_inc(S["fo_ready"], 1)
                        dve.wait_ge(S["fo_ready"], t)
                    if u == 1 and old:
                        head_shift(t - 2, own)
                    if u == 3 and old:
                        add(t - 2, own)
                if isinstance(t, int):
                    vec.sem_inc(S["step"], PER - own.n) if own.n < PER else None
                else:
                    assert own.n == PER, own.n

            in_turn(dve, prelude, body, older=True)

        @block.scalar
        def _(act):
            act.wait_ge(S["v_ready"], 2)
            act.wait_ge(S["ready"], 1)

            def keep_x(t):
                act.wait_ge(S["xt_made"], t + 1)
                nc.scalar.copy(xt[:], ps[:, X, :]).then_inc(S["xt_ready"], 1)

            def keep_q(t, par, e):
                act.wait_ge(S["projected"], 7 * t + e + 1)
                nc.scalar.copy(q[:, par, e, :], ps[:, X, :]).then_inc(S["q_ready"], 1)

            def keep_keys(t, par):
                act.wait_ge(S["projected"], 7 * t + 5)
                for h in range(2, 4):
                    r = slice(HP * h, HP * h + HD)
                    ins = nc.scalar.copy(keys[r, par, :, h, :], seqs(ps[r, X, :]))
                ins.then_inc(S["k_ready"], 1)

            def keep_v(t, par):
                act.wait_ge(S["projected"], 7 * t + 7)
                nc.scalar.copy(v[:, par, :, :, 0:HD], ps[:, X, 0:GROUP * D].rearrange("p (b h c) -> p b h c", b=GROUP, c=HD)).then_inc(S["v_ready"], 1)

            def prelude():
                keep_x(0)
                for e in range(SETS):
                    keep_q(0, 0, e)
                keep_keys(0, 0)
                keep_v(0, 0)

            def keep_turned(t, u):
                act.wait_ge(S["turned"], UNITS * t + u + 1)
                if started(t, u, 2):
                    act.wait_ge(S["valued"], UNITS * t + u - 1)
                nc.scalar.copy(probs_t[:, u % 2], heads(ps[:, TU + u % 2, :])).then_inc(S["odd_ready"], 1)

            def exponential(t, u):
                act.wait_ge(S["topped"], UNITS * t + u + 1)
                if started(t, u, 4):
                    act.wait_ge(S["turned"], UNITS * t + u - 3)
                for h in range(4):
                    ins = nc.scalar.activation(probs[:, u % 4, h], ps[:, SC + u % 2, h * N:(h + 1) * N], ACT.Exp, bias=top[:, u % 4, h:h + 1])
                ins.then_inc(S["exped"], 1)

            def body(t, par, cur, prev, nxt, old):
                for u in range(UNITS):
                    if u == 5 and prev:
                        act.wait_ge(S["gs_shifted"], t)
                        nc.scalar.activation(gs[:], gs[:], ACT.Exp).then_inc(S["gs_exped"], 1)
                    if u == 2 and old:
                        act.wait_ge(S["fg_shifted"], t - 1)
                        nc.scalar.activation(fg[:], fg[:], ACT.Exp).then_inc(S["fg_exped"], 1)
                    if cur:
                        exponential(t, u)
                    if u >= 2 and u % 2 == 1 and cur:
                        keep_turned(t, u - 2)
                    if u == 1 and prev:
                        keep_turned(t - 1, UNITS - 1)
                    if u == 4 and nxt:
                        keep_x(t + 1)
                    if 5 <= u <= 8 and nxt:
                        keep_q(t + 1, 1 - par, u - 5)
                    if u == 9 and nxt:
                        keep_keys(t + 1, 1 - par)
                    if u == 11 and nxt:
                        keep_v(t + 1, 1 - par)
                    if u == 10 and prev:
                        act.wait_ge(S["fx_made"], t)
                        nc.scalar.copy(fx_t[:], ps[:, Y, :]).then_inc(S["fx_t_ready"], 1)
                    if u == 0 and old:
                        act.wait_ge(S["fo_made"], t - 1)
                        nc.scalar.copy(fo_t[:], ps[:, Y, :]).then_inc(S["fo_t_ready"], 1)

            in_turn(act, prelude, body, older=True)

        @block.tensor
        def _(pe):
            mm = nc.tensor.matmul

            def turn_x(t):
                pe.wait_ge(S["normed"], t + 1)
                if started(t, 0, 1):
                    pe.wait_ge(S["v_ready"], t + 2)
                for b in range(GROUP):
                    ins = nc.tensor.transpose(ps[:, X, b * N:(b + 1) * N], xs[:, b, :], k.ident[:])
                ins.then_inc(S["xt_made"], 1)

            def project(t, n):
                if n == 0:
                    pe.wait_ge(S["xt_ready"], t + 1)
                elif n <= 4:
                    pe.wait_ge(S["q_ready"], 4 * t + n)
                elif n == 5:
                    pe.wait_ge(S["k_ready"], 2 * t + 2)
                else:
                    pe.wait_ge(S["live_ready"], t + 1)
                if n < 6:
                    wt = wq[:, n] if n < 4 else (wk, wsx)[n - 4][:]
                    ins = mm(ps[:, X, :], wt.rearrange("p h c -> p (h c)"), xt[:], start=True, stop=True)
                else:
                    for b in range(GROUP):
                        ins = mm(ps[:, X, b * D:(b + 1) * D], xt[:, b * N:(b + 1) * N], wv[:], start=True, stop=True)
                ins.then_inc(S["projected"], 1)

            def prelude():
                pe.wait_ge(S["ready"], 1)
                turn_x(0)
                for n in range(7):
                    project(0, n)

            def scores(t, par, u):
                b, e = u // SETS, u % SETS
                if u == 0:
                    pe.wait_ge(S["q_ready"], 4 * t + 4)
                    pe.wait_ge(S["k_ready"], 2 * t + 2)
                if started(t, u, 2):
                    pe.wait_ge(S["exped"], UNITS * t + u - 1)
                mm(ps[:, SC + u % 2, :], identb[:], causal[:].rearrange("p h n -> p (h n)"), start=True, stop=False)
                mm(ps[:, SC + u % 2, :], q[:, par, e, b * N:(b + 1) * N], keys[:, par, b].rearrange("p h n -> p (h n)"),
                   start=False, stop=True).then_inc(S["scored"], 1)

            def turn(t, u):
                pe.wait_ge(S["exped"], UNITS * t + u + 1)
                if started(t, u, 2):
                    pe.wait_ge(S[copied(u)], UNITS // 2 * t + u // 2)
                for h in range(4):
                    ins = nc.tensor.transpose(ps[:, TU + u % 2, h * N:(h + 1) * N], probs[:, u % 4, h], k.ident[:])
                ins.then_inc(S["turned"], 1)

            def values(t, par, u):
                b, e = u // SETS, u % SETS
                pe.wait_ge(S[copied(u)], UNITS // 2 * t + u // 2 + 1)
                if u == 0:
                    pe.wait_ge(S["v_ready"], t + 3)
                if e == 0 and started(t, b, 1):
                    pe.wait_ge(S["ot_ready"], GROUP * t + b)
                nc.tensor.sem_inc(S["apart"], 1)
                for h in range(4):
                    ins = mm(ps[HP * h:HP * h + HP, OT, e * N:(e + 1) * N], v[:, par, b, h, :], probs_t[:, u % 2, h],
                             start=True, stop=True, tile_position=(0, HP * h))
                ins.then_inc(S["valued"], 1)

            def turn_back(t, b):
                pe.wait_ge(S["ot_ready"], GROUP * t + b + 1)
                if started(t, b, 1):
                    pe.wait_ge(S["out_ready"], GROUP * t + b)
                for e in range(SETS):
                    ins = mm(ps[:, BACK, e * BC:(e + 1) * BC], ot[:, e], pick[:, e], start=True, stop=True)
                ins.then_inc(S["back"], 1)

            def turn_rows(t, made, ready):
                pe.wait_ge(S[ready], t + 1)
                for b in range(GROUP):
                    ins = nc.tensor.transpose(ps[:, Y, b * N:(b + 1) * N], fx[:, b, :], k.ident[:])
                ins.then_inc(S[made], 1)

            def body(t, par, cur, prev, nxt, old):
                for u in range(UNITS):
                    if cur:
                        scores(t, par, u)
                    if u >= 2 and cur:
                        turn(t, u - 2)
                    if u < 2 and prev:
                        turn(t - 1, UNITS + u - 2)
                    if u >= 3 and cur:
                        values(t, par, u - 3)
                    if u < 3 and prev:
                        values(t - 1, 1 - par, UNITS + u - 3)
                    if u == 4 and nxt:
                        turn_x(t + 1)
                    if 5 <= u <= 11 and nxt:
                        project(t + 1, u - 5)
                    if u in (7, 11, 15) and cur:
                        turn_back(t, u // 4 - 1)
                    if u == 3 and prev:
                        turn_back(t - 1, GROUP - 1)
                    if u == 10 and prev:
                        turn_rows(t - 1, "fx_made", "fx_ready")
                    if u == 11 and prev:
                        pe.wait_ge(S["fx_t_ready"], t)
                        mm(ps[0:D, Y, :], fc1[:], fx_t[:], start=True, stop=True).then_inc(S["h1_made"], 1)
                    if u == 12 and prev:
                        pe.wait_ge(S["h1_ready"], t)
                        for b in range(GROUP):
                            ins = mm(ps[:, Y, b * D:(b + 1) * D], h1_t[:, b * N:(b + 1) * N], fc2[:], start=True, stop=True)
                        ins.then_inc(S["h2_made"], 1)
                    if u == 0 and old:
                        turn_rows(t - 2, "fo_made", "fo_ready")
                    if u == 1 and old:
                        pe.wait_ge(S["fo_t_ready"], t - 1)
                        for b in range(GROUP):
                            ins = mm(ps[:, Y, b * HEADS:(b + 1) * HEADS], fo_t[:, b * N:(b + 1) * N], fgate_w[:], start=True, stop=True)
                        ins.then_inc(S["fg_made"], 1)

            in_turn(pe, prelude, body, older=True)


def fold_l1_ffn(k, wq, wk, wsx, wv, fc1, fc2, pick, fgate_w, gate_b, norms, causal, identb, resid, nhalf):
    nc, w = k.nc, k.w
    HEADS, SETS, HD, HP, A1 = 4, 4, 16, 32, D + 1
    OC = HEADS * (HD + 1)
    with Scope(nc, "l1fold") as s:
        hl = s.sb("hl", [D, A1])
        nat = s.sb("nat", [D, 8, D])
        turned = s.sb("turned", [D, 8, D])
        fgnat = s.sb("fgnat", [HEADS, D])
        gnat = s.sb("gnat", [HEADS * SETS, SETS, P])
        xs = s.sb("xs", [P, HEADS, A1])
        xt = s.sb("xt", [A1, TOK])
        sx = s.sb("sx", [A1, D])
        maskf = s.sb("maskf", [P, 4, N])
        ps = s.ps("ps", [P, 8, 512])
        zeroed, loaded, step, made, ready, masked = (s.sem(n) for n in "zeroed loaded step made ready masked".split())
        center_vector, center_scalar = center_parts(k, s)
        block = s.block()
        LOADS = 2 + HEADS * (SETS + 7 + 4) + 2

        def load_heads(eng, ns):
            for n in ns:
                r = slice(n * HD, (n + 1) * HD)
                for e in range(SETS):
                    eng.dma_start(nat[r, e, r], w["L1_ffn_wq"][n, e]).then_inc(loaded, 16)
                for m, name in ((4, "wk"), (5, "wv")):
                    eng.dma_start(nat[r, m, r], w[f"L1_ffn_{name}"][n]).then_inc(loaded, 16)
                for m, name in ((6, "fc1_w"), (7, "fc2_w")):
                    eng.dma_start(nat[r, m, r], w[f"L1_ffn_{name}"]).then_inc(loaded, 16)
                eng.dma_start(gnat[n * SETS:(n + 1) * SETS, :, n * HP:n * HP + HD],
                              w["L1_ffn_gate_w"][n].rearrange("g (e c) -> g e c", e=SETS)).then_inc(loaded, 16)
                for fc, name in ((fc1, "fc1_b"), (fc2, "fc2_b")):
                    eng.dma_start(fc[D:A1, r], w[f"L1_ffn_{name}"].rearrange("(o d) -> o d", o=1)).then_inc(loaded, 16)
                for m, name in enumerate(("ln_g", "ln_b", "fnorm_g", "fnorm_b")):
                    eng.dma_start(norms[:, m, 0, r], w[f"L1_ffn_{name}"].partition_broadcast(P)).then_inc(loaded, 16)

        @block.sync
        def _(sp):
            sp.wait_ge(zeroed, 1)
            sp.dma_start(hl[:, 0:D], w["L1_ffn_hl_w"].rearrange("n d i -> (n d) i")).then_inc(loaded, 16)
            sp.dma_start(hl[:, D:A1], w["L1_ffn_hl_b"].rearrange("n (d u) -> (n d) u", u=1)).then_inc(loaded, 16)
            load_heads(sp, (0, 1, 2))

        @block.scalar
        def _(act):
            act.wait_ge(zeroed, 1)
            center_scalar(act)
            load_heads(act, (3,))
            act.dma_start(fgnat[:], w["L1_ffn_fgate_w"]).then_inc(loaded, 16)
            act.dma_start(gate_b[:, 0, :], w["L1_ffn_gate_b"].rearrange("n e -> (n e)").partition_broadcast(P)).then_inc(loaded, 16)

        @block.gpsimd
        def _(pool):
            link = Link(pool, masked)
            link(nc.gpsimd.memset(maskf[:], 0.0))
            link(nc.gpsimd.affine_select(out=maskf[:], in_=maskf[:], compare_op=ALU.is_ge, fill=MASKED, base=0,
                                         pattern=[[0, 4], [-1, N]], channel_multiplier=1))

        @block.vector
        def _(dve):
            vec = nc.vector
            link = Link(dve, step)
            for buf in (nat, gnat, pick, fc1, fc2, wq, wk, wsx, wv, fgate_w):
                ins = vec.memset(buf[:], 0.0)
            link(ins)
            vec.sem_inc(zeroed, 1)
            center_vector(dve)
            for e in range(SETS):
                vec.tensor_copy(pick[:, e, 0:OC].rearrange("p (h c) -> p h c", h=HEADS), k.ident[:].rearrange("p (h c) -> p h c", h=HEADS)[:, :, 0:HD + 1])
            link(vec.memset(nhalf[:], -0.5))
            link(vec.tensor_copy(identb[:], k.ident[:]))
            link(vec.memset(xs[:, :, D:A1], 1.0))
            link(vec.tensor_tensor(xs[:, :, 0:D], k.xc[:, 0:HEADS, :], bc(k.rstd[:, 0:HEADS, :], [P, HEADS, D]), ALU.mult))
            vec.sem_inc(ready, 1)
            dve.wait_ge(masked, 2)
            link(vec.tensor_copy(causal[:], maskf[:]))
            dve.wait_ge(made, 1)
            link(vec.tensor_copy(turned[:], ps[0:D, 0, :].rearrange("p (n c) -> p n c", n=8)))
            link(vec.tensor_copy(fc1[0:D, :], ps[0:D, 0, 6 * D:7 * D]))
            link(vec.tensor_copy(fc2[0:D, :], ps[0:D, 0, 7 * D:8 * D]))
            link(vec.tensor_copy(sx[:], ps[0:A1, 1, 0:D]))
            link(vec.tensor_copy(wsx[0:A1, :, 0:HD], ps[0:A1, 1, 0:D].rearrange("p (h c) -> p h c", h=HEADS)))
            link(vec.memset(wsx[D:A1, :, HD:HD + 1], 1.0))
            link(vec.tensor_copy(fgate_w[0:D, :], ps[0:D, 3, 0:HEADS]))
            link(vec.tensor_copy(pick[:, :, OC:], ps[:, 2, 0:4 * HEADS * SETS].rearrange("p (e m) -> p e m", e=SETS)))
            link(vec.tensor_copy(xt[:], ps[0:A1, 4, :]))
            vec.sem_inc(ready, 1)
            dve.wait_ge(made, 2)
            f = ps[0:A1, 5, 0:6 * D].rearrange("p (n h c) -> p n h c", n=6, h=HEADS)
            link(vec.tensor_scalar(wq[0:A1, :, :, 0:HD], f[:, 0:4], HD ** 0.5, None, ALU.mult))
            link(vec.tensor_copy(wk[0:A1, :, 0:HD], f[:, 4]))
            link(vec.tensor_copy(wv[0:A1, :], ps[0:A1, 5, 5 * D:6 * D]))
            for n in range(HEADS):
                link(vec.tensor_copy(resid[:, n, :], ps[:, 6, n * D + n * HD:n * D + (n + 1) * HD]))

        @block.tensor
        def _(pe):
            mm = nc.tensor.matmul
            pe.wait_ge(loaded, 16 * LOADS)
            pe.wait_ge(ready, 1)
            for n in range(8):
                nc.tensor.transpose(ps[0:D, 0, n * D:(n + 1) * D], nat[:, n, :], k.ident[0:D, 0:D])
            nc.tensor.transpose(ps[0:A1, 1, 0:D], hl[:], k.ident[0:D, 0:D])
            nc.tensor.transpose(ps[0:D, 3, 0:HEADS], fgnat[:], k.ident[0:HEADS, 0:HEADS])
            for e in range(SETS):
                nc.tensor.transpose(ps[:, 2, 16 * e:16 * e + 16], gnat[:, e, :], k.ident[0:16, 0:16])
            for b in range(HEADS):
                ins = nc.tensor.transpose(ps[0:A1, 4, b * N:(b + 1) * N], xs[:, b, :], k.ident[:])
            ins.then_inc(made, 1)
            pe.wait_ge(ready, 2)
            mm(ps[0:A1, 5, 0:6 * D], hl[:], turned[:, 0:6].rearrange("p n c -> p (n c)"), start=True, stop=True)
            for b in range(HEADS):
                ins = mm(ps[:, 6, b * D:(b + 1) * D], xt[:, b * N:(b + 1) * N], sx[:], start=True, stop=True)
            ins.then_inc(made, 1)


def stage_l2_attn(k):
    nc, w = k.nc, k.w
    HEADS, HD = 8, 64
    PAIRS = HEADS // 2
    UNITS = GROUP * 2
    with Scope(nc, "l2a") as s:
        pair_map = s.sb("pair_map", [P, HEADS, HD])
        value_map = s.sb("value_map", [P, HEADS, D])
        with Scope(nc, "l2fold") as s1:
            nat = s1.sb("nat", [D, 4, HEADS, HD])
            turned = s1.sb("turned", [D, 4, HEADS, HD])
            ps = s1.ps("ps", [P, 8, 512])
            loaded, step, made, ready = (s1.sem(n) for n in "loaded step made ready".split())
            center_vector, center_scalar = center_parts(k, s1)
            block = s1.block()

            @block.scalar
            def _(act):
                center_scalar(act)

            @block.sync
            def _(sp):
                for n, name in enumerate(("q", "k", "v", "out")):
                    sp.dma_start(nat[:, n], w[f"L2_attn_weight_{name}"]).then_inc(loaded, 16)

            @block.tensor
            def _(pe):
                pe.wait_ge(loaded, 64)
                for n in range(4):
                    for h in range(HEADS):
                        ins = nc.tensor.transpose(ps[0:D, n, h * HD:(h + 1) * HD], nat[:, n, h], k.ident[0:D, 0:D])
                ins.then_inc(made, 1)
                pe.wait_ge(ready, 1)
                for h in range(HEADS):
                    nc.tensor.matmul(ps[0:D, 4, h * HD:(h + 1) * HD], turned[:, 0, h], turned[:, 1, h], start=True, stop=True)
                    ins = nc.tensor.matmul(ps[0:D, 5, h * HD:(h + 1) * HD], turned[:, 2, h], turned[:, 3, h], start=True, stop=True)
                ins.then_inc(made, 1)

            @block.vector
            def _(dve):
                link = Link(dve, step)
                nc.vector.memset(pair_map[D:P], 0.0)
                link(nc.vector.memset(value_map[D:P], 0.0))
                center_vector(dve)
                dve.wait_ge(made, 1)
                for n in range(4):
                    link(nc.vector.tensor_copy(turned[:, n], ps[0:D, n, :].rearrange("p (h c) -> p h c", h=HEADS)))
                nc.vector.sem_inc(ready, 1)
                dve.wait_ge(made, 2)
                link(nc.vector.tensor_scalar(pair_map[0:D], ps[0:D, 4, :].rearrange("p (h c) -> p h c", h=HEADS), HD ** -0.5, None, ALU.mult))
                link(nc.vector.tensor_copy(value_map[0:D], ps[0:D, 5, :].rearrange("p (h c) -> p h c", h=HEADS)))

        xs = s.sb("xs", [P, GROUP, 2, D])
        xh = s.sb("xh", [P, 2, 2, TOK])
        xm = s.sb("xm", [P, 2, PAIRS, TOK])
        top = s.sb("top", [P, 4, 4])
        probs = s.sb("probs", [P, 4, 4, N])
        total = s.sb("total", [P, 4, 4])
        rtotal = s.sb("rtotal", [P, 4, 4])
        weight = s.sb("weight", [P, 2, HEADS, 1])
        part = s.sb("part", [P, 2, HEADS, D])
        summed = s.sb("summed", [P, 2, D])
        ps = s.ps("ps", [P, 8, 512])
        SC, XV, WT, X, Y = 0, 2, 4, 6, 7
        names = "step zeroed normed xt_made xt_ready projected xm_ready scored topped exped inverted weighed taken xv_made".split()
        S = {n: s.sem(n) for n in names}
        block = s.block()

        def started(t, u, back):
            return not (isinstance(t, int) and t == 0 and u < back)

        @block.vector
        def _(dve):
            vec = nc.vector
            vec.memset(xh[:], 0.0).then_inc(S["zeroed"], 1)
            PER = 4 * GROUP

            def front(t, half):
                g = bass.ds(GROUP * t, GROUP)
                vec.tensor_tensor(xs[:, :, half, :], k.xc[:, g, :], bc(k.rstd[:, g, :], [P, GROUP, D]), ALU.mult).then_inc(S["normed"], 1)

            def prelude():
                front(0, 0)
                front(0, 1)

            def maximum(t, u):
                dve.wait_ge(S["scored"], UNITS * t + u + 1)
                vec.tensor_reduce(top[:, u % 4], ps[:, SC + u % 2, :].rearrange("p (a n) -> p a n", a=4), AX, ALU.max,
                                  negate=True).then_inc(S["topped"], 1)

            def invert(t, u):
                dve.wait_ge(S["exped"], UNITS * t + u + 1)
                if started(t, u, 4):
                    dve.wait_ge(S["weighed"], UNITS * t + u - 3)
                vec.reciprocal(rtotal[:, u % 4], total[:, u % 4]).then_inc(S["inverted"], 1)

            def combine(t, b, link):
                dve.wait_ge(S["weighed"], UNITS * t + 2 * b + 2)
                dve.wait_ge(S["xv_made"], GROUP * t + b + 1)
                link(vec.tensor_copy(weight[:, b % 2].rearrange("p h o -> p (h o)"), ps[:, WT + b % 2, 0:HEADS]))
                link(vec.tensor_tensor(part[:, b % 2], ps[:, XV + b % 2, :].rearrange("p (h d) -> p h d", h=HEADS),
                                       bc(weight[:, b % 2], [P, HEADS, D]), ALU.mult))
                vec.sem_inc(S["taken"], 1)

            def add(t, b, link):
                link(vec.tensor_reduce(summed[:, b % 2], part[:, b % 2].rearrange("p h d -> p d h"), AX, ALU.add))
                one = bass.ds(GROUP * t + b, 1)
                link(vec.tensor_tensor(k.h[:, one, :], k.h[:, one, :], summed[:, b % 2:b % 2 + 1, :], ALU.add))

            def body(t, par, cur, prev, nxt):
                link = Link(dve, S["step"], PER * t - PER // 2 if prev else 0)
                for u in range(UNITS):
                    if cur:
                        maximum(t, u)
                    if u >= 1 and cur:
                        invert(t, u - 1)
                    if u == 0 and prev:
                        invert(t - 1, UNITS - 1)
                    if u in (1, 3) and nxt:
                        front(t + 1, u // 2)
                    if u in (0, 2) and prev:
                        combine(t - 1, 2 + u // 2, link)
                    if u in (1, 3) and prev:
                        add(t - 1, 2 + u // 2, link)
                    if u in (4, 6) and cur:
                        combine(t, u // 2 - 2, link)
                    if u in (5, 7) and cur:
                        add(t, u // 2 - 2, link)

            in_turn(dve, prelude, body)

        @block.scalar
        def _(act):
            act.wait_ge(S["zeroed"], 1)

            def keep_x(t, par):
                act.wait_ge(S["xt_made"], t + 1)
                for half in range(2):
                    r = slice(D * half, D * half + D)
                    ins = nc.scalar.copy(xh[r, par, half, :], ps[r, X, :])
                ins.then_inc(S["xt_ready"], 1)

            def keep_projected(t, par, p):
                act.wait_ge(S["projected"], PAIRS * t + p + 1)
                nc.scalar.copy(xm[:, par, p, :], ps[:, (Y, X)[p % 2], :]).then_inc(S["xm_ready"], 1)

            def prelude():
                keep_x(0, 0)
                for p in range(PAIRS):
                    keep_projected(0, 0, p)

            def exponential(t, u):
                act.wait_ge(S["topped"], UNITS * t + u + 1)
                if started(t, u, 4):
                    act.wait_ge(S["weighed"], UNITS * t + u - 3)
                    act.wait_ge(S["inverted"], UNITS * t + u - 3)
                for a in range(4):
                    ins = nc.scalar.activation(probs[:, u % 4, a], ps[:, SC + u % 2, a * N:(a + 1) * N], ACT.Exp, bias=top[:, u % 4, a:a + 1],
                                               accum_out=total[:, u % 4, a:a + 1])
                ins.then_inc(S["exped"], 1)

            def body(t, par, cur, prev, nxt):
                for u in range(UNITS):
                    if cur:
                        exponential(t, u)
                    if u == 3 and nxt:
                        keep_x(t + 1, 1 - par)
                    if u >= 4 and nxt:
                        keep_projected(t + 1, 1 - par, u - 4)

            in_turn(act, prelude, body)

        @block.tensor
        def _(pe):
            mm = nc.tensor.matmul

            def turn_x(t):
                pe.wait_ge(S["normed"], 2 * t + 2)
                if started(t, 0, 1):
                    pe.wait_ge(S["xm_ready"], PAIRS * t)
                for b in range(GROUP):
                    ins = nc.tensor.transpose(ps[:, X, b * N:(b + 1) * N], xs[:, b].rearrange("p z d -> p (z d)"), k.ident[:])
                ins.then_inc(S["xt_made"], 1)

            def project(t, par, p):
                pe.wait_ge(S["xt_ready"], t + 1)
                if p >= 2:
                    pe.wait_ge(S["xm_ready"], PAIRS * t + p - 1)
                mm(ps[:, (Y, X)[p % 2], :], pair_map[:, 2 * p:2 * p + 2].rearrange("c h d -> c (h d)"), xh[:, par, 0, :],
                   start=True, stop=True).then_inc(S["projected"], 1)

            def prelude():
                turn_x(0)
                for p in range(PAIRS):
                    project(0, 0, p)

            def scores(t, par, u):
                b, half = u // 2, u % 2
                if u == 0:
                    pe.wait_ge(S["xm_ready"], PAIRS * t + PAIRS)
                if started(t, u, 2):
                    pe.wait_ge(S["exped"], UNITS * t + u - 1)
                mm(ps[:, SC + u % 2, :], xh[:, par, half, b * N:(b + 1) * N], xm[:, par, :, b * N:(b + 1) * N],
                   start=True, stop=True).then_inc(S["scored"], 1)

            def weigh(t, par, u):
                b = u // 2
                if u % 2 == 0 and started(t, b, 2):
                    pe.wait_ge(S["taken"], GROUP * t + b - 1)
                pe.wait_ge(S["inverted"], UNITS * t + u + 1)
                for a in range(4):
                    ins = mm(ps[:, WT + b % 2, 2 * a + u % 2:2 * a + u % 2 + 1], probs[:, u % 4, a, :], rtotal[:, u % 4, a:a + 1],
                             start=True, stop=True)
                ins.then_inc(S["weighed"], 1)
                if u % 2:
                    mm(ps[:, XV + b % 2, :], xh[:, par, 0, b * N:(b + 1) * N], value_map[:].rearrange("c h o -> c (h o)"),
                       start=True, stop=True).then_inc(S["xv_made"], 1)

            def body(t, par, cur, prev, nxt):
                for u in range(UNITS):
                    if cur:
                        scores(t, par, u)
                    if u >= 2 and cur:
                        weigh(t, par, u - 2)
                    if u < 2 and prev:
                        weigh(t - 1, 1 - par, UNITS + u - 2)
                    if u == 3 and nxt:
                        turn_x(t + 1)
                    if u >= 4 and nxt:
                        project(t + 1, 1 - par, u - 4)

            in_turn(pe, prelude, body)


def turn_all(k, tag, xt, router=None, logits=None, by_token=False):
    nc = k.nc
    with Scope(nc, f"turn{tag}") as s:
        xs = s.sb("xs", [P, 2, GROUP, P])
        xg = s.sb("xg", [P, 2, TOK])
        ps = s.ps("ps", [P, 4, 512])
        names = "step normed made ready kept routed taken".split()
        S = {n: s.sem(n) for n in names}
        block = s.block()
        E = router.shape[1] if router is not None else 0

        @block.vector
        def _(dve):
            link = Link(dve, S["step"])
            link(nc.vector.memset(xs[:], 0.0))
            link(nc.vector.memset(xs[:, :, :, D:D + 1], 1.0))
            with dve.Fori(0, GROUPS // 2) as i:
                for j in range(2):
                    dve.wait_ge(S["taken"], 2 * i + j + 1)
                    front_dve(k, dve, xs[:, j], 2 * i + j, S["normed"])
                for j in range(2):
                    t = 2 * i + j
                    g = bass.ds(GROUP * t, GROUP)
                    if E:
                        dve.wait_ge(S["ready"], t + 1)
                    if E:
                        nc.vector.tensor_copy(xt[:, g, :], xg[:, j].rearrange("p (b n) -> p b n", b=GROUP)).then_inc(S["kept"], 1)
                        dve.wait_ge(S["routed"], t + 1)
                        nc.vector.tensor_copy(logits[:, g, :], ps[:, 2 + j, 0:GROUP * E].rearrange("p (b e) -> p b e", b=GROUP)).then_inc(S["kept"], 1)

        @block.scalar
        def _(act):
            with act.Fori(0, GROUPS // 2) as i:
                for j in range(2):
                    t = 2 * i + j
                    act.wait_ge(S["made"], t + 1)
                    if E:
                        nc.scalar.copy(xg[:, j], ps[:, j, :]).then_inc(S["ready"], 1)
                    else:
                        g = bass.ds(GROUP * t, GROUP)
                        dst = xt[:, :, g].rearrange("p n b -> p b n") if by_token else xt[:, g, :]
                        nc.scalar.copy(dst, ps[:, j, :].rearrange("p (b n) -> p b n", b=GROUP)).then_inc(S["ready"], 1)

        @block.tensor
        def _(pe):
            nc.tensor.sem_inc(S["taken"], 2)
            with pe.Fori(0, GROUPS // 2) as i:
                for j in range(2):
                    t = 2 * i + j
                    pe.wait_ge(S["normed"], t + 1)
                    pe.wait_ge(S["taken"], t + 1)
                    for b in range(GROUP):
                        ins = nc.tensor.transpose(ps[:, j, b * N:(b + 1) * N], xs[:, j, b, :], k.ident[:])
                    ins.then_inc(S["made"], 1)
                for j in range(2):
                    t = 2 * i + j
                    pe.wait_ge(S["ready"], t + 1)
                    if E:
                        for b in range(GROUP):
                            ins = nc.tensor.matmul(ps[:, 2 + j, b * E:(b + 1) * E], xg[:, j, b * N:(b + 1) * N], router[:], start=True, stop=True)
                        ins.then_inc(S["routed"], 1)
                    nc.tensor.sem_inc(S["taken"], 1)


def route(k, tag, logits, share):
    nc = k.nc
    E = logits.shape[2]
    with Scope(nc, f"route{tag}") as s:
        shape = [P, SEQS, E]
        top = s.sb("top", [P, SEQS, 1])
        first = s.sb("first", [P, SEQS, 1])
        prob = s.sb("prob", shape)
        left = s.sb("left", shape)
        pick = s.sb("pick", [P, 2] + shape[1:])
        weight = s.sb("weight", [P, 1, E])
        step, shifted, exped, made = (s.sem(n) for n in "step shifted exped made".split())
        block = s.block()

        @block.gpsimd
        def _(pool):
            nc.gpsimd.iota(weight[:, 0, :], [[-1, E]], E, 0, allow_small_or_imprecise_dtypes=True).then_inc(made, 1)

        @block.scalar
        def _(act):
            act.wait_ge(shifted, 1)
            nc.scalar.activation(prob[:], prob[:], ACT.Exp).then_inc(exped, 1)

        @block.vector
        def _(dve):
            vec = nc.vector
            link = Link(dve, step)
            link(vec.tensor_reduce(top[:, :, 0], logits[:], AX, ALU.max))
            vec.tensor_tensor(prob[:], logits[:], bc(top[:], shape), ALU.subtract).then_inc(shifted, 1)
            dve.wait_ge(exped, 1)
            dve.wait_ge(made, 1)
            src = prob
            for n in range(2):
                link(vec.tensor_reduce(top[:, :, 0], src[:], AX, ALU.max))
                link(vec.tensor_tensor(pick[:, n], src[:], bc(top[:], shape), ALU.is_equal))
                link(vec.tensor_tensor(pick[:, n], pick[:, n], bc(weight[:], shape), ALU.mult))
                link(vec.tensor_reduce(first[:, :, 0], pick[:, n], AX, ALU.max))
                link(vec.tensor_tensor(pick[:, n], pick[:, n], bc(first[:], shape), ALU.is_equal))
                if n == 0:
                    link(vec.scalar_tensor_tensor(out=left[:], in0=pick[:, 0], scalar=-2.0, in1=prob[:], op0=ALU.mult, op1=ALU.add))
                    src = left
            link(vec.tensor_tensor(pick[:, 0], pick[:, 0], pick[:, 1], ALU.add))
            link(vec.tensor_tensor(prob[:], pick[:, 0], prob[:], ALU.mult))
            link(vec.tensor_reduce(top[:, :, 0], prob[:], AX, ALU.add))
            link(vec.reciprocal(top[:], top[:]))
            link(vec.tensor_tensor(share[:], prob[:], bc(top[:], shape), ALU.mult))


def mix_experts(k, tag, xt, share, w1, w2, b2, shared):
    nc = k.nc
    HC, E, PARTS = 2, 8, 3
    ALL = E + (1 if shared else 0)
    with Scope(nc, f"mix{tag}") as s:
        parts = s.sb("parts", [P, SEQS, PARTS * E], BF16)
        rest = s.sb("rest", [P, SEQS, E])
        now = s.sb("now", [P, GROUP, PARTS * E], BF16)
        parts_t = s.sb("parts_t", [P, TOK], BF16)
        identb = s.sb("identb", [P, P], BF16)
        pick_f = s.sb("pick_f", [P, E, P])
        pick = s.sb("pick", [P, E, P], BF16)
        b2x = s.sb("b2x", [P, D])
        b2rest = s.sb("b2rest", [P, D])
        b2_parts = s.sb("b2_parts", [P, PARTS, D], BF16)
        halves = s.sb("halves", [P, D])
        act_t = s.sb("act_t", [P, 3, HC, TOK])
        scaled = s.sb("scaled", [P, 2, HC, TOK])
        y_t = s.sb("y_t", [P, TOK])
        ps = s.ps("ps", [P, 8, 512])
        names = "parts_in parts_made parts_ready step picked loaded ready hidden active spread scaled output y_ready back added apart".split()
        S = {n: s.sem(n) for n in names}
        block = s.block()
        NH = ALL * HC
        HIDDEN, SPREAD, Y, BACK, TURN = 0, 3, 5, 6, 7
        turned = ps[0:PARTS * E, TURN, 0:TOK // 2].bitcast(BF16)
        HB = 3 if NH % 3 == 0 else 2

        @block.sync
        def _(sp):
            sp.wait_ge(S["ready"], 1)
            for n in range(PARTS):
                sp.dma_start(b2x[n * E:(n + 1) * E, :], b2).then_inc(S["loaded"], 16)

        @block.gpsimd
        def _(pool):
            link = Link(pool, S["picked"])
            link(nc.gpsimd.memset(pick_f[:], 0.0))
            for n in range(PARTS):
                link(nc.gpsimd.affine_select(out=pick_f[:], in_=pick_f[:], compare_op=ALU.not_equal, fill=1.0,
                                             base=-n * E, pattern=[[-1, E], [0, P]], channel_multiplier=1))

        @block.vector
        def _(dve):
            vec = nc.vector
            link = Link(dve, S["step"])
            link(vec.memset(b2x[:], 0.0))
            vec.sem_inc(S["ready"], 1)
            for n in range(2):
                link(vec.tensor_copy(halves[n * D:(n + 1) * D, :], k.ident[n * D:(n + 1) * D, n * D:(n + 1) * D]))
            dve.wait_ge(S["loaded"], 16 * PARTS)
            link(vec.tensor_copy(b2_parts[:, 0], b2x[:]))
            link(vec.tensor_tensor(b2rest[:], b2x[:], b2_parts[:, 0], ALU.subtract))
            link(vec.tensor_copy(b2_parts[:, 1], b2rest[:]))
            link(vec.tensor_tensor(b2rest[:], b2rest[:], b2_parts[:, 1], ALU.subtract))
            link(vec.tensor_copy(b2_parts[:, 2], b2rest[:]))
            dve.wait_ge(S["picked"], 1 + PARTS)
            link(vec.tensor_copy(pick[:], pick_f[:]))
            link(vec.tensor_copy(identb[:], k.ident[:]))
            link(vec.memset(parts_t[:], 0.0))
            link(vec.tensor_copy(parts[:, :, 0:E], share[:]))
            link(vec.tensor_tensor(rest[:], share[:], parts[:, :, 0:E], ALU.subtract))
            link(vec.tensor_copy(parts[:, :, E:2 * E], rest[:]))
            link(vec.tensor_tensor(rest[:], rest[:], parts[:, :, E:2 * E], ALU.subtract))
            link(vec.tensor_copy(parts[:, :, 2 * E:3 * E], rest[:]))
            vec.sem_inc(S["ready"], 1)

            def fetch_parts(t):
                vec.tensor_copy(now[:], parts[:, bass.ds(GROUP * t, GROUP), :]).then_inc(S["parts_in"], 1)

            def keep_parts(t):
                dve.wait_ge(S["parts_made"], t + 1)
                vec.tensor_copy(parts_t[0:PARTS * E, :], turned).then_inc(S["parts_ready"], 1)

            fetch_parts(0)
            keep_parts(0)

            def keep(t):
                g = bass.ds(GROUP * t, GROUP)
                dve.wait_ge(S["back"], t + 1)
                vec.tensor_tensor(k.h[:, g, :], k.h[:, g, :], ps[:, BACK, 0:GROUP * D].rearrange("p (b d) -> p b d", b=GROUP), ALU.add).then_inc(S["added"], 1)

            def group(t, first, last):
                for e in range(E):
                    if e == 1 and not first:
                        keep(t - 1)
                    if e == 2 and not last:
                        fetch_parts(t + 1)
                    dve.wait_ge(S["spread"], E * t + e + 1)
                    dve.wait_ge(S["active"], NH * t + HC * e + HC)
                    if e >= 2:
                        dve.wait_ge(S["output"], ALL * t + e - 1)
                    vec.tensor_tensor(scaled[:, e % 2], act_t[:, e % 3],
                                      bc(ps[:, SPREAD + e % 2, :].rearrange("p (o n) -> p o n", o=1), [P, HC, TOK]), ALU.mult).then_inc(S["scaled"], 1)
                if not last:
                    keep_parts(t + 1)
                dve.wait_ge(S["output"], ALL * t + ALL)
                if not first:
                    dve.wait_ge(S["back"], t)
                vec.tensor_copy(y_t[:], ps[:, Y, :]).then_inc(S["y_ready"], 1)

            group(0, True, False)
            with dve.Fori(1, GROUPS - 1) as t:
                group(t, False, False)
            group(GROUPS - 1, False, True)
            keep(GROUPS - 1)

        @block.scalar
        def _(act):
            with act.Fori(0, GROUPS) as t:
                for n in range(NH):
                    e, c = n // HC, n % HC
                    act.wait_ge(S["hidden"], NH * t + n + 1)
                    if n >= 3 * HC and c == 0:
                        act.wait_ge(S["scaled"], E * t + e - 2)
                    nc.scalar.activation(act_t[:, e % 3, c, :], ps[:, HIDDEN + n % HB, :], ACT.Gelu).then_inc(S["active"], 1)

        @block.tensor
        def _(pe):
            mm = nc.tensor.matmul
            pe.wait_ge(S["ready"], 2)

            def back(t):
                pe.wait_ge(S["y_ready"], t + 1)
                for b in range(GROUP):
                    ins = mm(ps[:, BACK, b * D:(b + 1) * D], y_t[:, b * N:(b + 1) * N], halves[:], start=True, stop=True)
                ins.then_inc(S["back"], 1)

            def turn_parts(t):
                pe.wait_ge(S["parts_in"], t + 1)
                if not (isinstance(t, int) and t == 0):
                    pe.wait_ge(S["parts_ready"], t)
                nc.tensor.sem_inc(S["apart"], 1)
                for b in range(GROUP):
                    ins = nc.tensor.transpose(turned[:, b * N:(b + 1) * N], now[:, b], identb[:])
                ins.then_inc(S["parts_made"], 1)

            def group(t, first, last):
                g = bass.ds(GROUP * t, GROUP)
                x = xt[:, g, :].rearrange("p b n -> p (b n)")

                def hidden(e):
                    for c in range(HC):
                        n = HC * e + c
                        if n >= HB:
                            pe.wait_ge(S["active"], NH * t + n - HB + 1)
                        mm(ps[:, HIDDEN + n % HB, :], w1[:, e, c * P:(c + 1) * P], x, start=True, stop=True).then_inc(S["hidden"], 1)

                def spread(e):
                    if e >= 2:
                        pe.wait_ge(S["scaled"], E * t + e - 1)
                    mm(ps[:, SPREAD + e % 2, :], pick[:, e, :], parts_t[:], start=True, stop=True).then_inc(S["spread"], 1)

                def output(e):
                    src = scaled[:, e % 2] if e < E else act_t[:, e % 3]
                    if e < E:
                        pe.wait_ge(S["scaled"], E * t + e + 1)
                    else:
                        pe.wait_ge(S["active"], NH * t + NH)
                    for c in range(HC):
                        ins = mm(ps[c * D:(c + 1) * D, Y, :], w2[:, e, c, :], src[:, c, :], start=(e == 0 and c == 1), stop=(e == ALL - 1),
                                 skip_group_check=True, tile_position=(0, c * D))
                    return ins.then_inc(S["output"], 1)

                hidden(0)
                pe.wait_ge(S["parts_ready"], t + 1)
                spread(0)
                if not first:
                    back(t - 1)
                for n in range(PARTS):
                    mm(ps[0:D, Y, :], b2_parts[:, n, :], parts_t[:], start=(n == 0), stop=False, skip_group_check=True, tile_position=(0, 0))
                for e in range(1, ALL):
                    hidden(e)
                    if e < E:
                        spread(e)
                    if e == 4 and not last:
                        turn_parts(t + 1)
                    output(e - 1)
                output(ALL - 1)

            turn_parts(0)
            group(0, True, False)
            with pe.Fori(1, GROUPS - 1) as t:
                group(t, False, False)
            group(GROUPS - 1, False, True)
            back(GROUPS - 1)


def stage_l2_ffn(k):
    nc, w = k.nc, k.w
    E, F, A1 = 8, 256, D + 1
    with Scope(nc, "l2f") as s:
        share = s.sb("share", [P, SEQS, E])
        xt = s.sb("xt", [P, SEQS, N])
        w1 = s.sb("w1", [P, E + 1, F])
        w2 = s.sb("w2", [P, E + 1, 2, D])
        with Scope(nc, "l2froute") as s1:
            wr = s1.sb("wr", [P, E])
            bshared = s1.sb("bshared", [P, 1, D])
            logits = s1.sb("logits", [P, SEQS, E])
            with Scope(nc, "l2fload") as s2:
                loaded, zeroed, added = s2.sem("loaded"), s2.sem("zeroed"), s2.sem("added")
                center_vector, center_scalar = center_parts(k, s2)
                block = s2.block()

                @block.scalar
                def _(act):
                    center_scalar(act)

                @block.sync
                def _(sp):
                    sp.wait_ge(zeroed, 1)
                    sp.dma_start(w1[0:D, 0:E], w["L2_ffn_W1p"].rearrange("e d f -> d e f")).then_inc(loaded, 16)
                    sp.dma_start(w1[0:D, E], w["L2_ffn_W1s"]).then_inc(loaded, 16)
                    sp.dma_start(w1[D:A1, 0:E], w["L2_ffn_b1p"].rearrange("(o e) f -> o e f", o=1)).then_inc(loaded, 16)
                    sp.dma_start(w1[D:A1, E], w["L2_ffn_b1s"].rearrange("(o f) -> o f", o=1)).then_inc(loaded, 16)
                    for c in range(2):
                        sp.dma_start(w2[:, 0:E, c], w["L2_ffn_W2p"].rearrange("e (c f) d -> c f e d", c=2)[c]).then_inc(loaded, 16)
                    sp.dma_start(w2[:, E], w["L2_ffn_W2s"].rearrange("(c f) d -> f c d", c=2)).then_inc(loaded, 16)
                    sp.dma_start(bshared[:, 0, :], w["L2_ffn_b2s"].partition_broadcast(P)).then_inc(loaded, 16)
                    sp.dma_start(wr[0:D, :], w["L2_ffn_Wr"]).then_inc(loaded, 16)

                @block.vector
                def _(dve):
                    nc.vector.memset(wr[D:P, :], 0.0)
                    nc.vector.memset(w1[D:P], 0.0).then_inc(zeroed, 1)
                    center_vector(dve)
                    dve.wait_ge(loaded, 144)
                    nc.vector.tensor_tensor(k.h[:], k.h[:], bc(bshared[:], [P, SEQS, D]), ALU.add).then_inc(added, 1)
                    dve.wait_ge(added, 1)
            turn_all(k, "l2f", xt, wr, logits)
            route(k, "l2f", logits, share)
        mix_experts(k, "l2f", xt, share, w1, w2, w["L2_ffn_b2p"], True)


def stage_neighbours(k, xt, mask):
    nc, w = k.nc, k.w
    A1, NEAR = D + 1, 17
    with Scope(nc, "knn") as s:
        wr = s.sb("wr", [A1, D])
        mean_t = s.sb("mean_t", [A1, SEQS])
        reprs = s.sb("reprs", [SEQS, D])
        sq = s.sb("sq", [SEQS, D])
        norm = s.sb("norm", [SEQS, 1])
        unit_t = s.sb("unit_t", [D, SEQS])
        sim = s.sb("sim", [SEQS, 1, SEQS])
        before = s.sb("before", [SEQS, SEQS, SEQS])
        tie = s.sb("tie", [SEQS, SEQS, SEQS])
        lower = s.sb("lower", [SEQS, SEQS, SEQS])
        rank = s.sb("rank", [SEQS, SEQS])
        ps = s.ps("ps", [SEQS, 4, 512])
        loaded, step, meaned, made, squared, rooted, united, lowered = (s.sem(n) for n in "loaded step meaned made squared rooted united lowered".split())
        block = s.block()

        @block.sync
        def _(sp):
            sp.dma_start(wr[0:D, :], w["L3_attn_W_repr"]).then_inc(loaded, 16)
            sp.dma_start(wr[D:A1, :], w["L3_attn_b_repr"].rearrange("(o d) -> o d", o=1)).then_inc(loaded, 16)

        @block.gpsimd
        def _(pool):
            link = Link(pool, lowered)
            link(nc.gpsimd.memset(lower[:], 1.0))
            link(nc.gpsimd.affine_select(out=lower[:], in_=lower[:], compare_op=ALU.is_gt, fill=0.0, base=0,
                                         pattern=[[1, SEQS], [-1, SEQS]], channel_multiplier=0))

        @block.scalar
        def _(act):
            act.wait_ge(squared, 1)
            nc.scalar.activation(norm[:], norm[:], ACT.Sqrt).then_inc(rooted, 1)

        @block.tensor
        def _(pe):
            pe.wait_ge(loaded, 32)
            pe.wait_ge(meaned, 1)
            nc.tensor.matmul(ps[:, 0, 0:D], mean_t[:], wr[:], start=True, stop=True).then_inc(made, 1)
            pe.wait_ge(united, 1)
            nc.tensor.transpose(ps[:, 1, 0:SEQS], reprs[:], k.ident[0:SEQS, 0:SEQS]).then_inc(made, 1)
            pe.wait_ge(united, 2)
            nc.tensor.matmul(ps[:, 2, 0:SEQS], unit_t[:], unit_t[:], start=True, stop=True).then_inc(made, 1)

        @block.vector
        def _(dve):
            vec = nc.vector
            link = Link(dve, step)
            link(vec.memset(mean_t[D:A1, :], 1.0))
            link(vec.tensor_reduce(mean_t[0:D, :], xt[0:D].rearrange("d n b -> d b n"), AX, ALU.add))
            link(vec.tensor_scalar(mean_t[0:D, :], mean_t[0:D, :], 1.0 / N, None, ALU.mult))
            vec.sem_inc(meaned, 1)
            dve.wait_ge(made, 1)
            link(vec.tensor_copy(reprs[:], ps[:, 0, 0:D]))
            link(vec.tensor_tensor(sq[:], reprs[:], reprs[:], ALU.mult))
            vec.tensor_reduce(norm[:], sq[:], AX, ALU.add).then_inc(squared, 1)
            dve.wait_ge(rooted, 1)
            link(vec.reciprocal(norm[:], norm[:]))
            vec.tensor_scalar(reprs[:], reprs[:], norm[:, 0:1], None, ALU.mult).then_inc(united, 1)
            dve.wait_ge(made, 2)
            vec.tensor_copy(unit_t[:], ps[:, 1, 0:SEQS]).then_inc(united, 1)
            dve.wait_ge(made, 3)
            link(vec.tensor_copy(sim[:, 0, :], ps[:, 2, 0:SEQS]))
            cube = [SEQS, SEQS, SEQS]
            mine = bc(sim[:, 0, :].rearrange("p (b o) -> p b o", o=1), cube)
            vec.tensor_tensor(before[:], bc(sim[:], cube), mine, ALU.is_gt)
            link(vec.tensor_tensor(tie[:], bc(sim[:], cube), mine, ALU.is_equal))
            dve.wait_ge(lowered, 2)
            link(vec.tensor_tensor(tie[:], tie[:], lower[:], ALU.mult))
            link(vec.tensor_tensor(before[:], before[:], tie[:], ALU.add))
            link(vec.tensor_reduce(rank[:], before[:], AX, ALU.add))
            link(vec.tensor_scalar(rank[:], rank[:], NEAR - 0.5, MASKED, ALU.is_gt, ALU.mult))
            link(vec.memset(mask[SEQS:P], 0.0))
            link(vec.tensor_copy(mask[0:SEQS], bc(rank[:].rearrange("p (o b) -> p o b", o=1), [SEQS, 8, SEQS])))


def stage_l3_attn(k):
    with Scope(k.nc, "l3") as s:
        xt = s.sb("xt", [P, N, SEQS])
        yt = s.sb("yt", [D, SEQS, N])
        mask = s.sb("mask", [P, 8, SEQS], BF16)
        turn_all(k, "l3a", xt, by_token=True)
        stage_neighbours(k, xt, mask)
        attend_sequences(k, xt, yt, mask)
        add_turned_back(k, "l3a", yt)


def attend_sequences(k, xt, yt, mask):
    nc, w = k.nc, k.w
    HEADS, HD = 8, 32
    NG = 8
    assert N // NG == GROUPS
    COLS = NG * SEQS
    UNITS = NG // 2
    PROJ = 6
    with Scope(nc, "l3a") as s:
        twice = s.sb("twice", [P, 2, SEQS], BF16)
        wqk = s.sb("wqk", [P, 2, 2, P])
        wv = s.sb("wv", [P, 2, 4, HD])
        wo = s.sb("wo", [P, 2, D])
        bo = s.sb("bo", [D, 1])
        xg = s.sb("xg", [P, COLS])
        q = s.sb("q", [P, 2, 2, COLS])
        keys = s.sb("keys", [P, 2, 2, NG, 4, SEQS])
        v = s.sb("v", [P, 2, NG, 4, 2, HD + 1])
        top = s.sb("top", [P, 2, HEADS, 1])
        probs = s.sb("probs", [P, 2, HEADS, SEQS])
        probs_t = s.sb("probs_t", [P, 2, 4, P])
        rden = s.sb("rden", [P, 2, HEADS, 1])
        mixed = s.sb("mixed", [P, 2, UNITS, HEADS, HD])
        mt = s.sb("mt", [P, 2, COLS])
        ps = s.ps("ps", [P, 8, 512])
        SC, TU, OUT, X, Y = 0, 2, 4, 5, 7
        names = ("loaded step zeroed v_laid x_in projected q_ready kv_ready topped scored shifted exped turned turned_ready valued inverted mixed_ready "
                 "mt_made mt_ready y_made y_kept apart").split()
        S = {n: s.sem(n) for n in names}
        block = s.block()

        def started(t, u, back):
            return not (isinstance(t, int) and t == 0 and u < back)

        @block.sync
        def _(sp):
            sp.wait_ge(S["zeroed"], 1)
            sp.dma_start(wqk[0:D], w["L3_attn_W_qkv"][:, 0:4 * P].rearrange("d (z g c) -> d z g c", z=2, g=2)).then_inc(S["loaded"], 16)
            for z in range(2):
                sp.dma_start(wv[0:D, z], w["L3_attn_W_qkv"][:, 4 * P:6 * P].rearrange("d (a z c) -> z d a c", z=2, c=HD)[z]).then_inc(S["loaded"], 16)
            sp.dma_start(wo[:], w["L3_attn_W_out"].rearrange("(g c) o -> c g o", g=2)).then_inc(S["loaded"], 16)
            sp.dma_start(bo[:], w["L3_attn_b_out"].rearrange("(o u) -> o u", u=1)).then_inc(S["loaded"], 16)

        @block.gpsimd
        def _(pool):
            nc.gpsimd.memset(v[:], 0.0).then_inc(S["v_laid"], 1)
            pool.wait_ge(S["v_laid"], 1)
            for z in range(2):
                nc.gpsimd.memset(v[D * z:D * z + D, :, :, :, z, HD:HD + 1], 1.0).then_inc(S["v_laid"], 1)

        @block.vector
        def _(dve):
            vec = nc.vector
            link = Link(dve, S["step"])
            vec.memset(wqk[:], 0.0)
            vec.memset(wv[:], 0.0)
            vec.memset(twice[:], 0.0)
            link(vec.memset(keys[:], 0.0))
            vec.sem_inc(S["zeroed"], 1)
            dve.wait_ge(S["v_laid"], 3)
            for z in range(2):
                link(vec.tensor_copy(twice[0:SEQS, z, :], k.ident[0:SEQS, 0:SEQS]))
            dve.wait_ge(S["loaded"], 16 * 5)
            link(vec.tensor_scalar(wqk[:, 0], wqk[:, 0], HD ** -0.5, None, ALU.mult))
            vec.sem_inc(S["step"], 1)

            def fetch(t):
                if started(t, 0, 1):
                    dve.wait_ge(S["projected"], PROJ * t)
                vec.tensor_copy(xg[:], xt[:, bass.ds(NG * t, NG), :].rearrange("p n b -> p (n b)")).then_inc(S["x_in"], 1)

            def keep_keys(t, par, g):
                dve.wait_ge(S["projected"], PROJ * t + 3 + g)
                for h in range(2):
                    r = slice(HD * h, HD * h + HD)
                    ins = vec.tensor_copy(keys[r, par, g, :, h, :], ps[r, X + g, :].rearrange("p (n b) -> p n b", n=NG))
                ins.then_inc(S["kv_ready"], 1)

            def keep_values(t, par, j):
                dve.wait_ge(S["projected"], PROJ * t + 5 + j)
                vec.tensor_copy(v[0:D, par, 4 * j:4 * j + 4, :, 0, 0:HD],
                                ps[0:D, X + j, :].rearrange("p (n a c) -> p n a c", n=4, c=HD)).then_inc(S["kv_ready"], 1)

            def prelude():
                fetch(0)
                for n in range(2):
                    keep_keys(0, 0, n)
                for n in range(2):
                    keep_values(0, 0, n)

            def shift(t, u):
                dve.wait_ge(S["scored"], UNITS * t + u + 1)
                bank = ps[:, SC + u % 2, :].rearrange("p (h b) -> p h b", h=HEADS)
                vec.tensor_reduce(top[:, u % 2, :, 0], bank, AX, ALU.max).then_inc(S["topped"], 1)
                dve.wait_ge(S["topped"], UNITS * t + u + 1)
                if started(t, u, 2):
                    dve.wait_ge(S["turned"], UNITS * t + u - 1)
                vec.tensor_tensor(probs[:, u % 2], bank, bc(top[:, u % 2], [P, HEADS, SEQS]), ALU.subtract).then_inc(S["shifted"], 1)

            def normalize(t, par, u):
                dve.wait_ge(S["valued"], UNITS * t + u + 1)
                o = ps[:, OUT, 0:HEADS * (HD + 1)].rearrange("p (h c) -> p h c", h=HEADS)
                vec.reciprocal(rden[:, u % 2], o[:, :, HD:HD + 1]).then_inc(S["inverted"], 1)
                dve.wait_ge(S["inverted"], UNITS * t + u + 1)
                vec.tensor_tensor(mixed[:, par, u], o[:, :, 0:HD], bc(rden[:, u % 2], [P, HEADS, HD]), ALU.mult).then_inc(S["mixed_ready"], 1)

            def keep_y(t):
                dve.wait_ge(S["y_made"], t + 1)
                vec.tensor_scalar(yt[:, :, bass.ds(NG * t, NG)].rearrange("p b n -> p n b"), ps[0:D, Y, :].rearrange("p (n b) -> p n b", n=NG),
                                  bo[:, 0:1], None, ALU.add).then_inc(S["y_kept"], 1)

            def body(t, par, cur, prev, nxt):
                for u in range(UNITS):
                    if cur:
                        shift(t, u)
                    if u == 0 and nxt:
                        fetch(t + 1)
                    if u == 1 and nxt:
                        keep_keys(t + 1, 1 - par, 0)
                        keep_keys(t + 1, 1 - par, 1)
                    if u >= 2 and nxt:
                        keep_values(t + 1, 1 - par, u - 2)
                    if u >= 2 and cur:
                        normalize(t, par, u - 2)
                    if u < 2 and prev:
                        normalize(t - 1, 1 - par, UNITS + u - 2)
                    if u == 3 and prev:
                        keep_y(t - 1)

            in_turn(dve, prelude, body)

        @block.scalar
        def _(act):
            act.wait_ge(S["zeroed"], 1)
            act.wait_ge(S["v_laid"], 3)

            def keep_q(t, par, g):
                act.wait_ge(S["projected"], PROJ * t + g + 1)
                nc.scalar.copy(q[:, par, g, :], ps[:, X + g, :]).then_inc(S["q_ready"], 1)

            def keep_keys(t, par, g):
                act.wait_ge(S["projected"], PROJ * t + 3 + g)
                for h in range(2, 4):
                    r = slice(HD * h, HD * h + HD)
                    ins = nc.scalar.copy(keys[r, par, g, :, h, :], ps[r, X + g, :].rearrange("p (n b) -> p n b", n=NG))
                ins.then_inc(S["kv_ready"], 1)

            def keep_values(t, par, j):
                act.wait_ge(S["projected"], PROJ * t + 5 + j)
                nc.scalar.copy(v[D:P, par, 4 * j:4 * j + 4, :, 1, 0:HD],
                               ps[D:P, X + j, :].rearrange("p (n a c) -> p n a c", n=4, c=HD)).then_inc(S["kv_ready"], 1)

            def prelude():
                for n in range(2):
                    keep_q(0, 0, n)
                for n in range(2):
                    keep_keys(0, 0, n)
                for n in range(2):
                    keep_values(0, 0, n)

            def exponential(t, u):
                act.wait_ge(S["shifted"], UNITS * t + u + 1)
                nc.scalar.activation(probs[:, u % 2], probs[:, u % 2], ACT.Exp).then_inc(S["exped"], 1)

            def keep_turned(t, u):
                act.wait_ge(S["turned"], UNITS * t + u + 1)
                if started(t, u, 2):
                    act.wait_ge(S["valued"], UNITS * t + u - 1)
                nc.scalar.copy(probs_t[:, u % 2], ps[:, TU + u % 2, :].rearrange("p (a c) -> p a c", a=4)).then_inc(S["turned_ready"], 1)

            def keep_mixed(t, g):
                act.wait_ge(S["mt_made"], 2 * t + g + 1)
                nc.scalar.copy(mt[:, g], ps[:, Y, :]).then_inc(S["mt_ready"], 1)

            def body(t, par, cur, prev, nxt):
                for u in range(UNITS):
                    if u == 0 and nxt:
                        keep_q(t + 1, 1 - par, 0)
                        keep_q(t + 1, 1 - par, 1)
                    if u >= 1 and cur:
                        keep_turned(t, u - 1)
                    if u == 0 and prev:
                        keep_turned(t - 1, UNITS - 1)
                    if cur:
                        exponential(t, u)
                    if u == 1 and nxt:
                        keep_keys(t + 1, 1 - par, 0)
                        keep_keys(t + 1, 1 - par, 1)
                    if u >= 2 and nxt:
                        keep_values(t + 1, 1 - par, u - 2)
                    if u >= 2 and prev:
                        keep_mixed(t - 1, u - 2)

            in_turn(act, prelude, body)

        @block.tensor
        def _(pe):
            mm = nc.tensor.matmul
            pe.wait_ge(S["step"], 5)

            def project(t, n):
                if n >= 4:
                    pe.wait_ge(S["x_in"], t + 1)
                if n < 2:
                    if started(t, 0, 1):
                        pe.wait_ge(S["kv_ready"], 8 * t)
                elif n < 4:
                    pe.wait_ge(S["q_ready"], 2 * t + n - 1)
                else:
                    pe.wait_ge(S["kv_ready"], 8 * t + 4)
                if n < 4:
                    x = xt[:, bass.ds(NG * t, NG), :].rearrange("p n b -> p (n b)")
                    ins = mm(ps[:, X + n % 2, :], wqk[:, n // 2, n % 2, :], x, start=True, stop=True)
                else:
                    for p in range(4 * (n - 4), 4 * (n - 4) + 4):
                        for z in range(2):
                            ins = mm(ps[D * z:D * z + D, X + n % 2, (p % 4) * P:(p % 4 + 1) * P], xg[:, p * SEQS:(p + 1) * SEQS],
                                     wv[:, z].rearrange("p a c -> p (a c)"), start=True, stop=True, tile_position=(0, D * z))
                ins.then_inc(S["projected"], 1)

            def prelude():
                for n in range(PROJ):
                    project(0, n)

            def scores(t, par, u):
                if u == 0:
                    pe.wait_ge(S["q_ready"], 2 * t + 2)
                    pe.wait_ge(S["kv_ready"], 8 * t + 8)
                if started(t, u, 2):
                    pe.wait_ge(S["shifted"], UNITS * t + u - 1)
                bank = ps[:, SC + u % 2, :]
                mm(bank, twice[:].rearrange("p z b -> p (z b)"), mask[:].rearrange("p s b -> p (s b)"), start=True, stop=False)
                for g in range(2):
                    for z in range(2):
                        n = 2 * u + z
                        ins = mm(bank[D * z:D * z + D, g * 256:(g + 1) * 256], q[:, par, g, n * SEQS:(n + 1) * SEQS],
                                 keys[:, par, g, n].rearrange("p h b -> p (h b)"), start=False, stop=(g == 1), tile_position=(0, D * z))
                ins.then_inc(S["scored"], 1)

            def turn(t, u):
                pe.wait_ge(S["exped"], UNITS * t + u + 1)
                if started(t, u, 2):
                    pe.wait_ge(S["turned_ready"], UNITS * t + u - 1)
                for a in range(4):
                    ins = nc.tensor.transpose(ps[:, TU + u % 2, a * P:(a + 1) * P], probs[:, u % 2, 2 * a:2 * a + 2].rearrange("p s b -> p (s b)"), k.ident[:])
                ins.then_inc(S["turned"], 1)

            def values(t, par, u):
                pe.wait_ge(S["turned_ready"], UNITS * t + u + 1)
                if started(t, u, 1):
                    pe.wait_ge(S["mixed_ready"], UNITS * t + u)
                nc.tensor.sem_inc(S["apart"], 1)
                W = 2 * (HD + 1)
                for a in range(4):
                    for z in range(2):
                        ins = mm(ps[D * z:D * z + D, OUT, a * W:(a + 1) * W], probs_t[:, u % 2, a, D * z:D * z + D],
                                 v[:, par, 2 * u + z, a].rearrange("p z c -> p (z c)"), start=True, stop=True, tile_position=(0, D * z))
                ins.then_inc(S["valued"], 1)

            def turn_mixed(t, par, g):
                pe.wait_ge(S["mixed_ready"], UNITS * t + UNITS)
                if g == 1:
                    pe.wait_ge(S["mt_ready"], 2 * t + 1)
                elif started(t, 0, 1):
                    pe.wait_ge(S["y_kept"], t)
                for u in range(UNITS):
                    ins = nc.tensor.transpose(ps[:, Y, u * P:(u + 1) * P], mixed[:, par, u, 4 * g:4 * g + 4].rearrange("p h c -> p (h c)"), k.ident[:])
                ins.then_inc(S["mt_made"], 1)

            def outputs(t):
                pe.wait_ge(S["mt_ready"], 2 * t + 2)
                for g in range(2):
                    ins = mm(ps[0:D, Y, :], wo[:, g, :], mt[:, g], start=(g == 0), stop=(g == 1))
                ins.then_inc(S["y_made"], 1)

            def body(t, par, cur, prev, nxt):
                for u in range(UNITS):
                    if cur:
                        scores(t, par, u)
                    if nxt:
                        project(t + 1, (0, 2, 4, 5)[u])
                    if u >= 1 and cur:
                        turn(t, u - 1)
                    if u == 0 and prev:
                        turn(t - 1, UNITS - 1)
                    if u < 2 and nxt:
                        project(t + 1, (1, 3)[u])
                    if u >= 2 and prev:
                        turn_mixed(t - 1, 1 - par, u - 2)
                    if u >= 2 and cur:
                        values(t, par, u - 2)
                    if u < 2 and prev:
                        values(t - 1, 1 - par, UNITS + u - 2)
                    if u == 3 and prev:
                        outputs(t - 1)

            in_turn(pe, prelude, body)


def add_turned_back(k, tag, yt):
    nc = k.nc
    with Scope(nc, f"back{tag}") as s:
        yg = s.sb("yg", [D, 2, TOK])
        ps = s.ps("ps", [P, 2, 512])
        ready, made, added, apart, free = (s.sem(n) for n in "ready made added apart free".split())
        block = s.block()

        @block.vector
        def _(dve):
            nc.vector.sem_inc(added, 2)
            with dve.Fori(0, GROUPS // 2) as i:
                for j in range(2):
                    t = 2 * i + j
                    g = bass.ds(GROUP * t, GROUP)
                    dve.wait_ge(made, t + 1)
                    nc.vector.tensor_tensor(k.h[:, g, :], k.h[:, g, :], ps[:, j, 0:GROUP * D].rearrange("p (b d) -> p b d", b=GROUP), ALU.add).then_inc(added, 1)

        @block.scalar
        def _(act):
            with act.Fori(0, GROUPS // 2) as i:
                for j in range(2):
                    t = 2 * i + j
                    act.wait_ge(free, t + 1)
                    nc.scalar.copy(yg[:, j], yt[:, bass.ds(GROUP * t, GROUP), :].rearrange("p b n -> p (b n)")).then_inc(ready, 1)

        @block.tensor
        def _(pe):
            nc.tensor.sem_inc(free, 2)
            with pe.Fori(0, GROUPS // 2) as i:
                for j in range(2):
                    t = 2 * i + j
                    pe.wait_ge(ready, t + 1)
                    pe.wait_ge(added, t + 1)
                    nc.tensor.sem_inc(apart, 1)
                    for b in range(GROUP):
                        ins = nc.tensor.transpose(ps[:, j, b * D:(b + 1) * D], yg[:, j, b * N:(b + 1) * N], k.ident[0:D, 0:D])
                    ins.then_inc(made, 1)
                    pe.wait_ge(made, t + 1)
                    nc.tensor.sem_inc(free, 1)


def stage_l3_ffn(k):
    nc, w = k.nc, k.w
    E, F, A1 = 8, 256, D + 1
    with Scope(nc, "l3f") as s:
        share = s.sb("share", [P, SEQS, E])
        xt = s.sb("xt", [P, SEQS, N])
        w1 = s.sb("w1", [P, E, F])
        w2 = s.sb("w2", [P, E, 2, D])
        with Scope(nc, "l3froute") as s1:
            wr = s1.sb("wr", [P, E])
            logits = s1.sb("logits", [P, SEQS, E])
            with Scope(nc, "l3fload") as s2:
                gain = s2.sb("gain", [E, 2, D])
                gain_t = s2.sb("gain_t", [D, E])
                shift_t = s2.sb("shift_t", [D, E, A1])
                ps = s2.ps("ps", [P, 6, 512])
                loaded, step, made, ready, zeroed = (s2.sem(n) for n in "loaded step made ready zeroed".split())
                center_vector, center_scalar = center_parts(k, s2)
                block = s2.block()

                @block.scalar
                def _(act):
                    center_scalar(act)

                @block.sync
                def _(sp):
                    sp.wait_ge(zeroed, 1)
                    sp.dma_start(w1[0:D], w["L3_ffn_W1"].rearrange("e d f -> d e f")).then_inc(loaded, 16)
                    sp.dma_start(w1[D:A1], w["L3_ffn_b1"].rearrange("(o e) f -> o e f", o=1)).then_inc(loaded, 16)
                    for c in range(2):
                        sp.dma_start(w2[:, :, c], w["L3_ffn_W2"].rearrange("e (c f) d -> c f e d", c=2)[c]).then_inc(loaded, 16)
                    sp.dma_start(wr[0:D, :], w["L3_ffn_Wr"]).then_inc(loaded, 16)
                    sp.dma_start(wr[D:A1, :], w["L3_ffn_br"].rearrange("(o e) -> o e", o=1)).then_inc(loaded, 16)
                    sp.dma_start(gain[:, 0, :], w["L3_ffn_ln_g"]).then_inc(loaded, 16)
                    sp.dma_start(gain[:, 1, :], w["L3_ffn_ln_b"]).then_inc(loaded, 16)

                @block.tensor
                def _(pe):
                    pe.wait_ge(loaded, 16 * 8)
                    for n in range(2):
                        ins = nc.tensor.transpose(ps[0:D, 0, E * n:E * n + E], gain[:, n, :], k.ident[0:E, 0:E])
                    ins.then_inc(made, 1)
                    pe.wait_ge(ready, 1)
                    for e in range(E):
                        ins = nc.tensor.matmul(ps[0:A1, 1 + e // 2, (e % 2) * F:(e % 2 + 1) * F], shift_t[:, e, :], w1[0:D, e, :], start=True, stop=True)
                    ins.then_inc(made, 1)

                @block.vector
                def _(dve):
                    vec = nc.vector
                    link = Link(dve, step)
                    link(vec.memset(wr[D:P, :], 0.0))
                    link(vec.memset(w1[D:P], 0.0))
                    vec.sem_inc(zeroed, 1)
                    link(vec.memset(shift_t[:], 0.0))
                    center_vector(dve)
                    dve.wait_ge(made, 1)
                    link(vec.tensor_copy(gain_t[:], ps[0:D, 0, 0:E]))
                    link(vec.tensor_copy(shift_t[:, :, D], ps[0:D, 0, E:2 * E]))
                    vec.sem_inc(ready, 1)
                    dve.wait_ge(made, 2)
                    row = w1[D:A1].rearrange("p (a z) f -> p a z f", z=2)
                    link(vec.tensor_tensor(row, row, ps[D:A1, 1:5, :].rearrange("p a (z f) -> p a z f", z=2), ALU.add))
                    for e in range(E):
                        link(vec.tensor_scalar(w1[0:D, e, :], w1[0:D, e, :], gain_t[:, e:e + 1], None, ALU.mult))
            turn_all(k, "l3fr", xt, wr, logits)
            route(k, "l3f", logits, share)
        inner_center(k)
        turn_all(k, "l3fx", xt)
        mix_experts(k, "l3f", xt, share, w1, w2, w["L3_ffn_b2"], False)


def inner_center(k):
    nc = k.nc
    with Scope(nc, "inner") as s:
        sq = s.sb("sq", [P, SEQS, D])
        mean = s.sb("mean", [P, SEQS, 1])
        std = s.sb("std", [P, SEQS, 1])
        eps = s.sb("eps", [P, 1])
        step, summed, rooted = s.sem("step"), s.sem("summed"), s.sem("rooted")
        block = s.block()

        @block.scalar
        def _(act):
            act.wait_ge(summed, 1)
            nc.scalar.activation(std[:], mean[:], ACT.Sqrt, bias=eps[:, 0:1], scale=1.0 / D).then_inc(rooted, 1)

        @block.vector
        def _(dve):
            vec = nc.vector
            link = Link(dve, step)
            full = [P, SEQS, D]
            link(vec.memset(eps[:], LN_EPS))
            link(vec.tensor_tensor(k.xc[:], k.xc[:], bc(k.rstd[:], full), ALU.mult))
            link(vec.tensor_reduce(mean[:, :, 0], k.xc[:], AX, ALU.add))
            link(vec.tensor_scalar(mean[:], mean[:], 1.0 / D, None, ALU.mult))
            link(vec.tensor_tensor(k.xc[:], k.xc[:], bc(mean[:], full), ALU.subtract))
            link(vec.tensor_tensor(sq[:], k.xc[:], k.xc[:], ALU.mult))
            vec.tensor_reduce(mean[:, :, 0], sq[:], AX, ALU.add).then_inc(summed, 1)
            dve.wait_ge(rooted, 1)
            link(vec.reciprocal(k.rstd[:], std[:]))


def stage_store(k):
    nc = k.nc
    with Scope(nc, "store") as s:
        stored = s.sem("stored")
        block = s.block()

        @block.sync
        def _(sp):
            sp.dma_start(k.out.rearrange("b n d -> n b d"), k.h[:]).then_inc(stored, 16)
            sp.wait_ge(stored, 16)


def build(nc, w, out):
    k = Core(nc, w, out)
    with ExitStack() as ctx:
        k.h = ctx.enter_context(nc.sbuf_tensor("h", [P, SEQS, D], F32))
        k.xc = ctx.enter_context(nc.sbuf_tensor("xc", [P, SEQS, D], F32))
        k.rstd = ctx.enter_context(nc.sbuf_tensor("rstd", [P, SEQS, 1], F32))
        k.ident = ctx.enter_context(nc.sbuf_tensor("ident", [P, P], F32))
        k.edge_score = ctx.enter_context(nc.sbuf_tensor("edge_score", [P, 1, 33], F32))
        k.edge_gate = ctx.enter_context(nc.sbuf_tensor("edge_gate", [P, 4, 1, 33], F32))
        k.last_edge = ctx.enter_context(nc.sbuf_tensor("last_edge", [P, N], F32))
        k.rows_landed = [ctx.enter_context(nc.semaphore(f"rows_landed{n}")) for n in range(3)]
        k.attr_fetched = ctx.enter_context(nc.semaphore("attr_fetched"))
        k.chunks_fetched = ctx.enter_context(nc.semaphore("chunks_fetched"))
        Scope.psum = ctx.enter_context(nc.psum_tensor("psum", [P, 8 * BANK], F32))
        stage_constants(k)
        for name, run, normed in TOWER:
            if normed:
                stage_center(k, name)
            run(k)
        stage_store(k)


TOWER = [("tok", stage_tokens, False), ("L0a", stage_l0_attn, False), ("L0f", stage_l0_ffn, False), ("L1a", stage_l1_attn, True), ("L1f", stage_l1_ffn, False), ("L2a", stage_l2_attn, False), ("L2f", stage_l2_ffn, False), ("L3a", stage_l3_attn, True), ("L3f", stage_l3_ffn, False)]


def kernel(**inputs):
    import numpy as _np
    import concourse.bacc as _bacc
    from concourse import mybir as _mybir
    from concourse.bass_utils import run_bass_kernel_spmd as _run

    nc = _bacc.Bacc("TRN2", target_bir_lowering=False, num_devices=1)
    arrays, w = {}, {}
    for name, value in inputs.items():
        a = _np.ascontiguousarray(value)
        arrays[f"in_{name}"] = a
        w[name] = nc.dram_tensor(f"in_{name}", a.shape, _mybir.dt.from_np(a.dtype), kind="ExternalInput").ap()
    out = nc.dram_tensor("out", (SEQS, N, D), F32, kind="ExternalOutput").ap()
    build(nc, w, out)
    r = _run(nc, [arrays], core_ids=[0])
    return r.results[0]["out"]
```
